# Optimizing a Trainium2 kernel written in Bass

```python
import numpy as np
import jax
import jax.numpy as jnp

def _softmax(x, axis=-1):
    return jax.nn.softmax(x, axis=axis)

def _gelu(x):
    return jax.nn.gelu(x, approximate=True)

def _silu(x):
    return jax.nn.silu(x)

def _sigmoid(x):
    return jax.nn.sigmoid(x)

def _layernorm(x, axis=-1, eps=1e-05):
    m = jnp.mean(x, axis=axis, keepdims=True)
    v = jnp.var(x, axis=axis, keepdims=True)
    return (x - m) / jnp.sqrt(v + eps)

def _scatter_add(tgt, idx, src, axis=0):
    return tgt.at[idx].add(src)

def _segment_sum(src, seg, n):
    return jax.ops.segment_sum(src, seg, n)
kernel_name = 'mk_sandwich_d4_jaxref_r8_a12822'

def setup_inputs(seed: int=0):
    np.random.seed(seed)
    _w = jnp.asarray

    def _L0_attn_setup():
        import jax, jax.numpy as jnp
        import numpy as np
        B, N, D = (4, 512, 128)
        H, DH = (16, 64)
        EPS = 1e-06
        key = jax.random.key(seed)
        ks = jax.random.split(key, 6)
        s = 1.0 / np.sqrt(D)
        return {'x': jax.random.normal(ks[0], (B, N, D), dtype=jnp.float32), 'Wq': jax.random.normal(ks[1], (D, H * DH), dtype=jnp.float32) * s, 'Wk': jax.random.normal(ks[2], (D, H * DH), dtype=jnp.float32) * s, 'Wv': jax.random.normal(ks[3], (D, H * DH), dtype=jnp.float32) * s, 'Wo': jax.random.normal(ks[4], (H * DH, D), dtype=jnp.float32) * s, 'bo': jnp.zeros((D,), dtype=jnp.float32)}
    _L0_attn_in = _L0_attn_setup()

    def _L0_ffn_setup():
        import jax, jax.numpy as jnp
        import numpy as np
        NUM_HEADS = 16
        TOP_K = 2
        key = jax.random.key(seed)
        ks = jax.random.split(key, 5)
        B, S, D, E = (4, 256, 128, 8)
        scale = 0.02
        return {'x': jax.random.normal(ks[0], (B, S, D), dtype=jnp.float32), 'W_qkv': jax.random.normal(ks[1], (D, 3 * D), dtype=jnp.float32) * scale, 'b_qkv': jnp.zeros((3 * D,), dtype=jnp.float32), 'W_gate': jax.random.normal(ks[2], (D, E), dtype=jnp.float32) * scale, 'b_gate': jnp.zeros((E,), dtype=jnp.float32), 'W_experts': jax.random.normal(ks[3], (E, D, D), dtype=jnp.float32) * scale, 'b_experts': jnp.zeros((E, D), dtype=jnp.float32)}
    _L0_ffn_in = _L0_ffn_setup()

    def _L1_attn_setup():
        import jax, jax.numpy as jnp
        import numpy as np
        D = 128
        key = jax.random.key(seed)
        k0, k1, k2, k3 = jax.random.split(key, 4)
        x = jax.random.normal(k0, (4, 256, D), dtype=jnp.float32)
        Wk = jax.random.normal(k1, (D, D), dtype=jnp.float32) * 0.02
        Wq = jax.random.normal(k2, (D, D), dtype=jnp.float32) * 0.02
        Wv = jax.random.normal(k3, (D, D), dtype=jnp.float32) * 0.02
        return {'x': x, 'Wk': Wk, 'Wq': Wq, 'Wv': Wv}
    _L1_attn_in = _L1_attn_setup()

    def _L1_ffn_setup():
        import jax, jax.numpy as jnp
        import numpy as np
        B, S, H = (2, 256, 128)
        E, I, K = (8, 512, 2)

        def _moe_forward(x, gate_w, wg, wu, wd):
            b, s, h = x.shape
            x_flat = x.reshape(-1, h)
            logits = x_flat @ gate_w.T
            top_v, top_i = jax.lax.top_k(logits, K)
            probs = jax.nn.softmax(top_v.astype(jnp.float32), axis=-1).astype(logits.dtype)
            one_hot = jax.nn.one_hot(top_i, E, dtype=probs.dtype)
            combine = jnp.einsum('tk,tke->et', probs, one_hot)

            def body(acc, ws):
                wge, wue, wde, we = ws
                hidden = jax.nn.silu(x_flat @ wge.T) * (x_flat @ wue.T)
                return (acc + we[:, None] * (hidden @ wde.T), None)
            out, _ = jax.lax.scan(body, jnp.zeros_like(x_flat), (wg, wu, wd, combine))
            return out.reshape(b, s, h)
        key = jax.random.key(seed)
        ks = jax.random.split(key, 5)
        scale_h = 1.0 / np.sqrt(H)
        scale_i = 1.0 / np.sqrt(I)
        x = jax.random.normal(ks[0], (B, S, H), dtype=jnp.float32)
        gate_w = jax.random.normal(ks[1], (E, H), dtype=jnp.float32) * scale_h
        wg = jax.random.normal(ks[2], (E, I, H), dtype=jnp.float32) * scale_h
        wu = jax.random.normal(ks[3], (E, I, H), dtype=jnp.float32) * scale_h
        wd = jax.random.normal(ks[4], (E, H, I), dtype=jnp.float32) * scale_i
        return {'x': x, 'gate_w': gate_w, 'wg': wg, 'wu': wu, 'wd': wd}
    _L1_ffn_in = _L1_ffn_setup()

    def _L2_attn_setup():
        import jax, jax.numpy as jnp
        import numpy as np
        D_MODEL = 128
        NUM_HEADS = 16
        D_HEAD = 64
        N_CTX = 256
        BATCH = 2
        SEQ = 256
        NEG = 10000000000.0
        key = jax.random.key(seed)
        kx, kk, kq, kv, ko = jax.random.split(key, 5)
        s = 1.0 / np.sqrt(D_MODEL)
        x = jax.random.normal(kx, (BATCH, SEQ, D_MODEL), dtype=jnp.float32)
        W_K = jax.random.normal(kk, (NUM_HEADS, D_HEAD, D_MODEL), dtype=jnp.float32) * s
        W_Q = jax.random.normal(kq, (NUM_HEADS, D_HEAD, D_MODEL), dtype=jnp.float32) * s
        W_V = jax.random.normal(kv, (NUM_HEADS, D_HEAD, D_MODEL), dtype=jnp.float32) * s
        W_O = jax.random.normal(ko, (D_MODEL, D_HEAD * NUM_HEADS), dtype=jnp.float32) * s
        return {'x': x, 'W_K': W_K, 'W_Q': W_Q, 'W_V': W_V, 'W_O': W_O}
    _L2_attn_in = _L2_attn_setup()

    def _L2_ffn_setup():
        import jax, jax.numpy as jnp
        import numpy as np
        DIM = 128
        DEPTH = 2
        HEADS = 8
        DIM_HEAD = 64
        WINDOW = 64
        INNER = HEADS * DIM_HEAD
        HID = int(DIM * 4 * 2 / 3)
        B, N = (2, 1024)
        QK_SCALE = 8.0

        def shift_token(t):
            t1, t2 = jnp.split(t, 2, axis=-1)
            t2 = jnp.pad(t2, ((0, 0), (1, 0), (0, 0)))[:, :-1]
            return jnp.concatenate([t1, t2], axis=-1)

        def l2norm(t):
            return t / jnp.clip(jnp.linalg.norm(t, axis=-1, keepdims=True), 1e-12)

        def rotate_half(x):
            x1, x2 = jnp.split(x, 2, axis=-1)
            return jnp.concatenate([-x2, x1], axis=-1)

        def rotary_xpos(q, k):
            n = q.shape[-2]
            half_idx = jnp.arange(0, DIM_HEAD, 2, dtype=jnp.float32)
            inv_freq = 1.0 / 10000.0 ** (half_idx / DIM_HEAD)
            t = jnp.arange(n, dtype=jnp.float32)
            freqs = t[:, None] * inv_freq[None, :]
            freqs = jnp.concatenate([freqs, freqs], axis=-1)
            base = (half_idx + 0.4 * DIM_HEAD) / (1.4 * DIM_HEAD)
            power = (t - n // 2) / float(WINDOW // 2)
            scale = base[None, :] ** power[:, None]
            scale = jnp.concatenate([scale, scale], axis=-1)
            cos, sin = (jnp.cos(freqs), jnp.sin(freqs))
            q = q * cos * scale + rotate_half(q) * sin * scale
            k = k * cos / scale + rotate_half(k) * sin / scale
            return (q, k)

        def local_attention(q, k, v):
            b, h, n, d = q.shape
            w = n // WINDOW
            bq = q.reshape(b, h, w, WINDOW, d) * QK_SCALE
            bk = k.reshape(b, h, w, WINDOW, d)
            bv = v.reshape(b, h, w, WINDOW, d)

            def look_around(t):
                p = jnp.pad(t, ((0, 0), (0, 0), (1, 0), (0, 0), (0, 0)))
                return jnp.concatenate([p[:, :, :w], p[:, :, 1:]], axis=3)
            bk, bv = (look_around(bk), look_around(bv))
            bt = jnp.arange(n).reshape(w, WINDOW)
            btp = jnp.pad(bt, ((1, 0), (0, 0)), constant_values=-1)
            btk = jnp.concatenate([btp[:w], btp[1:]], axis=1)
            sim = jnp.einsum('bhwid,bhwjd->bhwij', bq, bk)
            i = bt[:, :, None]
            j = btk[:, None, :]
            mask = (i < j) | (i > j + WINDOW) | (j == -1)
            sim = jnp.where(mask, -jnp.finfo(sim.dtype).max, sim)
            attn = jax.nn.softmax(sim, axis=-1)
            out = jnp.einsum('bhwij,bhwjd->bhwid', attn, bv)
            return out.reshape(b, h, n, d)

        def _layer(x, wqkv, qs, ksc, wo, lg, lb, w1, b1, w2, b2):
            b, n, _ = x.shape
            h = shift_token(x)
            qkv = h @ wqkv
            q, k, v = jnp.split(qkv, 3, axis=-1)
            to_heads = lambda t: t.reshape(b, n, HEADS, DIM_HEAD).transpose(0, 2, 1, 3)
            q, k, v = (to_heads(q), to_heads(k), to_heads(v))
            q = l2norm(q) * qs
            k = l2norm(k) * ksc
            q, k = rotary_xpos(q, k)
            o = local_attention(q, k, v)
            o = o.transpose(0, 2, 1, 3).reshape(b, n, INNER)
            x = x + o @ wo
            h = shift_token(x)
            mu = h.mean(-1, keepdims=True)
            var = h.var(-1, keepdims=True)
            h = (h - mu) / jnp.sqrt(var + 1e-05) * lg + lb
            h = h @ w1 + b1
            a, g = jnp.split(h, 2, axis=-1)
            h = a * jax.nn.gelu(g, approximate=False)
            x = x + h @ w2 + b2
            return x
        key = jax.random.key(seed)
        ks = jax.random.split(key, 6)
        return {'x': jax.random.normal(ks[0], (B, N, DIM), jnp.float32), 'wqkv': jax.random.normal(ks[1], (DEPTH, DIM, 3 * INNER), jnp.float32) * 0.02, 'q_scale': jnp.ones((DEPTH, DIM_HEAD), jnp.float32), 'k_scale': jnp.ones((DEPTH, DIM_HEAD), jnp.float32), 'wo': jax.random.normal(ks[2], (DEPTH, INNER, DIM), jnp.float32) * 0.02, 'ln_g': jnp.ones((DEPTH, DIM), jnp.float32), 'ln_b': jnp.zeros((DEPTH, DIM), jnp.float32), 'w1': jax.random.normal(ks[3], (DEPTH, DIM, 2 * HID), jnp.float32) * 0.02, 'b1': jnp.zeros((DEPTH, 2 * HID), jnp.float32), 'w2': jax.random.normal(ks[4], (DEPTH, HID, DIM), jnp.float32) * 0.02, 'b2': jnp.zeros((DEPTH, DIM), jnp.float32)}
    _L2_ffn_in = _L2_ffn_setup()

    def _L3_attn_setup():
        import jax, jax.numpy as jnp
        import numpy as np
        from jax import lax
        EPS = 1e-05

        def layer_norm(x, w, b):
            mu = x.mean(-1, keepdims=True)
            var = ((x - mu) ** 2).mean(-1, keepdims=True)
            return (x - mu) * lax.rsqrt(var + EPS) * w + b

        def causal_dw_conv(x, w, b):
            B, L, D = x.shape
            K = w.shape[1]
            xt = jnp.pad(x.transpose(0, 2, 1), ((0, 0), (0, 0), (K - 1, 0)))
            y = lax.conv_general_dilated(xt, w[:, None, :], (1,), 'VALID', dimension_numbers=('NCH', 'OIH', 'NCH'), feature_group_count=D)
            return (y + b[:, None]).transpose(0, 2, 1)

        def mamba_block(x, ln_w, ln_b, W_in, b_in, conv_w, conv_b, W_xproj, W_dt, b_dt, A_log, Dp, W_out, b_out):
            res = x
            x = layer_norm(x, ln_w, ln_b)
            xz = x @ W_in + b_in
            Di = xz.shape[-1] // 2
            xp, z = (xz[..., :Di], xz[..., Di:])
            xp = jax.nn.silu(causal_dw_conv(xp, conv_w, conv_b))
            dbl = xp @ W_xproj
            N = A_log.shape[-1]
            R = dbl.shape[-1] - 2 * N
            dt, Bm, Cm = (dbl[..., :R], dbl[..., R:R + N], dbl[..., R + N:])
            delta = jax.nn.softplus(dt @ W_dt + b_dt)
            A = -jnp.exp(A_log)
            dA = jnp.exp(delta[..., None] * A)
            dBx = delta[..., None] * Bm[:, :, None, :] * xp[..., None]

            def step(h, inp):
                dAt, dBxt, ct = inp
                h = dAt * h + dBxt
                return (h, jnp.einsum('bdn,bn->bd', h, ct))
            h0 = jnp.zeros((x.shape[0], Di, N), x.dtype)
            _, ys = lax.scan(step, h0, (dA.transpose(1, 0, 2, 3), dBx.transpose(1, 0, 2, 3), Cm.transpose(1, 0, 2)))
            y = ys.transpose(1, 0, 2) + xp * Dp
            y = y * jax.nn.silu(z)
            return res + y @ W_out + b_out
        B, L, Dm = (2, 128, 128)
        Di, N, R, K = (256, 16, 64, 4)
        key = jax.random.key(seed)
        ks = jax.random.split(key, 12)
        s_in = 1.0 / np.sqrt(Dm)
        s_di = 1.0 / np.sqrt(Di)
        A = jnp.broadcast_to(jnp.arange(1, N + 1, dtype=jnp.float32), (Di, N))
        return {'x': jax.random.normal(ks[0], (B, L, Dm), jnp.float32), 'ln_w': jnp.ones((2, Dm), jnp.float32), 'ln_b': jnp.zeros((2, Dm), jnp.float32), 'W_in': jax.random.normal(ks[1], (2, Dm, 2 * Di), jnp.float32) * s_in, 'b_in': jnp.zeros((2, 2 * Di), jnp.float32), 'conv_w': jax.random.normal(ks[2], (2, Di, K), jnp.float32) * 0.5, 'conv_b': jnp.zeros((2, Di), jnp.float32), 'W_xproj': jax.random.normal(ks[3], (2, Di, R + 2 * N), jnp.float32) * s_di, 'W_dt': jax.random.normal(ks[4], (2, R, Di), jnp.float32) * 0.02, 'b_dt': jnp.full((2, Di), -4.6, jnp.float32) + 0.1 * jax.random.normal(ks[5], (2, Di), jnp.float32), 'A_log': jnp.log(jnp.stack([A, A])), 'D': jnp.ones((2, Di), jnp.float32), 'W_out': jax.random.normal(ks[6], (2, Di, Dm), jnp.float32) * s_di, 'b_out': jnp.zeros((2, Dm), jnp.float32), 'Wg': jax.random.normal(ks[7], (2 * Dm, Dm), jnp.float32) / np.sqrt(2 * Dm), 'bg': jnp.zeros((Dm,), jnp.float32), 'Wv': jax.random.normal(ks[8], (2 * Dm, Dm), jnp.float32) / np.sqrt(2 * Dm), 'bv': jnp.zeros((Dm,), jnp.float32)}
    _L3_attn_in = _L3_attn_setup()

    def _L3_ffn_setup():
        import jax, jax.numpy as jnp
        import numpy as np
        E = 32
        H = 128
        I = 64
        G = 8
        TKG = 4
        TOPK = 8
        NSH = 2
        SCALE = 2.5
        key = jax.random.key(seed)
        ks = jax.random.split(key, 10)
        s = 0.02
        return {'hidden_states': jax.random.normal(ks[0], (2, 128, H), jnp.float32), 'gate_w': jax.random.normal(ks[1], (E, H), jnp.float32) * s, 'gate_bias': jax.random.normal(ks[2], (E,), jnp.float32) * s, 'w_gate': jax.random.normal(ks[3], (E, I, H), jnp.float32) * s, 'w_up': jax.random.normal(ks[4], (E, I, H), jnp.float32) * s, 'w_down': jax.random.normal(ks[5], (E, H, I), jnp.float32) * s, 'sh_gate': jax.random.normal(ks[6], (I * NSH, H), jnp.float32) * s, 'sh_up': jax.random.normal(ks[7], (I * NSH, H), jnp.float32) * s, 'sh_down': jax.random.normal(ks[8], (H, I * NSH), jnp.float32) * s}
    _L3_ffn_in = _L3_ffn_setup()
    _d = {'L0_attn_x': _L0_attn_in['x'], 'L0_attn_Wq': _L0_attn_in['Wq'], 'L0_attn_Wk': _L0_attn_in['Wk'], 'L0_attn_Wv': _L0_attn_in['Wv'], 'L0_attn_Wo': _L0_attn_in['Wo'], 'L0_attn_bo': _L0_attn_in['bo'], 'L0_ffn_W_qkv': _L0_ffn_in['W_qkv'], 'L0_ffn_b_qkv': _L0_ffn_in['b_qkv'], 'L0_ffn_W_gate': _L0_ffn_in['W_gate'], 'L0_ffn_b_gate': _L0_ffn_in['b_gate'], 'L0_ffn_W_experts': _L0_ffn_in['W_experts'], 'L0_ffn_b_experts': _L0_ffn_in['b_experts'], 'L1_attn_Wk': _L1_attn_in['Wk'], 'L1_attn_Wq': _L1_attn_in['Wq'], 'L1_attn_Wv': _L1_attn_in['Wv'], 'L1_ffn_gate_w': _L1_ffn_in['gate_w'], 'L1_ffn_wg': _L1_ffn_in['wg'], 'L1_ffn_wu': _L1_ffn_in['wu'], 'L1_ffn_wd': _L1_ffn_in['wd'], 'L2_attn_W_K': _L2_attn_in['W_K'], 'L2_attn_W_Q': _L2_attn_in['W_Q'], 'L2_attn_W_V': _L2_attn_in['W_V'], 'L2_attn_W_O': _L2_attn_in['W_O'], 'L2_ffn_wqkv': _L2_ffn_in['wqkv'], 'L2_ffn_q_scale': _L2_ffn_in['q_scale'], 'L2_ffn_k_scale': _L2_ffn_in['k_scale'], 'L2_ffn_wo': _L2_ffn_in['wo'], 'L2_ffn_ln_g': _L2_ffn_in['ln_g'], 'L2_ffn_ln_b': _L2_ffn_in['ln_b'], 'L2_ffn_w1': _L2_ffn_in['w1'], 'L2_ffn_b1': _L2_ffn_in['b1'], 'L2_ffn_w2': _L2_ffn_in['w2'], 'L2_ffn_b2': _L2_ffn_in['b2'], 'L3_attn_ln_w': _L3_attn_in['ln_w'], 'L3_attn_ln_b': _L3_attn_in['ln_b'], 'L3_attn_W_in': _L3_attn_in['W_in'], 'L3_attn_b_in': _L3_attn_in['b_in'], 'L3_attn_conv_w': _L3_attn_in['conv_w'], 'L3_attn_conv_b': _L3_attn_in['conv_b'], 'L3_attn_W_xproj': _L3_attn_in['W_xproj'], 'L3_attn_W_dt': _L3_attn_in['W_dt'], 'L3_attn_b_dt': _L3_attn_in['b_dt'], 'L3_attn_A_log': _L3_attn_in['A_log'], 'L3_attn_D': _L3_attn_in['D'], 'L3_attn_W_out': _L3_attn_in['W_out'], 'L3_attn_b_out': _L3_attn_in['b_out'], 'L3_attn_Wg': _L3_attn_in['Wg'], 'L3_attn_bg': _L3_attn_in['bg'], 'L3_attn_Wv': _L3_attn_in['Wv'], 'L3_attn_bv': _L3_attn_in['bv'], 'L3_ffn_gate_w': _L3_ffn_in['gate_w'], 'L3_ffn_gate_bias': _L3_ffn_in['gate_bias'], 'L3_ffn_w_gate': _L3_ffn_in['w_gate'], 'L3_ffn_w_up': _L3_ffn_in['w_up'], 'L3_ffn_w_down': _L3_ffn_in['w_down'], 'L3_ffn_sh_gate': _L3_ffn_in['sh_gate'], 'L3_ffn_sh_up': _L3_ffn_in['sh_up'], 'L3_ffn_sh_down': _L3_ffn_in['sh_down']}
    _x0 = _d['L0_attn_x']
    _d['L0_attn_x'] = jax.random.normal(jax.random.fold_in(jax.random.key(seed), 1), (2, 1024, 128), dtype=_x0.dtype)
    del _x0
    return _d

def reference(L0_attn_x, L0_attn_Wq, L0_attn_Wk, L0_attn_Wv, L0_attn_Wo, L0_attn_bo, L0_ffn_W_qkv, L0_ffn_b_qkv, L0_ffn_W_gate, L0_ffn_b_gate, L0_ffn_W_experts, L0_ffn_b_experts, L1_attn_Wk, L1_attn_Wq, L1_attn_Wv, L1_ffn_gate_w, L1_ffn_wg, L1_ffn_wu, L1_ffn_wd, L2_attn_W_K, L2_attn_W_Q, L2_attn_W_V, L2_attn_W_O, L2_ffn_wqkv, L2_ffn_q_scale, L2_ffn_k_scale, L2_ffn_wo, L2_ffn_ln_g, L2_ffn_ln_b, L2_ffn_w1, L2_ffn_b1, L2_ffn_w2, L2_ffn_b2, L3_attn_ln_w, L3_attn_ln_b, L3_attn_W_in, L3_attn_b_in, L3_attn_conv_w, L3_attn_conv_b, L3_attn_W_xproj, L3_attn_W_dt, L3_attn_b_dt, L3_attn_A_log, L3_attn_D, L3_attn_W_out, L3_attn_b_out, L3_attn_Wg, L3_attn_bg, L3_attn_Wv, L3_attn_bv, L3_ffn_gate_w, L3_ffn_gate_bias, L3_ffn_w_gate, L3_ffn_w_up, L3_ffn_w_down, L3_ffn_sh_gate, L3_ffn_sh_up, L3_ffn_sh_down):

    def _L0_attn_ref(x, Wq, Wk, Wv, Wo, bo):
        import jax, jax.numpy as jnp
        import numpy as np
        B, N, D = (4, 512, 128)
        H, DH = (16, 64)
        EPS = 1e-06

        def split_heads(t):
            b, n, _ = t.shape
            return t.reshape(b, n, H, DH).transpose(0, 2, 1, 3)
        q = split_heads(x @ Wq)
        k = split_heads(x @ Wk)
        v = split_heads(x @ Wv)
        q = jax.nn.elu(q) + 1.0
        k = jax.nn.elu(k) + 1.0
        k_sum = k.sum(axis=2)
        z = jnp.einsum('bhnd,bhd->bhn', q, k_sum)[..., None] + EPS
        kv = jnp.einsum('bhnd,bhne->bhde', k, v)
        out = jnp.einsum('bhnd,bhde->bhne', q, kv) / z
        out = out.transpose(0, 2, 1, 3).reshape(x.shape[0], x.shape[1], H * DH)
        return out @ Wo + bo

    def _L0_ffn_ref(x, W_qkv, b_qkv, W_gate, b_gate, W_experts, b_experts):
        import jax, jax.numpy as jnp
        import numpy as np
        NUM_HEADS = 16
        TOP_K = 2
        B, S, D = x.shape
        H = NUM_HEADS
        hd = D // H
        E = W_gate.shape[-1]
        qkv = (x @ W_qkv + b_qkv).reshape(B, S, 3, H, hd)
        q, k, v = (qkv[:, :, 0], qkv[:, :, 1], qkv[:, :, 2])
        attn = jnp.einsum('bqhd,bkhd->bhqk', q, k) / jnp.sqrt(jnp.asarray(hd, x.dtype))
        attn = jax.nn.softmax(attn, axis=-1)
        attn_out = jnp.einsum('bhqk,bkhd->bqhd', attn, v).reshape(B, S, D)
        gate = jax.nn.softmax(x @ W_gate + b_gate, axis=-1)
        top_g, top_i = jax.lax.top_k(gate, TOP_K)
        combine = jnp.sum(jax.nn.one_hot(top_i, E, dtype=x.dtype) * top_g[..., None], axis=2)
        expert_out = jnp.einsum('bsd,edf->bsef', x, W_experts) + b_experts
        moe_out = jnp.einsum('bsef,bse->bsf', expert_out, combine)
        return attn_out + moe_out

    def _L1_attn_ref(x, Wk, Wq, Wv):
        import jax, jax.numpy as jnp
        import numpy as np
        D = 128
        K = x @ Wk
        Q = x @ Wq
        V = x @ Wv
        N = Q.shape[-2]
        d = K.shape[-1]
        scores = jnp.einsum('bnd,bmd->bnm', Q, K) / jnp.sqrt(jnp.float32(d))
        causal = jnp.tril(jnp.ones((N, N), dtype=bool))
        scores = jnp.where(causal[None, :, :], scores, -jnp.inf)
        attn = jax.nn.softmax(scores, axis=-1)
        return attn @ V

    def _L1_ffn_ref(x, gate_w, wg, wu, wd):
        import jax, jax.numpy as jnp
        import numpy as np
        B, S, H = (2, 256, 128)
        E, I, K = (8, 512, 2)

        def _moe_forward(x, gate_w, wg, wu, wd):
            b, s, h = x.shape
            x_flat = x.reshape(-1, h)
            logits = x_flat @ gate_w.T
            top_v, top_i = jax.lax.top_k(logits, K)
            probs = jax.nn.softmax(top_v.astype(jnp.float32), axis=-1).astype(logits.dtype)
            one_hot = jax.nn.one_hot(top_i, E, dtype=probs.dtype)
            combine = jnp.einsum('tk,tke->et', probs, one_hot)

            def body(acc, ws):
                wge, wue, wde, we = ws
                hidden = jax.nn.silu(x_flat @ wge.T) * (x_flat @ wue.T)
                return (acc + we[:, None] * (hidden @ wde.T), None)
            out, _ = jax.lax.scan(body, jnp.zeros_like(x_flat), (wg, wu, wd, combine))
            return out.reshape(b, s, h)
        return _moe_forward(x, gate_w, wg, wu, wd)

    def _L2_attn_ref(x, W_K, W_Q, W_V, W_O):
        import jax, jax.numpy as jnp
        import numpy as np
        D_MODEL = 128
        NUM_HEADS = 16
        D_HEAD = 64
        N_CTX = 256
        BATCH = 2
        SEQ = 256
        NEG = 10000000000.0
        B, S, D = x.shape
        k = jnp.einsum('ihd,bpd->biph', W_K, x)
        q = jnp.einsum('ihd,bpd->biph', W_Q, x)
        v = jnp.einsum('ihd,bpd->biph', W_V, x)
        scores = jnp.einsum('biph,biqh->biqp', k, q)
        mask = jnp.tril(jnp.ones((S, S), dtype=scores.dtype))
        masked = scores * mask - NEG * (1.0 - mask)
        attn = jax.nn.softmax(masked / np.sqrt(D_HEAD), axis=-1)
        z = jnp.einsum('biph,biqp->biqh', v, attn)
        z_flat = jnp.transpose(z, (0, 2, 1, 3)).reshape(B, S, -1)
        out = jnp.einsum('df,bqf->bqd', W_O, z_flat)
        return out

    def _L2_ffn_ref(x, wqkv, q_scale, k_scale, wo, ln_g, ln_b, w1, b1, w2, b2):
        import jax, jax.numpy as jnp
        import numpy as np
        DIM = 128
        DEPTH = 2
        HEADS = 8
        DIM_HEAD = 64
        WINDOW = 64
        INNER = HEADS * DIM_HEAD
        HID = int(DIM * 4 * 2 / 3)
        B, N = (2, 1024)
        QK_SCALE = 8.0

        def shift_token(t):
            t1, t2 = jnp.split(t, 2, axis=-1)
            t2 = jnp.pad(t2, ((0, 0), (1, 0), (0, 0)))[:, :-1]
            return jnp.concatenate([t1, t2], axis=-1)

        def l2norm(t):
            return t / jnp.clip(jnp.linalg.norm(t, axis=-1, keepdims=True), 1e-12)

        def rotate_half(x):
            x1, x2 = jnp.split(x, 2, axis=-1)
            return jnp.concatenate([-x2, x1], axis=-1)

        def rotary_xpos(q, k):
            n = q.shape[-2]
            half_idx = jnp.arange(0, DIM_HEAD, 2, dtype=jnp.float32)
            inv_freq = 1.0 / 10000.0 ** (half_idx / DIM_HEAD)
            t = jnp.arange(n, dtype=jnp.float32)
            freqs = t[:, None] * inv_freq[None, :]
            freqs = jnp.concatenate([freqs, freqs], axis=-1)
            base = (half_idx + 0.4 * DIM_HEAD) / (1.4 * DIM_HEAD)
            power = (t - n // 2) / float(WINDOW // 2)
            scale = base[None, :] ** power[:, None]
            scale = jnp.concatenate([scale, scale], axis=-1)
            cos, sin = (jnp.cos(freqs), jnp.sin(freqs))
            q = q * cos * scale + rotate_half(q) * sin * scale
            k = k * cos / scale + rotate_half(k) * sin / scale
            return (q, k)

        def local_attention(q, k, v):
            b, h, n, d = q.shape
            w = n // WINDOW
            bq = q.reshape(b, h, w, WINDOW, d) * QK_SCALE
            bk = k.reshape(b, h, w, WINDOW, d)
            bv = v.reshape(b, h, w, WINDOW, d)

            def look_around(t):
                p = jnp.pad(t, ((0, 0), (0, 0), (1, 0), (0, 0), (0, 0)))
                return jnp.concatenate([p[:, :, :w], p[:, :, 1:]], axis=3)
            bk, bv = (look_around(bk), look_around(bv))
            bt = jnp.arange(n).reshape(w, WINDOW)
            btp = jnp.pad(bt, ((1, 0), (0, 0)), constant_values=-1)
            btk = jnp.concatenate([btp[:w], btp[1:]], axis=1)
            sim = jnp.einsum('bhwid,bhwjd->bhwij', bq, bk)
            i = bt[:, :, None]
            j = btk[:, None, :]
            mask = (i < j) | (i > j + WINDOW) | (j == -1)
            sim = jnp.where(mask, -jnp.finfo(sim.dtype).max, sim)
            attn = jax.nn.softmax(sim, axis=-1)
            out = jnp.einsum('bhwij,bhwjd->bhwid', attn, bv)
            return out.reshape(b, h, n, d)

        def _layer(x, wqkv, qs, ksc, wo, lg, lb, w1, b1, w2, b2):
            b, n, _ = x.shape
            h = shift_token(x)
            qkv = h @ wqkv
            q, k, v = jnp.split(qkv, 3, axis=-1)
            to_heads = lambda t: t.reshape(b, n, HEADS, DIM_HEAD).transpose(0, 2, 1, 3)
            q, k, v = (to_heads(q), to_heads(k), to_heads(v))
            q = l2norm(q) * qs
            k = l2norm(k) * ksc
            q, k = rotary_xpos(q, k)
            o = local_attention(q, k, v)
            o = o.transpose(0, 2, 1, 3).reshape(b, n, INNER)
            x = x + o @ wo
            h = shift_token(x)
            mu = h.mean(-1, keepdims=True)
            var = h.var(-1, keepdims=True)
            h = (h - mu) / jnp.sqrt(var + 1e-05) * lg + lb
            h = h @ w1 + b1
            a, g = jnp.split(h, 2, axis=-1)
            h = a * jax.nn.gelu(g, approximate=False)
            x = x + h @ w2 + b2
            return x
        for l in range(DEPTH):
            x = _layer(x, wqkv[l], q_scale[l], k_scale[l], wo[l], ln_g[l], ln_b[l], w1[l], b1[l], w2[l], b2[l])
        return x

    def _L3_attn_ref(x, ln_w, ln_b, W_in, b_in, conv_w, conv_b, W_xproj, W_dt, b_dt, A_log, D, W_out, b_out, Wg, bg, Wv, bv):
        import jax, jax.numpy as jnp
        import numpy as np
        from jax import lax
        EPS = 1e-05

        def layer_norm(x, w, b):
            mu = x.mean(-1, keepdims=True)
            var = ((x - mu) ** 2).mean(-1, keepdims=True)
            return (x - mu) * lax.rsqrt(var + EPS) * w + b

        def causal_dw_conv(x, w, b):
            B, L, D = x.shape
            K = w.shape[1]
            xt = jnp.pad(x.transpose(0, 2, 1), ((0, 0), (0, 0), (K - 1, 0)))
            y = lax.conv_general_dilated(xt, w[:, None, :], (1,), 'VALID', dimension_numbers=('NCH', 'OIH', 'NCH'), feature_group_count=D)
            return (y + b[:, None]).transpose(0, 2, 1)

        def mamba_block(x, ln_w, ln_b, W_in, b_in, conv_w, conv_b, W_xproj, W_dt, b_dt, A_log, Dp, W_out, b_out):
            res = x
            x = layer_norm(x, ln_w, ln_b)
            xz = x @ W_in + b_in
            Di = xz.shape[-1] // 2
            xp, z = (xz[..., :Di], xz[..., Di:])
            xp = jax.nn.silu(causal_dw_conv(xp, conv_w, conv_b))
            dbl = xp @ W_xproj
            N = A_log.shape[-1]
            R = dbl.shape[-1] - 2 * N
            dt, Bm, Cm = (dbl[..., :R], dbl[..., R:R + N], dbl[..., R + N:])
            delta = jax.nn.softplus(dt @ W_dt + b_dt)
            A = -jnp.exp(A_log)
            dA = jnp.exp(delta[..., None] * A)
            dBx = delta[..., None] * Bm[:, :, None, :] * xp[..., None]

            def step(h, inp):
                dAt, dBxt, ct = inp
                h = dAt * h + dBxt
                return (h, jnp.einsum('bdn,bn->bd', h, ct))
            h0 = jnp.zeros((x.shape[0], Di, N), x.dtype)
            _, ys = lax.scan(step, h0, (dA.transpose(1, 0, 2, 3), dBx.transpose(1, 0, 2, 3), Cm.transpose(1, 0, 2)))
            y = ys.transpose(1, 0, 2) + xp * Dp
            y = y * jax.nn.silu(z)
            return res + y @ W_out + b_out
        fwd = mamba_block(x, ln_w[0], ln_b[0], W_in[0], b_in[0], conv_w[0], conv_b[0], W_xproj[0], W_dt[0], b_dt[0], A_log[0], D[0], W_out[0], b_out[0])
        bwd = mamba_block(x[:, ::-1], ln_w[1], ln_b[1], W_in[1], b_in[1], conv_w[1], conv_b[1], W_xproj[1], W_dt[1], b_dt[1], A_log[1], D[1], W_out[1], b_out[1])
        bwd = bwd[:, ::-1]
        comb = jnp.concatenate([fwd, bwd], -1)
        gate = jax.nn.sigmoid(comb @ Wg + bg)
        value = comb @ Wv + bv
        return (gate * value + (1.0 - gate) * fwd + (1.0 - gate) * bwd) / 2.0

    def _L3_ffn_ref(hidden_states, gate_w, gate_bias, w_gate, w_up, w_down, sh_gate, sh_up, sh_down):
        import jax, jax.numpy as jnp
        import numpy as np
        E = 32
        H = 128
        I = 64
        G = 8
        TKG = 4
        TOPK = 8
        NSH = 2
        SCALE = 2.5
        B, S, Hd = hidden_states.shape
        h = hidden_states.reshape(-1, Hd)
        logits = h.astype(jnp.float32) @ gate_w.T
        scores = jax.nn.sigmoid(logits)
        sc = scores + gate_bias
        grp = sc.reshape(-1, G, E // G)
        group_scores = jax.lax.top_k(grp, 2)[0].sum(-1)
        gidx = jax.lax.top_k(group_scores, TKG)[1]
        gmask = jnp.sum(jax.nn.one_hot(gidx, G, dtype=sc.dtype), axis=1)
        smask = jnp.repeat(gmask, E // G, axis=1)
        masked = jnp.where(smask > 0, sc, jnp.zeros_like(sc))
        tki = jax.lax.top_k(masked, TOPK)[1]
        tkw = jnp.take_along_axis(scores, tki, axis=1)
        tkw = tkw / (tkw.sum(-1, keepdims=True) + 1e-20)
        tkw = tkw * SCALE
        combine = (jax.nn.one_hot(tki, E, dtype=tkw.dtype) * tkw[..., None]).sum(1)
        g = jax.nn.silu(jnp.einsum('th,eih->tei', h, w_gate))
        u = jnp.einsum('th,eih->tei', h, w_up)
        routed = jnp.einsum('tei,ehi->th', g * u * combine[:, :, None], w_down)
        sg = jax.nn.silu(h @ sh_gate.T)
        shared = sg * (h @ sh_up.T) @ sh_down.T
        return (routed + shared).reshape(B, S, Hd)
    x = L0_attn_x
    x = x + _layernorm(_L0_attn_ref(_layernorm(x, axis=-1), L0_attn_Wq, L0_attn_Wk, L0_attn_Wv, L0_attn_Wo, L0_attn_bo), axis=-1)
    x = x + _layernorm(_L0_ffn_ref(_layernorm(x, axis=-1), L0_ffn_W_qkv, L0_ffn_b_qkv, L0_ffn_W_gate, L0_ffn_b_gate, L0_ffn_W_experts, L0_ffn_b_experts), axis=-1)
    x = x + _layernorm(_L1_attn_ref(_layernorm(x, axis=-1), L1_attn_Wk, L1_attn_Wq, L1_attn_Wv), axis=-1)
    x = x + _layernorm(_L1_ffn_ref(_layernorm(x, axis=-1), L1_ffn_gate_w, L1_ffn_wg, L1_ffn_wu, L1_ffn_wd), axis=-1)
    x = x + _layernorm(_L2_attn_ref(_layernorm(x, axis=-1), L2_attn_W_K, L2_attn_W_Q, L2_attn_W_V, L2_attn_W_O), axis=-1)
    x = x + _layernorm(_L2_ffn_ref(_layernorm(x, axis=-1), L2_ffn_wqkv, L2_ffn_q_scale, L2_ffn_k_scale, L2_ffn_wo, L2_ffn_ln_g, L2_ffn_ln_b, L2_ffn_w1, L2_ffn_b1, L2_ffn_w2, L2_ffn_b2), axis=-1)
    x = x + _layernorm(_L3_attn_ref(_layernorm(x, axis=-1), L3_attn_ln_w, L3_attn_ln_b, L3_attn_W_in, L3_attn_b_in, L3_attn_conv_w, L3_attn_conv_b, L3_attn_W_xproj, L3_attn_W_dt, L3_attn_b_dt, L3_attn_A_log, L3_attn_D, L3_attn_W_out, L3_attn_b_out, L3_attn_Wg, L3_attn_bg, L3_attn_Wv, L3_attn_bv), axis=-1)
    x = x + _layernorm(_L3_ffn_ref(_layernorm(x, axis=-1), L3_ffn_gate_w, L3_ffn_gate_bias, L3_ffn_w_gate, L3_ffn_w_up, L3_ffn_w_down, L3_ffn_sh_gate, L3_ffn_sh_up, L3_ffn_sh_down), axis=-1)
    return x

_drawn_inputs = setup_inputs


def setup_inputs(seed=0):
    import zlib

    import numpy as np

    out = dict(_drawn_inputs(seed))
    spreads = {'L0_attn_bo': (0.0, 0.1),
     'L0_ffn_b_qkv': (0.0, 0.1),
     'L0_ffn_b_gate': (0.0, 0.1),
     'L0_ffn_b_experts': (0.0, 0.1),
     'L2_ffn_q_scale': (1.0, 0.6),
     'L2_ffn_k_scale': (1.0, 0.6),
     'L2_ffn_ln_g': (1.0, 0.6),
     'L2_ffn_ln_b': (0.0, 0.8),
     'L2_ffn_b1': (0.0, 0.8),
     'L2_ffn_b2': (0.0, 0.559),
     'L3_attn_ln_w': (1.0, 0.2),
     'L3_attn_ln_b': (0.0, 0.1),
     'L3_attn_b_in': (0.0, 0.1),
     'L3_attn_conv_b': (0.0, 0.367),
     'L3_attn_D': (1.0, 0.553),
     'L3_attn_b_out': (0.0, 0.327),
     'L3_attn_bg': (0.0, 0.49),
     'L3_attn_bv': (0.0, 0.48)}
    factors = {'L1_attn_Wk': 5.341,
     'L1_attn_Wq': 5.562,
     'L2_ffn_w1': 5.434,
     'L2_ffn_w2': 5.157,
     'L3_attn_W_dt': 64.0,
     'L3_attn_b_dt': 64.0}
    for name, (base, spread) in spreads.items():
        noise = np.random.default_rng([zlib.crc32(name.encode()), seed]).standard_normal(out[name].shape)
        drawn = base * np.exp(spread * noise) if base else spread * noise
        out[name] = jnp.asarray(drawn.astype(out[name].dtype))
    for name, factor in factors.items():
        out[name] = (out[name] * factor).astype(out[name].dtype)
    return out
```

```python
from contextlib import ExitStack

import numpy as np

import concourse.bass as bass
from concourse import mybir

F32 = mybir.dt.float32
BF16 = mybir.dt.bfloat16
U32 = mybir.dt.uint32
ALU = mybir.AluOpType
ACT = mybir.ActivationFunctionType
AX = mybir.AxisListType.X

P = 128
BATCH, SEQ = 2, 1024
TOKENS = BATCH * SEQ
NT = TOKENS // P
TPB = SEQ // P
BANK = 512
CPB = SEQ // BANK
LN_EPS = 1e-5
NEG = -1.0e30


class Phase:

    def __init__(self, nc, name):
        self.nc, self.name, self.ctx, self.sems = nc, name, ExitStack(), []

    def __enter__(self):
        self.ctx.__enter__()
        return self

    def __exit__(self, *e):
        self.ctx.__exit__(*e)
        nums = sorted(x.num for x in self.sems)
        while nums:
            n = 1
            while n < len(nums) and nums[n] == nums[0] + n:
                n += 1
            self.nc.gpsimd.sem_clear(range(nums[0], nums[0] + n))
            nums = nums[n:]

    def sb(self, name, shape, dt=F32):
        return self.ctx.enter_context(self.nc.sbuf_tensor(f"{self.name}_{name}", shape, dt))

    def ps(self, name, banks, dt=F32):
        return self.ctx.enter_context(self.nc.psum_tensor(f"{self.name}_{name}", [P, banks, BANK], dt))

    def sem(self, name):
        self.sems.append(self.ctx.enter_context(self.nc.semaphore(f"{self.name}_{name}")))
        return self.sems[-1]

    def block(self):
        return self.ctx.enter_context(self.nc.Block())


class Chain:

    def __init__(self, eng, sem):
        self.eng, self.sem, self.n = eng, sem, 0

    def step(self, ins):
        ins.then_inc(self.sem, 1)
        self.n += 1
        self.eng.wait_ge(self.sem, self.n)


def constants_phase(nc, m, dram):
    with Phase(nc, "const") as ph:
        loaded = ph.sem("loaded")
        zeroed = ph.sem("zeroed")
        made = ph.sem("made")
        block = ph.block()

        @block.sync
        def _(sp):
            sp.dma_start(m.X[:], dram["x"].rearrange("b (t p) d -> p (b t) d", p=P)).then_inc(loaded, 16)
            sp.wait_ge(loaded, 16)

        @block.vector
        def _(dve):
            chain = Chain(dve, made)
            nc.vector.memset(m.ones[:], 1.0)
            nc.vector.memset(m.neghalf[:], -0.5)
            nc.vector.memset(m.wide_ones[:], 1.0)
            chain.step(nc.vector.memset(m.blockdiag[:], 0.0))
            for h in range(2):
                nc.vector.memset(m.blockdiag[64 * h:64 * h + 64, 64 * h:64 * h + 64], 1.0)

        @block.gpsimd
        def _(pool):
            pool.memset(m.ident[:], 0.0).then_inc(zeroed, 1)
            pool.memset(m.causal[:], 0.0).then_inc(zeroed, 1)
            pool.memset(m.flip[:], 0.0).then_inc(zeroed, 1)
            pool.memset(m.band[:], 0.0).then_inc(zeroed, 1)
            pool.iota(m.iota8[:], pattern=[[1, 8]], base=0, channel_multiplier=0,
                      allow_small_or_imprecise_dtypes=True).then_inc(zeroed, 1)
            pool.wait_ge(zeroed, 5)
            pool.affine_select(out=m.ident[:], in_=m.ident[:], compare_op=ALU.not_equal, fill=1.0, base=0,
                               pattern=[[-1, P]], channel_multiplier=1).then_inc(zeroed, 1)
            pool.affine_select(out=m.flip[:], in_=m.flip[:], compare_op=ALU.not_equal, fill=1.0, base=1 - P,
                               pattern=[[1, P]], channel_multiplier=1).then_inc(zeroed, 1)
            pool.affine_select(out=m.causal[:], in_=m.causal[:], compare_op=ALU.is_ge, fill=NEG, base=0,
                               pattern=[[-1, P]], channel_multiplier=1).then_inc(zeroed, 1)
            pool.affine_select(out=m.band[:], in_=m.band[:], compare_op=ALU.is_ge, fill=NEG, base=64,
                               pattern=[[-1, 192]], channel_multiplier=1).then_inc(zeroed, 1)
            pool.wait_ge(zeroed, 9)
            pool.affine_select(out=m.band[:], in_=m.band[:], compare_op=ALU.is_ge, fill=NEG, base=0,
                               pattern=[[1, 192]], channel_multiplier=-1).then_inc(zeroed, 1)
            pool.tensor_copy(m.identb[:], m.ident[:])


def norm_phase(nc, m, name, add, norm, out=None):
    with Phase(nc, name) as ph:
        stats = ph.sb("stats", [P, 2, NT, 6])
        mv = ph.sb("mv", [P, 2, NT, 2])
        rstd = ph.sb("rstd", [P, 2, NT])
        shift = ph.sb("shift", [P, 2, NT])
        turned = ph.ps("turned", 2)
        stat_done, aggr_done, var_done, rstd_done, shift_done, norm_done = (
            [ph.sem(f"{s}{k}") for k in range(2)] for s in ("stat", "aggr", "var", "rstd", "shift", "norm"))
        x_added = ph.sem("x_added")
        turn_done = ph.sem("turn_done")
        turn_kept = ph.sem("turn_kept")
        block = ph.block()
        src = (m.Y, m.X)
        passes = [k for k, on in enumerate((add, norm)) if on]

        @block.vector
        def _(dve):
            for k in passes:
                for t in range(NT):
                    if k == 1 and add:
                        dve.wait_ge(x_added, t + 1)
                    nc.vector.bn_stats(stats[:, k, t, :], src[k][:, t, :]).then_inc(stat_done[k], 1)
                for t in range(NT):
                    dve.wait_ge(stat_done[k], t + 1)
                    nc.vector.bn_aggr(mv[:, k, t, :], stats[:, k, t, :]).then_inc(aggr_done[k], 1)
                dve.wait_ge(aggr_done[k], NT)
                nc.vector.tensor_scalar(rstd[:, k, :], mv[:, k, :, 1], LN_EPS, None, ALU.add).then_inc(var_done[k], 1)
                dve.wait_ge(rstd_done[k], 1)
                nc.vector.scalar_tensor_tensor(out=shift[:, k, :], in0=mv[:, k, :, 0], scalar=-1.0,
                                               in1=rstd[:, k, :], op0=ALU.mult, op1=ALU.mult).then_inc(shift_done[k], 1)
                if k == 0:
                    for t in range(NT):
                        dve.wait_ge(norm_done[0], t + 1)
                        nc.vector.tensor_tensor(m.X[:, t, :], m.X[:, t, :], m.XN[:, t, :], ALU.add).then_inc(x_added, 1)

        @block.gpsimd
        def _(pool):
            for k in passes:
                pool.wait_ge(var_done[k], 1)
                nc.gpsimd.tensor_tensor(rstd[:, k, :], rstd[:, k, :], m.neghalf[:], ALU.pow).then_inc(rstd_done[k], 1)

        @block.scalar
        def _(act):
            for k in passes:
                act.wait_ge(shift_done[k], 1)
                for t in range(NT):
                    if k == 1 and add:
                        act.wait_ge(x_added, t + 1)
                    nc.scalar.activation(m.XN[:, t, :], src[k][:, t, :], ACT.Identity, bias=shift[:, k, t:t + 1],
                                         scale=rstd[:, k, t:t + 1]).then_inc(norm_done[k], 1)
                if k == 1:
                    for c in range(NT // 4):
                        act.wait_ge(turn_done, 4 * (c + 1))
                        nc.scalar.activation(m.HT[:, c * BANK:(c + 1) * BANK], turned[:, c % 2, :],
                                             ACT.Copy).then_inc(turn_kept, 1)

        @block.tensor
        def _(pe):
            if norm:
                for t in range(NT):
                    pe.wait_ge(norm_done[1], t + 1)
                    if t % 4 == 0 and t >= 8:
                        pe.wait_ge(turn_kept, t // 4 - 1)
                    nc.tensor.transpose(turned[:, t // 4 % 2, t % 4 * P:(t % 4 + 1) * P], m.XN[:, t, :],
                                        m.ident[:]).then_inc(turn_done, 1)

        @block.sync
        def _(sp):
            if out is not None:
                sp.wait_ge(x_added, NT)
                sp.dma_start(out.rearrange("b (t p) d -> p (b t) d", p=P), m.X[:]).then_inc(m.stored, 16)
                sp.wait_ge(m.stored, 16)


class Memory:

    def __init__(self, nc, ctx):
        def sb(name, shape, dt=F32):
            return ctx.enter_context(nc.sbuf_tensor(name, shape, dt))
        self.X = sb("X", [P, NT, P])
        self.XN = sb("XN", [P, NT, P])
        self.Y = sb("Y", [P, NT, P])
        self.HT = sb("HT", [P, TOKENS])
        self.ident = sb("ident", [P, P])
        self.identb = sb("identb", [P, P], BF16)
        self.flip = sb("flip", [P, P])
        self.causal = sb("causal", [P, P])
        self.band = sb("band", [P, 192])
        self.blockdiag = sb("blockdiag", [P, P])
        self.ones = sb("ones", [P, P])
        self.neghalf = sb("neghalf", [P, NT])
        self.wide_ones = sb("wide_ones", [1, BANK])
        self.iota8 = sb("iota8", [P, 8])
        self.weights = sb("weights", [P, WCOLS])
        self.stored = ctx.enter_context(nc.semaphore("output_stored"))
        self.wsem = [ctx.enter_context(nc.semaphore(f"weights_loaded_{i}")) for i in range(8)]



PACKS = [
    [("Wq", P, 1024), ("Wk", P, 1024), ("Wv", P, 1024), ("Wo", P, 1024), ("bo", 1, P)],
    [("Wqkv", P, 384), ("bqkv", 1, 384), ("Wgate", P, 8), ("bgate", 1, 8), ("Wexp", P, 1024), ("bexp", 8, P)],
    [("Wq", P, P), ("Wk", P, P), ("Wv", P, P)],
    [("gate", P, 8), ("wg", P, 4096), ("wu", P, 4096), ("wd", P, 4096)],
    [("Wq", P, 1024), ("Wk", P, 1024), ("Wv", P, 1024), ("Wo", P, 1024)],
    [("wqkv", P, 2 * 1536), ("wo", P, 2 * 512), ("w1", P, 2 * 682), ("w2", P, 2 * 384), ("b1", P, 2 * 6),
     ("b2", 1, 2 * P), ("lng", P, 2), ("lnb", P, 2), ("qscale", 1, 2 * 64), ("kscale", 1, 2 * 64),
     ("cosq", P, 512), ("sinq", P, 512), ("cosk", P, 512), ("sink", P, 512)],
    [("lnw", P, 2), ("lnb", P, 2), ("Win", P, 2 * 512), ("bin", P, 2 * 4), ("convw", P, 2 * 8), ("convb", P, 2 * 2),
     ("Wx", P, 2 * 2 * 96), ("Wdt", 64, 2 * 256), ("bdt", P, 2 * 2), ("Alog", P, 2 * 2 * 16), ("D", P, 2 * 2),
     ("Wout", P, 2 * 2 * P), ("bout", P, 2), ("Wg", P, 2 * P), ("bg", P, 1), ("Wv", P, 2 * P), ("bv", P, 1)],
    [("gate", P, 32), ("bias", 1, 32), ("wg", P, 2048), ("wu", P, 2048), ("wd", P, 2048), ("sg", P, P),
     ("su", P, P), ("sd", P, P)],
]
WIDTHS = [sum(n for _, _, n in pack) for pack in PACKS]
WPART = [max(WIDTHS[0::2]), max(WIDTHS[1::2])]
WCOLS = sum(WPART)


def weight_views(m, s):
    views, at = {}, s % 2 * WPART[0]
    for name, rows, n in PACKS[s]:
        views[name] = m.weights[0:rows, at:at + n]
        at += n
    return views


def load_weights(sp, m, dram, s):
    if s < len(PACKS):
        at = s % 2 * WPART[0]
        sp.dma_start(m.weights[:, at:at + WIDTHS[s]], dram[f"w{s}"]).then_inc(m.wsem[s], 16)


def linear_attention_phase(nc, m, dram, s):
    w = weight_views(m, s)
    EPS = 1e-6
    with Phase(nc, "lin") as ph:
        keyexp = ph.sb("keyexp", [P, 2, BANK])
        keyrelu = ph.sb("keyrelu", [P, 2, BANK])
        key = ph.sb("key", [P, 2, 1024])
        val = ph.sb("val", [P, 2, 1024])
        kvT = ph.sb("kvT", [P, 8, P])
        ksum = ph.sb("ksum", [P, 8])
        ksumB = ph.sb("ksumB", [P, 8, P])
        mix = ph.sb("mix", [P, 8, P])
        qry = ph.sb("qry", [P, 2, BANK])
        den = ph.sb("den", [P, 2, BANK])
        rden = ph.sb("rden", [P, 2, BANK])
        qz = ph.sb("qz", [P, 2, BANK])
        proj = ph.ps("proj", 4)
        acc = ph.ps("acc", 3)
        small = ph.ps("small", 1)
        names = ("proj_done", "proj_kept", "exp_done", "relu_done", "key_done", "val_done", "tile_used", "kv_done",
                 "kvT_done", "ksum_done", "ksumB_done", "mix_psum", "mix_done", "q_psum", "q_exp", "q_relu",
                 "q_done", "z_psum", "den_done", "rden_done", "qz_done", "qz_used", "y_psum", "y_kept", "q_free")
        S = {n: ph.sem(n) for n in names}
        block = ph.block()
        UNITS = [(t, half) for t in range(TPB) for half in range(2)]

        @block.sync
        def _(sp):
            load_weights(sp, m, dram, s + 1)

        @block.tensor
        def _(pe):
            pe.wait_ge(m.wsem[s], 16)
            for b in range(BATCH):
                def accumulate(t):
                    g = b * TPB + t
                    pe.wait_ge(S["key_done"], 2 * (g + 1))
                    pe.wait_ge(S["val_done"], 2 * (g + 1))
                    if t == 0 and b > 0:
                        pe.wait_ge(S["y_kept"], 2 * b)
                        pe.wait_ge(S["ksum_done"], b)
                    for c in range(8):
                        nc.tensor.matmul(acc[:, c // 4, c % 4 * P:(c % 4 + 1) * P], val[:, g % 2, c * P:(c + 1) * P],
                                         key[:, g % 2, c * P:(c + 1) * P], start=(t == 0 and c % 4 == 0),
                                         stop=(t == TPB - 1), skip_group_check=True)
                        last = nc.tensor.matmul(acc[:, 2, c:c + 1], key[:, g % 2, c * P:(c + 1) * P], m.ones[:, 0:1],
                                                start=(t == 0 and c == 0), stop=(t == TPB - 1), skip_group_check=True)
                    last.then_inc(S["tile_used"], 1)

                for t in range(TPB):
                    g = b * TPB + t
                    for half in range(2):
                        for k, wt in enumerate((w["Wk"], w["Wv"])):
                            u = 4 * g + 2 * half + k
                            if u >= 4:
                                pe.wait_ge(S["proj_kept"], u - 3)
                            nc.tensor.matmul(proj[:, u % 4, :], m.HT[:, g * P:(g + 1) * P],
                                             wt[:, half * BANK:(half + 1) * BANK], start=True,
                                             stop=True).then_inc(S["proj_done"], 1)
                    if t >= 1:
                        accumulate(t - 1)
                accumulate(TPB - 1)
                pe.wait_ge(S["kvT_done"], b + 1)
                for c in range(8):
                    i = 8 * b + c
                    if i >= 4:
                        pe.wait_ge(S["mix_done"], i // 4)
                    nc.tensor.matmul(small[:, 0, c % 4 * P:(c % 4 + 1) * P], kvT[:, c, :], w["Wo"][:, c * P:(c + 1) * P],
                                     start=True, stop=True).then_inc(S["mix_psum"], 1)
                pe.wait_ge(S["proj_kept"], 4 * (b + 1) * TPB)
                pe.wait_ge(S["mix_done"], 2 * (b + 1))
                pe.wait_ge(S["ksumB_done"], b + 1)
                for half in range(2):
                    def query(c):
                        n = 16 * b + 8 * half + c
                        if n >= 2:
                            pe.wait_ge(S["q_free"], n - 1)
                        nc.tensor.matmul(proj[:, n % 2, :], w["Wq"][:, c * P:(c + 1) * P],
                                         m.HT[:, (CPB * b + half) * BANK:(CPB * b + half + 1) * BANK], start=True,
                                         stop=True).then_inc(S["q_psum"], 1)

                    def norm_sum(c):
                        n = 16 * b + 8 * half + c
                        pe.wait_ge(S["q_done"], n + 1)
                        if n >= 2:
                            pe.wait_ge(S["den_done"], n - 1)
                        nc.tensor.matmul(proj[:, 2 + n % 2, :], ksumB[:, c, :], qry[:, n % 2, :], start=True,
                                         stop=True).then_inc(S["z_psum"], 1)

                    def project(c):
                        n = 16 * b + 8 * half + c
                        pe.wait_ge(S["qz_done"], n + 1)
                        if c == 0 and 2 * b + half >= 1:
                            pe.wait_ge(S["y_kept"], 2 * b + half)
                        for j in range(4):
                            last = nc.tensor.matmul(acc[:, 0, j * P:(j + 1) * P], qz[:, n % 2, j * P:(j + 1) * P],
                                                    mix[:, c, :], start=(c == 0 and j == 0), stop=False,
                                                    skip_group_check=True)
                        last.then_inc(S["qz_used"], 1)

                    for c in range(10):
                        if c < 8:
                            query(c)
                        if 1 <= c <= 8:
                            norm_sum(c - 1)
                        if c >= 2:
                            project(c - 2)
                    for j in range(4):
                        last = nc.tensor.matmul(acc[:, 0, j * P:(j + 1) * P], m.ones[0:1, :], w["bo"], start=False,
                                                stop=True, skip_group_check=True)
                    last.then_inc(S["y_psum"], 1)

        @block.scalar
        def _(act):
            for b in range(BATCH):
                for t in range(TPB):
                    g = b * TPB + t
                    for half in range(2):
                        n = 2 * g + half
                        cols_ = slice(half * BANK, (half + 1) * BANK)
                        act.wait_ge(S["proj_done"], 2 * n + 1)
                        if n >= 2:
                            act.wait_ge(S["key_done"], n - 1)
                        nc.scalar.activation(keyexp[:, n % 2, :], proj[:, 2 * n % 4, :], ACT.Exp).then_inc(S["exp_done"], 1)
                        nc.scalar.activation(keyrelu[:, n % 2, :], proj[:, 2 * n % 4, :], ACT.Relu).then_inc(S["relu_done"], 1)
                        act.wait_ge(S["relu_done"], n + 1)
                        act.wait_ge(S["exp_done"], n + 1)
                        act.sem_inc(S["proj_kept"], 1)
                        act.wait_ge(S["proj_done"], 2 * n + 2)
                        if g >= 2:
                            act.wait_ge(S["tile_used"], g - 1)
                        nc.scalar.activation(val[:, g % 2, cols_], proj[:, (2 * n + 1) % 4, :],
                                             ACT.Copy).then_inc(S["val_done"], 1)
                        act.wait_ge(S["val_done"], n + 1)
                        act.sem_inc(S["proj_kept"], 1)
                for n in range(16 * b, 16 * b + 16):
                    act.wait_ge(S["q_psum"], n + 1)
                    if n >= 2:
                        act.wait_ge(S["q_done"], n - 1)
                    nc.scalar.activation(keyexp[:, n % 2, :], proj[:, n % 2, :], ACT.Exp).then_inc(S["q_exp"], 1)
                    nc.scalar.activation(keyrelu[:, n % 2, :], proj[:, n % 2, :], ACT.Relu).then_inc(S["q_free"], 1)
                    act.wait_ge(S["z_psum"], n + 1)
                    if n >= 2:
                        act.wait_ge(S["rden_done"], n - 1)
                    nc.scalar.activation(den[:, n % 2, :], proj[:, 2 + n % 2, :], ACT.Copy, bias=EPS).then_inc(S["den_done"], 1)

        @block.vector
        def _(dve):
            for b in range(BATCH):
                for t in range(TPB):
                    g = b * TPB + t
                    for half in range(2):
                        n = 2 * g + half
                        dve.wait_ge(S["relu_done"], n + 1)
                        dve.wait_ge(S["exp_done"], n + 1)
                        if g >= 2:
                            dve.wait_ge(S["tile_used"], g - 1)
                        nc.vector.scalar_tensor_tensor(out=key[:, g % 2, half * BANK:(half + 1) * BANK],
                                                       in0=keyexp[:, n % 2, :], scalar=1.0, in1=keyrelu[:, n % 2, :],
                                                       op0=ALU.min, op1=ALU.add).then_inc(S["key_done"], 1)
                dve.wait_ge(S["tile_used"], (b + 1) * TPB)
                nc.vector.tensor_copy(ksum[:], acc[:, 2, 0:8]).then_inc(S["ksum_done"], 1)
                for c in range(8):
                    last = nc.vector.tensor_tensor(kvT[:, c, :], acc[:, c // 4, c % 4 * P:(c % 4 + 1) * P],
                                                   m.blockdiag[:], ALU.mult)
                last.then_inc(S["kvT_done"], 1)
                dve.wait_ge(S["ksum_done"], b + 1)
                for c in range(8):
                    last = nc.vector.tensor_scalar(ksumB[:, c, :], m.blockdiag[:], ksum[:, c:c + 1], None, ALU.mult)
                last.then_inc(S["ksumB_done"], 1)
                for h in range(2):
                    dve.wait_ge(S["mix_psum"], 8 * b + 4 * (h + 1))
                    nc.vector.tensor_copy(mix[:, 4 * h:4 * h + 4, :], small[:, 0, :].rearrange("p (c n) -> p c n", c=4)).then_inc(S["mix_done"], 1)
                for half in range(2):
                    def features(n):
                        dve.wait_ge(S["q_exp"], n + 1)
                        dve.wait_ge(S["q_free"], n + 1)
                        if n >= 2:
                            dve.wait_ge(S["qz_done"], n - 1)
                        nc.vector.scalar_tensor_tensor(out=qry[:, n % 2, :], in0=keyexp[:, n % 2, :], scalar=1.0,
                                                       in1=keyrelu[:, n % 2, :], op0=ALU.min,
                                                       op1=ALU.add).then_inc(S["q_done"], 1)

                    def divide(n):
                        dve.wait_ge(S["den_done"], n + 1)
                        nc.vector.reciprocal(rden[:, n % 2, :], den[:, n % 2, :]).then_inc(S["rden_done"], 1)
                        dve.wait_ge(S["rden_done"], n + 1)
                        if n >= 2:
                            dve.wait_ge(S["qz_used"], n - 1)
                        nc.vector.tensor_tensor(qz[:, n % 2, :], qry[:, n % 2, :], rden[:, n % 2, :],
                                                ALU.mult).then_inc(S["qz_done"], 1)
                    n0 = 16 * b + 8 * half
                    features(n0)
                    for n in range(n0, n0 + 8):
                        if n + 1 < n0 + 8:
                            features(n + 1)
                        divide(n)
                    dve.wait_ge(S["y_psum"], 2 * b + half + 1)
                    nc.vector.tensor_copy(m.Y[:, b * TPB + 4 * half:b * TPB + 4 * half + 4, :],
                                          acc[:, 0, :].rearrange("p (j n) -> p j n", j=4)).then_inc(S["y_kept"], 1)


SLOTS = 64


def split3(nc, chain, src, hi, mid, lo, rest):
    chain.step(nc.vector.tensor_copy(hi, src))
    chain.step(nc.vector.tensor_tensor(rest, src, hi, ALU.subtract))
    chain.step(nc.vector.tensor_copy(mid, rest))
    chain.step(nc.vector.tensor_tensor(rest, rest, mid, ALU.subtract))
    chain.step(nc.vector.tensor_copy(lo, rest))


def small_head_attention(nc, m, dram, s):
    w = weight_views(m, s)
    with ExitStack() as keep:
        def kept(name, shape, dt):
            return keep.enter_context(nc.sbuf_tensor(name, shape, dt))
        kT = kept("heads_kT", [P, 8, TOKENS], BF16)
        qstack = kept("heads_qstack", [P, NT, 16, SLOTS], BF16)
        vaug = kept("heads_vaug", [P, NT, 16, 9], F32)

        with Phase(nc, "hprep") as ph:
            kstack = ph.sb("kstack", [P, 2, 16, SLOTS], BF16)
            qk = ph.sb("qk", [P, 2, 256])
            parts = ph.sb("parts", [P, 2, 3, 256], BF16)
            rest = ph.sb("rest", [P, 256])
            proj = ph.ps("proj", 2)
            turned = ph.ctx.enter_context(nc.psum_tensor("hprep_turned", [P, 2, 1024], BF16))
            cleared, proj_done, qk_done, v_done, parts_done, chain_sem, stack_act, stack_pool, turn_done, turn_kept = (
                ph.sem(x) for x in ("cleared", "proj_done", "qk_done", "v_done", "parts_done", "chain", "stack_act",
                                    "stack_pool", "turn_done", "turn_kept"))
            block = ph.block()

            @block.sync
            def _(sp):
                load_weights(sp, m, dram, s + 1)

            @block.tensor
            def _(pe):
                pe.wait_ge(m.wsem[s], 16)

                def turn(g):
                    pe.wait_ge(stack_act, g + 1)
                    pe.wait_ge(stack_pool, g + 1)
                    if g >= 2:
                        pe.wait_ge(turn_kept, g - 1)
                    for c in range(8):
                        last = nc.tensor.transpose(turned[:, g % 2, c * P:(c + 1) * P],
                                                   kstack[:, g % 2, 2 * c:2 * c + 2, :].rearrange("p h d -> p (h d)"),
                                                   m.identb[:])
                    last.then_inc(turn_done, 1)

                for g in range(NT):
                    if g >= 2:
                        pe.wait_ge(qk_done, g - 1)
                        pe.wait_ge(v_done, g - 1)
                    nc.tensor.matmul(proj[:, g % 2, 0:384], m.HT[:, g * P:(g + 1) * P], w["Wqkv"], start=True, stop=False)
                    nc.tensor.matmul(proj[:, g % 2, 0:384], m.ones[0:1, :], w["bqkv"], start=False,
                                     stop=True).then_inc(proj_done, 1)
                    if g >= 1:
                        turn(g - 1)
                turn(NT - 1)

            @block.scalar
            def _(act):
                act.wait_ge(cleared, 5)
                for g in range(NT):
                    act.wait_ge(proj_done, g + 1)
                    if g >= 2:
                        act.wait_ge(parts_done, g - 1)
                    nc.scalar.activation(qk[:, g % 2, :], proj[:, g % 2, 0:256], ACT.Copy).then_inc(qk_done, 1)
                    nc.scalar.activation(vaug[:, g, :, 0:8], proj[:, g % 2, 256:384].rearrange("p (h d) -> p h d", h=16),
                                         ACT.Copy).then_inc(v_done, 1)
                    act.wait_ge(parts_done, g + 1)
                    hi, mid, lo = (parts[:, g % 2, k, 0:P].rearrange("p (h d) -> p h d", h=16) for k in range(3))
                    for slot, part in enumerate((hi, hi, mid, mid, hi, lo)):
                        last = nc.scalar.activation(qstack[:, g, :, 8 * slot:8 * slot + 8], part, ACT.Copy)
                    last.then_inc(stack_act, 1)
                    if g >= 1:
                        act.wait_ge(turn_done, g)
                        nc.scalar.activation(kT[:, :, (g - 1) * P:g * P],
                                             turned[:, (g - 1) % 2, :].rearrange("p (c n) -> p c n", c=8),
                                             ACT.Copy).then_inc(turn_kept, 1)
                act.wait_ge(turn_done, NT)
                nc.scalar.activation(kT[:, :, (NT - 1) * P:NT * P],
                                     turned[:, (NT - 1) % 2, :].rearrange("p (c n) -> p c n", c=8),
                                     ACT.Copy).then_inc(turn_kept, 1)

            @block.gpsimd
            def _(pool):
                pool.wait_ge(cleared, 5)
                for g in range(NT):
                    pool.wait_ge(parts_done, g + 1)
                    if g >= 2:
                        pool.wait_ge(turn_done, g - 1)
                    hi, mid, lo = (parts[:, g % 2, k, P:2 * P].rearrange("p (h d) -> p h d", h=16) for k in range(3))
                    for slot, part in enumerate((hi, mid, hi, mid, lo, hi)):
                        last = nc.gpsimd.tensor_copy(kstack[:, g % 2, :, 8 * slot:8 * slot + 8], part)
                    last.then_inc(stack_pool, 1)

            @block.vector
            def _(dve):
                chain = Chain(dve, chain_sem)
                nc.vector.memset(kstack[:, :, :, 51:64], 0.0).then_inc(cleared, 1)
                nc.vector.memset(kstack[:, :, :, 48:51], 1.0).then_inc(cleared, 1)
                nc.vector.memset(qstack[:, 0:8, :, 48:64], 0.0).then_inc(cleared, 1)
                nc.vector.memset(qstack[:, 8:16, :, 48:64], 0.0).then_inc(cleared, 1)
                nc.vector.memset(vaug[:, :, :, 8], 1.0).then_inc(cleared, 1)
                for g in range(NT):
                    dve.wait_ge(qk_done, g + 1)
                    if g >= 2:
                        dve.wait_ge(stack_act, g - 1)
                        dve.wait_ge(stack_pool, g - 1)
                    split3(nc, chain, qk[:, g % 2, :], parts[:, g % 2, 0, :], parts[:, g % 2, 1, :],
                           parts[:, g % 2, 2, :], rest[:])
                    dve.sem_inc(parts_done, 1)

        with Phase(nc, "heads") as ph:
            qT = ph.sb("qT", [P, 2, 8, P], BF16)
            qmT = ph.sb("qmT", [P, 2, 8, P], BF16)
            halfmax = ph.sb("halfmax", [P, 2, 16, 2])
            negmax = ph.sb("negmax", [P, 16])
            rest = ph.sb("rest", [P, 16])
            probs = ph.sb("probs", [P, 3, 1024])
            rsum = ph.sb("rsum", [P, 2, 16])
            qmajor = ph.ps("qmajor", 2)
            kmajor = ph.ps("kmajor", 4)
            outp = ph.ps("outp", 1)
            turned = ph.ctx.enter_context(nc.psum_tensor("heads_turned", [P, 1, 1024], BF16))
            (t1_done, t1_kept, s_done, max_done, slots_done, t2_done, t2_kept, st_done, exp_done, pv_done, head_done,
             out_kept, chain_sem, rsum_done) = (
                ph.sem(x) for x in ("t1_done", "t1_kept", "s_done", "max_done", "slots_done", "t2_done", "t2_kept",
                                    "st_done", "exp_done", "pv_done", "head_done", "out_kept", "chain", "rsum_done"))
            block = ph.block()
            SC = float(8) ** -0.5

            @block.tensor
            def _(pe):
                def turn(g, done, n):
                    if n >= 1:
                        pe.wait_ge(t1_kept, (n + 1) // 2)
                        pe.wait_ge(t2_kept, n // 2)
                    for c in range(8):
                        last = nc.tensor.transpose(turned[:, 0, c * P:(c + 1) * P],
                                                   qstack[:, g, 2 * c:2 * c + 2, :].rearrange("p h d -> p (h d)"),
                                                   m.identb[:])
                    last.then_inc(done, 1)

                def scores(g, h):
                    c, j, b = h // 2, h % 2, g // TPB
                    if h == 0:
                        pe.wait_ge(t1_kept, g + 1)
                    for half in range(2):
                        n = 32 * g + 2 * h + half
                        if n >= 2:
                            pe.wait_ge(max_done, n - 1)
                        nc.tensor.matmul(qmajor[:, half, :], qT[64 * j:64 * j + 48, g % 2, c, :],
                                         kT[64 * j:64 * j + 48, c, b * SEQ + half * BANK:b * SEQ + (half + 1) * BANK],
                                         start=True, stop=True).then_inc(s_done, 1)

                def shifted(g, h):
                    c, j, b, n = h // 2, h % 2, g // TPB, 16 * g + h
                    if h == 0:
                        pe.wait_ge(t2_kept, g + 1)
                    if n >= 2:
                        pe.wait_ge(exp_done, n - 1)
                    for kc in range(TPB):
                        last = nc.tensor.matmul(kmajor[:, 2 * (n % 2) + kc // 4, kc % 4 * P:(kc % 4 + 1) * P],
                                                kT[64 * j:64 * j + 51, c, b * SEQ + kc * P:b * SEQ + (kc + 1) * P],
                                                qmT[64 * j:64 * j + 51, g % 2, c, :], start=True, stop=True)
                    last.then_inc(st_done, 1)

                def values(g, h):
                    b, n = g // TPB, 16 * g + h
                    pe.wait_ge(exp_done, n + 1)
                    if h == 0 and g >= 1:
                        pe.wait_ge(out_kept, g)
                    at = g % 2 * 256 + 9 * h
                    for kc in range(TPB):
                        last = nc.tensor.matmul(outp[:, 0, at:at + 9], probs[:, n % 3, kc * P:(kc + 1) * P],
                                                vaug[:, b * TPB + kc, h, :], start=(kc == 0), stop=(kc == TPB - 1))
                    last.then_inc(pv_done, 1)

                turn(0, t1_done, 0)
                for i in range(NT + 1):
                    for h in range(16):
                        if i < NT:
                            scores(i, h)
                        if h == 2 and i >= 1:
                            pe.wait_ge(slots_done, i)
                            turn(i - 1, t2_done, 2 * i - 1)
                        if i >= 1 and h >= 3:
                            shifted(i - 1, h - 3)
                            if h >= 4:
                                values(i - 1, h - 4)
                        if h == 8 and i + 1 < NT:
                            turn(i + 1, t1_done, 2 * i + 1 - (i == 0)) if i > 0 else turn(1, t1_done, 1)
                    if i >= 1:
                        for h in range(13, 16):
                            shifted(i - 1, h)
                            values(i - 1, h - 1)
                        values(i - 1, 15)

            @block.scalar
            def _(act):
                def keep1(g):
                    act.wait_ge(t1_done, g + 1)
                    if g >= 2:
                        act.wait_ge(s_done, 32 * (g - 1))
                    nc.scalar.activation(qT[:, g % 2, :, :], turned[:, 0, :].rearrange("p (c n) -> p c n", c=8),
                                         ACT.Copy).then_inc(t1_kept, 1)
                keep1(0)
                for i in range(NT + 1):
                    if i >= 1:
                        act.wait_ge(t2_done, i)
                        if i >= 3:
                            act.wait_ge(st_done, 16 * (i - 2))
                        nc.scalar.activation(qmT[:, (i - 1) % 2, :, :], turned[:, 0, :].rearrange("p (c n) -> p c n", c=8),
                                             ACT.Copy).then_inc(t2_kept, 1)
                    for h in range(16):
                        if h == 5 and i + 1 < NT:
                            keep1(i + 1)
                        if i >= 1:
                            n = 16 * (i - 1) + h
                            act.wait_ge(st_done, n + 1)
                            if n >= 3:
                                act.wait_ge(pv_done, n - 2)
                            nc.scalar.activation(probs[:, n % 3, :].rearrange("p (a n) -> p a n", a=2),
                                                 kmajor[:, 2 * (n % 2):2 * (n % 2) + 2, :], ACT.Exp,
                                                 scale=SC).then_inc(exp_done, 1)

            @block.vector
            def _(dve):
                chain = Chain(dve, chain_sem)

                def normalise(g):
                    dve.wait_ge(pv_done, 16 * (g + 1))
                    o = outp[:, 0, g % 2 * 256:g % 2 * 256 + 144].rearrange("p (h e) -> p h e", h=16)
                    nc.vector.reciprocal(rsum[:, g % 2, :], o[:, :, 8]).then_inc(rsum_done, 1)
                    dve.wait_ge(rsum_done, g + 1)
                    nc.vector.tensor_tensor(m.Y[:, g, :].rearrange("p (h d) -> p h d", h=16), o[:, :, 0:8],
                                            rsum[:, g % 2, :].unsqueeze(2).broadcast_to([P, 16, 8]),
                                            ALU.mult).then_inc(out_kept, 1)

                for g in range(NT):
                    for h in range(16):
                        for half in range(2):
                            dve.wait_ge(s_done, 32 * g + 2 * h + half + 1)
                            nc.vector.tensor_reduce(halfmax[:, g % 2, h, half:half + 1], qmajor[:, half, :], AX,
                                                    ALU.max).then_inc(max_done, 1)
                        if h == 2 and g >= 2:
                            normalise(g - 2)
                    dve.wait_ge(max_done, 32 * (g + 1))
                    chain.step(nc.vector.tensor_reduce(negmax[:], halfmax[:, g % 2, :, :], AX, ALU.max))
                    chain.step(nc.vector.tensor_scalar(negmax[:], negmax[:], -1.0, None, ALU.mult))
                    dve.wait_ge(t1_done, g + 1)
                    split3(nc, chain, negmax[:], qstack[:, g, :, 48], qstack[:, g, :, 49], qstack[:, g, :, 50], rest[:])
                    dve.sem_inc(slots_done, 1)
                normalise(NT - 2)
                normalise(NT - 1)


def top2_experts(nc, m, dram, s):
    w = weight_views(m, s)
    with Phase(nc, "moe0") as ph:
        gates = ph.sb("gates", [P, NT, 8])
        pick = ph.sb("pick", [P, NT, 8])
        pick2 = ph.sb("pick2", [P, NT, 8])
        stat = ph.sb("stat", [P, NT])
        top = ph.sb("top", [P, NT, 8])
        where = ph.sb("where", [P, NT, 8], U32)
        wheref = ph.sb("wheref", [P, NT, 2])
        gT = ph.sb("gT", [8, TOKENS])
        acc = ph.sb("acc", [P, 2, P])
        logits = ph.ps("logits", 1)
        expert = ph.ps("expert", 4)
        bias = ph.ps("bias", 2)
        turned = ph.ps("turned", 1)
        logits_done, chain_sem, combine_done, gt_done, gt_kept, ex_done, ex_kept, acc_sem, exp_in, exp_out = (
            ph.sem(x) for x in ("logits_done", "chain", "combine_done", "gt_done", "gt_kept", "ex_done", "ex_kept",
                                "acc", "exp_in", "exp_out"))
        block = ph.block()

        @block.tensor
        def _(pe):
            for g in range(NT):
                nc.tensor.matmul(logits[:, 0, 8 * g:8 * g + 8], m.HT[:, g * P:(g + 1) * P], w["Wgate"], start=True, stop=False)
                last = nc.tensor.matmul(logits[:, 0, 8 * g:8 * g + 8], m.ones[0:1, :], w["bgate"], start=False, stop=True)
            last.then_inc(logits_done, 1)

            def experts(g):
                if g >= 2:
                    pe.wait_ge(ex_kept, g - 1)
                for k in range(2):
                    last = nc.tensor.matmul(expert[:, 2 * (g % 2) + k, :], m.HT[:, g * P:(g + 1) * P],
                                            w["Wexp"][:, k * BANK:(k + 1) * BANK], start=True, stop=True)
                last.then_inc(ex_done, 1)
            experts(0)
            experts(1)
            pe.wait_ge(combine_done, 1)
            for g in range(NT):
                if g % 4 == 0 and g > 0:
                    pe.wait_ge(gt_kept, g // 4)
                nc.tensor.transpose(turned[0:8, 0, g % 4 * P:(g % 4 + 1) * P], gates[:, g, :], m.ident[:]).then_inc(gt_done, 1)
            for g in range(NT):
                pe.wait_ge(gt_kept, g // 4 + 1)
                if g >= 2:
                    pe.wait_ge(ex_kept, g - 1)
                nc.tensor.matmul(bias[:, g % 2, 0:P], gT[:, g * P:(g + 1) * P], w["bexp"], start=True,
                                 stop=True)
                if g >= 2:
                    experts(g)
                else:
                    nc.tensor.matmul(bias[:, g % 2, 0:P], gT[:, g * P:(g + 1) * P], w["bexp"],
                                     start=True, stop=True).then_inc(ex_done, 1)

        @block.scalar
        def _(act):
            act.wait_ge(exp_in, 1)
            nc.scalar.activation(gates[:], gates[:], ACT.Exp).then_inc(exp_out, 1)
            for c in range(4):
                act.wait_ge(gt_done, 4 * (c + 1))
                nc.scalar.activation(gT[:, c * BANK:(c + 1) * BANK], turned[0:8, 0, :], ACT.Copy).then_inc(gt_kept, 1)

        @block.vector
        def _(dve):
            chain = Chain(dve, chain_sem)

            def wide(a):
                return a.unsqueeze(2).broadcast_to([P, NT, 8])
            dve.wait_ge(logits_done, 1)
            lg = logits[:, 0, 0:8 * NT].rearrange("p (t e) -> p t e", e=8)
            chain.step(nc.vector.tensor_reduce(stat[:], lg, AX, ALU.max))
            nc.vector.tensor_tensor(gates[:], lg, wide(stat[:]), ALU.subtract).then_inc(exp_in, 1)
            dve.wait_ge(exp_out, 1)
            chain.step(nc.vector.tensor_reduce(stat[:], gates[:], AX, ALU.add))
            chain.step(nc.vector.reciprocal(stat[:], stat[:]))
            chain.step(nc.vector.tensor_tensor(gates[:], gates[:], wide(stat[:]), ALU.mult))
            top2_mask(nc, m, chain, gates, top, where, wheref, pick, pick2)
            nc.vector.tensor_tensor(gates[:], gates[:], pick[:], ALU.mult).then_inc(combine_done, 1)
            dve.wait_ge(combine_done, 1)
            adds = Chain(dve, acc_sem)
            for g in range(NT):
                dve.wait_ge(ex_done, g + 3 if g >= 2 else 4)
                for e in range(8):
                    src = expert[:, 2 * (g % 2) + e // 4, e % 4 * P:(e % 4 + 1) * P]
                    into = acc[:, e % 2, :]
                    prev = m.Y[:, g, :] if e == 0 else acc[:, 1 - e % 2, :]
                    adds.step(nc.vector.scalar_tensor_tensor(out=into, in0=src, scalar=gates[:, g, e:e + 1], in1=prev,
                                                             op0=ALU.mult, op1=ALU.add))
                adds.step(nc.vector.tensor_tensor(m.Y[:, g, :], acc[:, 1, :], bias[:, g % 2, 0:P], ALU.add))
                dve.sem_inc(ex_kept, 1)


def top2_mask(nc, m, chain, gates, top, where, wheref, pick, pick2):
    for g in range(NT):
        last = nc.vector.max(out=top[:, g, :], in_=gates[:, g, :])
    chain.step(last)
    for g in range(NT):
        last = nc.vector.max_index(where[:, g, :], top[:, g, :], gates[:, g, :])
    chain.step(last)
    chain.step(nc.vector.tensor_copy(wheref[:], where[:, :, 0:2]))
    index = m.iota8[:].unsqueeze(1).broadcast_to([P, NT, 8])
    chain.step(nc.vector.tensor_tensor(pick[:], index, wheref[:, :, 0:1].broadcast_to([P, NT, 8]), ALU.is_equal))
    chain.step(nc.vector.tensor_tensor(pick2[:], index, wheref[:, :, 1:2].broadcast_to([P, NT, 8]), ALU.is_equal))
    chain.step(nc.vector.tensor_tensor(pick[:], pick[:], pick2[:], ALU.add))


def attention_and_top2(nc, m, dram, s):
    small_head_attention(nc, m, dram, s)
    top2_experts(nc, m, dram, s)


def causal_attention(nc, m, dram, s, name, groups, heads, scale, out_proj):
    w = weight_views(m, s)
    D = P // heads
    GROUPS = [(b, c) for b in range(BATCH) for c in range(groups)]
    UNITS = [(g, h, i) for g in range(len(GROUPS)) for h in range(heads) for i in range(TPB)]
    PER = heads * TPB

    def blocks(n):
        return UNITS[n][2] + 1

    def fills(n):
        return (blocks(n) + 3) // 4

    first_fill = [sum(fills(k) for k in range(n)) for n in range(len(UNITS) + 1)]

    def schedule():
        events, k = [], 0
        for n in range(len(UNITS) + 2):
            if n < len(UNITS) and n % PER == 0:
                for part in range(6):
                    events.append(("project", (n // PER, part), k))
                    k += 1
            if n < len(UNITS):
                events.append(("scores", n, None))
            if 1 <= n <= len(UNITS):
                events.append(("transposes", n - 1, None))
            if n >= 2:
                events.append(("values", n - 2, k))
                k += 1
                if out_proj and (n - 1) % PER == 0:
                    g = (n - 2) // PER
                    for half in range(2):
                        events.append(("turn", (g, half), k))
                        k += 1
                    if (g + 1) % groups == 0:
                        for half in range(2):
                            events.append(("out", (g // groups, half), k))
                            k += 1
        return events

    EVENTS = schedule()

    with Phase(nc, name) as ph:
        qT = ph.sb("qT", [P, 2, SEQ])
        kT = ph.sb("kT", [P, 2, SEQ])
        v = ph.sb("v", [P, 2, TPB, P])
        probs = ph.sb("probs", [P, 2, SEQ])
        probsT = ph.sb("probsT", [P, 2, SEQ])
        negmax = ph.sb("negmax", [P, 2])
        rowmax = ph.sb("rowmax", [P, 2])
        rowsum = ph.sb("rowsum", [P, 4])
        rinv = ph.sb("rinv", [P, 1])
        z = ph.sb("z", [P, 2, TPB, P]) if out_proj else None
        zT = ph.sb("zT", [P, groups, SEQ]) if out_proj else None
        score = ph.ps("score", 4)
        turned = ph.ps("turned", 2)
        misc = ph.ps("misc", 2)
        misc_done, misc_kept, s_done, negmax_done, exp_done, t_done, t_kept, pv_done, chain_sem = (
            ph.sem(x) for x in ("misc_done", "misc_kept", "s_done", "negmax_done", "exp_done", "t_done", "t_kept",
                                "pv_done", "chain"))
        block = ph.block()

        def score_of(n):
            return score[:, 2 * (n % 2):2 * (n % 2) + 2, :].rearrange("p a n -> p (a n)")

        @block.sync
        def _(sp):
            load_weights(sp, m, dram, s + 1)

        @block.tensor
        def _(pe):
            pe.wait_ge(m.wsem[s], 16)
            for what, idx, k in EVENTS:
                if k is not None and k >= 2:
                    pe.wait_ge(misc_kept, k - 1)
                if what == "project":
                    g, part = idx
                    b, c = GROUPS[g]
                    if part < 4:
                        wt, half = w["Wq" if part < 2 else "Wk"], part % 2
                        nc.tensor.matmul(misc[:, k % 2, :], wt[:, c * P:(c + 1) * P],
                                         m.HT[:, b * SEQ + half * BANK:b * SEQ + (half + 1) * BANK], start=True,
                                         stop=True).then_inc(misc_done, 1)
                    else:
                        for j in range(4):
                            t = b * TPB + 4 * (part - 4) + j
                            last = nc.tensor.matmul(misc[:, k % 2, j * P:(j + 1) * P], m.HT[:, t * P:(t + 1) * P],
                                                    w["Wv"][:, c * P:(c + 1) * P], start=True, stop=True)
                        last.then_inc(misc_done, 1)
                        if part == 5:
                            pe.wait_ge(misc_kept, k + 1)
                elif what == "scores":
                    g, h, i = UNITS[idx]
                    if idx >= 2:
                        pe.wait_ge(exp_done, idx - 1)
                    wide = (i + 1) * P
                    for at in range(0, wide, BANK):
                        to = min(wide, at + BANK)
                        last = nc.tensor.matmul(score_of(idx)[:, at:to], qT[D * h:D * (h + 1), g % 2, i * P:(i + 1) * P],
                                                kT[D * h:D * (h + 1), g % 2, at:to], start=True, stop=True)
                    last.then_inc(s_done, 1)
                elif what == "transposes":
                    pe.wait_ge(exp_done, idx + 1)
                    for f in range(fills(idx)):
                        e = first_fill[idx] + f
                        if e >= 2:
                            pe.wait_ge(t_kept, e - 1)
                        for kb in range(4 * f, min(4 * f + 4, blocks(idx))):
                            last = nc.tensor.transpose(turned[:, e % 2, kb % 4 * P:(kb % 4 + 1) * P],
                                                       probs[:, idx % 2, kb * P:(kb + 1) * P], m.ident[:])
                        last.then_inc(t_done, 1)
                elif what == "values":
                    g, h, i = UNITS[idx]
                    pe.wait_ge(t_kept, first_fill[idx + 1])
                    for kb in range(i + 1):
                        last = nc.tensor.matmul(misc[:, k % 2, 0:D], probsT[:, idx % 2, kb * P:(kb + 1) * P],
                                                v[:, g % 2, kb, D * h:D * (h + 1)], start=(kb == 0), stop=(kb == i))
                    last.then_inc(misc_done, 1)
                elif what == "turn":
                    g, half = idx
                    for j in range(4):
                        last = nc.tensor.transpose(misc[:, k % 2, j * P:(j + 1) * P], z[:, g % 2, 4 * half + j, :],
                                                   m.ident[:])
                    last.then_inc(misc_done, 1)
                else:
                    b, half = idx
                    pe.wait_ge(misc_kept, k)
                    for j in range(4):
                        t = 4 * half + j
                        for c in range(groups):
                            last = nc.tensor.matmul(misc[:, k % 2, j * P:(j + 1) * P], zT[:, c, t * P:(t + 1) * P],
                                                    w["Wo"][:, c * P:(c + 1) * P], start=(c == 0), stop=(c == groups - 1))
                    last.then_inc(misc_done, 1)

        @block.scalar
        def _(act):
            def exps(n):
                act.wait_ge(negmax_done, n + 1)
                if n >= 2:
                    act.wait_ge(t_done, first_fill[n - 1])
                wide = blocks(n) * P
                nc.scalar.activation(probs[:, n % 2, 0:wide], score_of(n)[:, 0:wide], ACT.Exp,
                                     bias=negmax[:, n % 2:n % 2 + 1], scale=scale,
                                     accum_out=rowsum[:, n % 4:n % 4 + 1]).then_inc(exp_done, 1)

            def keep(n):
                if n >= 2:
                    act.wait_ge(pv_done, n - 1)
                for f in range(fills(n)):
                    act.wait_ge(t_done, first_fill[n] + f + 1)
                    at, to = 4 * f * P, min(4 * f + 4, blocks(n)) * P
                    nc.scalar.activation(probsT[:, n % 2, at:to], turned[:, (first_fill[n] + f) % 2, 0:to - at],
                                         ACT.Copy).then_inc(t_kept, 1)
            for n in range(len(UNITS) + 1):
                if n < len(UNITS):
                    exps(n)
                if n >= 1:
                    keep(n - 1)

        @block.vector
        def _(dve):
            chain = Chain(dve, chain_sem)
            for what, idx, k in EVENTS:
                if k is not None:
                    dve.wait_ge(misc_done, k + 1)
                if what == "project":
                    g, part = idx
                    if part < 4:
                        to = (qT if part < 2 else kT)[:, g % 2, part % 2 * BANK:(part % 2 + 1) * BANK]
                    else:
                        to = v[:, g % 2, 4 * (part - 4):4 * (part - 3), :].rearrange("p t n -> p (t n)")
                    nc.vector.tensor_copy(to, misc[:, k % 2, :]).then_inc(misc_kept, 1)
                elif what == "scores":
                    i = UNITS[idx][2]
                    dve.wait_ge(s_done, idx + 1)
                    diag = score_of(idx)[:, i * P:(i + 1) * P]
                    chain.step(nc.vector.tensor_tensor(diag, diag, m.causal[:], ALU.add))
                    chain.step(nc.vector.tensor_reduce(rowmax[:, idx % 2:idx % 2 + 1], score_of(idx)[:, 0:(i + 1) * P],
                                                       AX, ALU.max))
                    if idx >= 2:
                        dve.wait_ge(exp_done, idx - 1)
                    nc.vector.tensor_scalar(negmax[:, idx % 2:idx % 2 + 1], rowmax[:, idx % 2:idx % 2 + 1], -scale, None,
                                            ALU.mult).then_inc(negmax_done, 1)
                elif what == "values":
                    g, h, i = UNITS[idx]
                    dve.sem_inc(pv_done, 1)
                    chain.step(nc.vector.reciprocal(rinv[:], rowsum[:, idx % 4:idx % 4 + 1]))
                    if out_proj:
                        to = z[:, g % 2, i, D * h:D * (h + 1)]
                    else:
                        to = m.Y[:, GROUPS[g][0] * TPB + i, :]
                    chain.step(nc.vector.tensor_scalar(to, misc[:, k % 2, 0:D], rinv[:], None, ALU.mult))
                    dve.sem_inc(misc_kept, 1)
                elif what == "turn":
                    g, half = idx
                    nc.vector.tensor_copy(zT[:, GROUPS[g][1], half * BANK:(half + 1) * BANK],
                                          misc[:, k % 2, :]).then_inc(misc_kept, 1)
                elif what == "out":
                    b, half = idx
                    t = b * TPB + 4 * half
                    nc.vector.tensor_copy(m.Y[:, t:t + 4, :].rearrange("p t n -> p (t n)"),
                                          misc[:, k % 2, :]).then_inc(misc_kept, 1)


def causal_single_head(nc, m, dram, s):
    causal_attention(nc, m, dram, s, "one", 1, 1, float(P) ** -0.5, False)


def swiglu_experts(nc, m, dram, s):
    w = weight_views(m, s)
    E, IC = 8, 4
    UNITS = [(tc, e, ic) for tc in range(NT // 4) for e in range(E) for ic in range(IC)]
    with Phase(nc, "swiglu") as ph:
        logits = ph.sb("logits", [P, NT, 8])
        gates = ph.sb("gates", [P, NT, 8])
        pick = ph.sb("pick", [P, NT, 8])
        pick2 = ph.sb("pick2", [P, NT, 8])
        stat = ph.sb("stat", [P, NT])
        top = ph.sb("top", [P, NT, 8])
        where = ph.sb("where", [P, NT, 8], U32)
        wheref = ph.sb("wheref", [P, NT, 2])
        silu = ph.sb("silu", [P, 2, BANK])
        hidden = ph.sb("hidden", [P, 3, BANK])
        router = ph.ps("router", 1)
        gate_up = ph.ps("gate_up", 4)
        down = ph.ps("down", 2)
        (router_done, chain_sem, exp_in, exp_out, gu_done, silu_done, hid_done, down_done, y_done) = (
            ph.sem(x) for x in ("router_done", "chain", "exp_in", "exp_out", "gu_done", "silu_done", "hid_done",
                                "down_done", "y_done"))
        block = ph.block()

        @block.sync
        def _(sp):
            load_weights(sp, m, dram, s + 1)

        @block.tensor
        def _(pe):
            pe.wait_ge(m.wsem[s], 16)
            for g in range(NT):
                last = nc.tensor.matmul(router[:, 0, 8 * g:8 * g + 8], m.HT[:, g * P:(g + 1) * P], w["gate"], start=True,
                                        stop=True)
            last.then_inc(router_done, 1)
            for n in range(len(UNITS) + 1):
                if n < len(UNITS):
                    tc, e, ic = UNITS[n]
                    if n >= 2:
                        pe.wait_ge(hid_done, n - 1)
                    at = (e * IC + ic) * P
                    for k, wt in enumerate((w["wg"], w["wu"])):
                        nc.tensor.matmul(gate_up[:, 2 * (n % 2) + k, :], wt[:, at:at + P],
                                         m.HT[:, tc * BANK:(tc + 1) * BANK], start=True, stop=True).then_inc(gu_done, 1)
                if n >= 1:
                    tc, e, ic = UNITS[n - 1]
                    k = tc * E + e
                    pe.wait_ge(hid_done, n)
                    if ic == 0 and k >= 2:
                        pe.wait_ge(y_done, 4 * (k - 1))
                    at = (e * IC + ic) * P
                    for j in range(4):
                        last = nc.tensor.matmul(down[:, k % 2, j * P:(j + 1) * P],
                                                hidden[:, (n - 1) % 3, j * P:(j + 1) * P], w["wd"][:, at:at + P],
                                                start=(ic == 0 and j == 0), stop=(ic == IC - 1), skip_group_check=True)
                    last.then_inc(down_done, 1)

        @block.scalar
        def _(act):
            act.wait_ge(exp_in, 1)
            nc.scalar.activation(gates[:], gates[:], ACT.Exp).then_inc(exp_out, 1)
            for n in range(len(UNITS)):
                act.wait_ge(gu_done, 2 * n + 1)
                if n >= 2:
                    act.wait_ge(hid_done, n - 1)
                nc.scalar.activation(silu[:, n % 2, :], gate_up[:, 2 * (n % 2), :], ACT.Silu).then_inc(silu_done, 1)

        @block.vector
        def _(dve):
            chain = Chain(dve, chain_sem)

            def wide(a):
                return a.broadcast_to([P, NT, 8])
            dve.wait_ge(router_done, 1)
            chain.step(nc.vector.tensor_copy(logits[:].rearrange("p t e -> p (t e)"), router[:, 0, 0:8 * NT]))
            top2_mask(nc, m, chain, logits, top, where, wheref, pick, pick2)
            nc.vector.tensor_tensor(gates[:], logits[:], wide(top[:, :, 0:1]), ALU.subtract).then_inc(exp_in, 1)
            dve.wait_ge(exp_out, 1)
            chain.step(nc.vector.tensor_tensor(gates[:], gates[:], pick[:], ALU.mult))
            chain.step(nc.vector.tensor_reduce(stat[:], gates[:], AX, ALU.add))
            chain.step(nc.vector.reciprocal(stat[:], stat[:]))
            chain.step(nc.vector.tensor_tensor(gates[:], gates[:], wide(stat[:].unsqueeze(2)), ALU.mult))
            for n in range(len(UNITS) + 1):
                if n < len(UNITS):
                    dve.wait_ge(silu_done, n + 1)
                    dve.wait_ge(gu_done, 2 * n + 2)
                    if n >= 3:
                        dve.wait_ge(down_done, n - 2)
                    nc.vector.tensor_tensor(hidden[:, n % 3, :], gate_up[:, 2 * (n % 2) + 1, :], silu[:, n % 2, :],
                                            ALU.mult).then_inc(hid_done, 1)
                if n >= 1 and UNITS[n - 1][2] == IC - 1:
                    tc, e, _ = UNITS[n - 1]
                    k = tc * E + e
                    dve.wait_ge(down_done, n)
                    if e > 0:
                        dve.wait_ge(y_done, 4 * k)
                    for j in range(4):
                        t = 4 * tc + j
                        src, c = down[:, k % 2, j * P:(j + 1) * P], gates[:, t, e:e + 1]
                        if e == 0:
                            last = nc.vector.tensor_scalar(m.Y[:, t, :], src, c, None, ALU.mult)
                        else:
                            last = nc.vector.scalar_tensor_tensor(out=m.Y[:, t, :], in0=src, scalar=c,
                                                                  in1=m.Y[:, t, :], op0=ALU.mult, op1=ALU.add)
                        last.then_inc(y_done, 1)


def causal_sixteen_heads(nc, m, dram, s):
    causal_attention(nc, m, dram, s, "many", 8, 2, 0.125, True)


HID = 341
WIN = 64
LAYERS = 2
SPAN = P + WIN


def shift_tokens(nc, m, name, Z, ZS):
    with Phase(nc, name) as ph:
        moved, kept, first = ph.sem("moved"), ph.sem("kept"), ph.sem("first")
        block = ph.block()

        @block.vector
        def _(dve):
            nc.vector.tensor_copy(ZS[:, :, 0:WIN], Z[:, :, 0:WIN]).then_inc(kept, 1)

        @block.gpsimd
        def _(pool):
            for b in range(BATCH):
                nc.gpsimd.memset(ZS[0:1, b * TPB, WIN:P], 0.0).then_inc(first, 1)

        @block.sync
        def _(sp):
            sp.dma_start(ZS[1:P, :, WIN:P], Z[0:P - 1, :, WIN:P]).then_inc(moved, 16)
            for b in range(BATCH):
                t = b * TPB
                sp.dma_start(ZS[0:1, t + 1:t + TPB, WIN:P], Z[P - 1:P, t:t + TPB - 1, WIN:P]).then_inc(moved, 16)
            sp.wait_ge(moved, 16 * (1 + BATCH))


def rotary_scale_phase(nc, m, w, l, tables, scaled):
    with Phase(nc, f"tables{l}") as ph:
        rows = ph.ps("rows", 1)
        spread = ph.sb("spread", [P, 2, 64])
        rows_done, spread_done = ph.sem("rows_done"), ph.sem("spread_done")
        done = ph.sem("done")
        block = ph.block()

        @block.tensor
        def _(pe):
            for k, name in enumerate(("qscale", "kscale")):
                last = nc.tensor.matmul(rows[:, 0, 64 * k:64 * k + 64], m.ones[0:1, :], w[name][:, 64 * l:64 * l + 64],
                                        start=True, stop=True)
            last.then_inc(rows_done, 1)

        @block.vector
        def _(dve):
            dve.wait_ge(rows_done, 1)
            nc.vector.tensor_copy(spread[:], rows[:, 0, 0:P].rearrange("p (k d) -> p k d", k=2)).then_inc(spread_done, 1)
            dve.wait_ge(spread_done, 1)
            for k in range(2):
                cos, sin = (tables[2 * k + j].rearrange("p (t d) -> p t d", d=64) for j in range(2))
                nc.vector.tensor_tensor(scaled[:, 2 * k, :, :], cos,
                                        spread[:, k, :].unsqueeze(1).broadcast_to([P, TPB, 64]), ALU.mult).then_inc(done, 1)
                for half in range(2):
                    mine, other = slice(32 * half, 32 * half + 32), slice(32 - 32 * half, 64 - 32 * half)
                    nc.vector.tensor_tensor(scaled[:, 2 * k + 1, :, mine], sin[:, :, mine],
                                            spread[:, k, other].unsqueeze(1).broadcast_to([P, TPB, 32]),
                                            ALU.mult).then_inc(done, 1)


def rotary_qkv(nc, m, w, l, b, ZS, scaled, qT, kT, v, qnorm):
    with Phase(nc, f"qkv{l}{b}") as ph:
        HS = ph.sb("HS", [P, WIN + SEQ])
        squares = ph.sb("squares", [P, 2, 2, BANK])
        sumsq = ph.sb("sumsq", [P, 2, 16])
        rnorm = ph.sb("rnorm", [P, 2, 16])
        cospart = ph.sb("cospart", [P, 2, 2, BANK])
        sinpart = ph.sb("sinpart", [P, 2, 2, BANK])
        rotated = ph.sb("rotated", [P, 2, 2, BANK])
        proj = ph.ps("proj", 4)
        vps = ph.ps("vps", 2)
        turned = ph.ps("turned", 2)
        (hs_turned, hs_kept, cleared, qk_done, sq_done, sum_done, clamp_done, rnorm_done, cs_done, add_done, rot_done,
         t_done, t_kept, v_done, v_kept, qn_done) = (
            ph.sem(x) for x in ("hs_turned", "hs_kept", "cleared", "qk_done", "sq_done", "sum_done", "clamp_done",
                                "rnorm_done", "cs_done", "add_done", "rot_done", "t_done", "t_kept", "v_done", "v_kept",
                                "qn_done"))
        block = ph.block()
        wl = w["wqkv"][:, 1536 * l:1536 * (l + 1)]

        @block.tensor
        def _(pe):
            for half in range(2):
                for j in range(4):
                    last = nc.tensor.transpose(turned[:, half, j * P:(j + 1) * P], ZS[:, b * TPB + 4 * half + j, :],
                                               m.ident[:])
                last.then_inc(hs_turned, 1)
            pe.wait_ge(hs_kept, 2)
            pe.wait_ge(cleared, 2)

            def values(i):
                n = P if i < TPB else WIN
                if i >= 2:
                    pe.wait_ge(v_kept, i - 1)
                nc.tensor.matmul(vps[0:n, i % 2, :], HS[:, i * P:i * P + n], wl[:, 1024:1536], start=True,
                                 stop=True).then_inc(v_done, 1)

            def turn(i):
                for k in range(2):
                    pe.wait_ge(rot_done, 2 * i + k + 1)
                    if i >= 1:
                        pe.wait_ge(t_kept, 2 * i - 1 + k)
                    for c in range(4):
                        last = nc.tensor.transpose(turned[:, k, c * P:(c + 1) * P],
                                                   rotated[:, i % 2, k, c * P:(c + 1) * P], m.ident[:])
                    last.then_inc(t_done, 1)
            for i in range(TPB):
                if i >= 2:
                    pe.wait_ge(cs_done, 6 * (i - 1))
                    pe.wait_ge(sq_done, 2 * (i - 1))
                for k in range(2):
                    nc.tensor.matmul(proj[:, 2 * (i % 2) + k, :], HS[:, WIN + i * P:WIN + (i + 1) * P],
                                     wl[:, k * BANK:(k + 1) * BANK], start=True, stop=True).then_inc(qk_done, 1)
                values(i)
                if i >= 1:
                    turn(i - 1)
            values(TPB)
            turn(TPB - 1)

        @block.scalar
        def _(act):
            for half in range(2):
                act.wait_ge(hs_turned, half + 1)
                nc.scalar.activation(HS[:, WIN + half * BANK:WIN + (half + 1) * BANK], turned[:, half, :],
                                     ACT.Copy).then_inc(hs_kept, 1)

            def keep(i):
                for k, to in enumerate((qT[:, :, i * P:(i + 1) * P], kT[:, :, WIN + i * P:WIN + (i + 1) * P])):
                    act.wait_ge(t_done, 2 * i + k + 1)
                    nc.scalar.activation(to, turned[:, k, :].rearrange("p (c n) -> p c n", c=4), ACT.Copy).then_inc(t_kept, 1)

            def keep_v(i):
                n = P if i < TPB else WIN
                act.wait_ge(v_done, i + 1)
                nc.scalar.activation(v[0:n, i, :], vps[0:n, i % 2, :], ACT.Copy).then_inc(v_kept, 1)
            for i in range(TPB):
                for k in range(2):
                    act.wait_ge(qk_done, 2 * i + k + 1)
                    if i >= 2:
                        act.wait_ge(sum_done, i - 1)
                    nc.scalar.activation(squares[:, i % 2, k, :], proj[:, 2 * (i % 2) + k, :], ACT.Square).then_inc(sq_done, 1)
                keep_v(i)
                if i >= 1:
                    keep(i - 1)
            keep_v(TPB)
            keep(TPB - 1)

        def scale_k(dve, i):
            dve.wait_ge(rnorm_done, i + 1)
            nc.vector.tensor_scalar(qnorm[:, i, :], rnorm[:, i % 2, 0:8], 8.0, None, ALU.mult)
            dve.wait_ge(add_done, 2 * i + 1)
            dve.sem_inc(rot_done, 1)
            dve.wait_ge(add_done, 2 * i + 2)
            kr = rotated[:, i % 2, 1, :].rearrange("p (h d) -> p h d", d=64)
            nc.vector.tensor_tensor(kr, kr, rnorm[:, i % 2, 8:16].unsqueeze(2).broadcast_to([P, 8, 64]),
                                    ALU.mult).then_inc(qn_done, 1)
            dve.wait_ge(qn_done, i + 1)
            dve.sem_inc(rot_done, 1)

        @block.vector
        def _(dve):
            nc.vector.memset(HS[:, 0:WIN], 0.0).then_inc(cleared, 1)
            nc.vector.memset(kT[:, :, 0:WIN], 0.0).then_inc(cleared, 1)
            for i in range(TPB):
                dve.wait_ge(sq_done, 2 * i + 2)
                nc.vector.tensor_reduce(sumsq[:, i % 2, :], squares[:, i % 2, :, :].rearrange("p k (h d) -> p (k h) d", d=64),
                                        AX, ALU.add).then_inc(sum_done, 1)
                dve.wait_ge(sum_done, i + 1)
                if i >= 2:
                    dve.wait_ge(qn_done, i - 1)
                nc.vector.tensor_scalar(rnorm[:, i % 2, :], sumsq[:, i % 2, :], 1e-24, None, ALU.max).then_inc(clamp_done, 1)
                if i >= 2:
                    dve.wait_ge(add_done, 2 * (i - 1))
                for k in range(2):
                    src = proj[:, 2 * (i % 2) + k, :].rearrange("p (h d) -> p h d", d=64)
                    cos = scaled[:, 2 * k, i, :].unsqueeze(1).broadcast_to([P, 8, 64])
                    nc.vector.tensor_tensor(cospart[:, i % 2, k, :].rearrange("p (h d) -> p h d", d=64), src, cos,
                                            ALU.mult).then_inc(cs_done, 1)
                    for half in range(2):
                        mine, other = slice(32 * half, 32 * half + 32), slice(32 - 32 * half, 64 - 32 * half)
                        nc.vector.tensor_tensor(sinpart[:, i % 2, k, :].rearrange("p (h d) -> p h d", d=64)[:, :, mine],
                                                src[:, :, other],
                                                scaled[:, 2 * k + 1, i, mine].unsqueeze(1).broadcast_to([P, 8, 32]),
                                                ALU.mult).then_inc(cs_done, 1)
                if i >= 1:
                    scale_k(dve, i - 1)
            scale_k(dve, TPB - 1)

        @block.gpsimd
        def _(pool):
            for i in range(TPB):
                pool.wait_ge(clamp_done, i + 1)
                nc.gpsimd.tensor_tensor(rnorm[:, i % 2, :], rnorm[:, i % 2, :], m.neghalf[:], ALU.pow).then_inc(rnorm_done, 1)
                for k in range(2):
                    pool.wait_ge(cs_done, 6 * i + 3 * k + 3)
                    if i >= 2:
                        pool.wait_ge(t_done, 2 * (i - 2) + k + 1)
                    nc.gpsimd.tensor_tensor(rotated[:, i % 2, k, :], cospart[:, i % 2, k, :], sinpart[:, i % 2, k, :],
                                            ALU.add).then_inc(add_done, 1)


def local_attention(nc, m, w, l, b, Z, qT, kT, v, qnorm, band_first):
    with Phase(nc, f"local{l}{b}") as ph:
        probs = ph.sb("probs", [P, 2, 4, SPAN])
        probsT = ph.sb("probsT", [P, 2, 4, 2 * P])
        rowmax = ph.sb("rowmax", [P, 2, 4])
        negmax = ph.sb("negmax", [P, 2, 4])
        rowsum = ph.sb("rowsum", [P, 2, 8])
        o = ph.sb("o", [P, BANK])
        oT = ph.sb("oT", [P, BANK])
        score = ph.ps("score", 4)
        turned = ph.ps("turned", 2)
        outp = ph.ps("outp", 1)
        misc = ph.ps("misc", 1)
        (s_done, chain_sem, negmax_done, exp_done, t_done, t_kept, pv_done, o_done, ot_done, ot_kept, y_done, z_done) = (
            ph.sem(x) for x in ("s_done", "chain", "negmax_done", "exp_done", "t_done", "t_kept", "pv_done", "o_done",
                                "ot_done", "ot_kept", "y_done", "z_done"))
        block = ph.block()
        N = 2 * TPB
        wo = w["wo"][:, 512 * l:512 * (l + 1)]
        HEADS = [(c, j) for c in range(2) for j in range(2)]

        def score_at(n, c, j):
            return score[:, 2 * (n % 2) + j, 256 * c:256 * c + SPAN]

        @block.tensor
        def _(pe):
            def scores(n):
                i, q4 = n // 2, n % 2
                if n >= 2:
                    pe.wait_ge(exp_done, 4 * (n - 1))
                for j in range(2):
                    for c in range(2):
                        cc = 2 * q4 + c
                        last = nc.tensor.matmul(score_at(n, c, j), qT[64 * j:64 * j + 64, cc, i * P:(i + 1) * P],
                                                kT[64 * j:64 * j + 64, cc, i * P:i * P + SPAN], start=True, stop=True)
                last.then_inc(s_done, 1)

            def turn(n):
                pe.wait_ge(exp_done, 4 * (n + 1))
                for pair in range(2):
                    e = 2 * n + pair
                    if e >= 2:
                        pe.wait_ge(t_kept, e - 1)
                    for k in range(2):
                        hh = 2 * pair + k
                        nc.tensor.transpose(turned[:, e % 2, 256 * k:256 * k + P], probs[:, n % 2, hh, 0:P], m.ident[:])
                        last = nc.tensor.transpose(turned[0:WIN, e % 2, 256 * k + P:256 * k + 2 * P],
                                                   probs[:, n % 2, hh, P:SPAN], m.ident[:])
                    last.then_inc(t_done, 1)

            def values(n):
                i, q4 = n // 2, n % 2
                pe.wait_ge(t_kept, 2 * (n + 1))
                if q4 == 0 and i > 0:
                    pe.wait_ge(o_done, i)
                for hh, (c, j) in enumerate(HEADS):
                    h = 2 * (2 * q4 + c) + j
                    to = outp[:, 0, 64 * h:64 * h + 64]
                    nc.tensor.matmul(to, probsT[:, n % 2, hh, 0:P], v[:, i, 64 * h:64 * h + 64], start=True, stop=False)
                    last = nc.tensor.matmul(to, probsT[0:WIN, n % 2, hh, P:2 * P], v[0:WIN, i + 1, 64 * h:64 * h + 64],
                                            start=False, stop=True)
                last.then_inc(pv_done, 1)

            def project(i):
                pe.wait_ge(o_done, i + 1)
                if i > 0:
                    pe.wait_ge(z_done, i)
                for c in range(4):
                    last = nc.tensor.transpose(misc[:, 0, c * P:(c + 1) * P], o[:, c * P:(c + 1) * P], m.ident[:])
                last.then_inc(ot_done, 1)
                pe.wait_ge(ot_kept, i + 1)
                for c in range(4):
                    last = nc.tensor.matmul(misc[:, 0, 0:P], oT[:, c * P:(c + 1) * P], wo[:, c * P:(c + 1) * P],
                                            start=(c == 0), stop=(c == 3))
                last.then_inc(y_done, 1)
            for n in range(N + 3):
                if n < N:
                    scores(n)
                if 1 <= n <= N:
                    turn(n - 1)
                if 2 <= n <= N + 1:
                    values(n - 2)
                if n >= 4 and n % 2 == 0:
                    project(n // 2 - 2)

        @block.scalar
        def _(act):
            def keep(n):
                if n >= 2:
                    act.wait_ge(pv_done, n - 1)
                for pair in range(2):
                    e = 2 * n + pair
                    act.wait_ge(t_done, e + 1)
                    to, src = probsT[:, n % 2, 2 * pair:2 * pair + 2, :], turned[:, e % 2, :].rearrange("p (k q) -> p k q", k=2)
                    nc.scalar.activation(to[:, :, 0:P], src[:, :, 0:P], ACT.Copy)
                    nc.scalar.activation(to[0:WIN, :, P:2 * P], src[0:WIN, :, P:2 * P], ACT.Copy).then_inc(t_kept, 1)
            for n in range(N + 1):
                if n < N:
                    i, q4 = n // 2, n % 2
                    act.wait_ge(negmax_done, n + 1)
                    if n >= 2:
                        act.wait_ge(t_done, 2 * (n - 1))
                    if n >= 4:
                        act.wait_ge(o_done, i - 1)
                    for hh, (c, j) in enumerate(HEADS):
                        h = 2 * (2 * q4 + c) + j
                        nc.scalar.activation(probs[:, n % 2, hh, :], score_at(n, c, j), ACT.Exp,
                                             bias=negmax[:, n % 2, hh:hh + 1], scale=qnorm[:, i, h:h + 1],
                                             accum_out=rowsum[:, i % 2, h:h + 1]).then_inc(exp_done, 1)
                if n >= 1:
                    keep(n - 1)

        @block.vector
        def _(dve):
            chain = Chain(dve, chain_sem)

            def finish(i):
                dve.wait_ge(pv_done, 2 * (i + 1))
                if i > 0:
                    dve.wait_ge(ot_done, i)
                chain.step(nc.vector.reciprocal(rowsum[:, i % 2, :], rowsum[:, i % 2, :]))
                nc.vector.tensor_tensor(o[:].rearrange("p (h d) -> p h d", d=64),
                                        outp[:, 0, :].rearrange("p (h d) -> p h d", d=64),
                                        rowsum[:, i % 2, :].unsqueeze(2).broadcast_to([P, 8, 64]), ALU.mult).then_inc(o_done, 1)
                dve.wait_ge(ot_done, i + 1)
                nc.vector.tensor_copy(oT[:], misc[:, 0, :]).then_inc(ot_kept, 1)

            def add(i):
                dve.wait_ge(y_done, i + 1)
                t = b * TPB + i
                nc.vector.tensor_tensor(Z[:, t, :], misc[:, 0, 0:P], Z[:, t, :], ALU.add).then_inc(z_done, 1)
            for n in range(N):
                i, q4 = n // 2, n % 2
                dve.wait_ge(s_done, n + 1)
                band = band_first if i == 0 else m.band
                for j in range(2):
                    sj = score[:, 2 * (n % 2) + j, :].rearrange("p (c k) -> p c k", c=2)[:, :, 0:SPAN]
                    last = nc.vector.tensor_tensor(sj, sj, band[:].unsqueeze(1).broadcast_to([P, 2, SPAN]), ALU.add)
                chain.step(last)
                for j in range(2):
                    sj = score[:, 2 * (n % 2) + j, :].rearrange("p (c k) -> p c k", c=2)[:, :, 0:SPAN]
                    last = nc.vector.tensor_reduce(rowmax[:, n % 2, j:4:2], sj, AX, ALU.max)
                chain.step(last)
                if n >= 2:
                    dve.wait_ge(exp_done, 4 * (n - 1))
                q4n = qnorm[:, i, 4 * q4:4 * q4 + 4]
                nc.vector.scalar_tensor_tensor(out=negmax[:, n % 2, :], in0=rowmax[:, n % 2, :], scalar=-1.0, in1=q4n,
                                               op0=ALU.mult, op1=ALU.mult).then_inc(negmax_done, 1)
                if n >= 4 and n % 2 == 0:
                    if n >= 6:
                        add(n // 2 - 3)
                    finish(n // 2 - 2)
            for i in range(TPB - 2, TPB):
                add(i - 1)
                finish(i)
            add(TPB - 1)


def gated_mlp(nc, m, w, l, Z, ZS, into):
    with Phase(nc, f"mlp{l}") as ph:
        stats = ph.sb("stats", [P, NT, 6])
        mv = ph.sb("mv", [P, NT, 2])
        rstd = ph.sb("rstd", [P, NT])
        shift = ph.sb("shift", [P, NT])
        gelu = ph.sb("gelu", [P, 2, BANK])
        hidden = ph.sb("hidden", [P, 2, 3, BANK])
        turned = ph.ps("turned", 2)
        agp = ph.ps("agp", 4)
        down = ph.ps("down", 2)
        (stat_done, aggr_done, var_done, rstd_done, shift_done, norm_done, turn_done, turn_kept, ag_done, gelu_done,
         hid_done, down_done, z_done) = (
            ph.sem(x) for x in ("stat_done", "aggr_done", "var_done", "rstd_done", "shift_done", "norm_done",
                                "turn_done", "turn_kept", "ag_done", "gelu_done", "hid_done", "down_done", "z_done"))
        block = ph.block()
        w1 = w["w1"][:, 2 * HID * l:2 * HID * (l + 1)]
        w2 = w["w2"][:, 384 * l:384 * (l + 1)]
        b1 = w["b1"][:, 6 * l:6 * (l + 1)]
        b2 = w["b2"][:, P * l:P * (l + 1)]
        ROWS = [P, P, HID - 2 * P]
        UNITS = [(tc, c) for tc in range(NT // 4) for c in range(3)]

        @block.vector
        def _(dve):
            for t in range(NT):
                nc.vector.bn_stats(stats[:, t, :], ZS[:, t, :]).then_inc(stat_done, 1)
            for t in range(NT):
                dve.wait_ge(stat_done, t + 1)
                nc.vector.bn_aggr(mv[:, t, :], stats[:, t, :]).then_inc(aggr_done, 1)
            dve.wait_ge(aggr_done, NT)
            nc.vector.tensor_scalar(rstd[:], mv[:, :, 1], LN_EPS, None, ALU.add).then_inc(var_done, 1)
            dve.wait_ge(rstd_done, 1)
            nc.vector.scalar_tensor_tensor(out=shift[:], in0=mv[:, :, 0], scalar=-1.0, in1=rstd[:], op0=ALU.mult,
                                           op1=ALU.mult).then_inc(shift_done, 1)
            for c in range(NT // 4):
                dve.wait_ge(turn_done, c + 1)
                nc.vector.tensor_scalar(m.HT[:, c * BANK:(c + 1) * BANK], turned[:, c % 2, :], w["lng"][:, l:l + 1],
                                        w["lnb"][:, l:l + 1], ALU.mult, ALU.add).then_inc(turn_kept, 1)
            for n, (tc, c) in enumerate(UNITS):
                r = ROWS[c]
                dve.wait_ge(gelu_done, n + 1)
                dve.wait_ge(ag_done, 2 * n + 2)
                if tc >= 2:
                    dve.wait_ge(down_done, tc - 1)
                nc.vector.scalar_tensor_tensor(out=hidden[0:r, tc % 2, c, :], in0=agp[0:r, 2 * (n % 2), :],
                                               scalar=b1[0:r, c:c + 1], in1=gelu[0:r, n % 2, :], op0=ALU.add,
                                               op1=ALU.mult).then_inc(hid_done, 1)
                if c == 2:
                    dve.wait_ge(down_done, tc + 1)
                    nc.vector.tensor_tensor(into[:, 4 * tc:4 * tc + 4, :], down[:, tc % 2, :].rearrange("p (t n) -> p t n", t=4),
                                            Z[:, 4 * tc:4 * tc + 4, :], ALU.add).then_inc(z_done, 1)

        @block.gpsimd
        def _(pool):
            pool.wait_ge(var_done, 1)
            nc.gpsimd.tensor_tensor(rstd[:], rstd[:], m.neghalf[:], ALU.pow).then_inc(rstd_done, 1)

        @block.scalar
        def _(act):
            act.wait_ge(shift_done, 1)
            for t in range(NT):
                nc.scalar.activation(ZS[:, t, :], ZS[:, t, :], ACT.Identity, bias=shift[:, t:t + 1],
                                     scale=rstd[:, t:t + 1]).then_inc(norm_done, 1)
            for n, (tc, c) in enumerate(UNITS):
                r = ROWS[c]
                act.wait_ge(ag_done, 2 * n + 2)
                if n >= 2:
                    act.wait_ge(hid_done, n - 1)
                nc.scalar.activation(gelu[0:r, n % 2, :], agp[0:r, 2 * (n % 2) + 1, :], ACT.Gelu,
                                     bias=b1[0:r, 3 + c:4 + c]).then_inc(gelu_done, 1)

        @block.tensor
        def _(pe):
            for c in range(NT // 4):
                pe.wait_ge(norm_done, 4 * (c + 1))
                if c >= 2:
                    pe.wait_ge(turn_kept, c - 1)
                for j in range(4):
                    last = nc.tensor.transpose(turned[:, c % 2, j * P:(j + 1) * P], ZS[:, 4 * c + j, :], m.ident[:])
                last.then_inc(turn_done, 1)
            pe.wait_ge(turn_kept, NT // 4)

            def project(tc):
                pe.wait_ge(hid_done, 3 * (tc + 1))
                if tc >= 2:
                    pe.wait_ge(z_done, tc - 1)
                for j in range(4):
                    to = down[:, tc % 2, j * P:(j + 1) * P]
                    for c in range(3):
                        r = ROWS[c]
                        nc.tensor.matmul(to, hidden[0:r, tc % 2, c, j * P:(j + 1) * P], w2[0:r, c * P:(c + 1) * P],
                                         start=(c == 0), stop=False)
                    last = nc.tensor.matmul(to, m.ones[0:1, :], b2, start=False, stop=True)
                last.then_inc(down_done, 1)
            for n, (tc, c) in enumerate(UNITS):
                r = ROWS[c]
                if n >= 2:
                    pe.wait_ge(hid_done, n - 1)
                for k in range(2):
                    at = k * HID + c * P
                    nc.tensor.matmul(agp[0:r, 2 * (n % 2) + k, :], w1[:, at:at + r], m.HT[:, tc * BANK:(tc + 1) * BANK],
                                     start=True, stop=True).then_inc(ag_done, 1)
                if c == 2:
                    project(tc)


def local_transformer(nc, m, dram, s):
    w = weight_views(m, s)
    with ExitStack() as keep:
        def kept(name, shape):
            return keep.enter_context(nc.sbuf_tensor(f"loc_{name}", shape, F32))
        ZS = kept("ZS", [P, NT, P])
        scaled = kept("scaled", [P, 4, TPB, 64])
        qT = kept("qT", [P, 4, SEQ])
        kT = kept("kT", [P, 4, WIN + SEQ])
        v = kept("v", [P, TPB + 1, BANK])
        qnorm = kept("qnorm", [P, TPB, 8])
        band_first = kept("band_first", [P, SPAN])
        Z = m.XN
        with Phase(nc, "locfirst") as ph:
            copied = ph.sem("copied")
            block = ph.block()

            @block.sync
            def _(sp):
                sp.wait_ge(m.wsem[s], 16)
                load_weights(sp, m, dram, s + 1)

            @block.gpsimd
            def _(pool):
                nc.gpsimd.tensor_copy(band_first[:, WIN:SPAN], m.band[:, WIN:SPAN]).then_inc(copied, 1)
                nc.gpsimd.memset(band_first[:, 0:WIN], NEG).then_inc(copied, 1)
        tables = [w[k] for k in ("cosq", "sinq", "cosk", "sink")]
        for l in range(LAYERS):
            rotary_scale_phase(nc, m, w, l, tables, scaled)
            shift_tokens(nc, m, f"shifta{l}", Z, ZS)
            for b in range(BATCH):
                rotary_qkv(nc, m, w, l, b, ZS, scaled, qT, kT, v, qnorm)
                local_attention(nc, m, w, l, b, Z, qT, kT, v, qnorm, band_first)
            shift_tokens(nc, m, f"shiftb{l}", Z, ZS)
            gated_mlp(nc, m, w, l, Z, ZS, m.Y if l == 1 else Z)


DI, NS, RANK, TAPS = 256, 16, 64, 4
NCH = DI // P


def mamba_norm(nc, m, U):
    with Phase(nc, "mnorm") as ph:
        stats = ph.sb("stats", [P, NT, 6])
        mv = ph.sb("mv", [P, NT, 2])
        rstd = ph.sb("rstd", [P, NT])
        shift = ph.sb("shift", [P, NT])
        stat_done, aggr_done, var_done, rstd_done, shift_done, norm_done = (
            ph.sem(x) for x in ("stat_done", "aggr_done", "var_done", "rstd_done", "shift_done", "norm_done"))
        block = ph.block()

        @block.vector
        def _(dve):
            for t in range(NT):
                nc.vector.bn_stats(stats[:, t, :], m.XN[:, t, :]).then_inc(stat_done, 1)
            for t in range(NT):
                dve.wait_ge(stat_done, t + 1)
                nc.vector.bn_aggr(mv[:, t, :], stats[:, t, :]).then_inc(aggr_done, 1)
            dve.wait_ge(aggr_done, NT)
            nc.vector.tensor_scalar(rstd[:], mv[:, :, 1], LN_EPS, None, ALU.add).then_inc(var_done, 1)
            dve.wait_ge(rstd_done, 1)
            nc.vector.scalar_tensor_tensor(out=shift[:], in0=mv[:, :, 0], scalar=-1.0, in1=rstd[:], op0=ALU.mult,
                                           op1=ALU.mult).then_inc(shift_done, 1)

        @block.gpsimd
        def _(pool):
            pool.wait_ge(var_done, 1)
            nc.gpsimd.tensor_tensor(rstd[:], rstd[:], m.neghalf[:], ALU.pow).then_inc(rstd_done, 1)

        @block.scalar
        def _(act):
            act.wait_ge(shift_done, 1)
            for t in range(NT):
                nc.scalar.activation(U[:, t, :], m.XN[:, t, :], ACT.Identity, bias=shift[:, t:t + 1],
                                     scale=rstd[:, t:t + 1]).then_inc(norm_done, 1)


def mamba_setup(nc, m, dram, s, w, select, negA, Wx3):
    with Phase(nc, "msetup") as ph:
        sel_done, a_done, x_done = ph.sem("sel_done"), ph.sem("a_done"), ph.sem("x_done")
        block = ph.block()

        @block.sync
        def _(sp):
            sp.wait_ge(m.wsem[s], 16)
            load_weights(sp, m, dram, s + 1)

        @block.gpsimd
        def _(pool):
            nc.gpsimd.memset(select[:], 0.0).then_inc(sel_done, 1)
            for r in range(3):
                pool.wait_ge(sel_done, r + 1)
                nc.gpsimd.affine_select(out=select[:], in_=select[:], compare_op=ALU.not_equal, fill=1.0, base=-32 * r,
                                        pattern=[[-1, 2 * NS], [0, P]], channel_multiplier=1).then_inc(sel_done, 1)

        @block.scalar
        def _(act):
            act.wait_ge(m.wsem[s], 16)
            nc.scalar.activation(negA[:], w["Alog"], ACT.Exp).then_inc(a_done, 1)

        @block.vector
        def _(dve):
            dve.wait_ge(m.wsem[s], 16)
            for r in range(3):
                nc.vector.tensor_copy(Wx3[:, :, 2 * NS * r:2 * NS * (r + 1)],
                                      w["Wx"].rearrange("p (q n) -> p q n", n=RANK + 2 * NS)[:, :, RANK:RANK + 2 * NS]
                                      ).then_inc(x_done, 1)
            dve.wait_ge(a_done, 1)
            nc.vector.tensor_scalar(negA[:], negA[:], -1.0, None, ALU.mult).then_inc(x_done, 1)


def mamba_front(nc, m, w, d, b, U, xc, sz, delta, du, BC3, Wx3):
    with Phase(nc, f"front{d}{b}") as ph:
        UT = ph.sb("UT", [P, SEQ])
        padded = ph.sb("padded", [P, NCH, TAPS - 1 + SEQ])
        conv = ph.sb("conv", [P, NCH, SEQ])
        dt = ph.sb("dt", [RANK, SEQ])
        bchi = ph.sb("bchi", [96, SEQ], BF16)
        bcmid = ph.sb("bcmid", [96, SEQ], BF16)
        rest = ph.sb("rest", [96, SEQ])
        soft = ph.sb("soft", [P, 4, BANK])
        ring = ph.ps("ring", 4)
        dbl = ph.ps("dbl", 4)
        (turn_done, turn_kept, padded_clear, in_done, in_kept, conv_sem, conv_done, xc_done, dbl_done, dt_kept, dl_done,
         relu_done, abs_done, exp_done, ln_done, delta_done, chain_sem) = (
            ph.sem(x) for x in ("turn_done", "turn_kept", "padded_clear", "in_done", "in_kept", "conv_sem", "conv_done",
                                "xc_done", "dbl_done", "dt_kept", "dl_done", "relu_done", "abs_done", "exp_done",
                                "ln_done", "delta_done", "chain"))
        block = ph.block()
        Win = w["Win"][:, 2 * DI * d:2 * DI * (d + 1)]
        bin_ = w["bin"][:, 4 * d:4 * (d + 1)]
        bdt = w["bdt"][:, 2 * d:2 * (d + 1)]

        @block.tensor
        def _(pe):
            for half in range(2):
                for j in range(4):
                    i = 4 * half + j
                    t = b * TPB + (i if d == 0 else TPB - 1 - i)
                    to = dbl[:, half, j * P:(j + 1) * P]
                    if d == 0:
                        last = nc.tensor.transpose(to, U[:, t, :], m.ident[:])
                    else:
                        last = nc.tensor.matmul(to, U[:, t, :], m.flip[:], start=True, stop=True)
                last.then_inc(turn_done, 1)
            pe.wait_ge(turn_kept, 2)
            for u in range(8):
                if u >= 4:
                    pe.wait_ge(in_kept, u - 3)
                nc.tensor.matmul(ring[:, u % 4, :], Win[:, u // 2 * P:(u // 2 + 1) * P],
                                 UT[:, u % 2 * BANK:(u % 2 + 1) * BANK], start=True, stop=True).then_inc(in_done, 1)
            pe.wait_ge(xc_done, NCH)
            for half in range(2):
                rhs = [xc[:, ch, half * BANK:(half + 1) * BANK] for ch in range(NCH)]
                for ch in range(NCH):
                    q = (NCH * d + ch) * (RANK + 2 * NS)
                    last = nc.tensor.matmul(dbl[0:RANK, 2 * half, :], w["Wx"][:, q:q + RANK], rhs[ch], start=(ch == 0),
                                            stop=(ch == NCH - 1))
                last.then_inc(dbl_done, 1)
                for ch in range(NCH):
                    last = nc.tensor.matmul(dbl[0:96, 2 * half + 1, :], Wx3[:, NCH * d + ch, :], rhs[ch],
                                            start=(ch == 0), stop=(ch == NCH - 1))
                last.then_inc(dbl_done, 1)
            pe.wait_ge(in_kept, 8)
            for ch in range(NCH):
                for half in range(2):
                    pe.wait_ge(dt_kept, half + 1)
                    nc.tensor.matmul(ring[:, 2 * ch + half, :], w["Wdt"][:, DI * d + ch * P:DI * d + (ch + 1) * P],
                                     dt[:, half * BANK:(half + 1) * BANK], start=True, stop=True).then_inc(dl_done, 1)

        @block.scalar
        def _(act):
            act.wait_ge(padded_clear, 1)
            for u in range(8):
                act.wait_ge(in_done, u + 1)
                c, half = u // 2, u % 2
                if c < NCH:
                    nc.scalar.activation(padded[:, c, TAPS - 1 + half * BANK:TAPS - 1 + (half + 1) * BANK],
                                         ring[:, u % 4, :], ACT.Identity, bias=bin_[:, c:c + 1]).then_inc(in_kept, 1)
                else:
                    nc.scalar.activation(sz[:, c - NCH, half * BANK:(half + 1) * BANK], ring[:, u % 4, :], ACT.Silu,
                                         bias=bin_[:, c:c + 1]).then_inc(in_kept, 1)
            for ch in range(NCH):
                act.wait_ge(conv_done, ch + 1)
                nc.scalar.activation(xc[:, ch, :], conv[:, ch, :], ACT.Silu).then_inc(xc_done, 1)
            for half in range(2):
                act.wait_ge(dbl_done, 2 * half + 1)
                nc.scalar.activation(dt[:, half * BANK:(half + 1) * BANK], dbl[0:RANK, 2 * half, :],
                                     ACT.Copy).then_inc(dt_kept, 1)
            for u in range(4):
                act.wait_ge(dl_done, u + 1)
                nc.scalar.activation(soft[:, u, :], ring[:, u, :], ACT.Abs, bias=bdt[:, u // 2:u // 2 + 1]).then_inc(abs_done, 1)
            act.wait_ge(abs_done, 4)
            nc.scalar.activation(soft[:], soft[:], ACT.Exp, scale=-1.0).then_inc(exp_done, 1)
            act.wait_ge(exp_done, 1)
            nc.scalar.activation(soft[:], soft[:], ACT.Ln, bias=1.0).then_inc(ln_done, 1)

        @block.vector
        def _(dve):
            chain = Chain(dve, chain_sem)
            nc.vector.memset(padded[:, :, 0:TAPS - 1], 0.0).then_inc(padded_clear, 1)
            for half in range(2):
                dve.wait_ge(turn_done, half + 1)
                nc.vector.tensor_scalar(UT[:, half * BANK:(half + 1) * BANK], dbl[:, half, :], w["lnw"][:, d:d + 1],
                                        w["lnb"][:, d:d + 1], ALU.mult, ALU.add).then_inc(turn_kept, 1)
            for ch in range(NCH):
                dve.wait_ge(in_kept, 2 * ch + 2)
                taps = w["convw"][:, (NCH * d + ch) * TAPS:(NCH * d + ch + 1) * TAPS]
                cb = w["convb"][:, NCH * d + ch:NCH * d + ch + 1]
                chain.step(nc.vector.tensor_scalar(conv[:, ch, :], padded[:, ch, 0:SEQ], taps[:, 0:1], cb, ALU.mult, ALU.add))
                for k in range(1, TAPS):
                    chain.step(nc.vector.scalar_tensor_tensor(out=conv[:, ch, :], in0=padded[:, ch, k:k + SEQ],
                                                              scalar=taps[:, k:k + 1], in1=conv[:, ch, :],
                                                              op0=ALU.mult, op1=ALU.add))
                dve.sem_inc(conv_done, 1)
            for half in range(2):
                dve.wait_ge(dbl_done, 2 * half + 2)
                cols_ = slice(half * BANK, (half + 1) * BANK)
                src = dbl[0:96, 2 * half + 1, :]
                chain.step(nc.vector.tensor_copy(bchi[:, cols_], src))
                chain.step(nc.vector.tensor_tensor(rest[:, cols_], src, bchi[:, cols_], ALU.subtract))
                chain.step(nc.vector.tensor_copy(bcmid[:, cols_], rest[:, cols_]))
                chain.step(nc.vector.tensor_tensor(rest[:, cols_], rest[:, cols_], bcmid[:, cols_], ALU.subtract))
                nc.vector.tensor_copy(BC3[0:32, cols_], bchi[0:32, cols_])
                nc.vector.tensor_copy(BC3[32:64, cols_], bcmid[32:64, cols_])
                chain.step(nc.vector.tensor_copy(BC3[64:96, cols_], rest[64:96, cols_]))
            for u in range(4):
                dve.wait_ge(dl_done, u + 1)
                dve.wait_ge(abs_done, u + 1)
                nc.vector.tensor_scalar(delta[:, u // 2, u % 2 * BANK:(u % 2 + 1) * BANK], ring[:, u, :],
                                        bdt[:, u // 2:u // 2 + 1], 0.0, ALU.add, ALU.max).then_inc(relu_done, 1)
            dve.wait_ge(ln_done, 1)
            dve.wait_ge(relu_done, 4)
            dall = delta[:].rearrange("p c t -> p (c t)")
            chain.step(nc.vector.tensor_tensor(dall, dall, soft[:].rearrange("p u t -> p (u t)"), ALU.add))
            chain.step(nc.vector.tensor_tensor(du[:], delta[:], xc[:], ALU.mult))


def mamba_scan(nc, m, w, d, b, xc, sz, delta, du, BC3, select, negA, outT):
    with Phase(nc, f"scan{d}{b}") as ph:
        decay = ph.sb("decay", [P, 4, SEQ])
        state = ph.sb("state", [P, 4, SEQ])
        back = ph.sb("back", [P, TPB, P])
        bspread = ph.ps("bspread", 2)
        cspread = ph.ps("cspread", 2)
        yacc = ph.ps("yacc", 4)
        (b_done, c_done, dec_done, in_done, scan_done, hc_done, y_used, y_done, gate_sem, gated, out_done, back_kept,
         flip_done, fin) = (
            ph.sem(x) for x in ("b_done", "c_done", "dec_done", "in_done", "scan_done", "hc_done", "y_used", "y_done",
                                "gate_sem", "gated", "out_done", "back_kept", "flip_done", "fin"))
        block = ph.block()
        Wout = w["Wout"][:, NCH * P * d:NCH * P * (d + 1)]

        @block.tensor
        def _(pe):
            def spread(n):
                for to, q, done in ((bspread, n, b_done), (cspread, NS + n, c_done)):
                    if n >= 1:
                        if done is b_done:
                            pe.wait_ge(in_done, 2 * n)
                        else:
                            pe.wait_ge(hc_done, 2 * n)
                    for half in range(2):
                        last = nc.tensor.matmul(to[:, half, :], select[:, q, :], BC3[:, half * BANK:(half + 1) * BANK],
                                                start=True, stop=True)
                    last.then_inc(done, 1)

            def accumulate(n):
                for ch in range(NCH):
                    k = NCH * n + ch
                    pe.wait_ge(hc_done, k + 1)
                    for half in range(2):
                        last = nc.tensor.matmul(yacc[:, 2 * ch + half, :], m.ident[:],
                                                state[:, k % 4, half * BANK:(half + 1) * BANK], start=(n == 0),
                                                stop=(n == NS - 1))
                    last.then_inc(y_used, 1)
            for n in range(NS):
                spread(n)
                if n >= 1:
                    accumulate(n - 1)
            accumulate(NS - 1)
            if d == 0:
                for half in range(2):
                    pe.wait_ge(gated, NCH)
                    for ch in range(NCH):
                        last = nc.tensor.matmul(bspread[:, half, :], Wout[:, ch * P:(ch + 1) * P],
                                                du[:, ch, half * BANK:(half + 1) * BANK], start=(ch == 0),
                                                stop=(ch == NCH - 1))
                    last.then_inc(flip_done, 1)
            else:
                pe.wait_ge(gated, NCH)
                for half in range(2):
                    for j in range(4):
                        i = 4 * half + j
                        for ch in range(NCH):
                            last = nc.tensor.matmul(cspread[:, half, j * P:(j + 1) * P], du[:, ch, i * P:(i + 1) * P],
                                                    Wout[:, ch * P:(ch + 1) * P], start=(ch == 0), stop=(ch == NCH - 1))
                    last.then_inc(out_done, 1)
                pe.wait_ge(back_kept, 2)
                for half in range(2):
                    for j in range(4):
                        i = TPB - 1 - (4 * half + j)
                        last = nc.tensor.matmul(bspread[:, half, j * P:(j + 1) * P], back[:, i, :], m.flip[:],
                                                start=True, stop=True)
                    last.then_inc(flip_done, 1)

        @block.scalar
        def _(act):
            for k in range(NCH * NS):
                n, ch = k // NCH, k % NCH
                if k >= 4:
                    act.wait_ge(scan_done, k - 3)
                a = (NCH * d + ch) * NS + n
                nc.scalar.activation(decay[:, k % 4, :], delta[:, ch, :], ACT.Exp,
                                     scale=negA[:, a:a + 1]).then_inc(dec_done, 1)

        @block.vector
        def _(dve):
            for n in range(NS):
                for ch in range(NCH):
                    k = NCH * n + ch
                    if k >= 4:
                        dve.wait_ge(y_used, k - 3)
                    dve.wait_ge(b_done, n + 1)
                    nc.vector.tensor_tensor(state[:, k % 4, :], bspread[:].rearrange("p a t -> p (a t)"), du[:, ch, :],
                                            ALU.mult).then_inc(in_done, 1)
                for ch in range(NCH):
                    k = NCH * n + ch
                    dve.wait_ge(in_done, k + 1)
                    dve.wait_ge(dec_done, k + 1)
                    nc.vector.tensor_tensor_scan(state[:, k % 4, :], decay[:, k % 4, :], state[:, k % 4, :], 0.0,
                                                 ALU.mult, ALU.add).then_inc(scan_done, 1)
                for ch in range(NCH):
                    k = NCH * n + ch
                    dve.wait_ge(scan_done, k + 1)
                    dve.wait_ge(c_done, n + 1)
                    nc.vector.tensor_tensor(state[:, k % 4, :], cspread[:].rearrange("p a t -> p (a t)"),
                                            state[:, k % 4, :], ALU.mult).then_inc(hc_done, 1)
            dve.wait_ge(y_used, NCH * NS)
            for ch in range(NCH):
                nc.vector.scalar_tensor_tensor(out=du[:, ch, :], in0=xc[:, ch, :],
                                               scalar=w["D"][:, NCH * d + ch:NCH * d + ch + 1],
                                               in1=yacc[:, 2 * ch:2 * ch + 2, :].rearrange("p a t -> p (a t)"),
                                               op0=ALU.mult, op1=ALU.add).then_inc(gate_sem, 1)
                dve.wait_ge(gate_sem, ch + 1)
                nc.vector.tensor_tensor(du[:, ch, :], du[:, ch, :], sz[:, ch, :], ALU.mult).then_inc(gated, 1)
            if d == 1:
                for half in range(2):
                    dve.wait_ge(out_done, half + 1)
                    nc.vector.tensor_copy(back[:, 4 * half:4 * half + 4, :].rearrange("p t n -> p (t n)"),
                                          cspread[:, half, :]).then_inc(back_kept, 1)
            for half in range(2):
                dve.wait_ge(flip_done, half + 1)
                at = b * SEQ + half * BANK
                nc.vector.scalar_tensor_tensor(out=outT[:, d, at:at + BANK], in0=bspread[:, half, :],
                                               scalar=w["bout"][:, d:d + 1], in1=m.HT[:, at:at + BANK], op0=ALU.add,
                                               op1=ALU.add).then_inc(fin, 1)


def mamba_gate(nc, m, w, outT):
    with Phase(nc, "mgate") as ph:
        total = ph.sb("total", [P, 2, BANK])
        gate = ph.sb("gate", [P, 2, BANK])
        mixed = ph.sb("mixed", [P, 2, BANK])
        gv = ph.ps("gv", 4)
        turned = ph.ps("turned", 2)
        chain_sem, gv_done, gate_done, mixed_done, turn_done, y_done = (
            ph.sem(x) for x in ("chain", "gv_done", "gate_done", "mixed_done", "turn_done", "y_done"))
        block = ph.block()
        CH = NT // 4

        def keep(act, c):
            act.wait_ge(turn_done, c + 1)
            nc.scalar.activation(m.Y[:, 4 * c:4 * c + 4, :].rearrange("p t n -> p (t n)"), turned[:, c % 2, :],
                                 ACT.Copy).then_inc(y_done, 1)

        @block.tensor
        def _(pe):
            def turn(c):
                pe.wait_ge(mixed_done, c + 1)
                if c >= 2:
                    pe.wait_ge(y_done, c - 1)
                for j in range(4):
                    last = nc.tensor.transpose(turned[:, c % 2, j * P:(j + 1) * P], mixed[:, c % 2, j * P:(j + 1) * P],
                                               m.ident[:])
                last.then_inc(turn_done, 1)
            for c in range(CH):
                if c >= 2:
                    pe.wait_ge(mixed_done, c - 1)
                for k, wt in enumerate((w["Wg"], w["Wv"])):
                    for d in range(2):
                        last = nc.tensor.matmul(gv[:, 2 * (c % 2) + k, :], wt[:, d * P:(d + 1) * P],
                                                outT[:, d, c * BANK:(c + 1) * BANK], start=(d == 0), stop=(d == 1))
                    last.then_inc(gv_done, 1)
                if c >= 1:
                    turn(c - 1)
            turn(CH - 1)

        @block.scalar
        def _(act):
            for c in range(CH):
                act.wait_ge(gv_done, 2 * c + 1)
                if c >= 2:
                    act.wait_ge(mixed_done, c - 1)
                nc.scalar.activation(gate[:, c % 2, :], gv[:, 2 * (c % 2), :], ACT.Sigmoid,
                                     bias=w["bg"][:, 0:1]).then_inc(gate_done, 1)
                if c >= 1:
                    keep(act, c - 1)
            keep(act, CH - 1)

        @block.vector
        def _(dve):
            chain = Chain(dve, chain_sem)
            for c in range(CH):
                tot, mix = total[:, c % 2, :], mixed[:, c % 2, :]
                chain.step(nc.vector.tensor_tensor(tot, outT[:, 0, c * BANK:(c + 1) * BANK],
                                                   outT[:, 1, c * BANK:(c + 1) * BANK], ALU.add))
                dve.wait_ge(gv_done, 2 * c + 2)
                if c >= 2:
                    dve.wait_ge(turn_done, c - 1)
                chain.step(nc.vector.scalar_tensor_tensor(out=mix, in0=gv[:, 2 * (c % 2) + 1, :], scalar=w["bv"][:, 0:1],
                                                          in1=tot, op0=ALU.add, op1=ALU.subtract))
                dve.wait_ge(gate_done, c + 1)
                chain.step(nc.vector.tensor_tensor(mix, mix, gate[:, c % 2, :], ALU.mult))
                chain.step(nc.vector.tensor_tensor(mix, mix, tot, ALU.add))
                nc.vector.tensor_scalar(mix, mix, 0.5, None, ALU.mult).then_inc(mixed_done, 1)


def bidirectional_mamba(nc, m, dram, s):
    w = weight_views(m, s)
    with ExitStack() as keep:
        def kept(name, shape, dt=F32):
            return keep.enter_context(nc.sbuf_tensor(f"mamba_{name}", shape, dt))
        xc = kept("xc", [P, NCH, SEQ])
        sz = kept("sz", [P, NCH, SEQ])
        delta = kept("delta", [P, NCH, SEQ])
        du = kept("du", [P, NCH, SEQ])
        BC3 = kept("BC3", [96, SEQ], BF16)
        select = kept("select", [96, 2 * NS, P], BF16)
        negA = kept("negA", [P, 2 * NCH * NS])
        Wx3 = kept("Wx3", [P, 2 * NCH, 96])
        outT = kept("outT", [P, 2, TOKENS])
        mamba_setup(nc, m, dram, s, w, select, negA, Wx3)
        mamba_norm(nc, m, m.Y)
        for d in range(2):
            for b in range(BATCH):
                mamba_front(nc, m, w, d, b, m.Y, xc, sz, delta, du, BC3, Wx3)
                mamba_scan(nc, m, w, d, b, xc, sz, delta, du, BC3, select, negA, outT)
        mamba_gate(nc, m, w, outT)


def grouped_experts(nc, m, dram, s):
    w = weight_views(m, s)
    E, G, PERG, CH = 32, 8, 4, 16
    UNITS = [(tc, c) for tc in range(NT // 4) for c in range(CH + 1)]
    with Phase(nc, "grouped") as ph:
        scores = ph.sb("scores", [P, NT, E])
        biased = ph.sb("biased", [P, NT, E])
        biasB = ph.sb("biasB", [P, E])
        hi1, lo1, hi2, lo2, first, second = (ph.sb(f"pair{k}", [P, NT, G]) for k in range(6))
        group = ph.sb("group", [P, NT, G])
        top = ph.sb("top", [P, NT, 8])
        where = ph.sb("where", [P, NT, 8], U32)
        wheref = ph.sb("wheref", [P, NT, 4])
        same = ph.sb("same", [P, NT, G, 4])
        gmask = ph.sb("gmask", [P, NT, G])
        replaced = ph.sb("replaced", [P, NT, E])
        stat = ph.sb("stat", [P, NT])
        parts = ph.sb("parts", [P, NT, 3, E], BF16)
        partsT = ph.sb("partsT", [96, TOKENS], BF16)
        select = ph.sb("select", [96, CH, P], BF16)
        silu = ph.sb("silu", [P, 2, BANK])
        gated = ph.sb("gated", [P, 2, BANK])
        hidden = ph.sb("hidden", [P, 3, BANK])
        gate_up = ph.ps("gate_up", 4)
        spread = ph.ps("spread", 2)
        down = ph.ps("down", 1)
        turned = ph.ctx.enter_context(nc.psum_tensor("grouped_turned", [P, 1, 1024], BF16))
        (router_done, bias_done, chain_sem, sig_done, parts_done, turn_done, turn_kept, gu_done, silu_done, gated_done,
         hid_done, spread_done, down_done, y_done, sel_done) = (
            ph.sem(x) for x in ("router_done", "bias_done", "chain", "sig_done", "parts_done", "turn_done", "turn_kept",
                                "gu_done", "silu_done", "gated_done", "hid_done", "spread_done", "down_done", "y_done",
                                "sel_done"))
        block = ph.block()
        shared_w = (w["sg"], w["su"], w["sd"])

        @block.gpsimd
        def _(pool):
            nc.gpsimd.memset(select[:], 0.0).then_inc(sel_done, 1)
            for r in range(3):
                pool.wait_ge(sel_done, r + 1)
                nc.gpsimd.affine_select(out=select[:].rearrange("k c (j i) -> k c j i", j=2),
                                        in_=select[:].rearrange("k c (j i) -> k c j i", j=2),
                                        compare_op=ALU.not_equal, fill=1.0, base=-E * r,
                                        pattern=[[-2, CH], [-1, 2], [0, 64]], channel_multiplier=1).then_inc(sel_done, 1)

        @block.tensor
        def _(pe):
            pe.wait_ge(m.wsem[s], 16)
            nc.tensor.matmul(down[:, 0, 0:E], m.ones[0:1, :], w["bias"], start=True, stop=True).then_inc(bias_done, 1)
            for g in range(NT):
                last = nc.tensor.matmul(spread[:, 0, E * g:E * (g + 1)], m.HT[:, g * P:(g + 1) * P], w["gate"],
                                        start=True, stop=True)
            last.then_inc(router_done, 1)

            def gate_and_up(n):
                tc, c = UNITS[n]
                if n >= 2:
                    pe.wait_ge(gated_done, n - 1)
                for k in range(2):
                    wt = shared_w[k] if c == CH else w[("wg", "wu")[k]][:, c * P:(c + 1) * P]
                    nc.tensor.matmul(gate_up[:, 2 * (n % 2) + k, :], wt, m.HT[:, tc * BANK:(tc + 1) * BANK],
                                     start=True, stop=True).then_inc(gu_done, 1)
            gate_and_up(0)
            gate_and_up(1)
            pe.wait_ge(parts_done, 1)
            for half in range(2):
                if half:
                    pe.wait_ge(turn_kept, 1)
                for j in range(8):
                    g = 8 * half + j
                    last = nc.tensor.transpose(turned[0:96, 0, j * P:(j + 1) * P],
                                               parts[:, g, :, :].rearrange("p r e -> p (r e)"), m.identb[:])
                last.then_inc(turn_done, 1)
            pe.wait_ge(turn_kept, 2)
            pe.wait_ge(sel_done, 4)
            for n in range(len(UNITS) + 1):
                if n < len(UNITS):
                    tc, c = UNITS[n]
                    if n >= 2:
                        gate_and_up(n)
                        pe.wait_ge(hid_done, n - 1)
                    if c < CH:
                        nc.tensor.matmul(spread[:, n % 2, :], select[:, c, :], partsT[:, tc * BANK:(tc + 1) * BANK],
                                         start=True, stop=True).then_inc(spread_done, 1)
                    else:
                        nc.tensor.matmul(spread[:, n % 2, :], m.ones[0:1, :], m.wide_ones[0:1, :], start=True,
                                         stop=True).then_inc(spread_done, 1)
                if n >= 1:
                    tc, c = UNITS[n - 1]
                    pe.wait_ge(hid_done, n)
                    if c == 0 and tc > 0:
                        pe.wait_ge(y_done, tc)
                    for j in range(4):
                        wt = shared_w[2] if c == CH else w["wd"][:, c * P:(c + 1) * P]
                        last = nc.tensor.matmul(down[:, 0, j * P:(j + 1) * P], hidden[:, (n - 1) % 3, j * P:(j + 1) * P],
                                                wt, start=(c == 0 and j == 0), stop=(c == CH), skip_group_check=True)
                    last.then_inc(down_done, 1)

        @block.scalar
        def _(act):
            act.wait_ge(router_done, 1)
            nc.scalar.activation(scores[:].rearrange("p t e -> p (t e)"), spread[:, 0, :], ACT.Sigmoid).then_inc(sig_done, 1)
            for half in range(2):
                act.wait_ge(turn_done, half + 1)
                nc.scalar.activation(partsT[:, half * 1024:(half + 1) * 1024], turned[0:96, 0, :],
                                     ACT.Copy).then_inc(turn_kept, 1)
            for n in range(len(UNITS)):
                act.wait_ge(gu_done, 2 * n + 1)
                if n >= 2:
                    act.wait_ge(gated_done, n - 1)
                nc.scalar.activation(silu[:, n % 2, :], gate_up[:, 2 * (n % 2), :], ACT.Silu).then_inc(silu_done, 1)

        @block.vector
        def _(dve):
            chain = Chain(dve, chain_sem)

            def tt(out, a, b, op):
                chain.step(nc.vector.tensor_tensor(out, a, b, op))
            dve.wait_ge(bias_done, 1)
            chain.step(nc.vector.tensor_copy(biasB[:], down[:, 0, 0:E]))
            dve.wait_ge(sig_done, 1)
            tt(biased[:], scores[:], biasB[:].unsqueeze(1).broadcast_to([P, NT, E]), ALU.add)
            a, b, c, d = (biased[:].rearrange("p t (g k) -> p t g k", k=PERG)[:, :, :, k] for k in range(PERG))
            tt(hi1[:], a, b, ALU.max)
            tt(lo1[:], a, b, ALU.min)
            tt(hi2[:], c, d, ALU.max)
            tt(lo2[:], c, d, ALU.min)
            tt(first[:], hi1[:], hi2[:], ALU.max)
            tt(second[:], hi1[:], hi2[:], ALU.min)
            tt(lo1[:], lo1[:], lo2[:], ALU.max)
            tt(second[:], second[:], lo1[:], ALU.max)
            tt(group[:], first[:], second[:], ALU.add)
            for g in range(NT):
                last = nc.vector.max(out=top[:, g, :], in_=group[:, g, :])
            chain.step(last)
            for g in range(NT):
                last = nc.vector.max_index(where[:, g, :], top[:, g, :], group[:, g, :])
            chain.step(last)
            chain.step(nc.vector.tensor_copy(wheref[:], where[:, :, 0:4]))
            for k in range(4):
                tt(same[:, :, :, k], m.iota8[:].unsqueeze(1).broadcast_to([P, NT, G]),
                   wheref[:, :, k:k + 1].broadcast_to([P, NT, G]), ALU.is_equal)
            chain.step(nc.vector.tensor_reduce(gmask[:], same[:], AX, ALU.add))
            for k in range(PERG):
                bk = biased[:].rearrange("p t (g k) -> p t g k", k=PERG)[:, :, :, k]
                tt(bk, bk, gmask[:], ALU.mult)
            for g in range(NT):
                last = nc.vector.max(out=top[:, g, :], in_=biased[:, g, :])
            chain.step(last)
            for g in range(NT):
                last = nc.vector.match_replace(out=replaced[:, g, :], in_to_replace=top[:, g, :],
                                               in_values=biased[:, g, :], imm_value=-3.0e38)
            chain.step(last)
            tt(replaced[:], replaced[:], biased[:], ALU.not_equal)
            tt(scores[:], scores[:], replaced[:], ALU.mult)
            chain.step(nc.vector.tensor_reduce(stat[:], scores[:], AX, ALU.add))
            chain.step(nc.vector.tensor_scalar(stat[:], stat[:], 1e-20, None, ALU.add))
            chain.step(nc.vector.reciprocal(stat[:], stat[:]))
            chain.step(nc.vector.tensor_scalar(stat[:], stat[:], 2.5, None, ALU.mult))
            tt(scores[:], scores[:], stat[:].unsqueeze(2).broadcast_to([P, NT, E]), ALU.mult)
            split3(nc, chain, scores[:], parts[:, :, 0, :], parts[:, :, 1, :], parts[:, :, 2, :], replaced[:])
            dve.sem_inc(parts_done, 1)
            for n in range(len(UNITS) + 1):
                if n < len(UNITS):
                    dve.wait_ge(silu_done, n + 1)
                    dve.wait_ge(gu_done, 2 * n + 2)
                    nc.vector.tensor_tensor(gated[:, n % 2, :], gate_up[:, 2 * (n % 2) + 1, :], silu[:, n % 2, :],
                                            ALU.mult).then_inc(gated_done, 1)
                    dve.wait_ge(gated_done, n + 1)
                    dve.wait_ge(spread_done, n + 1)
                    if n >= 3:
                        dve.wait_ge(down_done, n - 2)
                    nc.vector.tensor_tensor(hidden[:, n % 3, :], spread[:, n % 2, :], gated[:, n % 2, :],
                                            ALU.mult).then_inc(hid_done, 1)
                if n >= 1 and UNITS[n - 1][1] == CH:
                    tc = UNITS[n - 1][0]
                    dve.wait_ge(down_done, n)
                    nc.vector.tensor_copy(m.Y[:, 4 * tc:4 * tc + 4, :].rearrange("p t n -> p (t n)"),
                                          down[:, 0, :]).then_inc(y_done, 1)


S0, S1 = 0, 8
PHASES = [linear_attention_phase, attention_and_top2, causal_single_head, swiglu_experts, causal_sixteen_heads, local_transformer, bidirectional_mamba, grouped_experts]



def program(nc, dram, out):
    with ExitStack() as ctx:
        m = Memory(nc, ctx)
        constants_phase(nc, m, dram)
        phases = PHASES
        with Phase(nc, "first") as ph:
            block = ph.block()

            @block.sync
            def _(sp):
                load_weights(sp, m, dram, S0)
        for s in range(S0, S1):
            norm_phase(nc, m, f"norm{s}", add=s > S0, norm=True)
            phases[s](nc, m, dram, s)
        norm_phase(nc, m, "last", add=True, norm=False, out=out)


def rotary_tables():
    half = np.arange(0, 64, 2, dtype=np.float32)
    inv = (1.0 / 10000.0 ** (half / 64)).astype(np.float32)
    t = np.arange(SEQ, dtype=np.float32)
    freqs = t[:, None] * inv[None, :]
    freqs = np.concatenate([freqs, freqs], -1)
    base = (half + 0.4 * 64) / (1.4 * 64)
    power = (t - SEQ // 2) / 32.0
    scale = (base[None, :] ** power[:, None]).astype(np.float32)
    scale = np.concatenate([scale, scale], -1)
    sign = np.concatenate([-np.ones(32, np.float32), np.ones(32, np.float32)])
    cos, sin = np.cos(freqs), np.sin(freqs) * sign
    fold = lambda a: np.ascontiguousarray(
        a.astype(np.float32).reshape(TPB, P, 64).transpose(1, 0, 2).reshape(P, TPB * 64))
    return fold(cos * scale), fold(sin * scale), fold(cos / scale), fold(sin / scale)


def packed(s, parts):
    out = np.zeros((P, WIDTHS[s]), np.float32)
    at = 0
    for name, rows, n in PACKS[s]:
        a = parts[name]
        out[0:a.shape[0], at:at + a.shape[1]] = a
        at += n
    return out


def row(a):
    return a.reshape(1, -1)


def cols(a):
    return a.reshape(-1, P).T


def chunks(a):
    return a.reshape(-1, P, a.shape[-1]).transpose(1, 0, 2).reshape(P, -1)


def layouts(i):
    flat = lambda a: a.transpose(1, 0, 2).reshape(a.shape[1], -1)
    w1 = i["L2_ffn_w1"]
    b1 = np.zeros((2, 6, P), np.float32)
    b1.reshape(2, 2, 3 * P)[:, :, 0:HID] = i["L2_ffn_b1"].reshape(2, 2, HID)
    w2 = np.zeros((2, 3 * P, P), np.float32)
    w2[:, 0:HID] = i["L2_ffn_w2"]
    cosq, sinq, cosk, sink = rotary_tables()
    return [
        {"Wq": i["L0_attn_Wq"], "Wk": i["L0_attn_Wk"], "Wv": i["L0_attn_Wv"], "Wo": chunks(i["L0_attn_Wo"]),
         "bo": row(i["L0_attn_bo"])},
        {"Wqkv": i["L0_ffn_W_qkv"], "bqkv": row(i["L0_ffn_b_qkv"]), "Wgate": i["L0_ffn_W_gate"],
         "bgate": row(i["L0_ffn_b_gate"]), "Wexp": flat(i["L0_ffn_W_experts"]), "bexp": i["L0_ffn_b_experts"]},
        {"Wq": i["L1_attn_Wq"], "Wk": i["L1_attn_Wk"], "Wv": i["L1_attn_Wv"]},
        {"gate": i["L1_ffn_gate_w"].T, "wg": i["L1_ffn_wg"].reshape(4096, P).T,
         "wu": i["L1_ffn_wu"].reshape(4096, P).T,
         "wd": i["L1_ffn_wd"].reshape(8, P, 4, P).transpose(3, 0, 2, 1).reshape(P, 4096)},
        {"Wq": i["L2_attn_W_Q"].reshape(1024, P).T, "Wk": i["L2_attn_W_K"].reshape(1024, P).T,
         "Wv": i["L2_attn_W_V"].reshape(1024, P).T, "Wo": chunks(i["L2_attn_W_O"].T)},
        {"wqkv": flat(i["L2_ffn_wqkv"]),
         "wo": i["L2_ffn_wo"].reshape(2, 4, P, P).transpose(2, 0, 1, 3).reshape(P, -1),
         "w1": flat(w1), "w2": w2.reshape(2, 3, P, P).transpose(2, 0, 1, 3).reshape(P, -1),
         "b1": cols(b1), "b2": row(i["L2_ffn_b2"]), "lng": cols(i["L2_ffn_ln_g"]), "lnb": cols(i["L2_ffn_ln_b"]),
         "qscale": row(i["L2_ffn_q_scale"]), "kscale": row(i["L2_ffn_k_scale"]),
         "cosq": cosq, "sinq": sinq, "cosk": cosk, "sink": sink},
        {"lnw": cols(i["L3_attn_ln_w"]), "lnb": cols(i["L3_attn_ln_b"]), "Win": flat(i["L3_attn_W_in"]),
         "bin": cols(i["L3_attn_b_in"]),
         "convw": i["L3_attn_conv_w"].reshape(2, 2, P, 4).transpose(2, 0, 1, 3).reshape(P, 16),
         "convb": cols(i["L3_attn_conv_b"]),
         "Wx": i["L3_attn_W_xproj"].reshape(2, 2, P, 96).transpose(2, 0, 1, 3).reshape(P, -1),
         "Wdt": flat(i["L3_attn_W_dt"]), "bdt": cols(i["L3_attn_b_dt"]),
         "Alog": i["L3_attn_A_log"].reshape(2, 2, P, 16).transpose(2, 0, 1, 3).reshape(P, -1),
         "D": cols(i["L3_attn_D"]),
         "Wout": i["L3_attn_W_out"].reshape(2, 2, P, P).transpose(2, 0, 1, 3).reshape(P, -1),
         "bout": cols(i["L3_attn_b_out"]), "Wg": chunks(i["L3_attn_Wg"]), "bg": cols(i["L3_attn_bg"]),
         "Wv": chunks(i["L3_attn_Wv"]), "bv": cols(i["L3_attn_bv"])},
        {"gate": i["L3_ffn_gate_w"].T, "bias": row(i["L3_ffn_gate_bias"]),
         "wg": i["L3_ffn_w_gate"].reshape(2048, P).T, "wu": i["L3_ffn_w_up"].reshape(2048, P).T,
         "wd": i["L3_ffn_w_down"].reshape(16, 2, P, 64).transpose(1, 3, 0, 2).reshape(P, 2048),
         "sg": i["L3_ffn_sh_gate"].T, "su": i["L3_ffn_sh_up"].T, "sd": i["L3_ffn_sh_down"].T},
    ]


_OUTS = [((BATCH, SEQ, P), "float32")]


def kernel(**inputs):
    import concourse.bacc as _bacc
    from concourse.bass_utils import run_bass_kernel_spmd as _run

    nc = _bacc.Bacc("TRN2", target_bir_lowering=False, num_devices=1)
    host = {k: np.asarray(v) for k, v in inputs.items()}
    feeds = {"x": np.ascontiguousarray(host["L0_attn_x"])}
    for s, parts in enumerate(layouts(host)):
        feeds[f"w{s}"] = packed(s, parts)
    dram = {k: nc.dram_tensor(f"in_{k}_dram", a.shape, mybir.dt.from_np(a.dtype), kind="ExternalInput").ap()
            for k, a in feeds.items()}
    outs = [nc.dram_tensor(f"out_{i}_dram", shape, mybir.dt.from_np(np.dtype(dtype)), kind="ExternalOutput").ap()
            for i, (shape, dtype) in enumerate(_OUTS)]
    program(nc, dram, outs[0])
    r = _run(nc, [{f"in_{k}_dram": a for k, a in feeds.items()}], core_ids=[0])
    return r.results[0]["out_0_dram"]
```

```python
from contextlib import ExitStack

import numpy as np

import concourse.bass as bass
from concourse import mybir

F32 = mybir.dt.float32
BF16 = mybir.dt.bfloat16
U32 = mybir.dt.uint32
ALU = mybir.AluOpType
ACT = mybir.ActivationFunctionType
AX = mybir.AxisListType.X

P = 128
BATCH, SEQ = 2, 1024
TOKENS = BATCH * SEQ
NT = TOKENS // P
TPB = SEQ // P
BANK = 512
CPB = SEQ // BANK
LN_EPS = 1e-5
NEG = -1.0e30


class Phase:

    def __init__(self, nc, name):
        self.nc, self.name, self.ctx, self.sems = nc, name, ExitStack(), []

    def __enter__(self):
        self.ctx.__enter__()
        return self

    def __exit__(self, *e):
        self.ctx.__exit__(*e)
        nums = sorted(x.num for x in self.sems)
        while nums:
            n = 1
            while n < len(nums) and nums[n] == nums[0] + n:
                n += 1
            self.nc.gpsimd.sem_clear(range(nums[0], nums[0] + n))
            nums = nums[n:]

    def sb(self, name, shape, dt=F32):
        return self.ctx.enter_context(self.nc.sbuf_tensor(f"{self.name}_{name}", shape, dt))

    def ps(self, name, banks, dt=F32):
        return self.ctx.enter_context(self.nc.psum_tensor(f"{self.name}_{name}", [P, banks, BANK], dt))

    def sem(self, name):
        self.sems.append(self.ctx.enter_context(self.nc.semaphore(f"{self.name}_{name}")))
        return self.sems[-1]

    def block(self):
        return self.ctx.enter_context(self.nc.Block())


class Chain:

    def __init__(self, eng, sem):
        self.eng, self.sem, self.n = eng, sem, 0

    def step(self, ins):
        ins.then_inc(self.sem, 1)
        self.n += 1
        self.eng.wait_ge(self.sem, self.n)


def constants_phase(nc, m, dram):
    with Phase(nc, "const") as ph:
        loaded = ph.sem("loaded")
        zeroed = ph.sem("zeroed")
        made = ph.sem("made")
        block = ph.block()

        @block.sync
        def _(sp):
            sp.dma_start(m.X[:], dram["x"].rearrange("b (t p) d -> p (b t) d", p=P)).then_inc(loaded, 16)
            sp.wait_ge(loaded, 16)

        @block.vector
        def _(dve):
            chain = Chain(dve, made)
            nc.vector.memset(m.ones[:], 1.0)
            nc.vector.memset(m.neghalf[:], -0.5)
            nc.vector.memset(m.wide_ones[:], 1.0)
            chain.step(nc.vector.memset(m.blockdiag[:], 0.0))
            for h in range(2):
                nc.vector.memset(m.blockdiag[64 * h:64 * h + 64, 64 * h:64 * h + 64], 1.0)

        @block.gpsimd
        def _(pool):
            pool.memset(m.ident[:], 0.0).then_inc(zeroed, 1)
            pool.memset(m.causal[:], 0.0).then_inc(zeroed, 1)
            pool.memset(m.flip[:], 0.0).then_inc(zeroed, 1)
            pool.memset(m.band[:], 0.0).then_inc(zeroed, 1)
            pool.iota(m.iota8[:], pattern=[[1, 8]], base=0, channel_multiplier=0,
                      allow_small_or_imprecise_dtypes=True).then_inc(zeroed, 1)
            pool.wait_ge(zeroed, 5)
            pool.affine_select(out=m.ident[:], in_=m.ident[:], compare_op=ALU.not_equal, fill=1.0, base=0,
                               pattern=[[-1, P]], channel_multiplier=1).then_inc(zeroed, 1)
            pool.affine_select(out=m.flip[:], in_=m.flip[:], compare_op=ALU.not_equal, fill=1.0, base=1 - P,
                               pattern=[[1, P]], channel_multiplier=1).then_inc(zeroed, 1)
            pool.affine_select(out=m.causal[:], in_=m.causal[:], compare_op=ALU.is_ge, fill=NEG, base=0,
                               pattern=[[-1, P]], channel_multiplier=1).then_inc(zeroed, 1)
            pool.affine_select(out=m.band[:], in_=m.band[:], compare_op=ALU.is_ge, fill=NEG, base=64,
                               pattern=[[-1, 192]], channel_multiplier=1).then_inc(zeroed, 1)
            pool.wait_ge(zeroed, 9)
            pool.affine_select(out=m.band[:], in_=m.band[:], compare_op=ALU.is_ge, fill=NEG, base=0,
                               pattern=[[1, 192]], channel_multiplier=-1).then_inc(zeroed, 1)
            pool.tensor_copy(m.identb[:], m.ident[:])
            pool.tensor_copy(m.causalb[:], m.causal[:])


def norm_phase(nc, m, name, add, norm, out=None):
    G = NT // 4
    with Phase(nc, name) as ph:
        stats = ph.sb("stats", [P, 2, NT, 6])
        mv = ph.sb("mv", [P, 2, NT, 2])
        rstd = ph.sb("rstd", [P, 2, NT])
        shift = ph.sb("shift", [P, 2, NT])
        turned = ph.ps("turned", 4)
        stat_done, aggr_done, var_done, rstd_done, shift_done, norm_done, own_done = (
            [ph.sem(f"{s}{k}") for k in range(2)] for s in ("stat", "aggr", "var", "rstd", "shift", "norm", "own"))
        x_added = ph.sem("x_added")
        turn_done = ph.sem("turn_done")
        turn_kept = ph.sem("turn_kept")
        block = ph.block()
        src = (m.Y, m.X)
        own = ([], [t for t in range(NT) if t % 4 in (0, 2)])
        act_tiles = [[t for t in range(NT) if t not in own[k]] for k in range(2)]
        HT_ACT = (0, 2)
        ORDER = sorted(((k, q) for k in range(2) if (add, norm)[k] for q in range(G)),
                       key=lambda kq: (kq[1] + 2 * kq[0] * add, kq[0]))

        def wait_normalised(eng, k, t):
            if t in own[k]:
                eng.wait_ge(own_done[k], own[k].index(t) + 1)
            else:
                eng.wait_ge(norm_done[k], act_tiles[k].index(t) + 1)

        @block.vector
        def _(dve):
            def statistics(k, q):
                group = range(4 * q, 4 * q + 4)
                for t in group:
                    if k == 1 and add:
                        dve.wait_ge(x_added, t + 1)
                    nc.vector.bn_stats(stats[:, k, t, :], src[k][:, t, :]).then_inc(stat_done[k], 1)
                for t in group:
                    dve.wait_ge(stat_done[k], t + 1)
                    nc.vector.bn_aggr(mv[:, k, t, :], stats[:, k, t, :]).then_inc(aggr_done[k], 1)
                dve.wait_ge(aggr_done[k], 4 * q + 4)
                nc.vector.tensor_scalar(rstd[:, k, 4 * q:4 * q + 4], mv[:, k, 4 * q:4 * q + 4, 1], LN_EPS, None,
                                        ALU.add).then_inc(var_done[k], 1)

            def apply(k, q):
                dve.wait_ge(rstd_done[k], q + 1)
                four = slice(4 * q, 4 * q + 4)
                nc.vector.scalar_tensor_tensor(out=shift[:, k, four], in0=mv[:, k, four, 0], scalar=-1.0,
                                               in1=rstd[:, k, four], op0=ALU.mult,
                                               op1=ALU.mult).then_inc(shift_done[k], 1)
                for t in range(4 * q, 4 * q + 4):
                    if t in own[k]:
                        dve.wait_ge(shift_done[k], q + 1)
                        if k == 1 and add:
                            dve.wait_ge(x_added, t + 1)
                        nc.vector.tensor_scalar(m.XN[:, t, :], src[k][:, t, :], rstd[:, k, t:t + 1],
                                                shift[:, k, t:t + 1], ALU.mult, ALU.add).then_inc(own_done[k], 1)

            def add_group(q):
                for t in range(4 * q, 4 * q + 4):
                    wait_normalised(dve, 0, t)
                    nc.vector.tensor_tensor(m.X[:, t, :], m.X[:, t, :], m.XN[:, t, :], ALU.add).then_inc(x_added, 1)

            lag = 2 if add else 0
            for step in range(G + 5):
                if add and step < G:
                    statistics(0, step)
                if norm and 0 <= step - lag - 2 < G and step - lag - 2 not in HT_ACT:
                    c = step - lag - 2
                    dve.wait_ge(turn_done, 4 * (c + 1))
                    nc.vector.tensor_copy(m.HT[:, c * BANK:(c + 1) * BANK], turned[:, c, :]).then_inc(turn_kept, 1)
                if norm and 0 <= step - lag < G:
                    statistics(1, step - lag)
                if add and 0 <= step - 1 < G:
                    apply(0, step - 1)
                if norm and 0 <= step - lag - 1 < G:
                    apply(1, step - lag - 1)
                if add and 0 <= step - 1 < G:
                    add_group(step - 1)

        @block.gpsimd
        def _(pool):
            for k, q in ORDER:
                pool.wait_ge(var_done[k], q + 1)
                nc.gpsimd.tensor_tensor(rstd[:, k, 4 * q:4 * q + 4], rstd[:, k, 4 * q:4 * q + 4], m.neghalf[:, 0:4],
                                        ALU.pow).then_inc(rstd_done[k], 1)

        @block.scalar
        def _(act):
            def copy_out(c):
                act.wait_ge(turn_done, 4 * (c + 1))
                nc.scalar.activation(m.HT[:, c * BANK:(c + 1) * BANK], turned[:, c, :], ACT.Copy).then_inc(turn_kept, 1)

            for k, q in ORDER:
                act.wait_ge(shift_done[k], q + 1)
                for t in range(4 * q, 4 * q + 4):
                    if t in act_tiles[k]:
                        if k == 1 and add:
                            act.wait_ge(x_added, t + 1)
                        nc.scalar.activation(m.XN[:, t, :], src[k][:, t, :], ACT.Identity, bias=shift[:, k, t:t + 1],
                                             scale=rstd[:, k, t:t + 1]).then_inc(norm_done[k], 1)
                if k == 1 and q - 1 in HT_ACT:
                    copy_out(q - 1)

        @block.tensor
        def _(pe):
            if norm:
                for t in range(NT):
                    wait_normalised(pe, 1, t)
                    nc.tensor.transpose(turned[:, t // 4, t % 4 * P:(t % 4 + 1) * P], m.XN[:, t, :],
                                        m.ident[:]).then_inc(turn_done, 1)

        @block.sync
        def _(sp):
            if out is not None:
                rows = out.rearrange("b (t p) d -> p (b t) d", p=P)
                for half in range(2):
                    tiles = slice(half * TPB, (half + 1) * TPB)
                    sp.wait_ge(x_added, (half + 1) * TPB)
                    sp.dma_start(rows[:, tiles, :], m.X[:, tiles, :]).then_inc(m.stored, 16)
                sp.wait_ge(m.stored, 32)


class Memory:

    def __init__(self, nc, ctx):
        def sb(name, shape, dt=F32):
            return ctx.enter_context(nc.sbuf_tensor(name, shape, dt))
        self.X = sb("X", [P, NT, P])
        self.XN = sb("XN", [P, NT, P])
        self.Y = sb("Y", [P, NT, P])
        self.HT = sb("HT", [P, TOKENS])
        self.ident = sb("ident", [P, P])
        self.identb = sb("identb", [P, P], BF16)
        self.flip = sb("flip", [P, P])
        self.causal = sb("causal", [P, P])
        self.causalb = sb("causalb", [P, P], BF16)
        self.band = sb("band", [P, 192])
        self.blockdiag = sb("blockdiag", [P, P])
        self.ones = sb("ones", [P, P])
        self.neghalf = sb("neghalf", [P, NT])
        self.wide_ones = sb("wide_ones", [1, BANK])
        self.iota8 = sb("iota8", [P, 8])
        self.weights = sb("weights", [P, WCOLS])
        self.stored = ctx.enter_context(nc.semaphore("output_stored"))
        self.wsem = [ctx.enter_context(nc.semaphore(f"weights_loaded_{i}")) for i in range(8)]



PACKS = [
    [("Wq", P, 1024), ("Wk", P, 1024), ("Wv", P, 1024), ("Wo", P, 1024), ("bo", 1, P)],
    [("Wqkv", P, 384), ("bqkv", 1, 384), ("Wgate", P, 8), ("bgate", 1, 8), ("Wexp", P, 1024), ("bexp", 8, P)],
    [("Wq", P, P), ("Wk", P, P), ("Wv", P, P)],
    [("gate", P, 8), ("wg", P, 4096), ("wu", P, 4096), ("wd", P, 4096)],
    [("Wq", P, 1024), ("Wk", P, 1024), ("Wv", P, 1024), ("Wo", P, 1024)],
    [("wqkv", P, 2 * 1536), ("wo", P, 2 * 512), ("w1", P, 2 * 682), ("w2", P, 2 * 384), ("b1", P, 2 * 6),
     ("b2", 1, 2 * P), ("lng", P, 2), ("lnb", P, 2), ("qscale", 1, 2 * 64), ("kscale", 1, 2 * 64),
     ("cosq", P, 512), ("sinq", P, 512), ("cosk", P, 512), ("sink", P, 512)],
    [("lnw", P, 2), ("lnb", P, 2), ("Win", P, 2 * 512), ("bin", P, 2 * 4), ("convw", P, 2 * 8), ("convb", P, 2 * 2),
     ("Wx", P, 2 * 2 * 96), ("Wdt", 64, 2 * 256), ("bdt", P, 2 * 2), ("Alog", P, 2 * 2 * 16), ("D", P, 2 * 2),
     ("Wout", P, 2 * 2 * P), ("bout", P, 2), ("Wg", P, 2 * P), ("bg", P, 1), ("Wv", P, 2 * P), ("bv", P, 1)],
    [("gate", P, 32), ("bias", 1, 32), ("wg", P, 2048), ("wu", P, 2048), ("wd", P, 2048), ("sg", P, P),
     ("su", P, P), ("sd", P, P)],
]
WIDTHS = [sum(n for _, _, n in pack) for pack in PACKS]
WPART = [max(WIDTHS[0::2]), max(WIDTHS[1::2])]
WCOLS = sum(WPART)


def weight_views(m, s):
    views, at = {}, s % 2 * WPART[0]
    for name, rows, n in PACKS[s]:
        views[name] = m.weights[0:rows, at:at + n]
        at += n
    return views


def load_weights(sp, m, dram, s):
    if s < len(PACKS):
        at = s % 2 * WPART[0]
        sp.dma_start(m.weights[:, at:at + WIDTHS[s]], dram[f"w{s}"]).then_inc(m.wsem[s], 16)


def linear_attention_phase(nc, m, dram, s):
    w = weight_views(m, s)
    EPS = 1e-6
    with Phase(nc, "lin") as ph:
        keyexp = ph.sb("keyexp", [P, 2, BANK])
        keyrelu = ph.sb("keyrelu", [P, 2, BANK])
        key = ph.sb("key", [P, 2, 1024])
        val = ph.sb("val", [P, 2, 1024])
        kvT = ph.sb("kvT", [P, 8, P])
        ksum = ph.sb("ksum", [P, 8])
        ksumB = ph.sb("ksumB", [P, 8, P])
        mix = ph.sb("mix", [P, 8, P])
        qry = ph.sb("qry", [P, 2, BANK])
        den = ph.sb("den", [P, 2, BANK])
        rden = ph.sb("rden", [P, 2, BANK])
        qz = ph.sb("qz", [P, 2, BANK])
        proj = ph.ps("proj", 4)
        acc = ph.ps("acc", 3)
        small = ph.ps("small", 1)
        names = ("proj_done", "proj_kept", "exp_done", "relu_done", "key_done", "val_done", "tile_used", "kv_done",
                 "kvT_done", "ksum_done", "ksumB_done", "mix_psum", "mix_done", "q_psum", "q_exp", "q_relu",
                 "q_done", "z_psum", "den_done", "rden_done", "qz_done", "qz_used", "y_psum", "y_kept", "q_free")
        S = {n: ph.sem(n) for n in names}
        block = ph.block()
        UNITS = [(t, half) for t in range(TPB) for half in range(2)]

        @block.sync
        def _(sp):
            load_weights(sp, m, dram, s + 1)

        @block.tensor
        def _(pe):
            pe.wait_ge(m.wsem[s], 16)
            for b in range(BATCH):
                def accumulate(t):
                    g = b * TPB + t
                    pe.wait_ge(S["key_done"], 2 * (g + 1))
                    pe.wait_ge(S["val_done"], 2 * (g + 1))
                    if t == 0 and b > 0:
                        pe.wait_ge(S["y_kept"], 2 * b)
                        pe.wait_ge(S["ksum_done"], b)
                    for c in range(8):
                        nc.tensor.matmul(acc[:, c // 4, c % 4 * P:(c % 4 + 1) * P], val[:, g % 2, c * P:(c + 1) * P],
                                         key[:, g % 2, c * P:(c + 1) * P], start=(t == 0 and c % 4 == 0),
                                         stop=(t == TPB - 1), skip_group_check=True)
                        last = nc.tensor.matmul(acc[:, 2, c:c + 1], key[:, g % 2, c * P:(c + 1) * P], m.ones[:, 0:1],
                                                start=(t == 0 and c == 0), stop=(t == TPB - 1), skip_group_check=True)
                    last.then_inc(S["tile_used"], 1)

                for t in range(TPB):
                    g = b * TPB + t
                    for half in range(2):
                        for k, wt in enumerate((w["Wk"], w["Wv"])):
                            u = 4 * g + 2 * half + k
                            if u >= 4:
                                pe.wait_ge(S["proj_kept"], u - 3)
                            nc.tensor.matmul(proj[:, u % 4, :], m.HT[:, g * P:(g + 1) * P],
                                             wt[:, half * BANK:(half + 1) * BANK], start=True,
                                             stop=True).then_inc(S["proj_done"], 1)
                    if t >= 1:
                        accumulate(t - 1)
                accumulate(TPB - 1)
                pe.wait_ge(S["kvT_done"], b + 1)
                for c in range(8):
                    i = 8 * b + c
                    if i >= 4:
                        pe.wait_ge(S["mix_done"], i // 4)
                    nc.tensor.matmul(small[:, 0, c % 4 * P:(c % 4 + 1) * P], kvT[:, c, :], w["Wo"][:, c * P:(c + 1) * P],
                                     start=True, stop=True).then_inc(S["mix_psum"], 1)
                pe.wait_ge(S["proj_kept"], 4 * (b + 1) * TPB)
                pe.wait_ge(S["mix_done"], 2 * (b + 1))
                pe.wait_ge(S["ksumB_done"], b + 1)
                for half in range(2):
                    def query(c):
                        n = 16 * b + 8 * half + c
                        if n >= 2:
                            pe.wait_ge(S["q_free"], n - 1)
                        nc.tensor.matmul(proj[:, n % 2, :], w["Wq"][:, c * P:(c + 1) * P],
                                         m.HT[:, (CPB * b + half) * BANK:(CPB * b + half + 1) * BANK], start=True,
                                         stop=True).then_inc(S["q_psum"], 1)

                    def norm_sum(c):
                        n = 16 * b + 8 * half + c
                        pe.wait_ge(S["q_done"], n + 1)
                        if n >= 2:
                            pe.wait_ge(S["den_done"], n - 1)
                        nc.tensor.matmul(proj[:, 2 + n % 2, :], ksumB[:, c, :], qry[:, n % 2, :], start=True,
                                         stop=True).then_inc(S["z_psum"], 1)

                    def project(c):
                        n = 16 * b + 8 * half + c
                        pe.wait_ge(S["qz_done"], n + 1)
                        if c == 0 and 2 * b + half >= 1:
                            pe.wait_ge(S["y_kept"], 2 * b + half)
                        for j in range(4):
                            last = nc.tensor.matmul(acc[:, 0, j * P:(j + 1) * P], qz[:, n % 2, j * P:(j + 1) * P],
                                                    mix[:, c, :], start=(c == 0 and j == 0), stop=False,
                                                    skip_group_check=True)
                        last.then_inc(S["qz_used"], 1)

                    for c in range(10):
                        if c < 8:
                            query(c)
                        if 1 <= c <= 8:
                            norm_sum(c - 1)
                        if c >= 2:
                            project(c - 2)
                    for j in range(4):
                        last = nc.tensor.matmul(acc[:, 0, j * P:(j + 1) * P], m.ones[0:1, :], w["bo"], start=False,
                                                stop=True, skip_group_check=True)
                    last.then_inc(S["y_psum"], 1)

        @block.scalar
        def _(act):
            for b in range(BATCH):
                for t in range(TPB):
                    g = b * TPB + t
                    for half in range(2):
                        n = 2 * g + half
                        cols_ = slice(half * BANK, (half + 1) * BANK)
                        act.wait_ge(S["proj_done"], 2 * n + 1)
                        if n >= 2:
                            act.wait_ge(S["key_done"], n - 1)
                        nc.scalar.activation(keyexp[:, n % 2, :], proj[:, 2 * n % 4, :], ACT.Exp).then_inc(S["exp_done"], 1)
                        nc.scalar.activation(keyrelu[:, n % 2, :], proj[:, 2 * n % 4, :], ACT.Relu).then_inc(S["relu_done"], 1)
                        act.wait_ge(S["relu_done"], n + 1)
                        act.wait_ge(S["exp_done"], n + 1)
                        act.sem_inc(S["proj_kept"], 1)
                        act.wait_ge(S["proj_done"], 2 * n + 2)
                        if g >= 2:
                            act.wait_ge(S["tile_used"], g - 1)
                        nc.scalar.activation(val[:, g % 2, cols_], proj[:, (2 * n + 1) % 4, :],
                                             ACT.Copy).then_inc(S["val_done"], 1)
                        act.wait_ge(S["val_done"], n + 1)
                        act.sem_inc(S["proj_kept"], 1)
                for n in range(16 * b, 16 * b + 16):
                    act.wait_ge(S["q_psum"], n + 1)
                    if n >= 2:
                        act.wait_ge(S["q_done"], n - 1)
                    nc.scalar.activation(keyexp[:, n % 2, :], proj[:, n % 2, :], ACT.Exp).then_inc(S["q_exp"], 1)
                    nc.scalar.activation(keyrelu[:, n % 2, :], proj[:, n % 2, :], ACT.Relu).then_inc(S["q_free"], 1)
                    act.wait_ge(S["z_psum"], n + 1)
                    if n >= 2:
                        act.wait_ge(S["rden_done"], n - 1)
                    nc.scalar.activation(den[:, n % 2, :], proj[:, 2 + n % 2, :], ACT.Copy, bias=EPS).then_inc(S["den_done"], 1)

        @block.vector
        def _(dve):
            for b in range(BATCH):
                for t in range(TPB):
                    g = b * TPB + t
                    for half in range(2):
                        n = 2 * g + half
                        dve.wait_ge(S["relu_done"], n + 1)
                        dve.wait_ge(S["exp_done"], n + 1)
                        if g >= 2:
                            dve.wait_ge(S["tile_used"], g - 1)
                        nc.vector.scalar_tensor_tensor(out=key[:, g % 2, half * BANK:(half + 1) * BANK],
                                                       in0=keyexp[:, n % 2, :], scalar=1.0, in1=keyrelu[:, n % 2, :],
                                                       op0=ALU.min, op1=ALU.add).then_inc(S["key_done"], 1)
                dve.wait_ge(S["tile_used"], (b + 1) * TPB)
                nc.vector.tensor_copy(ksum[:], acc[:, 2, 0:8]).then_inc(S["ksum_done"], 1)
                for c in range(8):
                    last = nc.vector.tensor_tensor(kvT[:, c, :], acc[:, c // 4, c % 4 * P:(c % 4 + 1) * P],
                                                   m.blockdiag[:], ALU.mult)
                last.then_inc(S["kvT_done"], 1)
                dve.wait_ge(S["ksum_done"], b + 1)
                for c in range(8):
                    last = nc.vector.tensor_scalar(ksumB[:, c, :], m.blockdiag[:], ksum[:, c:c + 1], None, ALU.mult)
                last.then_inc(S["ksumB_done"], 1)
                for h in range(2):
                    dve.wait_ge(S["mix_psum"], 8 * b + 4 * (h + 1))
                    nc.vector.tensor_copy(mix[:, 4 * h:4 * h + 4, :], small[:, 0, :].rearrange("p (c n) -> p c n", c=4)).then_inc(S["mix_done"], 1)
                for half in range(2):
                    def features(n):
                        dve.wait_ge(S["q_exp"], n + 1)
                        dve.wait_ge(S["q_free"], n + 1)
                        if n >= 2:
                            dve.wait_ge(S["qz_done"], n - 1)
                        nc.vector.scalar_tensor_tensor(out=qry[:, n % 2, :], in0=keyexp[:, n % 2, :], scalar=1.0,
                                                       in1=keyrelu[:, n % 2, :], op0=ALU.min,
                                                       op1=ALU.add).then_inc(S["q_done"], 1)

                    def divide(n):
                        dve.wait_ge(S["den_done"], n + 1)
                        nc.vector.reciprocal(rden[:, n % 2, :], den[:, n % 2, :]).then_inc(S["rden_done"], 1)
                        dve.wait_ge(S["rden_done"], n + 1)
                        if n >= 2:
                            dve.wait_ge(S["qz_used"], n - 1)
                        nc.vector.tensor_tensor(qz[:, n % 2, :], qry[:, n % 2, :], rden[:, n % 2, :],
                                                ALU.mult).then_inc(S["qz_done"], 1)
                    n0 = 16 * b + 8 * half
                    features(n0)
                    for n in range(n0, n0 + 8):
                        if n + 1 < n0 + 8:
                            features(n + 1)
                        divide(n)
                    dve.wait_ge(S["y_psum"], 2 * b + half + 1)
                    nc.vector.tensor_copy(m.Y[:, b * TPB + 4 * half:b * TPB + 4 * half + 4, :],
                                          acc[:, 0, :].rearrange("p (j n) -> p j n", j=4)).then_inc(S["y_kept"], 1)


SLOTS = 64


def split3(nc, chain, src, hi, mid, lo, rest):
    chain.step(nc.vector.tensor_copy(hi, src))
    chain.step(nc.vector.tensor_tensor(rest, src, hi, ALU.subtract))
    chain.step(nc.vector.tensor_copy(mid, rest))
    chain.step(nc.vector.tensor_tensor(rest, rest, mid, ALU.subtract))
    chain.step(nc.vector.tensor_copy(lo, rest))


def small_head_attention(nc, m, dram, s):
    w = weight_views(m, s)
    with ExitStack() as keep:
        def kept(name, shape, dt):
            return keep.enter_context(nc.sbuf_tensor(name, shape, dt))
        kT = kept("heads_kT", [P, 8, TOKENS], BF16)
        qstack = kept("heads_qstack", [P, NT, 16, SLOTS], BF16)
        vaug = kept("heads_vaug", [P, NT, 16, 9], F32)

        with Phase(nc, "hprep") as ph:
            kstack = ph.sb("kstack", [P, 2, 16, SLOTS], BF16)
            qk = ph.sb("qk", [P, 2, 256])
            parts = ph.sb("parts", [P, 2, 3, 256], BF16)
            rest = ph.sb("rest", [P, 256])
            proj = ph.ps("proj", 2)
            turned = ph.ctx.enter_context(nc.psum_tensor("hprep_turned", [P, 2, 1024], BF16))
            cleared, proj_done, qk_done, v_done, parts_done, chain_sem, stack_act, stack_pool, turn_done, turn_kept = (
                ph.sem(x) for x in ("cleared", "proj_done", "qk_done", "v_done", "parts_done", "chain", "stack_act",
                                    "stack_pool", "turn_done", "turn_kept"))
            block = ph.block()

            @block.sync
            def _(sp):
                load_weights(sp, m, dram, s + 1)

            @block.tensor
            def _(pe):
                pe.wait_ge(m.wsem[s], 16)

                def turn(g):
                    pe.wait_ge(stack_act, g + 1)
                    pe.wait_ge(stack_pool, g + 1)
                    if g >= 2:
                        pe.wait_ge(turn_kept, g - 1)
                    for c in range(8):
                        last = nc.tensor.transpose(turned[:, g % 2, c * P:(c + 1) * P],
                                                   kstack[:, g % 2, 2 * c:2 * c + 2, :].rearrange("p h d -> p (h d)"),
                                                   m.identb[:])
                    last.then_inc(turn_done, 1)

                for g in range(NT):
                    if g >= 2:
                        pe.wait_ge(qk_done, g - 1)
                        pe.wait_ge(v_done, g - 1)
                    nc.tensor.matmul(proj[:, g % 2, 0:384], m.HT[:, g * P:(g + 1) * P], w["Wqkv"], start=True, stop=False)
                    nc.tensor.matmul(proj[:, g % 2, 0:384], m.ones[0:1, :], w["bqkv"], start=False,
                                     stop=True).then_inc(proj_done, 1)
                    if g >= 1:
                        turn(g - 1)
                turn(NT - 1)

            @block.scalar
            def _(act):
                act.wait_ge(cleared, 5)
                for g in range(NT):
                    act.wait_ge(proj_done, g + 1)
                    if g >= 2:
                        act.wait_ge(parts_done, g - 1)
                    nc.scalar.activation(qk[:, g % 2, :], proj[:, g % 2, 0:256], ACT.Copy).then_inc(qk_done, 1)
                    nc.scalar.activation(vaug[:, g, :, 0:8], proj[:, g % 2, 256:384].rearrange("p (h d) -> p h d", h=16),
                                         ACT.Copy).then_inc(v_done, 1)
                    act.wait_ge(parts_done, g + 1)
                    hi, mid, lo = (parts[:, g % 2, k, 0:P].rearrange("p (h d) -> p h d", h=16) for k in range(3))
                    for slot, part in enumerate((hi, hi, mid, mid, hi, lo)):
                        last = nc.scalar.activation(qstack[:, g, :, 8 * slot:8 * slot + 8], part, ACT.Copy)
                    last.then_inc(stack_act, 1)
                    if g >= 1:
                        act.wait_ge(turn_done, g)
                        nc.scalar.activation(kT[:, :, (g - 1) * P:g * P],
                                             turned[:, (g - 1) % 2, :].rearrange("p (c n) -> p c n", c=8),
                                             ACT.Copy).then_inc(turn_kept, 1)
                act.wait_ge(turn_done, NT)
                nc.scalar.activation(kT[:, :, (NT - 1) * P:NT * P],
                                     turned[:, (NT - 1) % 2, :].rearrange("p (c n) -> p c n", c=8),
                                     ACT.Copy).then_inc(turn_kept, 1)

            @block.gpsimd
            def _(pool):
                pool.wait_ge(cleared, 5)
                for g in range(NT):
                    pool.wait_ge(parts_done, g + 1)
                    if g >= 2:
                        pool.wait_ge(turn_done, g - 1)
                    hi, mid, lo = (parts[:, g % 2, k, P:2 * P].rearrange("p (h d) -> p h d", h=16) for k in range(3))
                    for slot, part in enumerate((hi, mid, hi, mid, lo, hi)):
                        last = nc.gpsimd.tensor_copy(kstack[:, g % 2, :, 8 * slot:8 * slot + 8], part)
                    last.then_inc(stack_pool, 1)

            @block.vector
            def _(dve):
                chain = Chain(dve, chain_sem)
                nc.vector.memset(kstack[:, :, :, 51:64], 0.0).then_inc(cleared, 1)
                nc.vector.memset(kstack[:, :, :, 48:51], 1.0).then_inc(cleared, 1)
                nc.vector.memset(qstack[:, 0:8, :, 48:64], 0.0).then_inc(cleared, 1)
                nc.vector.memset(qstack[:, 8:16, :, 48:64], 0.0).then_inc(cleared, 1)
                nc.vector.memset(vaug[:, :, :, 8], 1.0).then_inc(cleared, 1)
                for g in range(NT):
                    dve.wait_ge(qk_done, g + 1)
                    if g >= 2:
                        dve.wait_ge(stack_act, g - 1)
                        dve.wait_ge(stack_pool, g - 1)
                    split3(nc, chain, qk[:, g % 2, :], parts[:, g % 2, 0, :], parts[:, g % 2, 1, :],
                           parts[:, g % 2, 2, :], rest[:])
                    dve.sem_inc(parts_done, 1)

        with Phase(nc, "heads") as ph:
            qT = ph.sb("qT", [P, 2, 8, P], BF16)
            qmT = ph.sb("qmT", [P, 2, 8, P], BF16)
            halfmax = ph.sb("halfmax", [P, 2, 16, 2])
            negmax = ph.sb("negmax", [P, 16])
            rest = ph.sb("rest", [P, 16])
            probs = ph.sb("probs", [P, 3, 1024])
            rsum = ph.sb("rsum", [P, 2, 16])
            qmajor = ph.ps("qmajor", 2)
            kmajor = ph.ps("kmajor", 4)
            outT = ph.sb("outT", [P, BANK])
            outp = ph.ps("outp", 1)
            turned32 = ph.ps("turned", 1)
            turned = turned32[:].bitcast(BF16)
            out_free, t3_done = ph.sem("out_free"), ph.sem("t3_done")
            (t1_done, t1_kept, s_done, max_done, slots_done, t2_done, t2_kept, st_done, exp_done, pv_done, head_done,
             out_kept, chain_sem, rsum_done) = (
                ph.sem(x) for x in ("t1_done", "t1_kept", "s_done", "max_done", "slots_done", "t2_done", "t2_kept",
                                    "st_done", "exp_done", "pv_done", "head_done", "out_kept", "chain", "rsum_done"))
            block = ph.block()
            SC = float(8) ** -0.5
            UNITS, LAG = 16 * NT, 22

            @block.tensor
            def _(pe):
                def turn(g, done, kept1, kept2, kept3):
                    if kept3 > 0:
                        pe.wait_ge(out_kept, kept3)
                    if kept1 > 0:
                        pe.wait_ge(t1_kept, kept1)
                    if kept2 > 0:
                        pe.wait_ge(t2_kept, kept2)
                    for c in range(8):
                        last = nc.tensor.transpose(turned[:, 0, c * P:(c + 1) * P],
                                                   qstack[:, g, 2 * c:2 * c + 2, :].rearrange("p h d -> p (h d)"),
                                                   m.identb[:])
                    last.then_inc(done, 1)

                def scores(unit):
                    g, h = unit // 16, unit % 16
                    c, j, b = h // 2, h % 2, g // TPB
                    if h == 0:
                        pe.wait_ge(t1_kept, g + 1)
                    for half in range(2):
                        n = 32 * g + 2 * h + half
                        if n >= 2:
                            pe.wait_ge(max_done, n - 1)
                        nc.tensor.matmul(qmajor[:, half, :], qT[64 * j:64 * j + 48, g % 2, c, :],
                                         kT[64 * j:64 * j + 48, c, b * SEQ + half * BANK:b * SEQ + (half + 1) * BANK],
                                         start=True, stop=True).then_inc(s_done, 1)

                def shifted(n):
                    g, h = n // 16, n % 16
                    c, j, b = h // 2, h % 2, g // TPB
                    if h == 0:
                        pe.wait_ge(t2_kept, g + 1)
                    if n >= 2:
                        pe.wait_ge(exp_done, n - 1)
                    for kc in range(TPB):
                        last = nc.tensor.matmul(kmajor[:, 2 * (n % 2) + kc // 4, kc % 4 * P:(kc % 4 + 1) * P],
                                                kT[64 * j:64 * j + 51, c, b * SEQ + kc * P:b * SEQ + (kc + 1) * P],
                                                qmT[64 * j:64 * j + 51, g % 2, c, :], start=True, stop=True)
                    last.then_inc(st_done, 1)

                def values(n):
                    g, h = n // 16, n % 16
                    b = g // TPB
                    pe.wait_ge(exp_done, n + 1)
                    if h == 0:
                        pe.wait_ge(out_free, g + 1)
                    rows, at = 32 * (h % 4), h // 4 * P
                    for kc in range(TPB):
                        last = nc.tensor.matmul(outp[rows:rows + 9, 0, at:at + P], vaug[:, b * TPB + kc, h, :],
                                                probs[:, n % 3, kc * P:(kc + 1) * P], start=(kc == 0),
                                                stop=(kc == TPB - 1))
                    last.then_inc(pv_done, 1)

                def turn_out(g):
                    pe.wait_ge(out_free, g + 2)
                    pe.wait_ge(t2_kept, g + 2 if g + 2 <= NT else NT)
                    pe.wait_ge(t1_kept, min(g + 3, NT))
                    if g >= 1:
                        pe.wait_ge(out_kept, g)
                    for c in range(4):
                        last = nc.tensor.transpose(turned32[:, 0, c * P:(c + 1) * P], outT[:, c * P:(c + 1) * P],
                                                   m.ident[:])
                    last.then_inc(t3_done, 1)

                turn(0, t1_done, 0, 0, 0)
                for n in range(16 * (NT + 2)):
                    g, h = n // 16, n % 16
                    if h == 3 and 1 <= g <= NT:
                        pe.wait_ge(slots_done, g)
                        turn(g - 1, t2_done, min(g + 1, NT), g - 1, g - 2)
                    if LAG <= n < UNITS + LAG:
                        shifted(n - LAG)
                    if n < UNITS:
                        scores(n)
                    if LAG + 2 <= n < UNITS + LAG + 2:
                        values(n - LAG - 2)
                    if h == 9 and g >= 2:
                        turn_out(g - 2)
                    if h == 13 and g + 1 < NT:
                        turn(g + 1, t1_done, g + 1, g, g - 1)

            @block.scalar
            def _(act):
                def keep1(g):
                    act.wait_ge(t1_done, g + 1)
                    if g >= 2:
                        act.wait_ge(s_done, 32 * (g - 1))
                    nc.scalar.activation(qT[:, g % 2, :, :], turned[:, 0, :].rearrange("p (c n) -> p c n", c=8),
                                         ACT.Copy).then_inc(t1_kept, 1)

                def keep2(g):
                    act.wait_ge(t2_done, g + 1)
                    if g >= 2:
                        act.wait_ge(st_done, 16 * (g - 1))
                    nc.scalar.activation(qmT[:, g % 2, :, :], turned[:, 0, :].rearrange("p (c n) -> p c n", c=8),
                                         ACT.Copy).then_inc(t2_kept, 1)
                keep1(0)
                act.wait_ge(out_free, 1)
                for n in range(16 * (NT + 2)):
                    g, h = n // 16, n % 16
                    if h == 3 and 1 <= g <= NT:
                        keep2(g - 1)
                    if LAG <= n < UNITS + LAG:
                        k = n - LAG
                        act.wait_ge(st_done, k + 1)
                        if k >= 3:
                            act.wait_ge(pv_done, k - 2)
                        nc.scalar.activation(probs[:, k % 3, :].rearrange("p (a n) -> p a n", a=2),
                                             kmajor[:, 2 * (k % 2):2 * (k % 2) + 2, :], ACT.Exp,
                                             scale=SC).then_inc(exp_done, 1)
                    if h == 8 and g >= 2:
                        act.wait_ge(pv_done, 16 * (g - 1))
                        if g >= 3:
                            act.wait_ge(t3_done, g - 2)
                        nc.scalar.activation(outT[:], outp[:, 0, :], ACT.Copy).then_inc(out_free, 1)
                    if h == 13 and g + 1 < NT:
                        keep1(g + 1)

            @block.vector
            def _(dve):
                chain = Chain(dve, chain_sem)

                def normalise(g):
                    dve.wait_ge(t3_done, g + 1)
                    o = turned32[:, 0, :].rearrange("p (h e) -> p h e", h=16)
                    nc.vector.reciprocal(rsum[:, g % 2, :], o[:, :, 8]).then_inc(rsum_done, 1)
                    dve.wait_ge(rsum_done, g + 1)
                    nc.vector.tensor_tensor(m.Y[:, g, :].rearrange("p (h d) -> p h d", h=16), o[:, :, 0:8],
                                            rsum[:, g % 2, :].unsqueeze(2).broadcast_to([P, 16, 8]),
                                            ALU.mult).then_inc(out_kept, 1)

                nc.vector.memset(outp[:], 0.0).then_inc(out_free, 1)
                for g in range(NT):
                    for h in range(16):
                        for half in range(2):
                            dve.wait_ge(s_done, 32 * g + 2 * h + half + 1)
                            nc.vector.tensor_reduce(halfmax[:, g % 2, h, half:half + 1], qmajor[:, half, :], AX,
                                                    ALU.max).then_inc(max_done, 1)
                        if h == 9 and g >= 2:
                            normalise(g - 2)
                    dve.wait_ge(max_done, 32 * (g + 1))
                    chain.step(nc.vector.tensor_reduce(negmax[:], halfmax[:, g % 2, :, :], AX, ALU.max))
                    chain.step(nc.vector.tensor_scalar(negmax[:], negmax[:], -1.0, None, ALU.mult))
                    dve.wait_ge(t1_done, g + 1)
                    split3(nc, chain, negmax[:], qstack[:, g, :, 48], qstack[:, g, :, 49], qstack[:, g, :, 50], rest[:])
                    dve.sem_inc(slots_done, 1)
                normalise(NT - 2)
                normalise(NT - 1)


def top2_experts(nc, m, dram, s):
    w = weight_views(m, s)
    E = 8
    UNITS = [(tc, e) for tc in range(NT // 4) for e in range(E)]
    with Phase(nc, "moe0") as ph:
        gates = ph.sb("gates", [P, NT, 8])
        pick = ph.sb("pick", [P, NT, 8])
        pick2 = ph.sb("pick2", [P, NT, 8])
        stat = ph.sb("stat", [P, NT])
        top = ph.sb("top", [P, NT, 8])
        where = ph.sb("where", [P, NT, 8], U32)
        wheref = ph.sb("wheref", [P, NT, 2])
        parts = ph.sb("parts", [P, NT, 3, 8], BF16)
        rest = ph.sb("rest", [P, NT, 8])
        partsT = ph.sb("partsT", [24, TOKENS], BF16)
        gT = ph.sb("gT", [8, TOKENS])
        select = ph.sb("select", [24, E, P], BF16)
        scaled = ph.sb("scaled", [P, 3, BANK])
        logits = ph.ps("logits", 1)
        spread = ph.ps("spread", 2)
        out = ph.ps("out", 2)
        turned = ph.ps("turned", 2)
        turnedb = ph.ctx.enter_context(nc.psum_tensor("moe0_turnedb", [P, 1, 1024], BF16))
        (logits_done, chain_sem, gates_done, parts_done, gt_done, gt_kept, pt_done, pt_kept, sel_done, spread_done,
         scaled_done, used, y_done, exp_in, exp_out) = (
            ph.sem(x) for x in ("logits_done", "chain", "gates_done", "parts_done", "gt_done", "gt_kept", "pt_done",
                                "pt_kept", "sel_done", "spread_done", "scaled_done", "used", "y_done", "exp_in",
                                "exp_out"))
        block = ph.block()

        @block.gpsimd
        def _(pool):
            nc.gpsimd.memset(select[:], 0.0).then_inc(sel_done, 1)
            for r in range(3):
                pool.wait_ge(sel_done, r + 1)
                nc.gpsimd.affine_select(out=select[:], in_=select[:], compare_op=ALU.not_equal, fill=1.0, base=-8 * r,
                                        pattern=[[-1, E], [0, P]], channel_multiplier=1).then_inc(sel_done, 1)

        @block.tensor
        def _(pe):
            for g in range(NT):
                nc.tensor.matmul(logits[:, 0, 8 * g:8 * g + 8], m.HT[:, g * P:(g + 1) * P], w["Wgate"], start=True, stop=False)
                last = nc.tensor.matmul(logits[:, 0, 8 * g:8 * g + 8], m.ones[0:1, :], w["bgate"], start=False, stop=True)
            last.then_inc(logits_done, 1)
            pe.wait_ge(gates_done, 1)
            for g in range(NT):
                if g % 4 == 0 and g >= 8:
                    pe.wait_ge(gt_kept, g // 4 - 1)
                nc.tensor.transpose(turned[0:8, g // 4 % 2, g % 4 * P:(g % 4 + 1) * P], gates[:, g, :],
                                    m.ident[:]).then_inc(gt_done, 1)
            pe.wait_ge(parts_done, 1)
            for half in range(2):
                if half:
                    pe.wait_ge(pt_kept, 1)
                for j in range(8):
                    last = nc.tensor.transpose(turnedb[0:24, 0, j * P:(j + 1) * P],
                                               parts[:, 8 * half + j, :, :].rearrange("p r e -> p (r e)"), m.identb[:])
                last.then_inc(pt_done, 1)
            pe.wait_ge(pt_kept, 2)
            pe.wait_ge(gt_kept, 4)
            pe.wait_ge(sel_done, 4)

            def spread_gate(n):
                tc, e = UNITS[n]
                if n >= 2:
                    pe.wait_ge(scaled_done, n - 1)
                nc.tensor.matmul(spread[:, n % 2, :], select[:, e, :], partsT[:, tc * BANK:(tc + 1) * BANK], start=True,
                                 stop=True).then_inc(spread_done, 1)
            spread_gate(0)
            for n, (tc, e) in enumerate(UNITS):
                if n + 1 < len(UNITS):
                    spread_gate(n + 1)
                if e == 0:
                    if tc >= 2:
                        pe.wait_ge(y_done, tc - 1)
                    for j in range(4):
                        t = 4 * tc + j
                        nc.tensor.matmul(out[:, tc % 2, j * P:(j + 1) * P], gT[:, t * P:(t + 1) * P], w["bexp"],
                                         start=(j == 0), stop=False, skip_group_check=True)
                pe.wait_ge(scaled_done, n + 1)
                for j in range(4):
                    last = nc.tensor.matmul(out[:, tc % 2, j * P:(j + 1) * P], scaled[:, n % 3, j * P:(j + 1) * P],
                                            w["Wexp"][:, e * P:(e + 1) * P], start=False, stop=(e == E - 1),
                                            skip_group_check=True)
                last.then_inc(used, 1)

        @block.scalar
        def _(act):
            act.wait_ge(exp_in, 1)
            nc.scalar.activation(gates[:], gates[:], ACT.Exp).then_inc(exp_out, 1)
            for c in range(4):
                act.wait_ge(gt_done, 4 * (c + 1))
                nc.scalar.activation(gT[:, c * BANK:(c + 1) * BANK], turned[0:8, c % 2, :], ACT.Copy).then_inc(gt_kept, 1)
            for half in range(2):
                act.wait_ge(pt_done, half + 1)
                nc.scalar.activation(partsT[:, half * 1024:(half + 1) * 1024], turnedb[0:24, 0, :],
                                     ACT.Copy).then_inc(pt_kept, 1)

        def add(dve, tc):
            dve.wait_ge(used, E * (tc + 1))
            y = m.Y[:, 4 * tc:4 * tc + 4, :].rearrange("p t n -> p (t n)")
            nc.vector.tensor_tensor(y, out[:, tc % 2, :], y, ALU.add).then_inc(y_done, 1)

        @block.vector
        def _(dve):
            chain = Chain(dve, chain_sem)

            def wide(a):
                return a.unsqueeze(2).broadcast_to([P, NT, 8])
            dve.wait_ge(logits_done, 1)
            lg = logits[:, 0, 0:8 * NT].rearrange("p (t e) -> p t e", e=8)
            chain.step(nc.vector.tensor_reduce(stat[:], lg, AX, ALU.max))
            nc.vector.tensor_tensor(gates[:], lg, wide(stat[:]), ALU.subtract).then_inc(exp_in, 1)
            dve.wait_ge(exp_out, 1)
            chain.step(nc.vector.tensor_reduce(stat[:], gates[:], AX, ALU.add))
            chain.step(nc.vector.reciprocal(stat[:], stat[:]))
            chain.step(nc.vector.tensor_tensor(gates[:], gates[:], wide(stat[:]), ALU.mult))
            top2_mask(nc, m, chain, gates, top, where, wheref, pick, pick2)
            nc.vector.tensor_tensor(gates[:], gates[:], pick[:], ALU.mult).then_inc(gates_done, 1)
            dve.wait_ge(gates_done, 1)
            split3(nc, chain, gates[:], parts[:, :, 0, :], parts[:, :, 1, :], parts[:, :, 2, :], rest[:])
            dve.sem_inc(parts_done, 1)
            for n, (tc, e) in enumerate(UNITS):
                dve.wait_ge(spread_done, n + 1)
                if n >= 3:
                    dve.wait_ge(used, n - 2)
                nc.vector.tensor_tensor(scaled[:, n % 3, :], spread[:, n % 2, :], m.HT[:, tc * BANK:(tc + 1) * BANK],
                                        ALU.mult).then_inc(scaled_done, 1)
                if e == 1 and tc >= 1:
                    add(dve, tc - 1)
            add(dve, NT // 4 - 1)


def top2_mask(nc, m, chain, gates, top, where, wheref, pick, pick2):
    for g in range(NT):
        last = nc.vector.max(out=top[:, g, :], in_=gates[:, g, :])
    chain.step(last)
    for g in range(NT):
        last = nc.vector.max_index(where[:, g, :], top[:, g, :], gates[:, g, :])
    chain.step(last)
    chain.step(nc.vector.tensor_copy(wheref[:], where[:, :, 0:2]))
    index = m.iota8[:].unsqueeze(1).broadcast_to([P, NT, 8])
    chain.step(nc.vector.tensor_tensor(pick[:], index, wheref[:, :, 0:1].broadcast_to([P, NT, 8]), ALU.is_equal))
    chain.step(nc.vector.tensor_tensor(pick2[:], index, wheref[:, :, 1:2].broadcast_to([P, NT, 8]), ALU.is_equal))
    chain.step(nc.vector.tensor_tensor(pick[:], pick[:], pick2[:], ALU.add))


def attention_and_top2(nc, m, dram, s):
    small_head_attention(nc, m, dram, s)
    top2_experts(nc, m, dram, s)


def causal_attention(nc, m, dram, s, name, groups, heads, scale, out_proj):
    w = weight_views(m, s)
    D = P // heads
    GROUPS = [(b, c) for b in range(BATCH) for c in range(groups)]
    MIXED = [i for pair in zip(range(TPB - 1, TPB // 2 - 1, -1), range(TPB // 2)) for i in pair]
    UNITS = [(g, h, i) for g in range(len(GROUPS)) for h in range(heads) for i in MIXED]
    PER = heads * TPB

    def blocks(n):
        return UNITS[n][2] + 1

    def fills(n):
        return (blocks(n) + 3) // 4

    first_fill = [sum(fills(k) for k in range(n)) for n in range(len(UNITS) + 1)]

    def schedule():
        events, k = [], 0

        def misc_event(what, idx):
            nonlocal k
            events.append((what, idx, k))
            k += 1

        ahead = [4 + part * (PER - 4) // 6 for part in range(6)]
        for part in range(6):
            misc_event("project", (0, part))
        for n in range(len(UNITS) + 9):
            g, at = n // PER, n % PER
            if n < len(UNITS):
                events.append(("scores", n, None))
            for part in range(6):
                if ahead[part] == at and g + 1 < len(GROUPS):
                    misc_event("project", (g + 1, part))
            if 2 <= n < len(UNITS) + 2:
                events.append(("transposes", n - 2, None))
            if 3 <= n < len(UNITS) + 3:
                misc_event("values", n - 3)
            if out_proj and g >= 1 and at in (3, 4):
                misc_event("turn", (g - 1, at - 3))
            if out_proj and g >= 1 and at in (6, 7) and g % groups == 0:
                misc_event("out", (g // groups - 1, at - 6))
        return events

    EVENTS = schedule()
    projected = {idx[0]: k + 1 for what, idx, k in EVENTS if what == "project"}
    z_whole = {UNITS[idx][0]: k + 1 for what, idx, k in EVENTS if what == "values"}
    zt_half = {idx: k + 1 for what, idx, k in EVENTS if what == "turn"}

    with Phase(nc, name) as ph:
        qT = ph.sb("qT", [P, 2, SEQ])
        kT = ph.sb("kT", [P, 2, SEQ])
        v = ph.sb("v", [P, 2, TPB, P])
        probs = ph.sb("probs", [P, 3, SEQ])
        probsT = ph.sb("probsT", [P, 2, SEQ])
        negmax = ph.sb("negmax", [P, 3])
        rowsum = ph.sb("rowsum", [P, 5])
        rinv = ph.sb("rinv", [P, 2])
        z = ph.sb("z", [P, 2, TPB, P]) if out_proj else None
        zT = ph.sb("zT", [P, groups, SEQ]) if out_proj else None
        score = ph.ps("score", 4)
        turned = ph.ps("turned", 2)
        misc = ph.ps("misc", 2)
        misc_done, misc_kept, s_done, negmax_done, exp_done, t_done, t_kept, pv_done, chain_sem = (
            ph.sem(x) for x in ("misc_done", "misc_kept", "s_done", "negmax_done", "exp_done", "t_done", "t_kept",
                                "pv_done", "chain"))
        block = ph.block()

        def score_of(n):
            return score[:, 2 * (n % 2):2 * (n % 2) + 2, :].rearrange("p a n -> p (a n)")

        @block.sync
        def _(sp):
            load_weights(sp, m, dram, s + 1)

        @block.tensor
        def _(pe):
            pe.wait_ge(m.wsem[s], 16)
            for what, idx, k in EVENTS:
                if k is not None and k >= 2:
                    pe.wait_ge(misc_kept, k - 1)
                if what == "project":
                    g, part = idx
                    b, c = GROUPS[g]
                    if part < 4:
                        wt, half = w["Wq" if part < 2 else "Wk"], part % 2
                        nc.tensor.matmul(misc[:, k % 2, :], wt[:, c * P:(c + 1) * P],
                                         m.HT[:, b * SEQ + half * BANK:b * SEQ + (half + 1) * BANK], start=True,
                                         stop=True).then_inc(misc_done, 1)
                    else:
                        for j in range(4):
                            t = b * TPB + 4 * (part - 4) + j
                            last = nc.tensor.matmul(misc[:, k % 2, j * P:(j + 1) * P], m.HT[:, t * P:(t + 1) * P],
                                                    w["Wv"][:, c * P:(c + 1) * P], start=True, stop=True)
                        last.then_inc(misc_done, 1)
                elif what == "scores":
                    g, h, i = UNITS[idx]
                    if idx % PER == 0:
                        pe.wait_ge(misc_kept, projected[g])
                    if idx >= 2:
                        pe.wait_ge(exp_done, idx - 1)
                    wide = (i + 1) * P
                    for at in range(0, wide, BANK):
                        to = min(wide, at + BANK)
                        nc.tensor.matmul(score_of(idx)[:, at:to], qT[D * h:D * (h + 1), g % 2, i * P:(i + 1) * P],
                                                kT[D * h:D * (h + 1), g % 2, at:to], start=True, stop=(to < wide),
                                                skip_group_check=True)
                    nc.tensor.matmul(score_of(idx)[:, i * P:wide], m.identb[:], m.causalb[:], start=False, stop=True,
                                     skip_group_check=True).then_inc(s_done, 1)
                elif what == "transposes":
                    pe.wait_ge(exp_done, idx + 1)
                    for f in range(fills(idx)):
                        e = first_fill[idx] + f
                        if e >= 2:
                            pe.wait_ge(t_kept, e - 1)
                        for kb in range(4 * f, min(4 * f + 4, blocks(idx))):
                            last = nc.tensor.transpose(turned[:, e % 2, kb % 4 * P:(kb % 4 + 1) * P],
                                                       probs[:, idx % 3, kb * P:(kb + 1) * P], m.ident[:])
                        last.then_inc(t_done, 1)
                elif what == "values":
                    g, h, i = UNITS[idx]
                    pe.wait_ge(t_kept, first_fill[idx + 1])
                    for kb in range(i + 1):
                        last = nc.tensor.matmul(misc[:, k % 2, 0:D], probsT[:, idx % 2, kb * P:(kb + 1) * P],
                                                v[:, g % 2, kb, D * h:D * (h + 1)], start=(kb == 0), stop=(kb == i))
                    last.then_inc(misc_done, 1)
                elif what == "turn":
                    g, half = idx
                    pe.wait_ge(misc_kept, z_whole[g])
                    for j in range(4):
                        last = nc.tensor.transpose(misc[:, k % 2, j * P:(j + 1) * P], z[:, g % 2, 4 * half + j, :],
                                                   m.ident[:])
                    last.then_inc(misc_done, 1)
                else:
                    b, half = idx
                    pe.wait_ge(misc_kept, zt_half[groups * (b + 1) - 1, half])
                    for j in range(4):
                        t = 4 * half + j
                        for c in range(groups):
                            last = nc.tensor.matmul(misc[:, k % 2, j * P:(j + 1) * P], zT[:, c, t * P:(t + 1) * P],
                                                    w["Wo"][:, c * P:(c + 1) * P], start=(c == 0), stop=(c == groups - 1))
                    last.then_inc(misc_done, 1)

        @block.scalar
        def _(act):
            def exps(n):
                act.wait_ge(negmax_done, n + 1)
                if n >= 3:
                    act.wait_ge(t_done, first_fill[n - 2])
                wide = blocks(n) * P
                nc.scalar.activation(probs[:, n % 3, 0:wide], score_of(n)[:, 0:wide], ACT.Exp,
                                     bias=negmax[:, n % 3:n % 3 + 1],
                                     accum_out=rowsum[:, n % 5:n % 5 + 1]).then_inc(exp_done, 1)

            def keep(n):
                if n >= 2:
                    act.wait_ge(pv_done, n - 1)
                for f in range(fills(n)):
                    act.wait_ge(t_done, first_fill[n] + f + 1)
                    at, to = 4 * f * P, min(4 * f + 4, blocks(n)) * P
                    nc.scalar.activation(probsT[:, n % 2, at:to], turned[:, (first_fill[n] + f) % 2, 0:to - at],
                                         ACT.Copy).then_inc(t_kept, 1)
            for n in range(len(UNITS) + 2):
                if n >= 2:
                    keep(n - 2)
                if n < len(UNITS):
                    exps(n)

        @block.vector
        def _(dve):
            chain = Chain(dve, chain_sem)
            for what, idx, k in EVENTS:
                if k is not None:
                    dve.wait_ge(misc_done, k + 1)
                if what == "project":
                    g, part = idx
                    if part < 4:
                        to = (qT if part < 2 else kT)[:, g % 2, part % 2 * BANK:(part % 2 + 1) * BANK]
                    else:
                        to = v[:, g % 2, 4 * (part - 4):4 * (part - 3), :].rearrange("p t n -> p (t n)")
                    if part < 2:
                        nc.vector.tensor_scalar(to, misc[:, k % 2, :], scale, None, ALU.mult).then_inc(misc_kept, 1)
                    else:
                        nc.vector.tensor_copy(to, misc[:, k % 2, :]).then_inc(misc_kept, 1)
                elif what == "scores":
                    i = UNITS[idx][2]
                    dve.wait_ge(s_done, idx + 1)
                    if idx >= 3:
                        dve.wait_ge(exp_done, idx - 2)
                    nc.vector.tensor_reduce(negmax[:, idx % 3:idx % 3 + 1], score_of(idx)[:, 0:(i + 1) * P], AX,
                                            ALU.max, negate=True).then_inc(negmax_done, 1)
                elif what == "values":
                    g, h, i = UNITS[idx]
                    dve.sem_inc(pv_done, 1)
                    r = rinv[:, idx % 2:idx % 2 + 1]
                    chain.step(nc.vector.reciprocal(r, rowsum[:, idx % 5:idx % 5 + 1]))
                    if out_proj:
                        to = z[:, g % 2, i, D * h:D * (h + 1)]
                    else:
                        to = m.Y[:, GROUPS[g][0] * TPB + i, :]
                    nc.vector.tensor_scalar(to, misc[:, k % 2, 0:D], r, None, ALU.mult).then_inc(misc_kept, 1)
                elif what == "turn":
                    g, half = idx
                    nc.vector.tensor_copy(zT[:, GROUPS[g][1], half * BANK:(half + 1) * BANK],
                                          misc[:, k % 2, :]).then_inc(misc_kept, 1)
                elif what == "out":
                    b, half = idx
                    t = b * TPB + 4 * half
                    nc.vector.tensor_copy(m.Y[:, t:t + 4, :].rearrange("p t n -> p (t n)"),
                                          misc[:, k % 2, :]).then_inc(misc_kept, 1)


def causal_single_head(nc, m, dram, s):
    causal_attention(nc, m, dram, s, "one", 1, 1, float(P) ** -0.5, False)


def swiglu_experts(nc, m, dram, s):
    w = weight_views(m, s)
    E, IC = 8, 4
    UNITS = [(tc, e, ic) for tc in range(NT // 4) for e in range(E) for ic in range(IC)]
    with Phase(nc, "swiglu") as ph:
        logits = ph.sb("logits", [P, NT, 8])
        gates = ph.sb("gates", [P, NT, 8])
        pick = ph.sb("pick", [P, NT, 8])
        pick2 = ph.sb("pick2", [P, NT, 8])
        stat = ph.sb("stat", [P, NT])
        top = ph.sb("top", [P, NT, 8])
        where = ph.sb("where", [P, NT, 8], U32)
        wheref = ph.sb("wheref", [P, NT, 2])
        silu = ph.sb("silu", [P, 2, BANK])
        hidden = ph.sb("hidden", [P, 3, BANK])
        router = ph.ps("router", 1)
        gate_up = ph.ps("gate_up", 4)
        down = ph.ps("down", 2)
        (router_done, chain_sem, exp_in, exp_out, gu_done, silu_done, hid_done, down_done, y_done) = (
            ph.sem(x) for x in ("router_done", "chain", "exp_in", "exp_out", "gu_done", "silu_done", "hid_done",
                                "down_done", "y_done"))
        block = ph.block()

        @block.sync
        def _(sp):
            load_weights(sp, m, dram, s + 1)

        @block.tensor
        def _(pe):
            pe.wait_ge(m.wsem[s], 16)
            for g in range(NT):
                last = nc.tensor.matmul(router[:, 0, 8 * g:8 * g + 8], m.HT[:, g * P:(g + 1) * P], w["gate"], start=True,
                                        stop=True)
            last.then_inc(router_done, 1)
            for n in range(len(UNITS) + 1):
                if n < len(UNITS):
                    tc, e, ic = UNITS[n]
                    if n >= 2:
                        pe.wait_ge(hid_done, n - 1)
                    at = (e * IC + ic) * P
                    for k, wt in enumerate((w["wg"], w["wu"])):
                        nc.tensor.matmul(gate_up[:, 2 * (n % 2) + k, :], wt[:, at:at + P],
                                         m.HT[:, tc * BANK:(tc + 1) * BANK], start=True, stop=True).then_inc(gu_done, 1)
                if n >= 1:
                    tc, e, ic = UNITS[n - 1]
                    k = tc * E + e
                    pe.wait_ge(hid_done, n)
                    if ic == 0 and k >= 2:
                        pe.wait_ge(y_done, 4 * (k - 1))
                    at = (e * IC + ic) * P
                    for j in range(4):
                        last = nc.tensor.matmul(down[:, k % 2, j * P:(j + 1) * P],
                                                hidden[:, (n - 1) % 3, j * P:(j + 1) * P], w["wd"][:, at:at + P],
                                                start=(ic == 0 and j == 0), stop=(ic == IC - 1), skip_group_check=True)
                    last.then_inc(down_done, 1)

        @block.scalar
        def _(act):
            act.wait_ge(exp_in, 1)
            nc.scalar.activation(gates[:], gates[:], ACT.Exp).then_inc(exp_out, 1)
            for n in range(len(UNITS)):
                act.wait_ge(gu_done, 2 * n + 1)
                if n >= 2:
                    act.wait_ge(hid_done, n - 1)
                nc.scalar.activation(silu[:, n % 2, :], gate_up[:, 2 * (n % 2), :], ACT.Silu).then_inc(silu_done, 1)

        @block.vector
        def _(dve):
            chain = Chain(dve, chain_sem)

            def wide(a):
                return a.broadcast_to([P, NT, 8])
            dve.wait_ge(router_done, 1)
            chain.step(nc.vector.tensor_copy(logits[:].rearrange("p t e -> p (t e)"), router[:, 0, 0:8 * NT]))
            top2_mask(nc, m, chain, logits, top, where, wheref, pick, pick2)
            nc.vector.tensor_tensor(gates[:], logits[:], wide(top[:, :, 0:1]), ALU.subtract).then_inc(exp_in, 1)
            dve.wait_ge(exp_out, 1)
            chain.step(nc.vector.tensor_tensor(gates[:], gates[:], pick[:], ALU.mult))
            chain.step(nc.vector.tensor_reduce(stat[:], gates[:], AX, ALU.add))
            chain.step(nc.vector.reciprocal(stat[:], stat[:]))
            chain.step(nc.vector.tensor_tensor(gates[:], gates[:], wide(stat[:].unsqueeze(2)), ALU.mult))
            for n in range(len(UNITS) + 1):
                if n < len(UNITS):
                    dve.wait_ge(silu_done, n + 1)
                    dve.wait_ge(gu_done, 2 * n + 2)
                    if n >= 3:
                        dve.wait_ge(down_done, n - 2)
                    nc.vector.tensor_tensor(hidden[:, n % 3, :], gate_up[:, 2 * (n % 2) + 1, :], silu[:, n % 2, :],
                                            ALU.mult).then_inc(hid_done, 1)
                if n >= 1 and UNITS[n - 1][2] == IC - 1:
                    tc, e, _ = UNITS[n - 1]
                    k = tc * E + e
                    dve.wait_ge(down_done, n)
                    if e > 0:
                        dve.wait_ge(y_done, 4 * k)
                    for j in range(4):
                        t = 4 * tc + j
                        src, c = down[:, k % 2, j * P:(j + 1) * P], gates[:, t, e:e + 1]
                        if e == 0:
                            last = nc.vector.tensor_scalar(m.Y[:, t, :], src, c, None, ALU.mult)
                        else:
                            last = nc.vector.scalar_tensor_tensor(out=m.Y[:, t, :], in0=src, scalar=c,
                                                                  in1=m.Y[:, t, :], op0=ALU.mult, op1=ALU.add)
                        last.then_inc(y_done, 1)


def causal_sixteen_heads(nc, m, dram, s):
    causal_attention(nc, m, dram, s, "many", 8, 2, 0.125, True)


HID = 341
WIN = 64
LAYERS = 2
SPAN = P + WIN


def shift_tokens(nc, m, name, Z, ZS):
    with Phase(nc, name) as ph:
        moved, kept, first = ph.sem("moved"), ph.sem("kept"), ph.sem("first")
        block = ph.block()

        @block.vector
        def _(dve):
            nc.vector.tensor_copy(ZS[:, :, 0:WIN], Z[:, :, 0:WIN]).then_inc(kept, 1)

        @block.gpsimd
        def _(pool):
            for b in range(BATCH):
                nc.gpsimd.memset(ZS[0:1, b * TPB, WIN:P], 0.0).then_inc(first, 1)

        @block.sync
        def _(sp):
            sp.dma_start(ZS[1:P, :, WIN:P], Z[0:P - 1, :, WIN:P]).then_inc(moved, 16)
            for b in range(BATCH):
                t = b * TPB
                sp.dma_start(ZS[0:1, t + 1:t + TPB, WIN:P], Z[P - 1:P, t:t + TPB - 1, WIN:P]).then_inc(moved, 16)
            sp.wait_ge(moved, 16 * (1 + BATCH))


def rotary_scale_phase(nc, m, w, l, tables, scaled):
    with Phase(nc, f"tables{l}") as ph:
        rows = ph.ps("rows", 1)
        spread = ph.sb("spread", [P, 2, 64])
        rows_done, spread_done = ph.sem("rows_done"), ph.sem("spread_done")
        done = ph.sem("done")
        block = ph.block()

        @block.tensor
        def _(pe):
            for k, name in enumerate(("qscale", "kscale")):
                last = nc.tensor.matmul(rows[:, 0, 64 * k:64 * k + 64], m.ones[0:1, :], w[name][:, 64 * l:64 * l + 64],
                                        start=True, stop=True)
            last.then_inc(rows_done, 1)

        @block.vector
        def _(dve):
            dve.wait_ge(rows_done, 1)
            nc.vector.tensor_copy(spread[:], rows[:, 0, 0:P].rearrange("p (k d) -> p k d", k=2)).then_inc(spread_done, 1)
            dve.wait_ge(spread_done, 1)
            for k in range(2):
                cos, sin = (tables[2 * k + j].rearrange("p (t d) -> p t d", d=64) for j in range(2))
                nc.vector.tensor_tensor(scaled[:, 2 * k, :, :], cos,
                                        spread[:, k, :].unsqueeze(1).broadcast_to([P, TPB, 64]), ALU.mult).then_inc(done, 1)
                for half in range(2):
                    mine, other = slice(32 * half, 32 * half + 32), slice(32 - 32 * half, 64 - 32 * half)
                    nc.vector.tensor_tensor(scaled[:, 2 * k + 1, :, mine], sin[:, :, mine],
                                            spread[:, k, other].unsqueeze(1).broadcast_to([P, TPB, 32]),
                                            ALU.mult).then_inc(done, 1)


def rotary_qkv(nc, m, w, l, b, ZS, scaled, qT, kT, v, qnorm):
    with Phase(nc, f"qkv{l}{b}") as ph:
        HS = ph.sb("HS", [P, WIN + SEQ])
        squares = ph.sb("squares", [P, 2, 2, BANK])
        sumsq = ph.sb("sumsq", [P, 2, 16])
        rnorm = ph.sb("rnorm", [P, 2, 16])
        cospart = ph.sb("cospart", [P, 2, 2, BANK])
        sinpart = ph.sb("sinpart", [P, 2, 2, BANK])
        rotated = ph.sb("rotated", [P, 2, 2, BANK])
        proj = ph.ps("proj", 4)
        vps = ph.ps("vps", 2)
        turned = ph.ps("turned", 2)
        (hs_turned, hs_kept, cleared, qk_done, sq_done, sum_done, clamp_done, rnorm_done, cs_done, add_done, rot_done,
         t_done, t_kept, v_done, v_kept, qn_done) = (
            ph.sem(x) for x in ("hs_turned", "hs_kept", "cleared", "qk_done", "sq_done", "sum_done", "clamp_done",
                                "rnorm_done", "cs_done", "add_done", "rot_done", "t_done", "t_kept", "v_done", "v_kept",
                                "qn_done"))
        block = ph.block()
        wl = w["wqkv"][:, 1536 * l:1536 * (l + 1)]

        @block.tensor
        def _(pe):
            for half in range(2):
                for j in range(4):
                    last = nc.tensor.transpose(turned[:, half, j * P:(j + 1) * P], ZS[:, b * TPB + 4 * half + j, :],
                                               m.ident[:])
                last.then_inc(hs_turned, 1)
            pe.wait_ge(hs_kept, 2)
            pe.wait_ge(cleared, 2)

            def values(i):
                n = P if i < TPB else WIN
                if i >= 2:
                    pe.wait_ge(v_kept, i - 1)
                nc.tensor.matmul(vps[0:n, i % 2, :], HS[:, i * P:i * P + n], wl[:, 1024:1536], start=True,
                                 stop=True).then_inc(v_done, 1)

            def turn(i):
                for k in range(2):
                    pe.wait_ge(rot_done, 2 * i + k + 1)
                    if i >= 1:
                        pe.wait_ge(t_kept, 2 * i - 1 + k)
                    for c in range(4):
                        last = nc.tensor.transpose(turned[:, k, c * P:(c + 1) * P],
                                                   rotated[:, i % 2, k, c * P:(c + 1) * P], m.ident[:])
                    last.then_inc(t_done, 1)
            for i in range(TPB):
                if i >= 2:
                    pe.wait_ge(cs_done, 6 * (i - 1))
                    pe.wait_ge(sq_done, 2 * (i - 1))
                for k in range(2):
                    nc.tensor.matmul(proj[:, 2 * (i % 2) + k, :], HS[:, WIN + i * P:WIN + (i + 1) * P],
                                     wl[:, k * BANK:(k + 1) * BANK], start=True, stop=True).then_inc(qk_done, 1)
                values(i)
                if i >= 1:
                    turn(i - 1)
            values(TPB)
            turn(TPB - 1)

        @block.scalar
        def _(act):
            for half in range(2):
                act.wait_ge(hs_turned, half + 1)
                nc.scalar.activation(HS[:, WIN + half * BANK:WIN + (half + 1) * BANK], turned[:, half, :],
                                     ACT.Copy).then_inc(hs_kept, 1)

            def keep(i):
                for k, to in enumerate((qT[:, :, i * P:(i + 1) * P], kT[:, :, WIN + i * P:WIN + (i + 1) * P])):
                    act.wait_ge(t_done, 2 * i + k + 1)
                    nc.scalar.activation(to, turned[:, k, :].rearrange("p (c n) -> p c n", c=4), ACT.Copy).then_inc(t_kept, 1)

            def keep_v(i):
                n = P if i < TPB else WIN
                act.wait_ge(v_done, i + 1)
                nc.scalar.activation(v[0:n, i, :], vps[0:n, i % 2, :], ACT.Copy).then_inc(v_kept, 1)
            for i in range(TPB):
                for k in range(2):
                    act.wait_ge(qk_done, 2 * i + k + 1)
                    if i >= 2:
                        act.wait_ge(sum_done, i - 1)
                    nc.scalar.activation(squares[:, i % 2, k, :], proj[:, 2 * (i % 2) + k, :], ACT.Square).then_inc(sq_done, 1)
                keep_v(i)
                if i >= 1:
                    keep(i - 1)
            keep_v(TPB)
            keep(TPB - 1)

        def scale_k(dve, i):
            dve.wait_ge(rnorm_done, i + 1)
            nc.vector.tensor_scalar(qnorm[:, i, :], rnorm[:, i % 2, 0:8], 8.0, None, ALU.mult)
            dve.wait_ge(add_done, 2 * i + 1)
            dve.sem_inc(rot_done, 1)
            dve.wait_ge(add_done, 2 * i + 2)
            kr = rotated[:, i % 2, 1, :].rearrange("p (h d) -> p h d", d=64)
            nc.vector.tensor_tensor(kr, kr, rnorm[:, i % 2, 8:16].unsqueeze(2).broadcast_to([P, 8, 64]),
                                    ALU.mult).then_inc(qn_done, 1)
            dve.wait_ge(qn_done, i + 1)
            dve.sem_inc(rot_done, 1)

        @block.vector
        def _(dve):
            nc.vector.memset(HS[:, 0:WIN], 0.0).then_inc(cleared, 1)
            nc.vector.memset(kT[:, :, 0:WIN], 0.0).then_inc(cleared, 1)
            for i in range(TPB):
                dve.wait_ge(sq_done, 2 * i + 2)
                nc.vector.tensor_reduce(sumsq[:, i % 2, :], squares[:, i % 2, :, :].rearrange("p k (h d) -> p (k h) d", d=64),
                                        AX, ALU.add).then_inc(sum_done, 1)
                dve.wait_ge(sum_done, i + 1)
                if i >= 2:
                    dve.wait_ge(qn_done, i - 1)
                nc.vector.tensor_scalar(rnorm[:, i % 2, :], sumsq[:, i % 2, :], 1e-24, None, ALU.max).then_inc(clamp_done, 1)
                if i >= 2:
                    dve.wait_ge(add_done, 2 * (i - 1))
                for k in range(2):
                    src = proj[:, 2 * (i % 2) + k, :].rearrange("p (h d) -> p h d", d=64)
                    cos = scaled[:, 2 * k, i, :].unsqueeze(1).broadcast_to([P, 8, 64])
                    nc.vector.tensor_tensor(cospart[:, i % 2, k, :].rearrange("p (h d) -> p h d", d=64), src, cos,
                                            ALU.mult).then_inc(cs_done, 1)
                    for half in range(2):
                        mine, other = slice(32 * half, 32 * half + 32), slice(32 - 32 * half, 64 - 32 * half)
                        nc.vector.tensor_tensor(sinpart[:, i % 2, k, :].rearrange("p (h d) -> p h d", d=64)[:, :, mine],
                                                src[:, :, other],
                                                scaled[:, 2 * k + 1, i, mine].unsqueeze(1).broadcast_to([P, 8, 32]),
                                                ALU.mult).then_inc(cs_done, 1)
                if i >= 1:
                    scale_k(dve, i - 1)
            scale_k(dve, TPB - 1)

        @block.gpsimd
        def _(pool):
            for i in range(TPB):
                pool.wait_ge(clamp_done, i + 1)
                nc.gpsimd.tensor_tensor(rnorm[:, i % 2, :], rnorm[:, i % 2, :], m.neghalf[:], ALU.pow).then_inc(rnorm_done, 1)
                for k in range(2):
                    pool.wait_ge(cs_done, 6 * i + 3 * k + 3)
                    if i >= 2:
                        pool.wait_ge(t_done, 2 * (i - 2) + k + 1)
                    nc.gpsimd.tensor_tensor(rotated[:, i % 2, k, :], cospart[:, i % 2, k, :], sinpart[:, i % 2, k, :],
                                            ALU.add).then_inc(add_done, 1)


def local_attention(nc, m, w, l, b, Z, qT, kT, v, qnorm, band_first):
    with Phase(nc, f"local{l}{b}") as ph:
        probs = ph.sb("probs", [P, 2, 4, SPAN])
        probsT = ph.sb("probsT", [P, 2, 4, 2 * P])
        rowmax = ph.sb("rowmax", [P, 2, 4])
        negmax = ph.sb("negmax", [P, 2, 4])
        rowsum = ph.sb("rowsum", [P, 2, 8])
        o = ph.sb("o", [P, BANK])
        oT = ph.sb("oT", [P, BANK])
        score = ph.ps("score", 4)
        turned = ph.ps("turned", 2)
        outp = ph.ps("outp", 1)
        misc = ph.ps("misc", 1)
        (s_done, chain_sem, negmax_done, exp_done, t_done, t_kept, pv_done, o_done, ot_done, ot_kept, y_done, z_done) = (
            ph.sem(x) for x in ("s_done", "chain", "negmax_done", "exp_done", "t_done", "t_kept", "pv_done", "o_done",
                                "ot_done", "ot_kept", "y_done", "z_done"))
        block = ph.block()
        N = 2 * TPB
        wo = w["wo"][:, 512 * l:512 * (l + 1)]
        HEADS = [(c, j) for c in range(2) for j in range(2)]

        def score_at(n, c, j):
            return score[:, 2 * (n % 2) + j, 256 * c:256 * c + SPAN]

        @block.tensor
        def _(pe):
            def scores(n):
                i, q4 = n // 2, n % 2
                if n >= 2:
                    pe.wait_ge(exp_done, 4 * (n - 1))
                for j in range(2):
                    for c in range(2):
                        cc = 2 * q4 + c
                        last = nc.tensor.matmul(score_at(n, c, j), qT[64 * j:64 * j + 64, cc, i * P:(i + 1) * P],
                                                kT[64 * j:64 * j + 64, cc, i * P:i * P + SPAN], start=True, stop=True)
                last.then_inc(s_done, 1)

            def turn(n):
                pe.wait_ge(exp_done, 4 * (n + 1))
                for pair in range(2):
                    e = 2 * n + pair
                    if e >= 2:
                        pe.wait_ge(t_kept, e - 1)
                    for k in range(2):
                        hh = 2 * pair + k
                        nc.tensor.transpose(turned[:, e % 2, 256 * k:256 * k + P], probs[:, n % 2, hh, 0:P], m.ident[:])
                        last = nc.tensor.transpose(turned[0:WIN, e % 2, 256 * k + P:256 * k + 2 * P],
                                                   probs[:, n % 2, hh, P:SPAN], m.ident[:])
                    last.then_inc(t_done, 1)

            def values(n):
                i, q4 = n // 2, n % 2
                pe.wait_ge(t_kept, 2 * (n + 1))
                if q4 == 0 and i > 0:
                    pe.wait_ge(o_done, i)
                for hh, (c, j) in enumerate(HEADS):
                    h = 2 * (2 * q4 + c) + j
                    to = outp[:, 0, 64 * h:64 * h + 64]
                    nc.tensor.matmul(to, probsT[:, n % 2, hh, 0:P], v[:, i, 64 * h:64 * h + 64], start=True, stop=False)
                    last = nc.tensor.matmul(to, probsT[0:WIN, n % 2, hh, P:2 * P], v[0:WIN, i + 1, 64 * h:64 * h + 64],
                                            start=False, stop=True)
                last.then_inc(pv_done, 1)

            def project(i):
                pe.wait_ge(o_done, i + 1)
                if i > 0:
                    pe.wait_ge(z_done, i)
                for c in range(4):
                    last = nc.tensor.transpose(misc[:, 0, c * P:(c + 1) * P], o[:, c * P:(c + 1) * P], m.ident[:])
                last.then_inc(ot_done, 1)
                pe.wait_ge(ot_kept, i + 1)
                for c in range(4):
                    last = nc.tensor.matmul(misc[:, 0, 0:P], oT[:, c * P:(c + 1) * P], wo[:, c * P:(c + 1) * P],
                                            start=(c == 0), stop=(c == 3))
                last.then_inc(y_done, 1)
            for n in range(N + 3):
                if n < N:
                    scores(n)
                if 1 <= n <= N:
                    turn(n - 1)
                if 2 <= n <= N + 1:
                    values(n - 2)
                if n >= 4 and n % 2 == 0:
                    project(n // 2 - 2)

        @block.scalar
        def _(act):
            def keep(n):
                if n >= 2:
                    act.wait_ge(pv_done, n - 1)
                for pair in range(2):
                    e = 2 * n + pair
                    act.wait_ge(t_done, e + 1)
                    to, src = probsT[:, n % 2, 2 * pair:2 * pair + 2, :], turned[:, e % 2, :].rearrange("p (k q) -> p k q", k=2)
                    nc.scalar.activation(to[:, :, 0:P], src[:, :, 0:P], ACT.Copy)
                    nc.scalar.activation(to[0:WIN, :, P:2 * P], src[0:WIN, :, P:2 * P], ACT.Copy).then_inc(t_kept, 1)
            for n in range(N + 1):
                if n < N:
                    i, q4 = n // 2, n % 2
                    act.wait_ge(negmax_done, n + 1)
                    if n >= 2:
                        act.wait_ge(t_done, 2 * (n - 1))
                    if n >= 4:
                        act.wait_ge(o_done, i - 1)
                    for hh, (c, j) in enumerate(HEADS):
                        h = 2 * (2 * q4 + c) + j
                        nc.scalar.activation(probs[:, n % 2, hh, :], score_at(n, c, j), ACT.Exp,
                                             bias=negmax[:, n % 2, hh:hh + 1], scale=qnorm[:, i, h:h + 1],
                                             accum_out=rowsum[:, i % 2, h:h + 1]).then_inc(exp_done, 1)
                if n >= 1:
                    keep(n - 1)

        @block.vector
        def _(dve):
            chain = Chain(dve, chain_sem)

            def finish(i):
                dve.wait_ge(pv_done, 2 * (i + 1))
                if i > 0:
                    dve.wait_ge(ot_done, i)
                chain.step(nc.vector.reciprocal(rowsum[:, i % 2, :], rowsum[:, i % 2, :]))
                nc.vector.tensor_tensor(o[:].rearrange("p (h d) -> p h d", d=64),
                                        outp[:, 0, :].rearrange("p (h d) -> p h d", d=64),
                                        rowsum[:, i % 2, :].unsqueeze(2).broadcast_to([P, 8, 64]), ALU.mult).then_inc(o_done, 1)
                dve.wait_ge(ot_done, i + 1)
                nc.vector.tensor_copy(oT[:], misc[:, 0, :]).then_inc(ot_kept, 1)

            def add(i):
                dve.wait_ge(y_done, i + 1)
                t = b * TPB + i
                nc.vector.tensor_tensor(Z[:, t, :], misc[:, 0, 0:P], Z[:, t, :], ALU.add).then_inc(z_done, 1)
            for n in range(N):
                i, q4 = n // 2, n % 2
                dve.wait_ge(s_done, n + 1)
                band = band_first if i == 0 else m.band
                for j in range(2):
                    sj = score[:, 2 * (n % 2) + j, :].rearrange("p (c k) -> p c k", c=2)[:, :, 0:SPAN]
                    last = nc.vector.tensor_tensor(sj, sj, band[:].unsqueeze(1).broadcast_to([P, 2, SPAN]), ALU.add)
                chain.step(last)
                for j in range(2):
                    sj = score[:, 2 * (n % 2) + j, :].rearrange("p (c k) -> p c k", c=2)[:, :, 0:SPAN]
                    last = nc.vector.tensor_reduce(rowmax[:, n % 2, j:4:2], sj, AX, ALU.max)
                chain.step(last)
                if n >= 2:
                    dve.wait_ge(exp_done, 4 * (n - 1))
                q4n = qnorm[:, i, 4 * q4:4 * q4 + 4]
                nc.vector.scalar_tensor_tensor(out=negmax[:, n % 2, :], in0=rowmax[:, n % 2, :], scalar=-1.0, in1=q4n,
                                               op0=ALU.mult, op1=ALU.mult).then_inc(negmax_done, 1)
                if n >= 4 and n % 2 == 0:
                    if n >= 6:
                        add(n // 2 - 3)
                    finish(n // 2 - 2)
            for i in range(TPB - 2, TPB):
                add(i - 1)
                finish(i)
            add(TPB - 1)


def gated_mlp(nc, m, w, l, Z, ZS, into):
    with Phase(nc, f"mlp{l}") as ph:
        stats = ph.sb("stats", [P, NT, 6])
        mv = ph.sb("mv", [P, NT, 2])
        rstd = ph.sb("rstd", [P, NT])
        shift = ph.sb("shift", [P, NT])
        gelu = ph.sb("gelu", [P, 2, BANK])
        hidden = ph.sb("hidden", [P, 2, 3, BANK])
        turned = ph.ps("turned", 2)
        agp = ph.ps("agp", 4)
        down = ph.ps("down", 2)
        (stat_done, aggr_done, var_done, rstd_done, shift_done, norm_done, turn_done, turn_kept, ag_done, gelu_done,
         hid_done, down_done, z_done) = (
            ph.sem(x) for x in ("stat_done", "aggr_done", "var_done", "rstd_done", "shift_done", "norm_done",
                                "turn_done", "turn_kept", "ag_done", "gelu_done", "hid_done", "down_done", "z_done"))
        block = ph.block()
        w1 = w["w1"][:, 2 * HID * l:2 * HID * (l + 1)]
        w2 = w["w2"][:, 384 * l:384 * (l + 1)]
        b1 = w["b1"][:, 6 * l:6 * (l + 1)]
        b2 = w["b2"][:, P * l:P * (l + 1)]
        ROWS = [P, P, HID - 2 * P]
        UNITS = [(tc, c) for tc in range(NT // 4) for c in range(3)]

        @block.vector
        def _(dve):
            for t in range(NT):
                nc.vector.bn_stats(stats[:, t, :], ZS[:, t, :]).then_inc(stat_done, 1)
            for t in range(NT):
                dve.wait_ge(stat_done, t + 1)
                nc.vector.bn_aggr(mv[:, t, :], stats[:, t, :]).then_inc(aggr_done, 1)
            dve.wait_ge(aggr_done, NT)
            nc.vector.tensor_scalar(rstd[:], mv[:, :, 1], LN_EPS, None, ALU.add).then_inc(var_done, 1)
            dve.wait_ge(rstd_done, 1)
            nc.vector.scalar_tensor_tensor(out=shift[:], in0=mv[:, :, 0], scalar=-1.0, in1=rstd[:], op0=ALU.mult,
                                           op1=ALU.mult).then_inc(shift_done, 1)
            for c in range(NT // 4):
                dve.wait_ge(turn_done, c + 1)
                nc.vector.tensor_scalar(m.HT[:, c * BANK:(c + 1) * BANK], turned[:, c % 2, :], w["lng"][:, l:l + 1],
                                        w["lnb"][:, l:l + 1], ALU.mult, ALU.add).then_inc(turn_kept, 1)
            for n, (tc, c) in enumerate(UNITS):
                r = ROWS[c]
                dve.wait_ge(gelu_done, n + 1)
                dve.wait_ge(ag_done, 2 * n + 2)
                if tc >= 2:
                    dve.wait_ge(down_done, tc - 1)
                nc.vector.scalar_tensor_tensor(out=hidden[0:r, tc % 2, c, :], in0=agp[0:r, 2 * (n % 2), :],
                                               scalar=b1[0:r, c:c + 1], in1=gelu[0:r, n % 2, :], op0=ALU.add,
                                               op1=ALU.mult).then_inc(hid_done, 1)
                if c == 2:
                    dve.wait_ge(down_done, tc + 1)
                    nc.vector.tensor_tensor(into[:, 4 * tc:4 * tc + 4, :], down[:, tc % 2, :].rearrange("p (t n) -> p t n", t=4),
                                            Z[:, 4 * tc:4 * tc + 4, :], ALU.add).then_inc(z_done, 1)

        @block.gpsimd
        def _(pool):
            pool.wait_ge(var_done, 1)
            nc.gpsimd.tensor_tensor(rstd[:], rstd[:], m.neghalf[:], ALU.pow).then_inc(rstd_done, 1)

        @block.scalar
        def _(act):
            act.wait_ge(shift_done, 1)
            for t in range(NT):
                nc.scalar.activation(ZS[:, t, :], ZS[:, t, :], ACT.Identity, bias=shift[:, t:t + 1],
                                     scale=rstd[:, t:t + 1]).then_inc(norm_done, 1)
            for n, (tc, c) in enumerate(UNITS):
                r = ROWS[c]
                act.wait_ge(ag_done, 2 * n + 2)
                if n >= 2:
                    act.wait_ge(hid_done, n - 1)
                nc.scalar.activation(gelu[0:r, n % 2, :], agp[0:r, 2 * (n % 2) + 1, :], ACT.Gelu,
                                     bias=b1[0:r, 3 + c:4 + c]).then_inc(gelu_done, 1)

        @block.tensor
        def _(pe):
            for c in range(NT // 4):
                pe.wait_ge(norm_done, 4 * (c + 1))
                if c >= 2:
                    pe.wait_ge(turn_kept, c - 1)
                for j in range(4):
                    last = nc.tensor.transpose(turned[:, c % 2, j * P:(j + 1) * P], ZS[:, 4 * c + j, :], m.ident[:])
                last.then_inc(turn_done, 1)
            pe.wait_ge(turn_kept, NT // 4)

            def project(tc):
                pe.wait_ge(hid_done, 3 * (tc + 1))
                if tc >= 2:
                    pe.wait_ge(z_done, tc - 1)
                for j in range(4):
                    to = down[:, tc % 2, j * P:(j + 1) * P]
                    for c in range(3):
                        r = ROWS[c]
                        nc.tensor.matmul(to, hidden[0:r, tc % 2, c, j * P:(j + 1) * P], w2[0:r, c * P:(c + 1) * P],
                                         start=(c == 0), stop=False)
                    last = nc.tensor.matmul(to, m.ones[0:1, :], b2, start=False, stop=True)
                last.then_inc(down_done, 1)
            for n, (tc, c) in enumerate(UNITS):
                r = ROWS[c]
                if n >= 2:
                    pe.wait_ge(hid_done, n - 1)
                for k in range(2):
                    at = k * HID + c * P
                    nc.tensor.matmul(agp[0:r, 2 * (n % 2) + k, :], w1[:, at:at + r], m.HT[:, tc * BANK:(tc + 1) * BANK],
                                     start=True, stop=True).then_inc(ag_done, 1)
                if c == 2:
                    project(tc)


def local_transformer(nc, m, dram, s):
    w = weight_views(m, s)
    with ExitStack() as keep:
        def kept(name, shape):
            return keep.enter_context(nc.sbuf_tensor(f"loc_{name}", shape, F32))
        ZS = kept("ZS", [P, NT, P])
        scaled = kept("scaled", [P, 4, TPB, 64])
        qT = kept("qT", [P, 4, SEQ])
        kT = kept("kT", [P, 4, WIN + SEQ])
        v = kept("v", [P, TPB + 1, BANK])
        qnorm = kept("qnorm", [P, TPB, 8])
        band_first = kept("band_first", [P, SPAN])
        Z = m.XN
        with Phase(nc, "locfirst") as ph:
            copied = ph.sem("copied")
            block = ph.block()

            @block.sync
            def _(sp):
                sp.wait_ge(m.wsem[s], 16)
                load_weights(sp, m, dram, s + 1)

            @block.gpsimd
            def _(pool):
                nc.gpsimd.tensor_copy(band_first[:, WIN:SPAN], m.band[:, WIN:SPAN]).then_inc(copied, 1)
                nc.gpsimd.memset(band_first[:, 0:WIN], NEG).then_inc(copied, 1)
        tables = [w[k] for k in ("cosq", "sinq", "cosk", "sink")]
        for l in range(LAYERS):
            rotary_scale_phase(nc, m, w, l, tables, scaled)
            shift_tokens(nc, m, f"shifta{l}", Z, ZS)
            for b in range(BATCH):
                rotary_qkv(nc, m, w, l, b, ZS, scaled, qT, kT, v, qnorm)
                local_attention(nc, m, w, l, b, Z, qT, kT, v, qnorm, band_first)
            shift_tokens(nc, m, f"shiftb{l}", Z, ZS)
            gated_mlp(nc, m, w, l, Z, ZS, m.Y if l == 1 else Z)


DI, NS, RANK, TAPS = 256, 16, 64, 4
NCH = DI // P


def mamba_norm(nc, m, U):
    with Phase(nc, "mnorm") as ph:
        stats = ph.sb("stats", [P, NT, 6])
        mv = ph.sb("mv", [P, NT, 2])
        rstd = ph.sb("rstd", [P, NT])
        shift = ph.sb("shift", [P, NT])
        stat_done, aggr_done, var_done, rstd_done, shift_done, norm_done = (
            ph.sem(x) for x in ("stat_done", "aggr_done", "var_done", "rstd_done", "shift_done", "norm_done"))
        block = ph.block()

        @block.vector
        def _(dve):
            for t in range(NT):
                nc.vector.bn_stats(stats[:, t, :], m.XN[:, t, :]).then_inc(stat_done, 1)
            for t in range(NT):
                dve.wait_ge(stat_done, t + 1)
                nc.vector.bn_aggr(mv[:, t, :], stats[:, t, :]).then_inc(aggr_done, 1)
            dve.wait_ge(aggr_done, NT)
            nc.vector.tensor_scalar(rstd[:], mv[:, :, 1], LN_EPS, None, ALU.add).then_inc(var_done, 1)
            dve.wait_ge(rstd_done, 1)
            nc.vector.scalar_tensor_tensor(out=shift[:], in0=mv[:, :, 0], scalar=-1.0, in1=rstd[:], op0=ALU.mult,
                                           op1=ALU.mult).then_inc(shift_done, 1)

        @block.gpsimd
        def _(pool):
            pool.wait_ge(var_done, 1)
            nc.gpsimd.tensor_tensor(rstd[:], rstd[:], m.neghalf[:], ALU.pow).then_inc(rstd_done, 1)

        @block.scalar
        def _(act):
            act.wait_ge(shift_done, 1)
            for t in range(NT):
                nc.scalar.activation(U[:, t, :], m.XN[:, t, :], ACT.Identity, bias=shift[:, t:t + 1],
                                     scale=rstd[:, t:t + 1]).then_inc(norm_done, 1)


def mamba_setup(nc, m, dram, s, w, select, negA, Wx3):
    with Phase(nc, "msetup") as ph:
        sel_done, a_done, x_done = ph.sem("sel_done"), ph.sem("a_done"), ph.sem("x_done")
        block = ph.block()

        @block.sync
        def _(sp):
            sp.wait_ge(m.wsem[s], 16)
            load_weights(sp, m, dram, s + 1)

        @block.gpsimd
        def _(pool):
            nc.gpsimd.memset(select[:], 0.0).then_inc(sel_done, 1)
            for r in range(3):
                pool.wait_ge(sel_done, r + 1)
                nc.gpsimd.affine_select(out=select[:], in_=select[:], compare_op=ALU.not_equal, fill=1.0, base=-32 * r,
                                        pattern=[[-1, 2 * NS], [0, P]], channel_multiplier=1).then_inc(sel_done, 1)

        @block.scalar
        def _(act):
            act.wait_ge(m.wsem[s], 16)
            nc.scalar.activation(negA[:], w["Alog"], ACT.Exp).then_inc(a_done, 1)

        @block.vector
        def _(dve):
            dve.wait_ge(m.wsem[s], 16)
            for r in range(3):
                nc.vector.tensor_copy(Wx3[:, :, 2 * NS * r:2 * NS * (r + 1)],
                                      w["Wx"].rearrange("p (q n) -> p q n", n=RANK + 2 * NS)[:, :, RANK:RANK + 2 * NS]
                                      ).then_inc(x_done, 1)
            dve.wait_ge(a_done, 1)
            nc.vector.tensor_scalar(negA[:], negA[:], -1.0, None, ALU.mult).then_inc(x_done, 1)


def mamba_front(nc, m, w, d, b, U, xc, sz, delta, du, BC3, Wx3):
    with Phase(nc, f"front{d}{b}") as ph:
        UT = ph.sb("UT", [P, SEQ])
        padded = ph.sb("padded", [P, NCH, TAPS - 1 + SEQ])
        conv = ph.sb("conv", [P, NCH, SEQ])
        dt = ph.sb("dt", [RANK, SEQ])
        bchi = ph.sb("bchi", [96, SEQ], BF16)
        bcmid = ph.sb("bcmid", [96, SEQ], BF16)
        rest = ph.sb("rest", [96, SEQ])
        soft = ph.sb("soft", [P, 4, BANK])
        ring = ph.ps("ring", 4)
        dbl = ph.ps("dbl", 4)
        (turn_done, turn_kept, padded_clear, in_done, in_kept, conv_sem, conv_done, xc_done, dbl_done, dt_kept, dl_done,
         relu_done, abs_done, exp_done, ln_done, delta_done, chain_sem) = (
            ph.sem(x) for x in ("turn_done", "turn_kept", "padded_clear", "in_done", "in_kept", "conv_sem", "conv_done",
                                "xc_done", "dbl_done", "dt_kept", "dl_done", "relu_done", "abs_done", "exp_done",
                                "ln_done", "delta_done", "chain"))
        block = ph.block()
        Win = w["Win"][:, 2 * DI * d:2 * DI * (d + 1)]
        bin_ = w["bin"][:, 4 * d:4 * (d + 1)]
        bdt = w["bdt"][:, 2 * d:2 * (d + 1)]

        @block.tensor
        def _(pe):
            for half in range(2):
                for j in range(4):
                    i = 4 * half + j
                    t = b * TPB + (i if d == 0 else TPB - 1 - i)
                    to = dbl[:, half, j * P:(j + 1) * P]
                    if d == 0:
                        last = nc.tensor.transpose(to, U[:, t, :], m.ident[:])
                    else:
                        last = nc.tensor.matmul(to, U[:, t, :], m.flip[:], start=True, stop=True)
                last.then_inc(turn_done, 1)
            pe.wait_ge(turn_kept, 2)
            for u in range(8):
                if u >= 4:
                    pe.wait_ge(in_kept, u - 3)
                nc.tensor.matmul(ring[:, u % 4, :], Win[:, u // 2 * P:(u // 2 + 1) * P],
                                 UT[:, u % 2 * BANK:(u % 2 + 1) * BANK], start=True, stop=True).then_inc(in_done, 1)
            pe.wait_ge(xc_done, NCH)
            for half in range(2):
                rhs = [xc[:, ch, half * BANK:(half + 1) * BANK] for ch in range(NCH)]
                for ch in range(NCH):
                    q = (NCH * d + ch) * (RANK + 2 * NS)
                    last = nc.tensor.matmul(dbl[0:RANK, 2 * half, :], w["Wx"][:, q:q + RANK], rhs[ch], start=(ch == 0),
                                            stop=(ch == NCH - 1))
                last.then_inc(dbl_done, 1)
                for ch in range(NCH):
                    last = nc.tensor.matmul(dbl[0:96, 2 * half + 1, :], Wx3[:, NCH * d + ch, :], rhs[ch],
                                            start=(ch == 0), stop=(ch == NCH - 1))
                last.then_inc(dbl_done, 1)
            pe.wait_ge(in_kept, 8)
            for ch in range(NCH):
                for half in range(2):
                    pe.wait_ge(dt_kept, half + 1)
                    nc.tensor.matmul(ring[:, 2 * ch + half, :], w["Wdt"][:, DI * d + ch * P:DI * d + (ch + 1) * P],
                                     dt[:, half * BANK:(half + 1) * BANK], start=True, stop=True).then_inc(dl_done, 1)

        @block.scalar
        def _(act):
            act.wait_ge(padded_clear, 1)
            for u in range(8):
                act.wait_ge(in_done, u + 1)
                c, half = u // 2, u % 2
                if c < NCH:
                    nc.scalar.activation(padded[:, c, TAPS - 1 + half * BANK:TAPS - 1 + (half + 1) * BANK],
                                         ring[:, u % 4, :], ACT.Identity, bias=bin_[:, c:c + 1]).then_inc(in_kept, 1)
                else:
                    nc.scalar.activation(sz[:, c - NCH, half * BANK:(half + 1) * BANK], ring[:, u % 4, :], ACT.Silu,
                                         bias=bin_[:, c:c + 1]).then_inc(in_kept, 1)
            for ch in range(NCH):
                act.wait_ge(conv_done, ch + 1)
                nc.scalar.activation(xc[:, ch, :], conv[:, ch, :], ACT.Silu).then_inc(xc_done, 1)
            for half in range(2):
                act.wait_ge(dbl_done, 2 * half + 1)
                nc.scalar.activation(dt[:, half * BANK:(half + 1) * BANK], dbl[0:RANK, 2 * half, :],
                                     ACT.Copy).then_inc(dt_kept, 1)
            for u in range(4):
                act.wait_ge(dl_done, u + 1)
                nc.scalar.activation(soft[:, u, :], ring[:, u, :], ACT.Abs, bias=bdt[:, u // 2:u // 2 + 1]).then_inc(abs_done, 1)
            act.wait_ge(abs_done, 4)
            nc.scalar.activation(soft[:], soft[:], ACT.Exp, scale=-1.0).then_inc(exp_done, 1)
            act.wait_ge(exp_done, 1)
            nc.scalar.activation(soft[:], soft[:], ACT.Ln, bias=1.0).then_inc(ln_done, 1)

        @block.vector
        def _(dve):
            chain = Chain(dve, chain_sem)
            nc.vector.memset(padded[:, :, 0:TAPS - 1], 0.0).then_inc(padded_clear, 1)
            for half in range(2):
                dve.wait_ge(turn_done, half + 1)
                nc.vector.tensor_scalar(UT[:, half * BANK:(half + 1) * BANK], dbl[:, half, :], w["lnw"][:, d:d + 1],
                                        w["lnb"][:, d:d + 1], ALU.mult, ALU.add).then_inc(turn_kept, 1)
            for ch in range(NCH):
                dve.wait_ge(in_kept, 2 * ch + 2)
                taps = w["convw"][:, (NCH * d + ch) * TAPS:(NCH * d + ch + 1) * TAPS]
                cb = w["convb"][:, NCH * d + ch:NCH * d + ch + 1]
                chain.step(nc.vector.tensor_scalar(conv[:, ch, :], padded[:, ch, 0:SEQ], taps[:, 0:1], cb, ALU.mult, ALU.add))
                for k in range(1, TAPS):
                    chain.step(nc.vector.scalar_tensor_tensor(out=conv[:, ch, :], in0=padded[:, ch, k:k + SEQ],
                                                              scalar=taps[:, k:k + 1], in1=conv[:, ch, :],
                                                              op0=ALU.mult, op1=ALU.add))
                dve.sem_inc(conv_done, 1)
            for half in range(2):
                dve.wait_ge(dbl_done, 2 * half + 2)
                cols_ = slice(half * BANK, (half + 1) * BANK)
                src = dbl[0:96, 2 * half + 1, :]
                chain.step(nc.vector.tensor_copy(bchi[:, cols_], src))
                chain.step(nc.vector.tensor_tensor(rest[:, cols_], src, bchi[:, cols_], ALU.subtract))
                chain.step(nc.vector.tensor_copy(bcmid[:, cols_], rest[:, cols_]))
                chain.step(nc.vector.tensor_tensor(rest[:, cols_], rest[:, cols_], bcmid[:, cols_], ALU.subtract))
                nc.vector.tensor_copy(BC3[0:32, cols_], bchi[0:32, cols_])
                nc.vector.tensor_copy(BC3[32:64, cols_], bcmid[32:64, cols_])
                chain.step(nc.vector.tensor_copy(BC3[64:96, cols_], rest[64:96, cols_]))
            for u in range(4):
                dve.wait_ge(dl_done, u + 1)
                dve.wait_ge(abs_done, u + 1)
                nc.vector.tensor_scalar(delta[:, u // 2, u % 2 * BANK:(u % 2 + 1) * BANK], ring[:, u, :],
                                        bdt[:, u // 2:u // 2 + 1], 0.0, ALU.add, ALU.max).then_inc(relu_done, 1)
            dve.wait_ge(ln_done, 1)
            dve.wait_ge(relu_done, 4)
            dall = delta[:].rearrange("p c t -> p (c t)")
            chain.step(nc.vector.tensor_tensor(dall, dall, soft[:].rearrange("p u t -> p (u t)"), ALU.add))
            chain.step(nc.vector.tensor_tensor(du[:], delta[:], xc[:], ALU.mult))


def mamba_scan(nc, m, w, d, b, xc, sz, delta, du, BC3, select, negA, outT):
    with Phase(nc, f"scan{d}{b}") as ph:
        decay = ph.sb("decay", [P, 4, SEQ])
        state = ph.sb("state", [P, 4, SEQ])
        back = ph.sb("back", [P, TPB, P])
        bspread = ph.ps("bspread", 2)
        cspread = ph.ps("cspread", 2)
        yacc = ph.ps("yacc", 4)
        (b_done, c_done, dec_done, in_done, scan_done, hc_done, y_used, y_done, gate_sem, gated, out_done, back_kept,
         flip_done, fin) = (
            ph.sem(x) for x in ("b_done", "c_done", "dec_done", "in_done", "scan_done", "hc_done", "y_used", "y_done",
                                "gate_sem", "gated", "out_done", "back_kept", "flip_done", "fin"))
        block = ph.block()
        Wout = w["Wout"][:, NCH * P * d:NCH * P * (d + 1)]

        @block.tensor
        def _(pe):
            def spread(n):
                for to, q, done in ((bspread, n, b_done), (cspread, NS + n, c_done)):
                    if n >= 1:
                        if done is b_done:
                            pe.wait_ge(in_done, 2 * n)
                        else:
                            pe.wait_ge(hc_done, 2 * n)
                    for half in range(2):
                        last = nc.tensor.matmul(to[:, half, :], select[:, q, :], BC3[:, half * BANK:(half + 1) * BANK],
                                                start=True, stop=True)
                    last.then_inc(done, 1)

            def accumulate(n):
                for ch in range(NCH):
                    k = NCH * n + ch
                    pe.wait_ge(hc_done, k + 1)
                    for half in range(2):
                        last = nc.tensor.matmul(yacc[:, 2 * ch + half, :], m.ident[:],
                                                state[:, k % 4, half * BANK:(half + 1) * BANK], start=(n == 0),
                                                stop=(n == NS - 1))
                    last.then_inc(y_used, 1)
            for n in range(NS):
                spread(n)
                if n >= 1:
                    accumulate(n - 1)
            accumulate(NS - 1)
            if d == 0:
                for half in range(2):
                    pe.wait_ge(gated, NCH)
                    for ch in range(NCH):
                        last = nc.tensor.matmul(bspread[:, half, :], Wout[:, ch * P:(ch + 1) * P],
                                                du[:, ch, half * BANK:(half + 1) * BANK], start=(ch == 0),
                                                stop=(ch == NCH - 1))
                    last.then_inc(flip_done, 1)
            else:
                pe.wait_ge(gated, NCH)
                for half in range(2):
                    for j in range(4):
                        i = 4 * half + j
                        for ch in range(NCH):
                            last = nc.tensor.matmul(cspread[:, half, j * P:(j + 1) * P], du[:, ch, i * P:(i + 1) * P],
                                                    Wout[:, ch * P:(ch + 1) * P], start=(ch == 0), stop=(ch == NCH - 1))
                    last.then_inc(out_done, 1)
                pe.wait_ge(back_kept, 2)
                for half in range(2):
                    for j in range(4):
                        i = TPB - 1 - (4 * half + j)
                        last = nc.tensor.matmul(bspread[:, half, j * P:(j + 1) * P], back[:, i, :], m.flip[:],
                                                start=True, stop=True)
                    last.then_inc(flip_done, 1)

        @block.scalar
        def _(act):
            for k in range(NCH * NS):
                n, ch = k // NCH, k % NCH
                if k >= 4:
                    act.wait_ge(scan_done, k - 3)
                a = (NCH * d + ch) * NS + n
                nc.scalar.activation(decay[:, k % 4, :], delta[:, ch, :], ACT.Exp,
                                     scale=negA[:, a:a + 1]).then_inc(dec_done, 1)

        @block.vector
        def _(dve):
            for n in range(NS):
                for ch in range(NCH):
                    k = NCH * n + ch
                    if k >= 4:
                        dve.wait_ge(y_used, k - 3)
                    dve.wait_ge(b_done, n + 1)
                    nc.vector.tensor_tensor(state[:, k % 4, :], bspread[:].rearrange("p a t -> p (a t)"), du[:, ch, :],
                                            ALU.mult).then_inc(in_done, 1)
                for ch in range(NCH):
                    k = NCH * n + ch
                    dve.wait_ge(in_done, k + 1)
                    dve.wait_ge(dec_done, k + 1)
                    nc.vector.tensor_tensor_scan(state[:, k % 4, :], decay[:, k % 4, :], state[:, k % 4, :], 0.0,
                                                 ALU.mult, ALU.add).then_inc(scan_done, 1)
                for ch in range(NCH):
                    k = NCH * n + ch
                    dve.wait_ge(scan_done, k + 1)
                    dve.wait_ge(c_done, n + 1)
                    nc.vector.tensor_tensor(state[:, k % 4, :], cspread[:].rearrange("p a t -> p (a t)"),
                                            state[:, k % 4, :], ALU.mult).then_inc(hc_done, 1)
            dve.wait_ge(y_used, NCH * NS)
            for ch in range(NCH):
                nc.vector.scalar_tensor_tensor(out=du[:, ch, :], in0=xc[:, ch, :],
                                               scalar=w["D"][:, NCH * d + ch:NCH * d + ch + 1],
                                               in1=yacc[:, 2 * ch:2 * ch + 2, :].rearrange("p a t -> p (a t)"),
                                               op0=ALU.mult, op1=ALU.add).then_inc(gate_sem, 1)
                dve.wait_ge(gate_sem, ch + 1)
                nc.vector.tensor_tensor(du[:, ch, :], du[:, ch, :], sz[:, ch, :], ALU.mult).then_inc(gated, 1)
            if d == 1:
                for half in range(2):
                    dve.wait_ge(out_done, half + 1)
                    nc.vector.tensor_copy(back[:, 4 * half:4 * half + 4, :].rearrange("p t n -> p (t n)"),
                                          cspread[:, half, :]).then_inc(back_kept, 1)
            for half in range(2):
                dve.wait_ge(flip_done, half + 1)
                at = b * SEQ + half * BANK
                nc.vector.scalar_tensor_tensor(out=outT[:, d, at:at + BANK], in0=bspread[:, half, :],
                                               scalar=w["bout"][:, d:d + 1], in1=m.HT[:, at:at + BANK], op0=ALU.add,
                                               op1=ALU.add).then_inc(fin, 1)


def mamba_gate(nc, m, w, outT):
    with Phase(nc, "mgate") as ph:
        total = ph.sb("total", [P, 2, BANK])
        gate = ph.sb("gate", [P, 2, BANK])
        mixed = ph.sb("mixed", [P, 2, BANK])
        gv = ph.ps("gv", 4)
        turned = ph.ps("turned", 2)
        chain_sem, gv_done, gate_done, mixed_done, turn_done, y_done = (
            ph.sem(x) for x in ("chain", "gv_done", "gate_done", "mixed_done", "turn_done", "y_done"))
        block = ph.block()
        CH = NT // 4

        def keep(act, c):
            act.wait_ge(turn_done, c + 1)
            nc.scalar.activation(m.Y[:, 4 * c:4 * c + 4, :].rearrange("p t n -> p (t n)"), turned[:, c % 2, :],
                                 ACT.Copy).then_inc(y_done, 1)

        @block.tensor
        def _(pe):
            def turn(c):
                pe.wait_ge(mixed_done, c + 1)
                if c >= 2:
                    pe.wait_ge(y_done, c - 1)
                for j in range(4):
                    last = nc.tensor.transpose(turned[:, c % 2, j * P:(j + 1) * P], mixed[:, c % 2, j * P:(j + 1) * P],
                                               m.ident[:])
                last.then_inc(turn_done, 1)
            for c in range(CH):
                if c >= 2:
                    pe.wait_ge(mixed_done, c - 1)
                for k, wt in enumerate((w["Wg"], w["Wv"])):
                    for d in range(2):
                        last = nc.tensor.matmul(gv[:, 2 * (c % 2) + k, :], wt[:, d * P:(d + 1) * P],
                                                outT[:, d, c * BANK:(c + 1) * BANK], start=(d == 0), stop=(d == 1))
                    last.then_inc(gv_done, 1)
                if c >= 1:
                    turn(c - 1)
            turn(CH - 1)

        @block.scalar
        def _(act):
            for c in range(CH):
                act.wait_ge(gv_done, 2 * c + 1)
                if c >= 2:
                    act.wait_ge(mixed_done, c - 1)
                nc.scalar.activation(gate[:, c % 2, :], gv[:, 2 * (c % 2), :], ACT.Sigmoid,
                                     bias=w["bg"][:, 0:1]).then_inc(gate_done, 1)
                if c >= 1:
                    keep(act, c - 1)
            keep(act, CH - 1)

        @block.vector
        def _(dve):
            chain = Chain(dve, chain_sem)
            for c in range(CH):
                tot, mix = total[:, c % 2, :], mixed[:, c % 2, :]
                chain.step(nc.vector.tensor_tensor(tot, outT[:, 0, c * BANK:(c + 1) * BANK],
                                                   outT[:, 1, c * BANK:(c + 1) * BANK], ALU.add))
                dve.wait_ge(gv_done, 2 * c + 2)
                if c >= 2:
                    dve.wait_ge(turn_done, c - 1)
                chain.step(nc.vector.scalar_tensor_tensor(out=mix, in0=gv[:, 2 * (c % 2) + 1, :], scalar=w["bv"][:, 0:1],
                                                          in1=tot, op0=ALU.add, op1=ALU.subtract))
                dve.wait_ge(gate_done, c + 1)
                chain.step(nc.vector.tensor_tensor(mix, mix, gate[:, c % 2, :], ALU.mult))
                chain.step(nc.vector.tensor_tensor(mix, mix, tot, ALU.add))
                nc.vector.tensor_scalar(mix, mix, 0.5, None, ALU.mult).then_inc(mixed_done, 1)


def bidirectional_mamba(nc, m, dram, s):
    w = weight_views(m, s)
    with ExitStack() as keep:
        def kept(name, shape, dt=F32):
            return keep.enter_context(nc.sbuf_tensor(f"mamba_{name}", shape, dt))
        xc = kept("xc", [P, NCH, SEQ])
        sz = kept("sz", [P, NCH, SEQ])
        delta = kept("delta", [P, NCH, SEQ])
        du = kept("du", [P, NCH, SEQ])
        BC3 = kept("BC3", [96, SEQ], BF16)
        select = kept("select", [96, 2 * NS, P], BF16)
        negA = kept("negA", [P, 2 * NCH * NS])
        Wx3 = kept("Wx3", [P, 2 * NCH, 96])
        outT = kept("outT", [P, 2, TOKENS])
        mamba_setup(nc, m, dram, s, w, select, negA, Wx3)
        mamba_norm(nc, m, m.Y)
        for d in range(2):
            for b in range(BATCH):
                mamba_front(nc, m, w, d, b, m.Y, xc, sz, delta, du, BC3, Wx3)
                mamba_scan(nc, m, w, d, b, xc, sz, delta, du, BC3, select, negA, outT)
        mamba_gate(nc, m, w, outT)


def grouped_experts(nc, m, dram, s):
    w = weight_views(m, s)
    E, G, PERG, CH = 32, 8, 4, 16
    UNITS = [(tc, c) for tc in range(NT // 4) for c in range(CH + 1)]
    with Phase(nc, "grouped") as ph:
        scores = ph.sb("scores", [P, NT, E])
        biased = ph.sb("biased", [P, NT, E])
        biasB = ph.sb("biasB", [P, E])
        hi1, lo1, hi2, lo2, first, second = (ph.sb(f"pair{k}", [P, NT, G]) for k in range(6))
        group = ph.sb("group", [P, NT, G])
        top = ph.sb("top", [P, NT, 8])
        where = ph.sb("where", [P, NT, 8], U32)
        wheref = ph.sb("wheref", [P, NT, 4])
        same = ph.sb("same", [P, NT, G, 4])
        gmask = ph.sb("gmask", [P, NT, G])
        replaced = ph.sb("replaced", [P, NT, E])
        stat = ph.sb("stat", [P, NT])
        parts = ph.sb("parts", [P, NT, 3, E], BF16)
        partsT = ph.sb("partsT", [96, TOKENS], BF16)
        select = ph.sb("select", [96, CH, P], BF16)
        silu = ph.sb("silu", [P, 2, BANK])
        gated = ph.sb("gated", [P, 2, BANK])
        hidden = ph.sb("hidden", [P, 3, BANK])
        gate_up = ph.ps("gate_up", 4)
        spread = ph.ps("spread", 2)
        down = ph.ps("down", 1)
        turned = ph.ctx.enter_context(nc.psum_tensor("grouped_turned", [P, 1, 1024], BF16))
        (router_done, bias_done, chain_sem, sig_done, parts_done, turn_done, turn_kept, gu_done, silu_done, gated_done,
         hid_done, spread_done, down_done, y_done, sel_done) = (
            ph.sem(x) for x in ("router_done", "bias_done", "chain", "sig_done", "parts_done", "turn_done", "turn_kept",
                                "gu_done", "silu_done", "gated_done", "hid_done", "spread_done", "down_done", "y_done",
                                "sel_done"))
        block = ph.block()
        shared_w = (w["sg"], w["su"], w["sd"])

        @block.gpsimd
        def _(pool):
            nc.gpsimd.memset(select[:], 0.0).then_inc(sel_done, 1)
            for r in range(3):
                pool.wait_ge(sel_done, r + 1)
                nc.gpsimd.affine_select(out=select[:].rearrange("k c (j i) -> k c j i", j=2),
                                        in_=select[:].rearrange("k c (j i) -> k c j i", j=2),
                                        compare_op=ALU.not_equal, fill=1.0, base=-E * r,
                                        pattern=[[-2, CH], [-1, 2], [0, 64]], channel_multiplier=1).then_inc(sel_done, 1)

        @block.tensor
        def _(pe):
            pe.wait_ge(m.wsem[s], 16)
            nc.tensor.matmul(down[:, 0, 0:E], m.ones[0:1, :], w["bias"], start=True, stop=True).then_inc(bias_done, 1)
            for g in range(NT):
                last = nc.tensor.matmul(spread[:, 0, E * g:E * (g + 1)], m.HT[:, g * P:(g + 1) * P], w["gate"],
                                        start=True, stop=True)
            last.then_inc(router_done, 1)

            def gate_and_up(n):
                tc, c = UNITS[n]
                if n >= 2:
                    pe.wait_ge(gated_done, n - 1)
                for k in range(2):
                    wt = shared_w[k] if c == CH else w[("wg", "wu")[k]][:, c * P:(c + 1) * P]
                    nc.tensor.matmul(gate_up[:, 2 * (n % 2) + k, :], wt, m.HT[:, tc * BANK:(tc + 1) * BANK],
                                     start=True, stop=True).then_inc(gu_done, 1)
            gate_and_up(0)
            gate_and_up(1)
            pe.wait_ge(parts_done, 1)
            for half in range(2):
                if half:
                    pe.wait_ge(turn_kept, 1)
                for j in range(8):
                    g = 8 * half + j
                    last = nc.tensor.transpose(turned[0:96, 0, j * P:(j + 1) * P],
                                               parts[:, g, :, :].rearrange("p r e -> p (r e)"), m.identb[:])
                last.then_inc(turn_done, 1)
            pe.wait_ge(turn_kept, 2)
            pe.wait_ge(sel_done, 4)
            for n in range(len(UNITS) + 1):
                if n < len(UNITS):
                    tc, c = UNITS[n]
                    if n >= 2:
                        gate_and_up(n)
                        pe.wait_ge(hid_done, n - 1)
                    if c < CH:
                        nc.tensor.matmul(spread[:, n % 2, :], select[:, c, :], partsT[:, tc * BANK:(tc + 1) * BANK],
                                         start=True, stop=True).then_inc(spread_done, 1)
                    else:
                        nc.tensor.matmul(spread[:, n % 2, :], m.ones[0:1, :], m.wide_ones[0:1, :], start=True,
                                         stop=True).then_inc(spread_done, 1)
                if n >= 1:
                    tc, c = UNITS[n - 1]
                    pe.wait_ge(hid_done, n)
                    if c == 0 and tc > 0:
                        pe.wait_ge(y_done, tc)
                    for j in range(4):
                        wt = shared_w[2] if c == CH else w["wd"][:, c * P:(c + 1) * P]
                        last = nc.tensor.matmul(down[:, 0, j * P:(j + 1) * P], hidden[:, (n - 1) % 3, j * P:(j + 1) * P],
                                                wt, start=(c == 0 and j == 0), stop=(c == CH), skip_group_check=True)
                    last.then_inc(down_done, 1)

        @block.scalar
        def _(act):
            act.wait_ge(router_done, 1)
            nc.scalar.activation(scores[:].rearrange("p t e -> p (t e)"), spread[:, 0, :], ACT.Sigmoid).then_inc(sig_done, 1)
            for half in range(2):
                act.wait_ge(turn_done, half + 1)
                nc.scalar.activation(partsT[:, half * 1024:(half + 1) * 1024], turned[0:96, 0, :],
                                     ACT.Copy).then_inc(turn_kept, 1)
            for n in range(len(UNITS)):
                act.wait_ge(gu_done, 2 * n + 1)
                if n >= 2:
                    act.wait_ge(gated_done, n - 1)
                nc.scalar.activation(silu[:, n % 2, :], gate_up[:, 2 * (n % 2), :], ACT.Silu).then_inc(silu_done, 1)

        @block.vector
        def _(dve):
            chain = Chain(dve, chain_sem)

            def tt(out, a, b, op):
                chain.step(nc.vector.tensor_tensor(out, a, b, op))
            dve.wait_ge(bias_done, 1)
            chain.step(nc.vector.tensor_copy(biasB[:], down[:, 0, 0:E]))
            dve.wait_ge(sig_done, 1)
            tt(biased[:], scores[:], biasB[:].unsqueeze(1).broadcast_to([P, NT, E]), ALU.add)
            a, b, c, d = (biased[:].rearrange("p t (g k) -> p t g k", k=PERG)[:, :, :, k] for k in range(PERG))
            tt(hi1[:], a, b, ALU.max)
            tt(lo1[:], a, b, ALU.min)
            tt(hi2[:], c, d, ALU.max)
            tt(lo2[:], c, d, ALU.min)
            tt(first[:], hi1[:], hi2[:], ALU.max)
            tt(second[:], hi1[:], hi2[:], ALU.min)
            tt(lo1[:], lo1[:], lo2[:], ALU.max)
            tt(second[:], second[:], lo1[:], ALU.max)
            tt(group[:], first[:], second[:], ALU.add)
            for g in range(NT):
                last = nc.vector.max(out=top[:, g, :], in_=group[:, g, :])
            chain.step(last)
            for g in range(NT):
                last = nc.vector.max_index(where[:, g, :], top[:, g, :], group[:, g, :])
            chain.step(last)
            chain.step(nc.vector.tensor_copy(wheref[:], where[:, :, 0:4]))
            for k in range(4):
                tt(same[:, :, :, k], m.iota8[:].unsqueeze(1).broadcast_to([P, NT, G]),
                   wheref[:, :, k:k + 1].broadcast_to([P, NT, G]), ALU.is_equal)
            chain.step(nc.vector.tensor_reduce(gmask[:], same[:], AX, ALU.add))
            for k in range(PERG):
                bk = biased[:].rearrange("p t (g k) -> p t g k", k=PERG)[:, :, :, k]
                tt(bk, bk, gmask[:], ALU.mult)
            for g in range(NT):
                last = nc.vector.max(out=top[:, g, :], in_=biased[:, g, :])
            chain.step(last)
            for g in range(NT):
                last = nc.vector.match_replace(out=replaced[:, g, :], in_to_replace=top[:, g, :],
                                               in_values=biased[:, g, :], imm_value=-3.0e38)
            chain.step(last)
            tt(replaced[:], replaced[:], biased[:], ALU.not_equal)
            tt(scores[:], scores[:], replaced[:], ALU.mult)
            chain.step(nc.vector.tensor_reduce(stat[:], scores[:], AX, ALU.add))
            chain.step(nc.vector.tensor_scalar(stat[:], stat[:], 1e-20, None, ALU.add))
            chain.step(nc.vector.reciprocal(stat[:], stat[:]))
            chain.step(nc.vector.tensor_scalar(stat[:], stat[:], 2.5, None, ALU.mult))
            tt(scores[:], scores[:], stat[:].unsqueeze(2).broadcast_to([P, NT, E]), ALU.mult)
            split3(nc, chain, scores[:], parts[:, :, 0, :], parts[:, :, 1, :], parts[:, :, 2, :], replaced[:])
            dve.sem_inc(parts_done, 1)
            for n in range(len(UNITS) + 1):
                if n < len(UNITS):
                    dve.wait_ge(silu_done, n + 1)
                    dve.wait_ge(gu_done, 2 * n + 2)
                    nc.vector.tensor_tensor(gated[:, n % 2, :], gate_up[:, 2 * (n % 2) + 1, :], silu[:, n % 2, :],
                                            ALU.mult).then_inc(gated_done, 1)
                    dve.wait_ge(gated_done, n + 1)
                    dve.wait_ge(spread_done, n + 1)
                    if n >= 3:
                        dve.wait_ge(down_done, n - 2)
                    nc.vector.tensor_tensor(hidden[:, n % 3, :], spread[:, n % 2, :], gated[:, n % 2, :],
                                            ALU.mult).then_inc(hid_done, 1)
                if n >= 1 and UNITS[n - 1][1] == CH:
                    tc = UNITS[n - 1][0]
                    dve.wait_ge(down_done, n)
                    nc.vector.tensor_copy(m.Y[:, 4 * tc:4 * tc + 4, :].rearrange("p t n -> p (t n)"),
                                          down[:, 0, :]).then_inc(y_done, 1)


S0, S1 = 0, 8
PHASES = [linear_attention_phase, attention_and_top2, causal_single_head, swiglu_experts, causal_sixteen_heads, local_transformer, bidirectional_mamba, grouped_experts]



def program(nc, dram, out):
    with ExitStack() as ctx:
        m = Memory(nc, ctx)
        constants_phase(nc, m, dram)
        phases = PHASES
        with Phase(nc, "first") as ph:
            block = ph.block()

            @block.sync
            def _(sp):
                load_weights(sp, m, dram, S0)
        for s in range(S0, S1):
            norm_phase(nc, m, f"norm{s}", add=s > S0, norm=True)
            phases[s](nc, m, dram, s)
        norm_phase(nc, m, "last", add=True, norm=False, out=out)


def rotary_tables():
    half = np.arange(0, 64, 2, dtype=np.float32)
    inv = (1.0 / 10000.0 ** (half / 64)).astype(np.float32)
    t = np.arange(SEQ, dtype=np.float32)
    freqs = t[:, None] * inv[None, :]
    freqs = np.concatenate([freqs, freqs], -1)
    base = (half + 0.4 * 64) / (1.4 * 64)
    power = (t - SEQ // 2) / 32.0
    scale = (base[None, :] ** power[:, None]).astype(np.float32)
    scale = np.concatenate([scale, scale], -1)
    sign = np.concatenate([-np.ones(32, np.float32), np.ones(32, np.float32)])
    cos, sin = np.cos(freqs), np.sin(freqs) * sign
    fold = lambda a: np.ascontiguousarray(
        a.astype(np.float32).reshape(TPB, P, 64).transpose(1, 0, 2).reshape(P, TPB * 64))
    return fold(cos * scale), fold(sin * scale), fold(cos / scale), fold(sin / scale)


def packed(s, parts):
    out = np.zeros((P, WIDTHS[s]), np.float32)
    at = 0
    for name, rows, n in PACKS[s]:
        a = parts[name]
        out[0:a.shape[0], at:at + a.shape[1]] = a
        at += n
    return out


def row(a):
    return a.reshape(1, -1)


def cols(a):
    return a.reshape(-1, P).T


def chunks(a):
    return a.reshape(-1, P, a.shape[-1]).transpose(1, 0, 2).reshape(P, -1)


def layouts(i):
    flat = lambda a: a.transpose(1, 0, 2).reshape(a.shape[1], -1)
    w1 = i["L2_ffn_w1"]
    b1 = np.zeros((2, 6, P), np.float32)
    b1.reshape(2, 2, 3 * P)[:, :, 0:HID] = i["L2_ffn_b1"].reshape(2, 2, HID)
    w2 = np.zeros((2, 3 * P, P), np.float32)
    w2[:, 0:HID] = i["L2_ffn_w2"]
    cosq, sinq, cosk, sink = rotary_tables()
    return [
        {"Wq": i["L0_attn_Wq"], "Wk": i["L0_attn_Wk"], "Wv": i["L0_attn_Wv"], "Wo": chunks(i["L0_attn_Wo"]),
         "bo": row(i["L0_attn_bo"])},
        {"Wqkv": i["L0_ffn_W_qkv"], "bqkv": row(i["L0_ffn_b_qkv"]), "Wgate": i["L0_ffn_W_gate"],
         "bgate": row(i["L0_ffn_b_gate"]), "Wexp": flat(i["L0_ffn_W_experts"]), "bexp": i["L0_ffn_b_experts"]},
        {"Wq": i["L1_attn_Wq"], "Wk": i["L1_attn_Wk"], "Wv": i["L1_attn_Wv"]},
        {"gate": i["L1_ffn_gate_w"].T, "wg": i["L1_ffn_wg"].reshape(4096, P).T,
         "wu": i["L1_ffn_wu"].reshape(4096, P).T,
         "wd": i["L1_ffn_wd"].reshape(8, P, 4, P).transpose(3, 0, 2, 1).reshape(P, 4096)},
        {"Wq": i["L2_attn_W_Q"].reshape(1024, P).T, "Wk": i["L2_attn_W_K"].reshape(1024, P).T,
         "Wv": i["L2_attn_W_V"].reshape(1024, P).T, "Wo": chunks(i["L2_attn_W_O"].T)},
        {"wqkv": flat(i["L2_ffn_wqkv"]),
         "wo": i["L2_ffn_wo"].reshape(2, 4, P, P).transpose(2, 0, 1, 3).reshape(P, -1),
         "w1": flat(w1), "w2": w2.reshape(2, 3, P, P).transpose(2, 0, 1, 3).reshape(P, -1),
         "b1": cols(b1), "b2": row(i["L2_ffn_b2"]), "lng": cols(i["L2_ffn_ln_g"]), "lnb": cols(i["L2_ffn_ln_b"]),
         "qscale": row(i["L2_ffn_q_scale"]), "kscale": row(i["L2_ffn_k_scale"]),
         "cosq": cosq, "sinq": sinq, "cosk": cosk, "sink": sink},
        {"lnw": cols(i["L3_attn_ln_w"]), "lnb": cols(i["L3_attn_ln_b"]), "Win": flat(i["L3_attn_W_in"]),
         "bin": cols(i["L3_attn_b_in"]),
         "convw": i["L3_attn_conv_w"].reshape(2, 2, P, 4).transpose(2, 0, 1, 3).reshape(P, 16),
         "convb": cols(i["L3_attn_conv_b"]),
         "Wx": i["L3_attn_W_xproj"].reshape(2, 2, P, 96).transpose(2, 0, 1, 3).reshape(P, -1),
         "Wdt": flat(i["L3_attn_W_dt"]), "bdt": cols(i["L3_attn_b_dt"]),
         "Alog": i["L3_attn_A_log"].reshape(2, 2, P, 16).transpose(2, 0, 1, 3).reshape(P, -1),
         "D": cols(i["L3_attn_D"]),
         "Wout": i["L3_attn_W_out"].reshape(2, 2, P, P).transpose(2, 0, 1, 3).reshape(P, -1),
         "bout": cols(i["L3_attn_b_out"]), "Wg": chunks(i["L3_attn_Wg"]), "bg": cols(i["L3_attn_bg"]),
         "Wv": chunks(i["L3_attn_Wv"]), "bv": cols(i["L3_attn_bv"])},
        {"gate": i["L3_ffn_gate_w"].T, "bias": row(i["L3_ffn_gate_bias"]),
         "wg": i["L3_ffn_w_gate"].reshape(2048, P).T, "wu": i["L3_ffn_w_up"].reshape(2048, P).T,
         "wd": i["L3_ffn_w_down"].reshape(16, 2, P, 64).transpose(1, 3, 0, 2).reshape(P, 2048),
         "sg": i["L3_ffn_sh_gate"].T, "su": i["L3_ffn_sh_up"].T, "sd": i["L3_ffn_sh_down"].T},
    ]


_OUTS = [((BATCH, SEQ, P), "float32")]


def kernel(**inputs):
    import concourse.bacc as _bacc
    from concourse.bass_utils import run_bass_kernel_spmd as _run

    nc = _bacc.Bacc("TRN2", target_bir_lowering=False, num_devices=1)
    host = {k: np.asarray(v) for k, v in inputs.items()}
    feeds = {"x": np.ascontiguousarray(host["L0_attn_x"])}
    for s, parts in enumerate(layouts(host)):
        feeds[f"w{s}"] = packed(s, parts)
    dram = {k: nc.dram_tensor(f"in_{k}_dram", a.shape, mybir.dt.from_np(a.dtype), kind="ExternalInput").ap()
            for k, a in feeds.items()}
    outs = [nc.dram_tensor(f"out_{i}_dram", shape, mybir.dt.from_np(np.dtype(dtype)), kind="ExternalOutput").ap()
            for i, (shape, dtype) in enumerate(_OUTS)]
    program(nc, dram, outs[0])
    r = _run(nc, [{f"in_{k}_dram": a for k, a in feeds.items()}], core_ids=[0])
    return r.results[0]["out_0_dram"]
```

```python
from contextlib import ExitStack

import numpy as np

import concourse.bass as bass
from concourse import mybir

F32 = mybir.dt.float32
BF16 = mybir.dt.bfloat16
U32 = mybir.dt.uint32
ALU = mybir.AluOpType
ACT = mybir.ActivationFunctionType
AX = mybir.AxisListType.X

P = 128
BATCH, SEQ = 2, 1024
TOKENS = BATCH * SEQ
NT = TOKENS // P
TPB = SEQ // P
BANK = 512
CPB = SEQ // BANK
LN_EPS = 1e-5
NEG = -1.0e30


class Phase:

    def __init__(self, nc, name):
        self.nc, self.name, self.ctx, self.sems = nc, name, ExitStack(), []

    def __enter__(self):
        self.ctx.__enter__()
        return self

    def __exit__(self, *e):
        self.ctx.__exit__(*e)
        nums = sorted(x.num for x in self.sems)
        while nums:
            n = 1
            while n < len(nums) and nums[n] == nums[0] + n:
                n += 1
            self.nc.gpsimd.sem_clear(range(nums[0], nums[0] + n))
            nums = nums[n:]

    def sb(self, name, shape, dt=F32):
        return self.ctx.enter_context(self.nc.sbuf_tensor(f"{self.name}_{name}", shape, dt))

    def ps(self, name, banks, dt=F32):
        return self.ctx.enter_context(self.nc.psum_tensor(f"{self.name}_{name}", [P, banks, BANK], dt))

    def sem(self, name):
        self.sems.append(self.ctx.enter_context(self.nc.semaphore(f"{self.name}_{name}")))
        return self.sems[-1]

    def block(self):
        return self.ctx.enter_context(self.nc.Block())


class Chain:

    def __init__(self, eng, sem):
        self.eng, self.sem, self.n = eng, sem, 0

    def step(self, ins):
        ins.then_inc(self.sem, 1)
        self.n += 1
        self.eng.wait_ge(self.sem, self.n)


def constants_phase(nc, m, dram):
    with Phase(nc, "const") as ph:
        loaded = ph.sem("loaded")
        zeroed = ph.sem("zeroed")
        made = ph.sem("made")
        block = ph.block()

        @block.sync
        def _(sp):
            sp.dma_start(m.X[:], dram["x"].rearrange("b (t p) d -> p (b t) d", p=P)).then_inc(loaded, 16)
            sp.wait_ge(loaded, 16)

        @block.vector
        def _(dve):
            chain = Chain(dve, made)
            nc.vector.memset(m.ones[:], 1.0)
            nc.vector.memset(m.neghalf[:], -0.5)
            chain.step(nc.vector.memset(m.blockdiag[:], 0.0))
            for h in range(2):
                nc.vector.memset(m.blockdiag[64 * h:64 * h + 64, 64 * h:64 * h + 64], 1.0)

        @block.gpsimd
        def _(pool):
            pool.memset(m.ident[:], 0.0).then_inc(zeroed, 1)
            pool.memset(m.causal[:], 0.0).then_inc(zeroed, 1)
            pool.memset(m.flip[:], 0.0).then_inc(zeroed, 1)
            pool.memset(m.band[:], 0.0).then_inc(zeroed, 1)
            pool.iota(m.iota8[:], pattern=[[1, 8]], base=0, channel_multiplier=0,
                      allow_small_or_imprecise_dtypes=True).then_inc(zeroed, 1)
            pool.wait_ge(zeroed, 5)
            pool.affine_select(out=m.ident[:], in_=m.ident[:], compare_op=ALU.not_equal, fill=1.0, base=0,
                               pattern=[[-1, P]], channel_multiplier=1).then_inc(zeroed, 1)
            pool.affine_select(out=m.flip[:], in_=m.flip[:], compare_op=ALU.not_equal, fill=1.0, base=1 - P,
                               pattern=[[1, P]], channel_multiplier=1).then_inc(zeroed, 1)
            pool.affine_select(out=m.causal[:], in_=m.causal[:], compare_op=ALU.is_ge, fill=NEG, base=0,
                               pattern=[[-1, P]], channel_multiplier=1).then_inc(zeroed, 1)
            pool.affine_select(out=m.band[:], in_=m.band[:], compare_op=ALU.is_ge, fill=NEG, base=64,
                               pattern=[[-1, 192]], channel_multiplier=1).then_inc(zeroed, 1)
            pool.wait_ge(zeroed, 9)
            pool.affine_select(out=m.band[:], in_=m.band[:], compare_op=ALU.is_ge, fill=NEG, base=0,
                               pattern=[[1, 192]], channel_multiplier=-1).then_inc(zeroed, 1)
            pool.tensor_copy(m.identb[:], m.ident[:])
            pool.tensor_copy(m.causalb[:], m.causal[:])


def norm_phase(nc, m, name, add, norm, out=None):
    G = NT // 4
    with Phase(nc, name) as ph:
        stats = ph.sb("stats", [P, 2, NT, 6])
        mv = ph.sb("mv", [P, 2, NT, 2])
        rstd = ph.sb("rstd", [P, 2, NT])
        shift = ph.sb("shift", [P, 2, NT])
        turned = ph.ps("turned", 4)
        stat_done, aggr_done, var_done, rstd_done, shift_done, norm_done, own_done = (
            [ph.sem(f"{s}{k}") for k in range(2)] for s in ("stat", "aggr", "var", "rstd", "shift", "norm", "own"))
        x_added = ph.sem("x_added")
        turn_done = ph.sem("turn_done")
        turn_kept = ph.sem("turn_kept")
        block = ph.block()
        src = (m.Y, m.X)
        own = ([], [t for t in range(NT) if t % 4 == 0])
        act_tiles = [[t for t in range(NT) if t not in own[k]] for k in range(2)]
        HT_ACT = (0, 2)
        ORDER = sorted(((k, q) for k in range(2) if (add, norm)[k] for q in range(G)),
                       key=lambda kq: (kq[1] + 2 * kq[0] * add, kq[0]))

        def wait_normalised(eng, k, t):
            if t in own[k]:
                eng.wait_ge(own_done[k], own[k].index(t) + 1)
            else:
                eng.wait_ge(norm_done[k], act_tiles[k].index(t) + 1)

        @block.vector
        def _(dve):
            def statistics(k, q):
                group = range(4 * q, 4 * q + 4)
                for t in group:
                    if k == 1 and add:
                        dve.wait_ge(x_added, t + 1)
                    nc.vector.bn_stats(stats[:, k, t, :], src[k][:, t, :]).then_inc(stat_done[k], 1)
                for t in group:
                    dve.wait_ge(stat_done[k], t + 1)
                    nc.vector.bn_aggr(mv[:, k, t, :], stats[:, k, t, :]).then_inc(aggr_done[k], 1)
                dve.wait_ge(aggr_done[k], 4 * q + 4)
                nc.vector.tensor_scalar(rstd[:, k, 4 * q:4 * q + 4], mv[:, k, 4 * q:4 * q + 4, 1], LN_EPS, None,
                                        ALU.add).then_inc(var_done[k], 1)

            def apply(k, q):
                dve.wait_ge(rstd_done[k], q + 1)
                four = slice(4 * q, 4 * q + 4)
                nc.vector.scalar_tensor_tensor(out=shift[:, k, four], in0=mv[:, k, four, 0], scalar=-1.0,
                                               in1=rstd[:, k, four], op0=ALU.mult,
                                               op1=ALU.mult).then_inc(shift_done[k], 1)
                for t in range(4 * q, 4 * q + 4):
                    if t in own[k]:
                        dve.wait_ge(shift_done[k], q + 1)
                        if k == 1 and add:
                            dve.wait_ge(x_added, t + 1)
                        nc.vector.tensor_scalar(m.XN[:, t, :], src[k][:, t, :], rstd[:, k, t:t + 1],
                                                shift[:, k, t:t + 1], ALU.mult, ALU.add).then_inc(own_done[k], 1)

            def add_group(q):
                for t in range(4 * q, 4 * q + 4):
                    wait_normalised(dve, 0, t)
                    nc.vector.tensor_tensor(m.X[:, t, :], m.X[:, t, :], m.XN[:, t, :], ALU.add).then_inc(x_added, 1)

            lag = 2 if add else 0
            for step in range(G + 5):
                if add and step < G:
                    statistics(0, step)
                if add and 0 <= step - 1 < G:
                    apply(0, step - 1)
                if add and 0 <= step - 2 < G:
                    add_group(step - 2)
                if norm and 0 <= step - lag < G:
                    statistics(1, step - lag)
                if norm and 0 <= step - lag - 1 < G:
                    apply(1, step - lag - 1)
                if norm and 0 <= step - lag - 2 < G and step - lag - 2 not in HT_ACT:
                    c = step - lag - 2
                    dve.wait_ge(turn_done, 4 * (c + 1))
                    nc.vector.tensor_copy(m.HT[:, c * BANK:(c + 1) * BANK], turned[:, c, :]).then_inc(turn_kept, 1)

        @block.gpsimd
        def _(pool):
            for k, q in ORDER:
                pool.wait_ge(var_done[k], q + 1)
                nc.gpsimd.tensor_tensor(rstd[:, k, 4 * q:4 * q + 4], rstd[:, k, 4 * q:4 * q + 4], m.neghalf[:, 0:4],
                                        ALU.pow).then_inc(rstd_done[k], 1)

        @block.scalar
        def _(act):
            def copy_out(c):
                act.wait_ge(turn_done, 4 * (c + 1))
                nc.scalar.activation(m.HT[:, c * BANK:(c + 1) * BANK], turned[:, c, :], ACT.Copy).then_inc(turn_kept, 1)

            for k, q in ORDER:
                act.wait_ge(shift_done[k], q + 1)
                for t in range(4 * q, 4 * q + 4):
                    if t in act_tiles[k]:
                        if k == 1 and add:
                            act.wait_ge(x_added, t + 1)
                        nc.scalar.activation(m.XN[:, t, :], src[k][:, t, :], ACT.Identity, bias=shift[:, k, t:t + 1],
                                             scale=rstd[:, k, t:t + 1]).then_inc(norm_done[k], 1)
                if k == 1 and q - 1 in HT_ACT:
                    copy_out(q - 1)

        @block.tensor
        def _(pe):
            if norm:
                for t in range(NT):
                    wait_normalised(pe, 1, t)
                    nc.tensor.transpose(turned[:, t // 4, t % 4 * P:(t % 4 + 1) * P], m.XN[:, t, :],
                                        m.ident[:]).then_inc(turn_done, 1)

        @block.sync
        def _(sp):
            if out is not None:
                rows = out.rearrange("b (t p) d -> p (b t) d", p=P)
                for half in range(2):
                    tiles = slice(half * TPB, (half + 1) * TPB)
                    sp.wait_ge(x_added, (half + 1) * TPB)
                    sp.dma_start(rows[:, tiles, :], m.X[:, tiles, :]).then_inc(m.stored, 16)
                sp.wait_ge(m.stored, 32)


class Memory:

    def __init__(self, nc, ctx):
        def sb(name, shape, dt=F32):
            return ctx.enter_context(nc.sbuf_tensor(name, shape, dt))
        self.X = sb("X", [P, NT, P])
        self.XN = sb("XN", [P, NT, P])
        self.Y = sb("Y", [P, NT, P])
        self.HT = sb("HT", [P, TOKENS])
        self.ident = sb("ident", [P, P])
        self.identb = sb("identb", [P, P], BF16)
        self.flip = sb("flip", [P, P])
        self.causal = sb("causal", [P, P])
        self.causalb = sb("causalb", [P, P], BF16)
        self.band = sb("band", [P, 192])
        self.blockdiag = sb("blockdiag", [P, P])
        self.ones = sb("ones", [P, P])
        self.neghalf = sb("neghalf", [P, NT])
        self.iota8 = sb("iota8", [P, 8])
        self.weights = sb("weights", [P, WCOLS])
        self.stored = ctx.enter_context(nc.semaphore("output_stored"))
        self.wsem = [ctx.enter_context(nc.semaphore(f"weights_loaded_{i}")) for i in range(8)]



PACKS = [
    [("Wq", P, 1024), ("Wk", P, 1024), ("Wv", P, 1024), ("Wo", P, 1024), ("bo", 1, P)],
    [("Wqkv", P, 384), ("bqkv", 1, 384), ("Wgate", P, 8), ("bgate", 1, 8), ("Wexp", P, 1024), ("bexp", 8, P)],
    [("Wq", P, P), ("Wk", P, P), ("Wv", P, P)],
    [("gate", P, 8), ("wg", P, 4096), ("wu", P, 4096), ("wd", P, 4096)],
    [("Wq", P, 1024), ("Wk", P, 1024), ("Wv", P, 1024), ("Wo", P, 1024)],
    [("wqkv", P, 2 * 1536), ("wo", P, 2 * 512), ("w1", P, 2 * 682), ("w2", P, 2 * 384), ("b1", P, 2 * 6),
     ("b2", 1, 2 * P), ("lng", P, 2), ("lnb", P, 2), ("qscale", 1, 2 * 64), ("kscale", 1, 2 * 64),
     ("cosq", P, 512), ("sinq", P, 512), ("cosk", P, 512), ("sink", P, 512)],
    [("lnw", P, 2), ("lnb", P, 2), ("Win", P, 2 * 512), ("bin", P, 2 * 4), ("convw", P, 2 * 8), ("convb", P, 2 * 2),
     ("Wx", P, 2 * 2 * 96), ("Wdt", 64, 2 * 256), ("bdt", P, 2 * 2), ("Alog", P, 2 * 2 * 16), ("D", P, 2 * 2),
     ("Wout", P, 2 * 2 * P), ("bout", P, 2), ("Wg", P, 2 * P), ("bg", P, 1), ("Wv", P, 2 * P), ("bv", P, 1)],
    [("gate", P, 32), ("bias", 1, 32), ("wg", P, 2048), ("wu", P, 2048), ("wd", P, 2048), ("sg", P, P),
     ("su", P, P), ("sd", P, P)],
]
WIDTHS = [sum(n for _, _, n in pack) for pack in PACKS]
WPART = [max(WIDTHS[0::2]), max(WIDTHS[1::2])]
WCOLS = sum(WPART)


def weight_views(m, s):
    views, at = {}, s % 2 * WPART[0]
    for name, rows, n in PACKS[s]:
        views[name] = m.weights[0:rows, at:at + n]
        at += n
    return views


def load_weights(sp, m, dram, s):
    if s < len(PACKS):
        at = s % 2 * WPART[0]
        sp.dma_start(m.weights[:, at:at + WIDTHS[s]], dram[f"w{s}"]).then_inc(m.wsem[s], 16)


def linear_attention_phase(nc, m, dram, s):
    w = weight_views(m, s)
    EPS = 1e-6
    with Phase(nc, "lin") as ph:
        keyexp = ph.sb("keyexp", [P, 2, BANK])
        keyrelu = ph.sb("keyrelu", [P, 2, BANK])
        key = ph.sb("key", [P, 2, 1024])
        val = ph.sb("val", [P, 2, 1024])
        kvT = ph.sb("kvT", [P, 8, P])
        ksum = ph.sb("ksum", [P, 8])
        keytotal = ph.sb("keytotal", [P, 1024])
        ksum2 = ph.sb("ksum2", [P, 8, 2])
        mix = ph.sb("mix", [P, 8, P])
        qry = ph.sb("qry", [P, 2, 8, BANK])
        zsum = ph.sb("zsum", [P, 64])
        zrest = ph.sb("zrest", [P, 64])
        zparts = ph.sb("zparts", [P, 4, 3, 16], BF16)
        zT = ph.sb("zT", [48, 2, BANK], BF16)
        select = ph.sb("select", [48, 16, 64], BF16)
        qz = ph.sb("qz", [P, 2, BANK])
        proj = ph.ps("proj", 4)
        acc = ph.ps("acc", 3)
        small = ph.ps("small", 1)
        turned = small[:].bitcast(BF16)
        names = ("proj_done", "proj_kept", "exp_done", "relu_done", "key_done", "val_done", "tile_used", "kvT_done",
                 "total_done", "ksum_psum", "ksum_done", "ksum2_done", "mix_psum", "mix_done", "q_psum", "q_exp",
                 "q_free", "q_done", "z_psum", "chain", "parts_done", "zt_psum", "zt_kept", "spread_done", "sel_done",
                 "qz_done", "qz_used", "y_psum", "y_kept")
        S = {n: ph.sem(n) for n in names}
        block = ph.block()
        UNITS = [(t, half) for t in range(TPB) for half in range(2)]

        @block.sync
        def _(sp):
            load_weights(sp, m, dram, s + 1)

        @block.tensor
        def _(pe):
            pe.wait_ge(m.wsem[s], 16)
            for b in range(BATCH):
                def accumulate(t):
                    g = b * TPB + t
                    pe.wait_ge(S["key_done"], 2 * (g + 1))
                    pe.wait_ge(S["val_done"], 2 * (g + 1))
                    if t == 0 and b > 0:
                        pe.wait_ge(S["y_kept"], 2 * b)
                    for c in range(8):
                        last = nc.tensor.matmul(acc[:, c // 4, c % 4 * P:(c % 4 + 1) * P], val[:, g % 2, c * P:(c + 1) * P],
                                                key[:, g % 2, c * P:(c + 1) * P], start=(t == 0 and c % 4 == 0),
                                                stop=(t == TPB - 1), skip_group_check=True)
                    last.then_inc(S["tile_used"], 1)

                for t in range(TPB):
                    g = b * TPB + t
                    for half in range(2):
                        for k, wt in enumerate((w["Wk"], w["Wv"])):
                            u = 4 * g + 2 * half + k
                            if u >= 4:
                                pe.wait_ge(S["proj_kept"], u - 3)
                            nc.tensor.matmul(proj[:, u % 4, :], m.HT[:, g * P:(g + 1) * P],
                                             wt[:, half * BANK:(half + 1) * BANK], start=True,
                                             stop=True).then_inc(S["proj_done"], 1)
                    if t >= 1:
                        accumulate(t - 1)
                accumulate(TPB - 1)
                pe.wait_ge(S["total_done"], (b + 1) * TPB)
                for c in range(8):
                    last = nc.tensor.matmul(acc[:, 2, c:c + 1], keytotal[:, c * P:(c + 1) * P], m.ones[:, 0:1],
                                            start=True, stop=True)
                last.then_inc(S["ksum_psum"], 1)

                def mixes():
                    pe.wait_ge(S["kvT_done"], b + 1)
                    for c in range(8):
                        i = 8 * b + c
                        if i >= 4:
                            pe.wait_ge(S["mix_done"], i // 4)
                        nc.tensor.matmul(small[:, 0, c % 4 * P:(c % 4 + 1) * P], kvT[:, c, :], w["Wo"][:, c * P:(c + 1) * P],
                                         start=True, stop=True).then_inc(S["mix_psum"], 1)

                def query(u):
                    n, half, c = 16 * b + u, u // 8, u % 8
                    if u >= 2:
                        pe.wait_ge(S["q_free"], n - 1)
                    nc.tensor.matmul(proj[:, u % 2, :], w["Wq"][:, c * P:(c + 1) * P],
                                     m.HT[:, (CPB * b + half) * BANK:(CPB * b + half + 1) * BANK], start=True,
                                     stop=True).then_inc(S["q_psum"], 1)

                def norm_sum(u):
                    half, c = u // 8, u % 8
                    pe.wait_ge(S["q_done"], 16 * b + u + 1)
                    if u == 0:
                        pe.wait_ge(S["ksum2_done"], b + 1)
                    for j in range(4):
                        at = 16 * j + 2 * c
                        last = nc.tensor.matmul(acc[:, 1 + half, at:at + 2], qry[:, half, c, j * P:(j + 1) * P],
                                                ksum2[:, c, :], start=True, stop=True)
                    last.then_inc(S["z_psum"], 1)

                def turn_z(half):
                    pe.wait_ge(S["parts_done"], 2 * b + half + 1)
                    if half == 0:
                        pe.wait_ge(S["mix_done"], 2 * (b + 1))
                    else:
                        pe.wait_ge(S["zt_kept"], 2 * b + 1)
                    for j in range(4):
                        last = nc.tensor.transpose(turned[0:48, 0, j * P:(j + 1) * P],
                                                   zparts[:, j, :, :].rearrange("p r h -> p (r h)"), m.identb[:])
                    last.then_inc(S["zt_psum"], 1)

                def spread(u):
                    half, c = u // 8, u % 8
                    if c == 0:
                        pe.wait_ge(S["zt_kept"], 2 * b + half + 1)
                    if u >= 2:
                        pe.wait_ge(S["qz_done"], 16 * b + u - 1)
                    nc.tensor.matmul(proj[:, 2 + u % 2, :], select[:, 2 * c:2 * c + 2, :].rearrange("p h d -> p (h d)"),
                                     zT[:, half, :], start=True, stop=True).then_inc(S["spread_done"], 1)

                def project(u):
                    half, c = u // 8, u % 8
                    pe.wait_ge(S["qz_done"], 16 * b + u + 1)
                    for j in range(4):
                        last = nc.tensor.matmul(acc[:, half, j * P:(j + 1) * P], qz[:, u % 2, j * P:(j + 1) * P],
                                                mix[:, c, :], start=(c == 0 and j == 0), stop=False,
                                                skip_group_check=True)
                    last.then_inc(S["qz_used"], 1)
                    if c == 7:
                        for j in range(4):
                            last = nc.tensor.matmul(acc[:, half, j * P:(j + 1) * P], m.ones[0:1, :], w["bo"],
                                                    start=False, stop=True, skip_group_check=True)
                        last.then_inc(S["y_psum"], 1)

                pe.wait_ge(S["proj_kept"], 4 * (b + 1) * TPB)
                if b == 0:
                    pe.wait_ge(S["sel_done"], 4)
                for u in range(27):
                    if u < 16:
                        query(u)
                    if u == 1:
                        mixes()
                    if 1 <= u <= 16:
                        norm_sum(u - 1)
                    if u in (10, 18):
                        turn_z((u - 10) // 8)
                    if 10 <= u < 26:
                        spread(u - 10)
                    if 11 <= u:
                        project(u - 11)

        @block.scalar
        def _(act):
            for b in range(BATCH):
                for t in range(TPB):
                    g = b * TPB + t
                    for half in range(2):
                        n = 2 * g + half
                        cols_ = slice(half * BANK, (half + 1) * BANK)
                        act.wait_ge(S["proj_done"], 2 * n + 1)
                        if n >= 2:
                            act.wait_ge(S["key_done"], n - 1)
                        nc.scalar.activation(keyexp[:, n % 2, :], proj[:, 2 * n % 4, :], ACT.Exp).then_inc(S["exp_done"], 1)
                        nc.scalar.activation(keyrelu[:, n % 2, :], proj[:, 2 * n % 4, :], ACT.Relu).then_inc(S["relu_done"], 1)
                        act.wait_ge(S["relu_done"], n + 1)
                        act.wait_ge(S["exp_done"], n + 1)
                        act.sem_inc(S["proj_kept"], 1)
                        act.wait_ge(S["proj_done"], 2 * n + 2)
                        if g >= 2:
                            act.wait_ge(S["tile_used"], g - 1)
                        nc.scalar.activation(val[:, g % 2, cols_], proj[:, (2 * n + 1) % 4, :],
                                             ACT.Copy).then_inc(S["val_done"], 1)
                        act.wait_ge(S["val_done"], n + 1)
                        act.sem_inc(S["proj_kept"], 1)
                def keep_z(half):
                    act.wait_ge(S["zt_psum"], 2 * b + half + 1)
                    nc.scalar.activation(zT[:, half, :], turned[0:48, 0, 0:BANK], ACT.Copy).then_inc(S["zt_kept"], 1)

                for u in range(16):
                    n = 16 * b + u
                    act.wait_ge(S["q_psum"], n + 1)
                    if u >= 2:
                        act.wait_ge(S["q_done"], n - 1)
                    nc.scalar.activation(keyexp[:, n % 2, :], proj[:, n % 2, :], ACT.Exp).then_inc(S["q_exp"], 1)
                    nc.scalar.activation(keyrelu[:, n % 2, :], proj[:, n % 2, :], ACT.Relu).then_inc(S["q_free"], 1)
                    if u == 10:
                        keep_z(0)
                keep_z(1)

        @block.gpsimd
        def _(pool):
            nc.gpsimd.memset(select[:], 0.0).then_inc(S["sel_done"], 1)
            for r in range(3):
                pool.wait_ge(S["sel_done"], r + 1)
                nc.gpsimd.affine_select(out=select[:], in_=select[:], compare_op=ALU.not_equal, fill=1.0, base=-16 * r,
                                        pattern=[[-1, 16], [0, 64]], channel_multiplier=1).then_inc(S["sel_done"], 1)
            for b in range(BATCH):
                for t in range(TPB):
                    g = b * TPB + t
                    pool.wait_ge(S["key_done"], 2 * (g + 1))
                    if t == 0:
                        if b > 0:
                            pool.wait_ge(S["ksum_psum"], b)
                        nc.gpsimd.tensor_copy(keytotal[:], key[:, g % 2, :]).then_inc(S["total_done"], 1)
                    else:
                        pool.wait_ge(S["total_done"], g)
                        nc.gpsimd.tensor_tensor(keytotal[:], keytotal[:], key[:, g % 2, :],
                                                ALU.add).then_inc(S["total_done"], 1)

        @block.vector
        def _(dve):
            chain = Chain(dve, S["chain"])
            for b in range(BATCH):
                for t in range(TPB):
                    g = b * TPB + t
                    for half in range(2):
                        n = 2 * g + half
                        dve.wait_ge(S["relu_done"], n + 1)
                        dve.wait_ge(S["exp_done"], n + 1)
                        if g >= 2:
                            dve.wait_ge(S["tile_used"], g - 1)
                            dve.wait_ge(S["total_done"], g - 1)
                        nc.vector.scalar_tensor_tensor(out=key[:, g % 2, half * BANK:(half + 1) * BANK],
                                                       in0=keyexp[:, n % 2, :], scalar=1.0, in1=keyrelu[:, n % 2, :],
                                                       op0=ALU.min, op1=ALU.add).then_inc(S["key_done"], 1)
                def features(u):
                    n = 16 * b + u
                    dve.wait_ge(S["q_exp"], n + 1)
                    dve.wait_ge(S["q_free"], n + 1)
                    nc.vector.scalar_tensor_tensor(out=qry[:, u // 8, u % 8, :], in0=keyexp[:, n % 2, :], scalar=1.0,
                                                   in1=keyrelu[:, n % 2, :], op0=ALU.min,
                                                   op1=ALU.add).then_inc(S["q_done"], 1)

                def invert(half):
                    dve.wait_ge(S["z_psum"], 16 * b + 8 * half + 8)
                    if 2 * b + half > 0:
                        dve.wait_ge(S["zt_psum"], 2 * b + half)
                    chain.step(nc.vector.tensor_scalar(zsum[:], acc[:, 1 + half, 0:64], EPS, None, ALU.add))
                    chain.step(nc.vector.reciprocal(zsum[:], zsum[:]))
                    hi, mid, lo = (zparts[:, :, r, :] for r in range(3))
                    split3(nc, chain, zsum[:].rearrange("p (j h) -> p j h", h=16), hi, mid, lo,
                           zrest[:].rearrange("p (j h) -> p j h", h=16))
                    dve.sem_inc(S["parts_done"], 1)

                def divide(u):
                    n = 16 * b + u
                    dve.wait_ge(S["spread_done"], n + 1)
                    if n >= 2:
                        dve.wait_ge(S["qz_used"], n - 1)
                    nc.vector.tensor_tensor(qz[:, u % 2, :], qry[:, u // 8, u % 8, :], proj[:, 2 + u % 2, :],
                                            ALU.mult).then_inc(S["qz_done"], 1)

                def keep_y(half):
                    dve.wait_ge(S["y_psum"], 2 * b + half + 1)
                    nc.vector.tensor_copy(m.Y[:, b * TPB + 4 * half:b * TPB + 4 * half + 4, :],
                                          acc[:, half, :].rearrange("p (j n) -> p j n", j=4)).then_inc(S["y_kept"], 1)

                dve.wait_ge(S["tile_used"], (b + 1) * TPB)
                for c in range(8):
                    last = nc.vector.tensor_tensor(kvT[:, c, :], acc[:, c // 4, c % 4 * P:(c % 4 + 1) * P],
                                                   m.blockdiag[:], ALU.mult)
                last.then_inc(S["kvT_done"], 1)
                dve.wait_ge(S["ksum_psum"], b + 1)
                nc.vector.tensor_copy(ksum[:], acc[:, 2, 0:8]).then_inc(S["ksum_done"], 1)
                dve.wait_ge(S["ksum_done"], b + 1)
                for h in range(2):
                    last = nc.vector.tensor_scalar(ksum2[:, :, h], ksum[:], m.blockdiag[:, 64 * h:64 * h + 1], None,
                                                   ALU.mult)
                last.then_inc(S["ksum2_done"], 1)
                for u in range(26):
                    if u < 16:
                        features(u)
                    if u == 0:
                        for h in range(2):
                            dve.wait_ge(S["mix_psum"], 8 * b + 4 * (h + 1))
                            nc.vector.tensor_copy(mix[:, 4 * h:4 * h + 4, :],
                                                  small[:, 0, :].rearrange("p (c n) -> p c n", c=4)).then_inc(S["mix_done"], 1)
                    if u in (8, 16):
                        invert(u // 8 - 1)
                    if u == 19:
                        keep_y(0)
                    if u >= 10:
                        divide(u - 10)
                keep_y(1)


SLOTS = 64
BUFS, OWN = 7, 5
POOL_SLOTS = 3


def split3(nc, chain, src, hi, mid, lo, rest):
    chain.step(nc.vector.tensor_copy(hi, src))
    chain.step(nc.vector.tensor_tensor(rest, src, hi, ALU.subtract))
    chain.step(nc.vector.tensor_copy(mid, rest))
    chain.step(nc.vector.tensor_tensor(rest, rest, mid, ALU.subtract))
    chain.step(nc.vector.tensor_copy(lo, rest))


def small_head_attention(nc, m, dram, s, router):
    w = weight_views(m, s)
    with ExitStack() as keep:
        def kept(name, shape, dt):
            return keep.enter_context(nc.sbuf_tensor(name, shape, dt))
        kT = kept("heads_kT", [P, 8, TOKENS], BF16)
        qstack = kept("heads_qstack", [P, NT, 16, SLOTS], BF16)
        vaug = kept("heads_vaug", [P, NT, 16, 9], F32)

        with Phase(nc, "hprep") as ph:
            kstack = ph.sb("kstack", [P, 2, 16, SLOTS], BF16)
            qk = ph.sb("qk", [P, 2, 256])
            parts = ph.sb("parts", [P, 2, 3, 256], BF16)
            rest = ph.sb("rest", [P, 256])
            bias = ph.sb("bias", [P, 384])
            proj = ph.ps("proj", 2)
            turned = ph.ctx.enter_context(nc.psum_tensor("hprep_turned", [P, 2, 1024], BF16))
            cleared, proj_done, qk_done, v_done, parts_done, chain_sem, stack_act, stack_pool, stack_dve, turn_done, turn_kept, bias_done, bias_kept = (
                ph.sem(x) for x in ("cleared", "proj_done", "qk_done", "v_done", "parts_done", "chain", "stack_act",
                                    "stack_pool", "stack_dve", "turn_done", "turn_kept", "bias_done", "bias_kept"))
            block = ph.block()

            @block.sync
            def _(sp):
                load_weights(sp, m, dram, s + 1)

            @block.tensor
            def _(pe):
                pe.wait_ge(m.wsem[s], 16)

                def turn(g):
                    pe.wait_ge(stack_act, g + 1)
                    pe.wait_ge(stack_pool, g + 1)
                    pe.wait_ge(stack_dve, g + 1)
                    if g >= 2:
                        pe.wait_ge(turn_kept, g - 1)
                    for c in range(8):
                        last = nc.tensor.transpose(turned[:, g % 2, c * P:(c + 1) * P],
                                                   kstack[:, g % 2, 2 * c:2 * c + 2, :].rearrange("p h d -> p (h d)"),
                                                   m.identb[:])
                    last.then_inc(turn_done, 1)

                nc.tensor.matmul(proj[:, 1, 0:384], m.ones[0:1, :], w["bqkv"], start=True,
                                 stop=True).then_inc(bias_done, 1)
                for g in range(NT):
                    if g == 1:
                        pe.wait_ge(bias_kept, 1)
                    if g >= 2:
                        pe.wait_ge(qk_done, g - 1)
                        pe.wait_ge(v_done, g - 1)
                    nc.tensor.matmul(proj[:, g % 2, 0:384], m.HT[:, g * P:(g + 1) * P], w["Wqkv"], start=True,
                                     stop=True).then_inc(proj_done, 1)
                    if g >= 2:
                        turn(g - 2)
                turn(NT - 2)
                turn(NT - 1)

            @block.scalar
            def _(act):
                def stack(g):
                    act.wait_ge(parts_done, g + 1)
                    hi, mid, lo = (parts[:, g % 2, k, 0:P].rearrange("p (h d) -> p h d", h=16) for k in range(3))
                    for slot, part in enumerate((hi, hi, mid, mid, hi, lo)):
                        last = nc.scalar.activation(qstack[:, g, :, 8 * slot:8 * slot + 8], part, ACT.Copy)
                    last.then_inc(stack_act, 1)

                def keep_turned(g):
                    act.wait_ge(turn_done, g + 1)
                    nc.scalar.activation(kT[:, :, g * P:(g + 1) * P], turned[:, g % 2, :].rearrange("p (c n) -> p c n", c=8),
                                         ACT.Copy).then_inc(turn_kept, 1)
                act.wait_ge(cleared, 5)
                for g in range(NT):
                    stack(g)
                    if g >= 2:
                        keep_turned(g - 2)
                keep_turned(NT - 2)
                keep_turned(NT - 1)

            @block.gpsimd
            def _(pool):
                pool.wait_ge(cleared, 5)
                for g in range(NT):
                    pool.wait_ge(parts_done, g + 1)
                    if g >= 2:
                        pool.wait_ge(turn_done, g - 1)
                    hi, mid, lo = (parts[:, g % 2, k, P:2 * P].rearrange("p (h d) -> p h d", h=16) for k in range(3))
                    for slot, part in enumerate((hi, mid, hi, mid, lo, hi)[:POOL_SLOTS]):
                        last = nc.gpsimd.tensor_copy(kstack[:, g % 2, :, 8 * slot:8 * slot + 8], part)
                    last.then_inc(stack_pool, 1)

            @block.vector
            def _(dve):
                chain = Chain(dve, chain_sem)
                nc.vector.memset(kstack[:, :, :, 51:64], 0.0).then_inc(cleared, 1)
                nc.vector.memset(kstack[:, :, :, 48:51], 1.0).then_inc(cleared, 1)
                nc.vector.memset(qstack[:, 0:8, :, 48:64], 0.0).then_inc(cleared, 1)
                nc.vector.memset(qstack[:, 8:16, :, 48:64], 0.0).then_inc(cleared, 1)
                nc.vector.memset(vaug[:, :, :, 8], 1.0).then_inc(cleared, 1)
                dve.wait_ge(bias_done, 1)
                nc.vector.tensor_copy(bias[:], proj[:, 1, 0:384]).then_inc(bias_kept, 1)
                dve.wait_ge(bias_kept, 1)
                for g in range(NT):
                    dve.wait_ge(proj_done, g + 1)
                    nc.vector.tensor_tensor(qk[:, g % 2, :], proj[:, g % 2, 0:256], bias[:, 0:256],
                                            ALU.add).then_inc(qk_done, 1)
                    nc.vector.tensor_tensor(vaug[:, g, :, 0:8], proj[:, g % 2, 256:384].rearrange("p (h d) -> p h d", h=16),
                                            bias[:, 256:384].rearrange("p (h d) -> p h d", h=16),
                                            ALU.add).then_inc(v_done, 1)
                    dve.wait_ge(qk_done, g + 1)
                    if g >= 2:
                        dve.wait_ge(stack_act, g - 1)
                        dve.wait_ge(stack_pool, g - 1)
                    split3(nc, chain, qk[:, g % 2, :], parts[:, g % 2, 0, :], parts[:, g % 2, 1, :],
                           parts[:, g % 2, 2, :], rest[:])
                    dve.sem_inc(parts_done, 1)
                    if g >= 2:
                        dve.wait_ge(turn_done, g - 1)
                    hi, mid, lo = (parts[:, g % 2, k, P:2 * P].rearrange("p (h d) -> p h d", h=16) for k in range(3))
                    for slot, part in list(enumerate((hi, mid, hi, mid, lo, hi)))[POOL_SLOTS:]:
                        last = nc.vector.tensor_copy(kstack[:, g % 2, :, 8 * slot:8 * slot + 8], part)
                    last.then_inc(stack_dve, 1)

        with Phase(nc, "heads") as ph:
            qT = ph.sb("qT", [P, 2, 8, P], BF16)
            qmT = ph.sb("qmT", [P, 2, 8, P], BF16)
            halfmax = ph.sb("halfmax", [P, 2, 16, 2])
            negmax = ph.sb("negmax", [P, 16])
            rest = ph.sb("rest", [P, 16])
            probs_own = ph.sb("probs", [P, OWN, 1024])
            probs_xn = m.XN[:].rearrange("p (a t) n -> p a (t n)", a=BUFS - OWN)
            rsum = ph.sb("rsum", [P, 2, 16])
            qmajor = ph.ps("qmajor", 2)
            kmajor = ph.ps("kmajor", 4)
            outT = ph.sb("outT", [P, BANK])
            outp = ph.ps("outp", 1)
            turned32 = ph.ps("turned", 1)
            turned = turned32[:].bitcast(BF16)
            out_free, t3_done = ph.sem("out_free"), ph.sem("t3_done")
            logits_done, exp_in, exp_out, gates_done = (
                ph.sem(x) for x in ("logits_done", "exp_in", "exp_out", "gates_done"))
            (t1_done, t1_kept, s_done, max_done, slots_done, t2_done, t2_kept, st_done, exp_done, pv_done, head_done,
             out_kept, chain_sem, rsum_done) = (
                ph.sem(x) for x in ("t1_done", "t1_kept", "s_done", "max_done", "slots_done", "t2_done", "t2_kept",
                                    "st_done", "exp_done", "pv_done", "head_done", "out_kept", "chain", "rsum_done"))
            block = ph.block()
            SC = float(8) ** -0.5
            UNITS, LAG = 16 * NT, 23

            def probs_of(k):
                return probs_own[:, k % BUFS, :] if k % BUFS < OWN else probs_xn[:, k % BUFS - OWN, :]

            @block.tensor
            def _(pe):
                def turn(g, done, kept1, kept2, kept3):
                    if kept3 > 0:
                        pe.wait_ge(out_kept, kept3)
                    if kept1 > 0:
                        pe.wait_ge(t1_kept, kept1)
                    if kept2 > 0:
                        pe.wait_ge(t2_kept, kept2)
                    for c in range(8):
                        last = nc.tensor.transpose(turned[:, 0, c * P:(c + 1) * P],
                                                   qstack[:, g, 2 * c:2 * c + 2, :].rearrange("p h d -> p (h d)"),
                                                   m.identb[:])
                    last.then_inc(done, 1)

                def scores(unit, half):
                    g, h = unit // 16, unit % 16
                    c, j, b = h // 2, h % 2, g // TPB
                    if h == 0 and half == 0:
                        pe.wait_ge(t1_kept, g + 1)
                    if 2 * unit + half >= 2:
                        pe.wait_ge(max_done, 2 * unit + half - 1)
                    nc.tensor.matmul(qmajor[:, half, :], qT[64 * j:64 * j + 48, g % 2, c, :],
                                     kT[64 * j:64 * j + 48, c, b * SEQ + half * BANK:b * SEQ + (half + 1) * BANK],
                                     start=True, stop=True).then_inc(s_done, 1)

                def shifted(k, half):
                    g, h = k // 16, k % 16
                    c, j, b = h // 2, h % 2, g // TPB
                    if h == 0 and half == 0:
                        pe.wait_ge(t2_kept, g + 1)
                    if k >= 2 and half == 0:
                        pe.wait_ge(exp_done, k - 1)
                    for kc in range(4 * half, 4 * half + 4):
                        last = nc.tensor.matmul(kmajor[:, 2 * (k % 2) + kc // 4, kc % 4 * P:(kc % 4 + 1) * P],
                                                kT[64 * j:64 * j + 51, c, b * SEQ + kc * P:b * SEQ + (kc + 1) * P],
                                                qmT[64 * j:64 * j + 51, g % 2, c, :], start=True, stop=True)
                    if half == 1:
                        last.then_inc(st_done, 1)

                def values(q):
                    g, c = q // 4, q % 4
                    b = g // TPB
                    pe.wait_ge(exp_done, 4 * q + 4)
                    if c == 0:
                        pe.wait_ge(out_free, g + 1)
                    for kc in range(TPB):
                        for j in range(4):
                            last = nc.tensor.matmul(outp[32 * j:32 * j + 9, 0, c * P:(c + 1) * P],
                                                    vaug[:, b * TPB + kc, 4 * c + j, :],
                                                    probs_of(4 * q + j)[:, kc * P:(kc + 1) * P], start=(kc == 0),
                                                    stop=(kc == TPB - 1), skip_group_check=True)
                    last.then_inc(pv_done, 1)

                def turn_out(g):
                    pe.wait_ge(out_free, g + 2)
                    pe.wait_ge(t2_kept, g + 2 if g + 2 <= NT else NT)
                    pe.wait_ge(t1_kept, min(g + 3, NT))
                    if g >= 1:
                        pe.wait_ge(out_kept, g)
                    for c in range(4):
                        last = nc.tensor.transpose(turned32[:, 0, c * P:(c + 1) * P], outT[:, c * P:(c + 1) * P],
                                                   m.ident[:])
                    last.then_inc(t3_done, 1)

                turn(0, t1_done, 0, 0, 0)
                for n in range(16 * (NT + 2)):
                    g, h = n // 16, n % 16
                    if h == 3 and 1 <= g <= NT:
                        pe.wait_ge(slots_done, g)
                        turn(g - 1, t2_done, min(g + 1, NT), g - 1, g - 2)
                    for half in range(2):
                        if n < UNITS:
                            scores(n, half)
                        if LAG <= n < UNITS + LAG:
                            shifted(n - LAG, half)
                    if n == UNITS + 1:
                        pe.wait_ge(max_done, 2 * UNITS)
                        for t in range(NT):
                            to = qmajor[:, 0, 8 * t:8 * t + 8]
                            nc.tensor.matmul(to, m.HT[:, t * P:(t + 1) * P], w["Wgate"], start=True, stop=False)
                            last = nc.tensor.matmul(to, m.ones[0:1, :], w["bgate"], start=False, stop=True)
                        last.then_inc(logits_done, 1)
                    if n >= LAG + 5 and (n - LAG - 5) % 4 == 0 and (n - LAG - 5) // 4 < UNITS // 4:
                        values((n - LAG - 5) // 4)
                    if h == 11 and g >= 2:
                        turn_out(g - 2)
                    if h == 13 and g + 1 < NT:
                        turn(g + 1, t1_done, g + 1, g, g - 1)

            @block.scalar
            def _(act):
                def keep1(g):
                    act.wait_ge(t1_done, g + 1)
                    if g >= 2:
                        act.wait_ge(s_done, 32 * (g - 1))
                    nc.scalar.activation(qT[:, g % 2, :, :], turned[:, 0, :].rearrange("p (c n) -> p c n", c=8),
                                         ACT.Copy).then_inc(t1_kept, 1)

                def keep2(g):
                    act.wait_ge(t2_done, g + 1)
                    if g >= 2:
                        act.wait_ge(st_done, 16 * (g - 1))
                    nc.scalar.activation(qmT[:, g % 2, :, :], turned[:, 0, :].rearrange("p (c n) -> p c n", c=8),
                                         ACT.Copy).then_inc(t2_kept, 1)
                keep1(0)
                act.wait_ge(out_free, 1)
                for n in range(16 * (NT + 2)):
                    g, h = n // 16, n % 16
                    if h == 3 and 1 <= g <= NT:
                        keep2(g - 1)
                    if LAG <= n < UNITS + LAG:
                        k = n - LAG
                        act.wait_ge(st_done, k + 1)
                        if k >= BUFS:
                            act.wait_ge(pv_done, (k - BUFS) // 4 + 1)
                        nc.scalar.activation(probs_of(k).rearrange("p (a n) -> p a n", a=2),
                                             kmajor[:, 2 * (k % 2):2 * (k % 2) + 2, :], ACT.Exp,
                                             scale=SC).then_inc(exp_done, 1)
                    if h == 9 and g >= 2:
                        act.wait_ge(pv_done, 4 * (g - 1))
                        if g >= 3:
                            act.wait_ge(t3_done, g - 2)
                        nc.scalar.activation(outT[:], outp[:, 0, :], ACT.Copy).then_inc(out_free, 1)
                    if h == 13 and g + 1 < NT:
                        keep1(g + 1)
                    if n == UNITS + 6:
                        act.wait_ge(exp_in, 1)
                        nc.scalar.activation(router.gates[:], router.gates[:], ACT.Exp).then_inc(exp_out, 1)

            @block.vector
            def _(dve):
                chain = Chain(dve, chain_sem)

                def normalise(g):
                    dve.wait_ge(t3_done, g + 1)
                    o = turned32[:, 0, :].rearrange("p (h e) -> p h e", h=16)
                    nc.vector.reciprocal(rsum[:, g % 2, :], o[:, :, 8]).then_inc(rsum_done, 1)
                    dve.wait_ge(rsum_done, g + 1)
                    nc.vector.tensor_tensor(m.Y[:, g, :].rearrange("p (h d) -> p h d", h=16), o[:, :, 0:8],
                                            rsum[:, g % 2, :].unsqueeze(2).broadcast_to([P, 16, 8]),
                                            ALU.mult).then_inc(out_kept, 1)

                nc.vector.memset(outp[:], 0.0).then_inc(out_free, 1)
                for g in range(NT):
                    for h in range(16):
                        for half in range(2):
                            dve.wait_ge(s_done, 32 * g + 2 * h + half + 1)
                            nc.vector.tensor_reduce(halfmax[:, g % 2, h, half:half + 1], qmajor[:, half, :], AX,
                                                    ALU.max).then_inc(max_done, 1)
                        if h == 11 and g >= 2:
                            normalise(g - 2)
                    dve.wait_ge(max_done, 32 * (g + 1))
                    chain.step(nc.vector.tensor_reduce(negmax[:], halfmax[:, g % 2, :, :], AX, ALU.max))
                    chain.step(nc.vector.tensor_scalar(negmax[:], negmax[:], -1.0, None, ALU.mult))
                    dve.wait_ge(t1_done, g + 1)
                    split3(nc, chain, negmax[:], qstack[:, g, :, 48], qstack[:, g, :, 49], qstack[:, g, :, 50], rest[:])
                    dve.sem_inc(slots_done, 1)
                dve.wait_ge(logits_done, 1)
                lg = qmajor[:, 0, 0:8 * NT].rearrange("p (t e) -> p t e", e=8)
                top2_gates(nc, m, dve, chain, lg, router, exp_in, exp_out, gates_done)
                normalise(NT - 2)
                normalise(NT - 1)


class Router:

    def __init__(self, nc, ctx):
        def sb(name, shape, dt=F32):
            return ctx.enter_context(nc.sbuf_tensor(f"router_{name}", shape, dt))
        self.gates = sb("gates", [P, NT, 8])
        self.pick = sb("pick", [P, NT, 8])
        self.pick2 = sb("pick2", [P, NT, 8])
        self.stat = sb("stat", [P, NT])
        self.top = sb("top", [P, NT, 8])
        self.where = sb("where", [P, NT, 8], U32)
        self.wheref = sb("wheref", [P, NT, 2])
        self.parts = sb("parts", [P, NT, 3, 8], BF16)
        self.rest = sb("rest", [P, NT, 8])


def top2_gates(nc, m, dve, chain, logits, r, exp_in, exp_out, gates_done):
    def wide(a):
        return a.unsqueeze(2).broadcast_to([P, NT, 8])
    chain.step(nc.vector.tensor_reduce(r.stat[:], logits, AX, ALU.max))
    nc.vector.tensor_tensor(r.gates[:], logits, wide(r.stat[:]), ALU.subtract).then_inc(exp_in, 1)
    dve.wait_ge(exp_out, 1)
    chain.step(nc.vector.tensor_reduce(r.stat[:], r.gates[:], AX, ALU.add))
    chain.step(nc.vector.reciprocal(r.stat[:], r.stat[:]))
    chain.step(nc.vector.tensor_tensor(r.gates[:], r.gates[:], wide(r.stat[:]), ALU.mult))
    top2_mask(nc, m, chain, r.gates, r.top, r.where, r.wheref, r.pick, r.pick2)
    nc.vector.tensor_tensor(r.gates[:], r.gates[:], r.pick[:], ALU.mult).then_inc(gates_done, 1)
    dve.wait_ge(gates_done, 1)
    split3(nc, chain, r.gates[:], r.parts[:, :, 0, :], r.parts[:, :, 1, :], r.parts[:, :, 2, :], r.rest[:])


def top2_experts(nc, m, dram, s, router):
    w = weight_views(m, s)
    E = 8
    UNITS = [(tc, e) for tc in range(NT // 4) for e in range(E)]
    with Phase(nc, "moe0") as ph:
        gates, parts = router.gates, router.parts
        partsT = ph.sb("partsT", [24, TOKENS], BF16)
        gT = ph.sb("gT", [8, TOKENS])
        select = ph.sb("select", [24, E, P], BF16)
        scaled = ph.sb("scaled", [P, 3, BANK])
        spread = ph.ps("spread", 2)
        out = ph.ps("out", 2)
        turned = ph.ps("turned", 2)
        turnedb = ph.ctx.enter_context(nc.psum_tensor("moe0_turnedb", [P, 1, 1024], BF16))
        gt_done, gt_kept, pt_done, pt_kept, sel_done, spread_done, scaled_done, used, y_done = (
            ph.sem(x) for x in ("gt_done", "gt_kept", "pt_done", "pt_kept", "sel_done", "spread_done", "scaled_done",
                                "used", "y_done"))
        block = ph.block()

        @block.gpsimd
        def _(pool):
            nc.gpsimd.memset(select[:], 0.0).then_inc(sel_done, 1)
            for r in range(3):
                pool.wait_ge(sel_done, r + 1)
                nc.gpsimd.affine_select(out=select[:], in_=select[:], compare_op=ALU.not_equal, fill=1.0, base=-8 * r,
                                        pattern=[[-1, E], [0, P]], channel_multiplier=1).then_inc(sel_done, 1)

        @block.tensor
        def _(pe):
            for g in range(NT):
                if g % 4 == 0 and g >= 8:
                    pe.wait_ge(gt_kept, g // 4 - 1)
                nc.tensor.transpose(turned[0:8, g // 4 % 2, g % 4 * P:(g % 4 + 1) * P], gates[:, g, :],
                                    m.ident[:]).then_inc(gt_done, 1)
            for half in range(2):
                if half:
                    pe.wait_ge(pt_kept, 1)
                for j in range(8):
                    last = nc.tensor.transpose(turnedb[0:24, 0, j * P:(j + 1) * P],
                                               parts[:, 8 * half + j, :, :].rearrange("p r e -> p (r e)"), m.identb[:])
                last.then_inc(pt_done, 1)
            pe.wait_ge(pt_kept, 2)
            pe.wait_ge(gt_kept, 4)
            pe.wait_ge(sel_done, 4)

            def spread_gate(n):
                tc, e = UNITS[n]
                if n >= 2:
                    pe.wait_ge(scaled_done, n - 1)
                nc.tensor.matmul(spread[:, n % 2, :], select[:, e, :], partsT[:, tc * BANK:(tc + 1) * BANK], start=True,
                                 stop=True).then_inc(spread_done, 1)
            spread_gate(0)
            for n, (tc, e) in enumerate(UNITS):
                if n + 1 < len(UNITS):
                    spread_gate(n + 1)
                if e == 0:
                    if tc >= 2:
                        pe.wait_ge(y_done, tc - 1)
                    for j in range(4):
                        t = 4 * tc + j
                        nc.tensor.matmul(out[:, tc % 2, j * P:(j + 1) * P], gT[:, t * P:(t + 1) * P], w["bexp"],
                                         start=(j == 0), stop=False, skip_group_check=True)
                pe.wait_ge(scaled_done, n + 1)
                for j in range(4):
                    last = nc.tensor.matmul(out[:, tc % 2, j * P:(j + 1) * P], scaled[:, n % 3, j * P:(j + 1) * P],
                                            w["Wexp"][:, e * P:(e + 1) * P], start=False, stop=(e == E - 1),
                                            skip_group_check=True)
                last.then_inc(used, 1)

        @block.scalar
        def _(act):
            for c in range(4):
                act.wait_ge(gt_done, 4 * (c + 1))
                nc.scalar.activation(gT[:, c * BANK:(c + 1) * BANK], turned[0:8, c % 2, :], ACT.Copy).then_inc(gt_kept, 1)
            for half in range(2):
                act.wait_ge(pt_done, half + 1)
                nc.scalar.activation(partsT[:, half * 1024:(half + 1) * 1024], turnedb[0:24, 0, :],
                                     ACT.Copy).then_inc(pt_kept, 1)

        def add(dve, tc):
            dve.wait_ge(used, E * (tc + 1))
            y = m.Y[:, 4 * tc:4 * tc + 4, :].rearrange("p t n -> p (t n)")
            nc.vector.tensor_tensor(y, out[:, tc % 2, :], y, ALU.add).then_inc(y_done, 1)

        @block.vector
        def _(dve):
            for n, (tc, e) in enumerate(UNITS):
                dve.wait_ge(spread_done, n + 1)
                if n >= 3:
                    dve.wait_ge(used, n - 2)
                nc.vector.tensor_tensor(scaled[:, n % 3, :], spread[:, n % 2, :], m.HT[:, tc * BANK:(tc + 1) * BANK],
                                        ALU.mult).then_inc(scaled_done, 1)
                if e == 1 and tc >= 1:
                    add(dve, tc - 1)
            add(dve, NT // 4 - 1)


def top2_mask(nc, m, chain, gates, top, where, wheref, pick, pick2):
    for g in range(NT):
        last = nc.vector.max(out=top[:, g, :], in_=gates[:, g, :])
    chain.step(last)
    for g in range(NT):
        last = nc.vector.max_index(where[:, g, :], top[:, g, :], gates[:, g, :])
    chain.step(last)
    chain.step(nc.vector.tensor_copy(wheref[:], where[:, :, 0:2]))
    index = m.iota8[:].unsqueeze(1).broadcast_to([P, NT, 8])
    chain.step(nc.vector.tensor_tensor(pick[:], index, wheref[:, :, 0:1].broadcast_to([P, NT, 8]), ALU.is_equal))
    chain.step(nc.vector.tensor_tensor(pick2[:], index, wheref[:, :, 1:2].broadcast_to([P, NT, 8]), ALU.is_equal))
    chain.step(nc.vector.tensor_tensor(pick[:], pick[:], pick2[:], ALU.add))


def attention_and_top2(nc, m, dram, s):
    with ExitStack() as keep:
        router = Router(nc, keep)
        small_head_attention(nc, m, dram, s, router)
        top2_experts(nc, m, dram, s, router)


def causal_attention(nc, m, dram, s, name, groups, heads, scale, out_proj):
    w = weight_views(m, s)
    D = P // heads
    GROUPS = [(b, c) for b in range(BATCH) for c in range(groups)]
    MIXED = [i for pair in zip(range(TPB - 1, TPB // 2 - 1, -1), range(TPB // 2)) for i in pair]
    UNITS = [(g, h, i) for g in range(len(GROUPS)) for h in range(heads) for i in MIXED]
    PER = heads * TPB

    def blocks(n):
        return UNITS[n][2] + 1

    def fills(n):
        return (blocks(n) + 3) // 4

    first_fill = [sum(fills(k) for k in range(n)) for n in range(len(UNITS) + 1)]

    def schedule():
        events, k = [], 0

        def misc_event(what, idx):
            nonlocal k
            events.append((what, idx, k))
            k += 1

        ahead = [4 + part * (PER - 4) // 6 for part in range(6)]
        for part in range(6):
            misc_event("project", (0, part))
        for n in range(len(UNITS) + 9):
            g, at = n // PER, n % PER
            if n < len(UNITS):
                events.append(("scores", n, None))
            for part in range(6):
                if ahead[part] == at and g + 1 < len(GROUPS):
                    misc_event("project", (g + 1, part))
            if 2 <= n < len(UNITS) + 2:
                events.append(("transposes", n - 2, None))
            if 3 <= n < len(UNITS) + 3:
                misc_event("values", n - 3)
            if out_proj and g >= 1 and at in (3, 4):
                misc_event("turn", (g - 1, at - 3))
            if out_proj and g >= 1 and at in (6, 7) and g % groups == 0:
                misc_event("out", (g // groups - 1, at - 6))
        return events

    EVENTS = schedule()
    projected = {idx[0]: k + 1 for what, idx, k in EVENTS if what == "project"}
    z_whole = {UNITS[idx][0]: k + 1 for what, idx, k in EVENTS if what == "values"}
    zt_half = {idx: k + 1 for what, idx, k in EVENTS if what == "turn"}

    with Phase(nc, name) as ph:
        qT = ph.sb("qT", [P, 2, SEQ])
        kT = ph.sb("kT", [P, 2, SEQ])
        v = ph.sb("v", [P, 2, TPB, P])
        probs = ph.sb("probs", [P, 3, SEQ])
        probsT = ph.sb("probsT", [P, 2, SEQ])
        negmax = ph.sb("negmax", [P, 3])
        rowsum = ph.sb("rowsum", [P, 5])
        rinv = ph.sb("rinv", [P, 2])
        z = ph.sb("z", [P, 2, TPB, P]) if out_proj else None
        zT = ph.sb("zT", [P, groups, SEQ]) if out_proj else None
        score = ph.ps("score", 4)
        turned = ph.ps("turned", 2)
        misc = ph.ps("misc", 2)
        misc_done, misc_kept, s_done, negmax_done, exp_done, t_done, t_kept, pv_done, chain_sem = (
            ph.sem(x) for x in ("misc_done", "misc_kept", "s_done", "negmax_done", "exp_done", "t_done", "t_kept",
                                "pv_done", "chain"))
        block = ph.block()

        def score_of(n):
            return score[:, 2 * (n % 2):2 * (n % 2) + 2, :].rearrange("p a n -> p (a n)")

        @block.sync
        def _(sp):
            load_weights(sp, m, dram, s + 1)

        @block.tensor
        def _(pe):
            pe.wait_ge(m.wsem[s], 16)
            for what, idx, k in EVENTS:
                if k is not None and k >= 2:
                    pe.wait_ge(misc_kept, k - 1)
                if what == "project":
                    g, part = idx
                    b, c = GROUPS[g]
                    if part < 4:
                        wt, half = w["Wq" if part < 2 else "Wk"], part % 2
                        nc.tensor.matmul(misc[:, k % 2, :], wt[:, c * P:(c + 1) * P],
                                         m.HT[:, b * SEQ + half * BANK:b * SEQ + (half + 1) * BANK], start=True,
                                         stop=True).then_inc(misc_done, 1)
                    else:
                        for j in range(4):
                            t = b * TPB + 4 * (part - 4) + j
                            last = nc.tensor.matmul(misc[:, k % 2, j * P:(j + 1) * P], m.HT[:, t * P:(t + 1) * P],
                                                    w["Wv"][:, c * P:(c + 1) * P], start=True, stop=True)
                        last.then_inc(misc_done, 1)
                elif what == "scores":
                    g, h, i = UNITS[idx]
                    if idx % PER == 0:
                        pe.wait_ge(misc_kept, projected[g])
                    if idx >= 2:
                        pe.wait_ge(exp_done, idx - 1)
                    wide = (i + 1) * P
                    for at in range(0, wide, BANK):
                        to = min(wide, at + BANK)
                        nc.tensor.matmul(score_of(idx)[:, at:to], qT[D * h:D * (h + 1), g % 2, i * P:(i + 1) * P],
                                                kT[D * h:D * (h + 1), g % 2, at:to], start=True, stop=(to < wide),
                                                skip_group_check=True)
                    nc.tensor.matmul(score_of(idx)[:, i * P:wide], m.identb[:], m.causalb[:], start=False, stop=True,
                                     skip_group_check=True).then_inc(s_done, 1)
                elif what == "transposes":
                    pe.wait_ge(exp_done, idx + 1)
                    for f in range(fills(idx)):
                        e = first_fill[idx] + f
                        if e >= 2:
                            pe.wait_ge(t_kept, e - 1)
                        for kb in range(4 * f, min(4 * f + 4, blocks(idx))):
                            last = nc.tensor.transpose(turned[:, e % 2, kb % 4 * P:(kb % 4 + 1) * P],
                                                       probs[:, idx % 3, kb * P:(kb + 1) * P], m.ident[:])
                        last.then_inc(t_done, 1)
                elif what == "values":
                    g, h, i = UNITS[idx]
                    pe.wait_ge(t_kept, first_fill[idx + 1])
                    for kb in range(i + 1):
                        last = nc.tensor.matmul(misc[:, k % 2, 0:D], probsT[:, idx % 2, kb * P:(kb + 1) * P],
                                                v[:, g % 2, kb, D * h:D * (h + 1)], start=(kb == 0), stop=(kb == i))
                    last.then_inc(misc_done, 1)
                elif what == "turn":
                    g, half = idx
                    pe.wait_ge(misc_kept, z_whole[g])
                    for j in range(4):
                        last = nc.tensor.transpose(misc[:, k % 2, j * P:(j + 1) * P], z[:, g % 2, 4 * half + j, :],
                                                   m.ident[:])
                    last.then_inc(misc_done, 1)
                else:
                    b, half = idx
                    pe.wait_ge(misc_kept, zt_half[groups * (b + 1) - 1, half])
                    for j in range(4):
                        t = 4 * half + j
                        for c in range(groups):
                            last = nc.tensor.matmul(misc[:, k % 2, j * P:(j + 1) * P], zT[:, c, t * P:(t + 1) * P],
                                                    w["Wo"][:, c * P:(c + 1) * P], start=(c == 0), stop=(c == groups - 1))
                    last.then_inc(misc_done, 1)

        @block.scalar
        def _(act):
            def exps(n):
                act.wait_ge(negmax_done, n + 1)
                if n >= 3:
                    act.wait_ge(t_done, first_fill[n - 2])
                wide = blocks(n) * P
                nc.scalar.activation(probs[:, n % 3, 0:wide], score_of(n)[:, 0:wide], ACT.Exp,
                                     bias=negmax[:, n % 3:n % 3 + 1],
                                     accum_out=rowsum[:, n % 5:n % 5 + 1]).then_inc(exp_done, 1)

            def keep(n):
                if n >= 2:
                    act.wait_ge(pv_done, n - 1)
                for f in range(fills(n)):
                    act.wait_ge(t_done, first_fill[n] + f + 1)
                    at, to = 4 * f * P, min(4 * f + 4, blocks(n)) * P
                    nc.scalar.activation(probsT[:, n % 2, at:to], turned[:, (first_fill[n] + f) % 2, 0:to - at],
                                         ACT.Copy).then_inc(t_kept, 1)
            for n in range(len(UNITS) + 2):
                if n >= 2:
                    keep(n - 2)
                if n < len(UNITS):
                    exps(n)

        @block.vector
        def _(dve):
            chain = Chain(dve, chain_sem)
            for what, idx, k in EVENTS:
                if k is not None:
                    dve.wait_ge(misc_done, k + 1)
                if what == "project":
                    g, part = idx
                    if part < 4:
                        to = (qT if part < 2 else kT)[:, g % 2, part % 2 * BANK:(part % 2 + 1) * BANK]
                    else:
                        to = v[:, g % 2, 4 * (part - 4):4 * (part - 3), :].rearrange("p t n -> p (t n)")
                    if part < 2:
                        nc.vector.tensor_scalar(to, misc[:, k % 2, :], scale, None, ALU.mult).then_inc(misc_kept, 1)
                    else:
                        nc.vector.tensor_copy(to, misc[:, k % 2, :]).then_inc(misc_kept, 1)
                elif what == "scores":
                    i = UNITS[idx][2]
                    dve.wait_ge(s_done, idx + 1)
                    if idx >= 3:
                        dve.wait_ge(exp_done, idx - 2)
                    nc.vector.tensor_reduce(negmax[:, idx % 3:idx % 3 + 1], score_of(idx)[:, 0:(i + 1) * P], AX,
                                            ALU.max, negate=True).then_inc(negmax_done, 1)
                elif what == "values":
                    g, h, i = UNITS[idx]
                    dve.sem_inc(pv_done, 1)
                    r = rinv[:, idx % 2:idx % 2 + 1]
                    chain.step(nc.vector.reciprocal(r, rowsum[:, idx % 5:idx % 5 + 1]))
                    if out_proj:
                        to = z[:, g % 2, i, D * h:D * (h + 1)]
                    else:
                        to = m.Y[:, GROUPS[g][0] * TPB + i, :]
                    nc.vector.tensor_scalar(to, misc[:, k % 2, 0:D], r, None, ALU.mult).then_inc(misc_kept, 1)
                elif what == "turn":
                    g, half = idx
                    nc.vector.tensor_copy(zT[:, GROUPS[g][1], half * BANK:(half + 1) * BANK],
                                          misc[:, k % 2, :]).then_inc(misc_kept, 1)
                elif what == "out":
                    b, half = idx
                    t = b * TPB + 4 * half
                    nc.vector.tensor_copy(m.Y[:, t:t + 4, :].rearrange("p t n -> p (t n)"),
                                          misc[:, k % 2, :]).then_inc(misc_kept, 1)


def causal_single_head(nc, m, dram, s):
    causal_attention(nc, m, dram, s, "one", 1, 1, float(P) ** -0.5, False)


def swiglu_experts(nc, m, dram, s):
    w = weight_views(m, s)
    E, IC = 8, 4
    UNITS = [(tc, e, ic) for tc in range(NT // 4) for e in range(E) for ic in range(IC)]
    with Phase(nc, "swiglu") as ph:
        logits = ph.sb("logits", [P, NT, 8])
        gates = ph.sb("gates", [P, NT, 8])
        pick = ph.sb("pick", [P, NT, 8])
        pick2 = ph.sb("pick2", [P, NT, 8])
        stat = ph.sb("stat", [P, NT])
        top = ph.sb("top", [P, NT, 8])
        where = ph.sb("where", [P, NT, 8], U32)
        wheref = ph.sb("wheref", [P, NT, 2])
        silu = ph.sb("silu", [P, 2, BANK])
        hidden = ph.sb("hidden", [P, 3, BANK])
        router = ph.ps("router", 1)
        gate_up = ph.ps("gate_up", 4)
        down = ph.ps("down", 2)
        (router_done, chain_sem, exp_in, exp_out, gu_done, silu_done, hid_done, down_done, y_done) = (
            ph.sem(x) for x in ("router_done", "chain", "exp_in", "exp_out", "gu_done", "silu_done", "hid_done",
                                "down_done", "y_done"))
        block = ph.block()

        @block.sync
        def _(sp):
            load_weights(sp, m, dram, s + 1)

        @block.tensor
        def _(pe):
            pe.wait_ge(m.wsem[s], 16)
            for g in range(NT):
                last = nc.tensor.matmul(router[:, 0, 8 * g:8 * g + 8], m.HT[:, g * P:(g + 1) * P], w["gate"], start=True,
                                        stop=True)
            last.then_inc(router_done, 1)
            for n in range(len(UNITS) + 1):
                if n < len(UNITS):
                    tc, e, ic = UNITS[n]
                    if n >= 2:
                        pe.wait_ge(hid_done, n - 1)
                    at = (e * IC + ic) * P
                    for k, wt in enumerate((w["wg"], w["wu"])):
                        nc.tensor.matmul(gate_up[:, 2 * (n % 2) + k, :], wt[:, at:at + P],
                                         m.HT[:, tc * BANK:(tc + 1) * BANK], start=True, stop=True).then_inc(gu_done, 1)
                if n >= 1:
                    tc, e, ic = UNITS[n - 1]
                    k = tc * E + e
                    pe.wait_ge(hid_done, n)
                    if ic == 0 and k >= 2:
                        pe.wait_ge(y_done, 4 * (k - 1))
                    at = (e * IC + ic) * P
                    for j in range(4):
                        last = nc.tensor.matmul(down[:, k % 2, j * P:(j + 1) * P],
                                                hidden[:, (n - 1) % 3, j * P:(j + 1) * P], w["wd"][:, at:at + P],
                                                start=(ic == 0 and j == 0), stop=(ic == IC - 1), skip_group_check=True)
                    last.then_inc(down_done, 1)

        @block.scalar
        def _(act):
            act.wait_ge(exp_in, 1)
            nc.scalar.activation(gates[:], gates[:], ACT.Exp).then_inc(exp_out, 1)
            for n in range(len(UNITS)):
                act.wait_ge(gu_done, 2 * n + 1)
                if n >= 2:
                    act.wait_ge(hid_done, n - 1)
                nc.scalar.activation(silu[:, n % 2, :], gate_up[:, 2 * (n % 2), :], ACT.Silu).then_inc(silu_done, 1)

        @block.vector
        def _(dve):
            chain = Chain(dve, chain_sem)

            def wide(a):
                return a.broadcast_to([P, NT, 8])
            dve.wait_ge(router_done, 1)
            chain.step(nc.vector.tensor_copy(logits[:].rearrange("p t e -> p (t e)"), router[:, 0, 0:8 * NT]))
            top2_mask(nc, m, chain, logits, top, where, wheref, pick, pick2)
            nc.vector.tensor_tensor(gates[:], logits[:], wide(top[:, :, 0:1]), ALU.subtract).then_inc(exp_in, 1)
            dve.wait_ge(exp_out, 1)
            chain.step(nc.vector.tensor_tensor(gates[:], gates[:], pick[:], ALU.mult))
            chain.step(nc.vector.tensor_reduce(stat[:], gates[:], AX, ALU.add))
            chain.step(nc.vector.reciprocal(stat[:], stat[:]))
            chain.step(nc.vector.tensor_tensor(gates[:], gates[:], wide(stat[:].unsqueeze(2)), ALU.mult))
            for n in range(len(UNITS) + 1):
                if n < len(UNITS):
                    dve.wait_ge(silu_done, n + 1)
                    dve.wait_ge(gu_done, 2 * n + 2)
                    if n >= 3:
                        dve.wait_ge(down_done, n - 2)
                    nc.vector.tensor_tensor(hidden[:, n % 3, :], gate_up[:, 2 * (n % 2) + 1, :], silu[:, n % 2, :],
                                            ALU.mult).then_inc(hid_done, 1)
                if n >= 1 and UNITS[n - 1][2] == IC - 1:
                    tc, e, _ = UNITS[n - 1]
                    k = tc * E + e
                    dve.wait_ge(down_done, n)
                    if e > 0:
                        dve.wait_ge(y_done, 4 * k)
                    for j in range(4):
                        t = 4 * tc + j
                        src, c = down[:, k % 2, j * P:(j + 1) * P], gates[:, t, e:e + 1]
                        if e == 0:
                            last = nc.vector.tensor_scalar(m.Y[:, t, :], src, c, None, ALU.mult)
                        else:
                            last = nc.vector.scalar_tensor_tensor(out=m.Y[:, t, :], in0=src, scalar=c,
                                                                  in1=m.Y[:, t, :], op0=ALU.mult, op1=ALU.add)
                        last.then_inc(y_done, 1)


def causal_sixteen_heads(nc, m, dram, s):
    causal_attention(nc, m, dram, s, "many", 8, 2, 0.125, True)


HID = 341
WIN = 64
LAYERS = 2
SPAN = P + WIN


def shift_tokens(nc, m, name, Z, ZS):
    with Phase(nc, name) as ph:
        moved, kept, first = ph.sem("moved"), ph.sem("kept"), ph.sem("first")
        block = ph.block()

        @block.vector
        def _(dve):
            nc.vector.tensor_copy(ZS[:, :, 0:WIN], Z[:, :, 0:WIN]).then_inc(kept, 1)

        @block.gpsimd
        def _(pool):
            for b in range(BATCH):
                nc.gpsimd.memset(ZS[0:1, b * TPB, WIN:P], 0.0).then_inc(first, 1)

        @block.sync
        def _(sp):
            sp.dma_start(ZS[1:P, :, WIN:P], Z[0:P - 1, :, WIN:P]).then_inc(moved, 16)
            for b in range(BATCH):
                t = b * TPB
                sp.dma_start(ZS[0:1, t + 1:t + TPB, WIN:P], Z[P - 1:P, t:t + TPB - 1, WIN:P]).then_inc(moved, 16)
            sp.wait_ge(moved, 16 * (1 + BATCH))


def rotary_scale_phase(nc, m, w, l, tables, scaled):
    with Phase(nc, f"tables{l}") as ph:
        rows = ph.ps("rows", 1)
        spread = ph.sb("spread", [P, 2, 64])
        rows_done, spread_done = ph.sem("rows_done"), ph.sem("spread_done")
        done = ph.sem("done")
        block = ph.block()

        @block.tensor
        def _(pe):
            for k, name in enumerate(("qscale", "kscale")):
                last = nc.tensor.matmul(rows[:, 0, 64 * k:64 * k + 64], m.ones[0:1, :], w[name][:, 64 * l:64 * l + 64],
                                        start=True, stop=True)
            last.then_inc(rows_done, 1)

        @block.vector
        def _(dve):
            dve.wait_ge(rows_done, 1)
            nc.vector.tensor_copy(spread[:], rows[:, 0, 0:P].rearrange("p (k d) -> p k d", k=2)).then_inc(spread_done, 1)
            dve.wait_ge(spread_done, 1)
            for k in range(2):
                cos, sin = (tables[2 * k + j].rearrange("p (t d) -> p t d", d=64) for j in range(2))
                nc.vector.tensor_tensor(scaled[:, 2 * k, :, :], cos,
                                        spread[:, k, :].unsqueeze(1).broadcast_to([P, TPB, 64]), ALU.mult).then_inc(done, 1)
                for half in range(2):
                    mine, other = slice(32 * half, 32 * half + 32), slice(32 - 32 * half, 64 - 32 * half)
                    nc.vector.tensor_tensor(scaled[:, 2 * k + 1, :, mine], sin[:, :, mine],
                                            spread[:, k, other].unsqueeze(1).broadcast_to([P, TPB, 32]),
                                            ALU.mult).then_inc(done, 1)


def rotary_qkv(nc, m, w, l, b, Z, scaled, qT, kT, v, qnorm):
    with Phase(nc, f"qkv{l}{b}") as ph:
        HS = ph.sb("HS", [P, WIN + SEQ])
        squares = ph.sb("squares", [P, 2, BANK])
        sumsq = ph.sb("sumsq", [P, 2, 16])
        rnorm = ph.sb("rnorm", [P, 2, 16])
        cospart = ph.sb("cospart", [P, 2, 2, BANK])
        sinpart = ph.sb("sinpart", [P, 2, 2, BANK])
        rotated = ph.sb("rotated", [P, 3, 2, BANK])
        proj = ph.ps("proj", 4)
        vps = ph.ps("vps", 2)
        turned = ph.ps("turned", 2)
        (hs_turned, hs_kept, cleared, qk_done, sq_done, sum_done, clamp_done, rnorm_done, cs_done, addq_done, addk_done,
         t_done, t_kept, v_done, v_kept, qn_done) = (
            ph.sem(x) for x in ("hs_turned", "hs_kept", "cleared", "qk_done", "sq_done", "sum_done", "clamp_done",
                                "rnorm_done", "cs_done", "addq_done", "addk_done", "t_done", "t_kept", "v_done", "v_kept",
                                "qn_done"))
        block = ph.block()
        wl = w["wqkv"][:, 1536 * l:1536 * (l + 1)]

        @block.tensor
        def _(pe):
            for half in range(2):
                for j in range(4):
                    last = nc.tensor.transpose(turned[:, half, j * P:(j + 1) * P], Z[:, b * TPB + 4 * half + j, :],
                                               m.ident[:])
                last.then_inc(hs_turned, 1)
            pe.wait_ge(hs_kept, 2)
            pe.wait_ge(cleared, 3)

            def values(i):
                n = P if i < TPB else WIN
                if i >= 2:
                    pe.wait_ge(v_kept, i - 1)
                nc.tensor.matmul(vps[0:n, i % 2, :], HS[:, i * P:i * P + n], wl[:, 1024:1536], start=True,
                                 stop=True).then_inc(v_done, 1)

            def turn(i):
                for k in range(2):
                    pe.wait_ge((addq_done, qn_done)[k], i + 1)
                    if i >= 1:
                        pe.wait_ge(t_kept, 2 * i - 1 + k)
                    for c in range(4):
                        last = nc.tensor.transpose(turned[:, k, c * P:(c + 1) * P],
                                                   rotated[:, i % 3, k, c * P:(c + 1) * P], m.ident[:])
                    last.then_inc(t_done, 1)
            for i in range(TPB):
                if i >= 2:
                    pe.wait_ge(cs_done, 3 * (i - 1))
                    pe.wait_ge(sq_done, 2 * (i - 1))
                for k in range(2):
                    nc.tensor.matmul(proj[:, 2 * (i % 2) + k, :], HS[:, WIN + i * P:WIN + (i + 1) * P],
                                     wl[:, k * BANK:(k + 1) * BANK], start=True, stop=True).then_inc(qk_done, 1)
                values(i)
                if i >= 2:
                    turn(i - 2)
            values(TPB)
            turn(TPB - 2)
            turn(TPB - 1)

        @block.scalar
        def _(act):
            for half in range(2):
                act.wait_ge(hs_turned, half + 1)
                at, n = WIN + half * BANK, BANK - half
                nc.scalar.activation(HS[0:WIN, at:at + BANK], turned[0:WIN, half, :], ACT.Copy)
                nc.scalar.activation(HS[WIN:P, at + 1:at + 1 + n], turned[WIN:P, half, 0:n],
                                     ACT.Copy).then_inc(hs_kept, 1)

            def keep(i):
                for k, to in enumerate((qT[:, :, i * P:(i + 1) * P], kT[:, :, WIN + i * P:WIN + (i + 1) * P])):
                    act.wait_ge(t_done, 2 * i + k + 1)
                    nc.scalar.activation(to, turned[:, k, :].rearrange("p (c n) -> p c n", c=4), ACT.Copy).then_inc(t_kept, 1)

            def keep_v(i):
                n = P if i < TPB else WIN
                act.wait_ge(v_done, i + 1)
                nc.scalar.activation(v[0:n, i, :], vps[0:n, i % 2, :], ACT.Copy).then_inc(v_kept, 1)
            for i in range(TPB):
                for k in range(2):
                    act.wait_ge(qk_done, 2 * i + k + 1)
                    if i >= 1:
                        act.wait_ge(sum_done, i)
                    nc.scalar.activation(squares[:, k, :], proj[:, 2 * (i % 2) + k, :], ACT.Square).then_inc(sq_done, 1)
                keep_v(i)
                if i >= 2:
                    keep(i - 2)
            keep_v(TPB)
            keep(TPB - 2)
            keep(TPB - 1)

        def scale_k(dve, i):
            dve.wait_ge(rnorm_done, i + 1)
            nc.vector.tensor_scalar(qnorm[:, i, :], rnorm[:, i % 2, 0:8], 8.0, None, ALU.mult)
            dve.wait_ge(addk_done, i + 1)
            kr = rotated[:, i % 3, 1, :].rearrange("p (h d) -> p h d", d=64)
            nc.vector.tensor_tensor(kr, kr, rnorm[:, i % 2, 8:16].unsqueeze(2).broadcast_to([P, 8, 64]),
                                    ALU.mult).then_inc(qn_done, 1)

        @block.vector
        def _(dve):
            nc.vector.memset(HS[:, 0:WIN], 0.0).then_inc(cleared, 1)
            nc.vector.memset(HS[WIN:P, WIN:WIN + 1], 0.0).then_inc(cleared, 1)
            nc.vector.memset(kT[:, :, 0:WIN], 0.0).then_inc(cleared, 1)
            for i in range(TPB):
                dve.wait_ge(sq_done, 2 * i + 2)
                nc.vector.tensor_reduce(sumsq[:, i % 2, :], squares[:].rearrange("p k (h d) -> p (k h) d", d=64),
                                        AX, ALU.add).then_inc(sum_done, 1)
                dve.wait_ge(sum_done, i + 1)
                if i >= 2:
                    dve.wait_ge(qn_done, i - 1)
                nc.vector.tensor_scalar(rnorm[:, i % 2, :], sumsq[:, i % 2, :], 1e-24, None, ALU.max).then_inc(clamp_done, 1)
                if i >= 2:
                    dve.wait_ge(addq_done, i - 1)
                    dve.wait_ge(addk_done, i - 1)
                src = proj[:, 2 * (i % 2):2 * (i % 2) + 2, :].rearrange("p k (h d) -> p k h d", d=64)
                cos = scaled[:, 0::2, i, :].unsqueeze(2).broadcast_to([P, 2, 8, 64])
                nc.vector.tensor_tensor(cospart[:, i % 2, :, :].rearrange("p k (h d) -> p k h d", d=64), src, cos,
                                        ALU.mult).then_inc(cs_done, 1)
                for half in range(2):
                    mine, other = slice(32 * half, 32 * half + 32), slice(32 - 32 * half, 64 - 32 * half)
                    nc.vector.tensor_tensor(sinpart[:, i % 2, :, :].rearrange("p k (h d) -> p k h d", d=64)[:, :, :, mine],
                                            src[:, :, :, other],
                                            scaled[:, 1::2, i, mine].unsqueeze(2).broadcast_to([P, 2, 8, 32]),
                                            ALU.mult).then_inc(cs_done, 1)
                dve.wait_ge(cs_done, 3 * i + 3)
                if i >= 3:
                    dve.wait_ge(t_done, 2 * (i - 3) + 2)
                nc.vector.tensor_tensor(rotated[:, i % 3, 1, :], cospart[:, i % 2, 1, :], sinpart[:, i % 2, 1, :],
                                        ALU.add).then_inc(addk_done, 1)
                if i >= 1:
                    scale_k(dve, i - 1)
            scale_k(dve, TPB - 1)

        @block.gpsimd
        def _(pool):
            for i in range(TPB):
                pool.wait_ge(clamp_done, i + 1)
                nc.gpsimd.tensor_tensor(rnorm[:, i % 2, :], rnorm[:, i % 2, :], m.neghalf[:], ALU.pow).then_inc(rnorm_done, 1)
                pool.wait_ge(cs_done, 3 * i + 3)
                if i >= 3:
                    pool.wait_ge(t_done, 2 * (i - 3) + 1)
                nc.gpsimd.tensor_tensor(rotated[:, i % 3, 0, :], cospart[:, i % 2, 0, :], sinpart[:, i % 2, 0, :],
                                        ALU.add).then_inc(addq_done, 1)


def local_attention(nc, m, w, l, b, Z, qT, kT, v, qnorm, band_first):
    with Phase(nc, f"local{l}{b}") as ph:
        probs = ph.sb("probs", [P, 3, 4, SPAN])
        probsT = ph.sb("probsT", [P, 2, 4, 2 * P])
        rowmax = ph.sb("rowmax", [P, 3, 4])
        negmax = ph.sb("negmax", [P, 3, 4])
        rowsum = ph.sb("rowsum", [P, 3, 8])
        o = ph.sb("o", [P, BANK])
        oT = ph.sb("oT", [P, BANK])
        score = ph.ps("score", 4)
        turned = ph.ps("turned", 2)
        outp = ph.ps("outp", 1)
        misc = ph.ps("misc", 1)
        (s_done, chain_sem, negmax_done, exp_done, t_done, t_kept, pv_done, o_done, ot_done, ot_kept, y_done, z_done) = (
            ph.sem(x) for x in ("s_done", "chain", "negmax_done", "exp_done", "t_done", "t_kept", "pv_done", "o_done",
                                "ot_done", "ot_kept", "y_done", "z_done"))
        block = ph.block()
        N = 2 * TPB
        wo = w["wo"][:, 512 * l:512 * (l + 1)]
        HEADS = [(c, j) for c in range(2) for j in range(2)]

        def score_at(n, c, j):
            return score[:, 2 * (n % 2) + j, 256 * c:256 * c + SPAN]

        @block.tensor
        def _(pe):
            def scores(n):
                i, q4 = n // 2, n % 2
                if n >= 2:
                    pe.wait_ge(exp_done, 4 * (n - 1))
                for c in range(2):
                    for j in range(2):
                        cc = 2 * q4 + c
                        last = nc.tensor.matmul(score_at(n, c, j), qT[64 * j:64 * j + 64, cc, i * P:(i + 1) * P],
                                                kT[64 * j:64 * j + 64, cc, i * P:i * P + SPAN], start=True, stop=True)
                last.then_inc(s_done, 1)

            def turn(n):
                pe.wait_ge(exp_done, 4 * (n + 1))
                for pair in range(2):
                    e = 2 * n + pair
                    if e >= 2:
                        pe.wait_ge(t_kept, e - 1)
                    for k in range(2):
                        hh = 2 * pair + k
                        nc.tensor.transpose(turned[:, e % 2, 256 * k:256 * k + P], probs[:, n % 3, hh, 0:P], m.ident[:])
                        last = nc.tensor.transpose(turned[0:WIN, e % 2, 256 * k + P:256 * k + 2 * P],
                                                   probs[:, n % 3, hh, P:SPAN], m.ident[:])
                    last.then_inc(t_done, 1)

            def values(n):
                i, q4 = n // 2, n % 2
                pe.wait_ge(t_kept, 2 * (n + 1))
                if q4 == 0 and i > 0:
                    pe.wait_ge(o_done, i)
                for hh, (c, j) in enumerate(HEADS):
                    h = 2 * (2 * q4 + c) + j
                    to = outp[:, 0, 64 * h:64 * h + 64]
                    nc.tensor.matmul(to, probsT[:, n % 2, hh, 0:P], v[:, i, 64 * h:64 * h + 64], start=True, stop=False)
                    last = nc.tensor.matmul(to, probsT[0:WIN, n % 2, hh, P:2 * P], v[0:WIN, i + 1, 64 * h:64 * h + 64],
                                            start=False, stop=True)
                last.then_inc(pv_done, 1)

            def turn_out(i):
                pe.wait_ge(o_done, i + 1)
                if i > 0:
                    pe.wait_ge(z_done, i)
                for c in range(4):
                    last = nc.tensor.transpose(misc[:, 0, c * P:(c + 1) * P], o[:, c * P:(c + 1) * P], m.ident[:])
                last.then_inc(ot_done, 1)

            def project(i):
                pe.wait_ge(ot_kept, i + 1)
                for c in range(4):
                    last = nc.tensor.matmul(misc[:, 0, 0:P], oT[:, c * P:(c + 1) * P], wo[:, c * P:(c + 1) * P],
                                            start=(c == 0), stop=(c == 3))
                last.then_inc(y_done, 1)
            for n in range(N + 5):
                if n < N:
                    scores(n)
                if n >= 6 and n % 2 == 0:
                    project((n - 6) // 2)
                if 2 <= n < N + 2:
                    turn(n - 2)
                if n >= 5 and n % 2 == 1 and (n - 5) // 2 < TPB:
                    turn_out((n - 5) // 2)
                if 3 <= n < N + 3:
                    values(n - 3)

        @block.scalar
        def _(act):
            def keep(n):
                if n >= 2:
                    act.wait_ge(pv_done, n - 1)
                for pair in range(2):
                    e = 2 * n + pair
                    act.wait_ge(t_done, e + 1)
                    to, src = probsT[:, n % 2, 2 * pair:2 * pair + 2, :], turned[:, e % 2, :].rearrange("p (k q) -> p k q", k=2)
                    nc.scalar.activation(to[:, :, 0:P], src[:, :, 0:P], ACT.Copy)
                    nc.scalar.activation(to[0:WIN, :, P:2 * P], src[0:WIN, :, P:2 * P], ACT.Copy).then_inc(t_kept, 1)
            for n in range(N + 2):
                if n >= 2:
                    keep(n - 2)
                if n < N:
                    i, q4 = n // 2, n % 2
                    act.wait_ge(negmax_done, n + 1)
                    if n >= 3:
                        act.wait_ge(t_done, 2 * (n - 2))
                    if n >= 6:
                        act.wait_ge(o_done, i - 2)
                    for hh, (c, j) in enumerate(HEADS):
                        h = 2 * (2 * q4 + c) + j
                        nc.scalar.activation(probs[:, n % 3, hh, :], score_at(n, c, j), ACT.Exp,
                                             bias=negmax[:, n % 3, hh:hh + 1], scale=qnorm[:, i, h:h + 1],
                                             accum_out=rowsum[:, i % 3, h:h + 1]).then_inc(exp_done, 1)

        @block.vector
        def _(dve):
            chain = Chain(dve, chain_sem)

            def finish(i):
                dve.wait_ge(pv_done, 2 * (i + 1))
                if i > 0:
                    dve.wait_ge(ot_done, i)
                chain.step(nc.vector.reciprocal(rowsum[:, i % 3, :], rowsum[:, i % 3, :]))
                nc.vector.tensor_tensor(o[:].rearrange("p (h d) -> p h d", d=64),
                                        outp[:, 0, :].rearrange("p (h d) -> p h d", d=64),
                                        rowsum[:, i % 3, :].unsqueeze(2).broadcast_to([P, 8, 64]), ALU.mult).then_inc(o_done, 1)

            def keep_turned(i):
                dve.wait_ge(ot_done, i + 1)
                nc.vector.tensor_copy(oT[:], misc[:, 0, :]).then_inc(ot_kept, 1)

            def add(i):
                dve.wait_ge(y_done, i + 1)
                t = b * TPB + i
                nc.vector.tensor_tensor(Z[:, t, :], misc[:, 0, 0:P], Z[:, t, :], ALU.add).then_inc(z_done, 1)

            def maxima(n):
                i, q4 = n // 2, n % 2
                dve.wait_ge(s_done, n + 1)
                band = band_first if i == 0 else m.band
                for j in range(2):
                    sj = score[:, 2 * (n % 2) + j, :].rearrange("p (c k) -> p c k", c=2)[:, :, 0:SPAN]
                    last = nc.vector.tensor_tensor(sj, sj, band[:].unsqueeze(1).broadcast_to([P, 2, SPAN]), ALU.add)
                chain.step(last)
                for j in range(2):
                    sj = score[:, 2 * (n % 2) + j, :].rearrange("p (c k) -> p c k", c=2)[:, :, 0:SPAN]
                    last = nc.vector.tensor_reduce(rowmax[:, n % 3, j:4:2], sj, AX, ALU.max, negate=True)
                chain.step(last)
                if n >= 3:
                    dve.wait_ge(exp_done, 4 * (n - 2))
                nc.vector.tensor_tensor(negmax[:, n % 3, :], rowmax[:, n % 3, :], qnorm[:, i, 4 * q4:4 * q4 + 4],
                                        ALU.mult).then_inc(negmax_done, 1)
            for n in range(N + 5):
                if n < N:
                    maxima(n)
                if n >= 6 and n % 2 == 0:
                    add((n - 6) // 2)
                if n >= 4 and n % 2 == 0 and (n - 4) // 2 < TPB:
                    finish((n - 4) // 2)
                if n >= 5 and n % 2 == 1 and (n - 5) // 2 < TPB:
                    keep_turned((n - 5) // 2)


def gated_mlp(nc, m, w, l, Z, ZS, into):
    with Phase(nc, f"mlp{l}") as ph:
        stats = ph.sb("stats", [P, NT, 6])
        mv = ph.sb("mv", [P, NT, 2])
        rstd = ph.sb("rstd", [P, NT])
        shift = ph.sb("shift", [P, NT])
        gelu = ph.sb("gelu", [P, 2, BANK])
        hidden = ph.sb("hidden", [P, 2, 3, BANK])
        turned = ph.ps("turned", 2)
        agp = ph.ps("agp", 4)
        down = ph.ps("down", 2)
        (stat_done, aggr_done, var_done, rstd_done, shift_done, norm_done, turn_done, turn_kept, ag_done, gelu_done,
         hid_done, down_done, z_done) = (
            ph.sem(x) for x in ("stat_done", "aggr_done", "var_done", "rstd_done", "shift_done", "norm_done",
                                "turn_done", "turn_kept", "ag_done", "gelu_done", "hid_done", "down_done", "z_done"))
        block = ph.block()
        w1 = w["w1"][:, 2 * HID * l:2 * HID * (l + 1)]
        w2 = w["w2"][:, 384 * l:384 * (l + 1)]
        b1 = w["b1"][:, 6 * l:6 * (l + 1)]
        b2 = w["b2"][:, P * l:P * (l + 1)]
        ROWS = [P, P, HID - 2 * P]
        UNITS = [(tc, c) for tc in range(NT // 4) for c in range(3)]

        @block.vector
        def _(dve):
            def add(tc):
                dve.wait_ge(down_done, tc + 1)
                nc.vector.tensor_tensor(into[:, 4 * tc:4 * tc + 4, :], down[:, tc % 2, :].rearrange("p (t n) -> p t n", t=4),
                                        Z[:, 4 * tc:4 * tc + 4, :], ALU.add).then_inc(z_done, 1)

            for q in range(NT // 4 + 1):
                if q < NT // 4:
                    for t in range(4 * q, 4 * q + 4):
                        nc.vector.bn_stats(stats[:, t, :], ZS[:, t, :]).then_inc(stat_done, 1)
                    for t in range(4 * q, 4 * q + 4):
                        dve.wait_ge(stat_done, t + 1)
                        nc.vector.bn_aggr(mv[:, t, :], stats[:, t, :]).then_inc(aggr_done, 1)
                    dve.wait_ge(aggr_done, 4 * q + 4)
                    nc.vector.tensor_scalar(rstd[:, 4 * q:4 * q + 4], mv[:, 4 * q:4 * q + 4, 1], LN_EPS, None,
                                            ALU.add).then_inc(var_done, 1)
                if q >= 1:
                    four = slice(4 * q - 4, 4 * q)
                    dve.wait_ge(rstd_done, q)
                    nc.vector.scalar_tensor_tensor(out=shift[:, four], in0=mv[:, four, 0], scalar=-1.0,
                                                   in1=rstd[:, four], op0=ALU.mult, op1=ALU.mult).then_inc(shift_done, 1)
            for c in range(NT // 4):
                dve.wait_ge(turn_done, c + 1)
                nc.vector.tensor_scalar(m.HT[:, c * BANK:(c + 1) * BANK], turned[:, c % 2, :], w["lng"][:, l:l + 1],
                                        w["lnb"][:, l:l + 1], ALU.mult, ALU.add).then_inc(turn_kept, 1)
            for n, (tc, c) in enumerate(UNITS):
                r = ROWS[c]
                dve.wait_ge(gelu_done, n + 1)
                dve.wait_ge(ag_done, 2 * n + 2)
                if tc >= 2:
                    dve.wait_ge(down_done, tc - 1)
                nc.vector.scalar_tensor_tensor(out=hidden[0:r, tc % 2, c, :], in0=agp[0:r, 2 * (n % 2), :],
                                               scalar=b1[0:r, c:c + 1], in1=gelu[0:r, n % 2, :], op0=ALU.add,
                                               op1=ALU.mult).then_inc(hid_done, 1)
                if c == 1 and tc >= 1:
                    add(tc - 1)
            add(NT // 4 - 1)

        @block.gpsimd
        def _(pool):
            for q in range(NT // 4):
                pool.wait_ge(var_done, q + 1)
                nc.gpsimd.tensor_tensor(rstd[:, 4 * q:4 * q + 4], rstd[:, 4 * q:4 * q + 4], m.neghalf[:, 0:4],
                                        ALU.pow).then_inc(rstd_done, 1)

        @block.scalar
        def _(act):
            for t in range(NT):
                if t % 4 == 0:
                    act.wait_ge(shift_done, t // 4 + 1)
                nc.scalar.activation(ZS[:, t, :], ZS[:, t, :], ACT.Identity, bias=shift[:, t:t + 1],
                                     scale=rstd[:, t:t + 1]).then_inc(norm_done, 1)
            for n, (tc, c) in enumerate(UNITS):
                r = ROWS[c]
                act.wait_ge(ag_done, 2 * n + 2)
                if n >= 2:
                    act.wait_ge(hid_done, n - 1)
                nc.scalar.activation(gelu[0:r, n % 2, :], agp[0:r, 2 * (n % 2) + 1, :], ACT.Gelu,
                                     bias=b1[0:r, 3 + c:4 + c]).then_inc(gelu_done, 1)

        @block.tensor
        def _(pe):
            for c in range(NT // 4):
                pe.wait_ge(norm_done, 4 * (c + 1))
                if c >= 2:
                    pe.wait_ge(turn_kept, c - 1)
                for j in range(4):
                    last = nc.tensor.transpose(turned[:, c % 2, j * P:(j + 1) * P], ZS[:, 4 * c + j, :], m.ident[:])
                last.then_inc(turn_done, 1)

            def project(tc):
                pe.wait_ge(hid_done, 3 * (tc + 1))
                if tc >= 2:
                    pe.wait_ge(z_done, tc - 1)
                for j in range(4):
                    to = down[:, tc % 2, j * P:(j + 1) * P]
                    for c in range(3):
                        r = ROWS[c]
                        nc.tensor.matmul(to, hidden[0:r, tc % 2, c, j * P:(j + 1) * P], w2[0:r, c * P:(c + 1) * P],
                                         start=(c == 0), stop=False)
                    last = nc.tensor.matmul(to, m.ones[0:1, :], b2, start=False, stop=True)
                last.then_inc(down_done, 1)
            for n, (tc, c) in enumerate(UNITS):
                r = ROWS[c]
                if c == 0:
                    pe.wait_ge(turn_kept, tc + 1)
                if n >= 2:
                    pe.wait_ge(hid_done, n - 1)
                for k in range(2):
                    at = k * HID + c * P
                    nc.tensor.matmul(agp[0:r, 2 * (n % 2) + k, :], w1[:, at:at + r], m.HT[:, tc * BANK:(tc + 1) * BANK],
                                     start=True, stop=True).then_inc(ag_done, 1)
                if c == 0 and tc >= 1:
                    project(tc - 1)
            project(NT // 4 - 1)


def local_transformer(nc, m, dram, s):
    w = weight_views(m, s)
    with ExitStack() as keep:
        def kept(name, shape):
            return keep.enter_context(nc.sbuf_tensor(f"loc_{name}", shape, F32))
        ZS = kept("ZS", [P, NT, P])
        scaled = kept("scaled", [P, 4, TPB, 64])
        qT = kept("qT", [P, 4, SEQ])
        kT = kept("kT", [P, 4, WIN + SEQ])
        v = kept("v", [P, TPB + 1, BANK])
        qnorm = kept("qnorm", [P, TPB, 8])
        band_first = kept("band_first", [P, SPAN])
        Z = m.XN
        with Phase(nc, "locfirst") as ph:
            copied = ph.sem("copied")
            block = ph.block()

            @block.sync
            def _(sp):
                sp.wait_ge(m.wsem[s], 16)
                load_weights(sp, m, dram, s + 1)

            @block.gpsimd
            def _(pool):
                nc.gpsimd.tensor_copy(band_first[:, WIN:SPAN], m.band[:, WIN:SPAN]).then_inc(copied, 1)
                nc.gpsimd.memset(band_first[:, 0:WIN], NEG).then_inc(copied, 1)
        tables = [w[k] for k in ("cosq", "sinq", "cosk", "sink")]
        for l in range(LAYERS):
            rotary_scale_phase(nc, m, w, l, tables, scaled)
            for b in range(BATCH):
                rotary_qkv(nc, m, w, l, b, Z, scaled, qT, kT, v, qnorm)
                local_attention(nc, m, w, l, b, Z, qT, kT, v, qnorm, band_first)
            shift_tokens(nc, m, f"shift{l}", Z, ZS)
            gated_mlp(nc, m, w, l, Z, ZS, m.Y if l == 1 else Z)


DI, NS, RANK, TAPS = 256, 16, 64, 4
NCH = DI // P


def mamba_setup(nc, m, dram, s, w, U, negA, Wx3):
    G = NT // 4
    with Phase(nc, "msetup") as ph:
        stats = ph.sb("stats", [P, NT, 6])
        mv = ph.sb("mv", [P, NT, 2])
        rstd = ph.sb("rstd", [P, NT])
        shift = ph.sb("shift", [P, NT])
        (a_done, neg_done, x_done, stat_done, aggr_done, var_done, rstd_done, shift_done, norm_done,
         own_done) = (
            ph.sem(x) for x in ("a_done", "neg_done", "x_done", "stat_done", "aggr_done", "var_done",
                                "rstd_done", "shift_done", "norm_done", "own_done"))
        block = ph.block()

        @block.sync
        def _(sp):
            sp.wait_ge(m.wsem[s], 16)
            load_weights(sp, m, dram, s + 1)

        @block.gpsimd
        def _(pool):
            for q in range(G):
                pool.wait_ge(var_done, q + 1)
                nc.gpsimd.tensor_tensor(rstd[:, 4 * q:4 * q + 4], rstd[:, 4 * q:4 * q + 4], m.neghalf[:, 0:4],
                                        ALU.pow).then_inc(rstd_done, 1)

        @block.vector
        def _(dve):
            for q in range(G + 1):
                if q < G:
                    for t in range(4 * q, 4 * q + 4):
                        nc.vector.bn_stats(stats[:, t, :], m.XN[:, t, :]).then_inc(stat_done, 1)
                    for t in range(4 * q, 4 * q + 4):
                        dve.wait_ge(stat_done, t + 1)
                        nc.vector.bn_aggr(mv[:, t, :], stats[:, t, :]).then_inc(aggr_done, 1)
                    dve.wait_ge(aggr_done, 4 * q + 4)
                    nc.vector.tensor_scalar(rstd[:, 4 * q:4 * q + 4], mv[:, 4 * q:4 * q + 4, 1], LN_EPS, None,
                                            ALU.add).then_inc(var_done, 1)
                if q >= 1:
                    four = slice(4 * q - 4, 4 * q)
                    dve.wait_ge(rstd_done, q)
                    nc.vector.scalar_tensor_tensor(out=shift[:, four], in0=mv[:, four, 0], scalar=-1.0,
                                                   in1=rstd[:, four], op0=ALU.mult, op1=ALU.mult).then_inc(shift_done, 1)
                    dve.wait_ge(shift_done, q)
                    for t in (4 * q - 3, 4 * q - 1):
                        nc.vector.tensor_scalar(U[:, t, :], m.XN[:, t, :], rstd[:, t:t + 1], shift[:, t:t + 1], ALU.mult,
                                                ALU.add).then_inc(own_done, 1)
            dve.wait_ge(m.wsem[s], 16)
            for r in range(3):
                nc.vector.tensor_copy(Wx3[:, :, 2 * NS * r:2 * NS * (r + 1)],
                                      w["Wx"].rearrange("p (q n) -> p q n", n=RANK + 2 * NS)[:, :, RANK:RANK + 2 * NS]
                                      ).then_inc(x_done, 1)
            dve.wait_ge(a_done, 1)
            nc.vector.tensor_scalar(negA[:], negA[:], -1.0, None, ALU.mult).then_inc(neg_done, 1)

        @block.scalar
        def _(act):
            act.wait_ge(m.wsem[s], 16)
            nc.scalar.activation(negA[:], w["Alog"], ACT.Exp).then_inc(a_done, 1)
            for q in range(G):
                act.wait_ge(shift_done, q + 1)
                for t in (4 * q, 4 * q + 2):
                    nc.scalar.activation(U[:, t, :], m.XN[:, t, :], ACT.Identity, bias=shift[:, t:t + 1],
                                         scale=rstd[:, t:t + 1]).then_inc(norm_done, 1)


def mamba_front(nc, m, w, d, b, U, xc, sz, delta, du, BC3, Wx3, select):
    INS = [(0, 0), (1, 0), (0, 1), (1, 1), (2, 0), (2, 1), (3, 0), (3, 1)]
    CONVS = DELTAS = [(0, 0), (1, 0), (0, 1), (1, 1)]

    def part(half):
        return slice(half * BANK, (half + 1) * BANK)
    with Phase(nc, f"front{d}{b}") as ph:
        UT = ph.sb("UT", [P, SEQ])
        padded = ph.sb("padded", [P, NCH, TAPS - 1 + SEQ])
        conv = ph.sb("conv", [P, NCH, SEQ])
        dt = ph.sb("dt", [RANK, SEQ])
        bchi = ph.sb("bchi", [96, SEQ], BF16)
        bcmid = ph.sb("bcmid", [96, SEQ], BF16)
        rest = ph.sb("rest", [96, SEQ])
        soft = ph.sb("soft", [P, 4, BANK])
        ring = ph.ps("ring", 4)
        dbl = ph.ps("dbl", 4)
        (turn_done, turn_kept, padded_clear, in_done, in_kept, conv_sem, conv_done, xc_done, dbl_done, dt_kept, dl_done,
         relu_done, abs_done, exp_done, ln_done, delta_done, chain_sem) = (
            ph.sem(x) for x in ("turn_done", "turn_kept", "padded_clear", "in_done", "in_kept", "conv_sem", "conv_done",
                                "xc_done", "dbl_done", "dt_kept", "dl_done", "relu_done", "abs_done", "exp_done",
                                "ln_done", "delta_done", "chain"))
        sel_done = ph.sem("sel_done")
        block = ph.block()
        Win = w["Win"][:, 2 * DI * d:2 * DI * (d + 1)]
        bin_ = w["bin"][:, 4 * d:4 * (d + 1)]
        bdt = w["bdt"][:, 2 * d:2 * (d + 1)]

        @block.tensor
        def _(pe):
            for half in range(2):
                for j in range(4):
                    i = 4 * half + j
                    t = b * TPB + (i if d == 0 else TPB - 1 - i)
                    to = dbl[:, half, j * P:(j + 1) * P]
                    if d == 0:
                        last = nc.tensor.transpose(to, U[:, t, :], m.ident[:])
                    else:
                        last = nc.tensor.matmul(to, U[:, t, :], m.flip[:], start=True, stop=True)
                last.then_inc(turn_done, 1)
            for u, (c, half) in enumerate(INS):
                pe.wait_ge(turn_kept, half + 1)
                if u >= 4:
                    pe.wait_ge(in_kept, u - 3)
                nc.tensor.matmul(ring[:, u % 4, :], Win[:, c * P:(c + 1) * P], UT[:, part(half)], start=True,
                                 stop=True).then_inc(in_done, 1)
            for half in range(2):
                pe.wait_ge(xc_done, NCH * (half + 1))
                pe.wait_ge(turn_kept, 2)
                rhs = [xc[:, ch, part(half)] for ch in range(NCH)]
                for ch in range(NCH):
                    q = (NCH * d + ch) * (RANK + 2 * NS)
                    last = nc.tensor.matmul(dbl[0:RANK, 2 * half, :], w["Wx"][:, q:q + RANK], rhs[ch], start=(ch == 0),
                                            stop=(ch == NCH - 1))
                last.then_inc(dbl_done, 1)
                for ch in range(NCH):
                    last = nc.tensor.matmul(dbl[0:96, 2 * half + 1, :], Wx3[:, NCH * d + ch, :], rhs[ch],
                                            start=(ch == 0), stop=(ch == NCH - 1))
                last.then_inc(dbl_done, 1)
                pe.wait_ge(in_kept, 8)
                pe.wait_ge(dt_kept, half + 1)
                for ch in range(NCH):
                    nc.tensor.matmul(ring[:, 2 * ch + half, :], w["Wdt"][:, DI * d + ch * P:DI * d + (ch + 1) * P],
                                     dt[:, part(half)], start=True, stop=True).then_inc(dl_done, 1)

        @block.scalar
        def _(act):
            act.wait_ge(padded_clear, 1)
            for u, (c, half) in enumerate(INS):
                act.wait_ge(in_done, u + 1)
                if c < NCH:
                    nc.scalar.activation(padded[:, c, TAPS - 1 + half * BANK:TAPS - 1 + (half + 1) * BANK],
                                         ring[:, u % 4, :], ACT.Identity, bias=bin_[:, c:c + 1]).then_inc(in_kept, 1)
                else:
                    nc.scalar.activation(sz[:, c - NCH, part(half)], ring[:, u % 4, :], ACT.Silu,
                                         bias=bin_[:, c:c + 1]).then_inc(in_kept, 1)

            def silu(k):
                ch, half = CONVS[k]
                act.wait_ge(conv_done, k + 1)
                nc.scalar.activation(xc[:, ch, part(half)], conv[:, ch, part(half)], ACT.Silu).then_inc(xc_done, 1)

            def keep_dt(half):
                act.wait_ge(dbl_done, 2 * half + 1)
                nc.scalar.activation(dt[:, part(half)], dbl[0:RANK, 2 * half, :], ACT.Copy).then_inc(dt_kept, 1)

            def absolute(k):
                ch, half = DELTAS[k]
                act.wait_ge(dl_done, k + 1)
                nc.scalar.activation(soft[:, 2 * ch + half, :], ring[:, 2 * ch + half, :], ACT.Abs,
                                     bias=bdt[:, ch:ch + 1]).then_inc(abs_done, 1)
            for k in range(3):
                silu(k)
            keep_dt(0)
            silu(3)
            absolute(0)
            absolute(1)
            keep_dt(1)
            absolute(2)
            absolute(3)
            act.wait_ge(abs_done, 4)
            nc.scalar.activation(soft[:], soft[:], ACT.Exp, scale=-1.0).then_inc(exp_done, 1)
            act.wait_ge(exp_done, 1)
            for ch in range(NCH):
                nc.scalar.activation(soft[:, 2 * ch:2 * ch + 2, :], soft[:, 2 * ch:2 * ch + 2, :], ACT.Ln,
                                     bias=1.0).then_inc(ln_done, 1)

        if (d, b) == (0, 0):
            @block.gpsimd
            def _(pool):
                nc.gpsimd.memset(select[:], 0.0).then_inc(sel_done, 1)
                for r in range(3):
                    pool.wait_ge(sel_done, r + 1)
                    nc.gpsimd.affine_select(out=select[:], in_=select[:], compare_op=ALU.not_equal, fill=1.0,
                                            base=-32 * r, pattern=[[-1, 2 * NS], [0, P]],
                                            channel_multiplier=1).then_inc(sel_done, 1)

        @block.vector
        def _(dve):
            chain = Chain(dve, chain_sem)
            nc.vector.memset(padded[:, :, 0:TAPS - 1], 0.0).then_inc(padded_clear, 1)
            for half in range(2):
                dve.wait_ge(turn_done, half + 1)
                nc.vector.tensor_scalar(UT[:, half * BANK:(half + 1) * BANK], dbl[:, half, :], w["lnw"][:, d:d + 1],
                                        w["lnb"][:, d:d + 1], ALU.mult, ALU.add).then_inc(turn_kept, 1)
            for k, (ch, half) in enumerate(CONVS):
                dve.wait_ge(in_kept, k + 1)
                taps = w["convw"][:, (NCH * d + ch) * TAPS:(NCH * d + ch + 1) * TAPS]
                cb = w["convb"][:, NCH * d + ch:NCH * d + ch + 1]
                to = conv[:, ch, part(half)]
                tap = [padded[:, ch, half * BANK + j:(half + 1) * BANK + j] for j in range(TAPS)]
                chain.step(nc.vector.tensor_scalar(to, tap[0], taps[:, 0:1], cb, ALU.mult, ALU.add))
                for j in range(1, TAPS):
                    chain.step(nc.vector.scalar_tensor_tensor(out=to, in0=tap[j], scalar=taps[:, j:j + 1], in1=to,
                                                              op0=ALU.mult, op1=ALU.add))
                dve.sem_inc(conv_done, 1)
            for half in range(2):
                dve.wait_ge(dbl_done, 2 * half + 2)
                src = dbl[0:96, 2 * half + 1, :]
                at = part(half)
                chain.step(nc.vector.tensor_copy(bchi[:, at], src))
                chain.step(nc.vector.tensor_tensor(rest[:, at], src, bchi[:, at], ALU.subtract))
                chain.step(nc.vector.tensor_copy(bcmid[:, at], rest[:, at]))
                chain.step(nc.vector.tensor_tensor(rest[:, at], rest[:, at], bcmid[:, at], ALU.subtract))
                nc.vector.tensor_copy(BC3[0:32, at], bchi[0:32, at])
                nc.vector.tensor_copy(BC3[32:64, at], bcmid[32:64, at])
                chain.step(nc.vector.tensor_copy(BC3[64:96, at], rest[64:96, at]))
                for k in range(NCH * half, NCH * half + NCH):
                    ch = DELTAS[k][0]
                    dve.wait_ge(dl_done, k + 1)
                    dve.wait_ge(abs_done, k + 1)
                    nc.vector.tensor_scalar(delta[:, ch, at], ring[:, 2 * ch + half, :], bdt[:, ch:ch + 1], 0.0,
                                            ALU.add, ALU.max).then_inc(relu_done, 1)
            dve.wait_ge(relu_done, 4)
            for ch in range(NCH):
                dve.wait_ge(ln_done, ch + 1)
                chain.step(nc.vector.tensor_tensor(delta[:, ch, :], delta[:, ch, :],
                                                   soft[:, 2 * ch:2 * ch + 2, :].rearrange("p u t -> p (u t)"), ALU.add))
                chain.step(nc.vector.tensor_tensor(du[:, ch, :], delta[:, ch, :], xc[:, ch, :], ALU.mult))


def mamba_scan(nc, m, w, d, b, xc, sz, delta, du, BC3, select, negA, outT):
    LAST = NCH * NS - 1
    STATES, DECAYS = 6, 3
    with Phase(nc, f"scan{d}{b}") as ph:
        decay = ph.sb("decay", [P, DECAYS, SEQ])
        state = ph.sb("state", [P, STATES, SEQ])
        crow = ph.sb("crow", [P, 2, SEQ])
        back = decay[:, 0, :].rearrange("p (t n) -> p t n", t=TPB)
        bspread = ph.ps("bspread", 2)
        cspread = ph.ps("cspread", 2)
        yacc = ph.ps("yacc", 4)
        (b_done, c_done, c_kept, dec_done, in_done, scan_done, hc_done, y_used, y_done, hc_last, gate_sem, gated, out_done, back_kept,
         flip_done, fin) = (
            ph.sem(x) for x in ("b_done", "c_done", "c_kept", "dec_done", "in_done", "scan_done", "hc_done", "y_used", "y_done",
                                "hc_last", "gate_sem", "gated", "out_done", "back_kept", "flip_done", "fin"))
        block = ph.block()
        Wout = w["Wout"][:, NCH * P * d:NCH * P * (d + 1)]

        @block.tensor
        def _(pe):
            def spread(n):
                for to, q, done in ((bspread, n, b_done), (cspread, NS + n, c_done)):
                    if n >= 1:
                        if done is b_done:
                            pe.wait_ge(in_done, 2 * n)
                        else:
                            pe.wait_ge(c_kept, n)
                    for half in range(2):
                        last = nc.tensor.matmul(to[:, half, :], select[:, q, :], BC3[:, half * BANK:(half + 1) * BANK],
                                                start=True, stop=True)
                    last.then_inc(done, 1)

            def accumulate(n):
                for ch in range(NCH):
                    k = NCH * n + ch
                    if k == LAST:
                        pe.wait_ge(hc_last, 1)
                        pe.wait_ge(hc_done, LAST)
                    else:
                        pe.wait_ge(hc_done, k + 1)
                    for half in range(2):
                        last = nc.tensor.matmul(yacc[:, 2 * ch + half, :], m.ident[:],
                                                state[:, k % STATES, half * BANK:(half + 1) * BANK], start=(n == 0),
                                                stop=(n == NS - 1))
                    last.then_inc(y_used, 1)
            for n in range(NS):
                spread(n)
                if n >= 2:
                    accumulate(n - 2)
            accumulate(NS - 2)
            accumulate(NS - 1)
            if d == 0:
                for half in range(2):
                    pe.wait_ge(gated, NCH * (half + 1))
                    for ch in range(NCH):
                        last = nc.tensor.matmul(bspread[:, half, :], Wout[:, ch * P:(ch + 1) * P],
                                                du[:, ch, half * BANK:(half + 1) * BANK], start=(ch == 0),
                                                stop=(ch == NCH - 1))
                    last.then_inc(flip_done, 1)
            else:
                for half in range(2):
                    pe.wait_ge(gated, NCH * (half + 1))
                    for j in range(4):
                        i = 4 * half + j
                        for ch in range(NCH):
                            last = nc.tensor.matmul(cspread[:, half, j * P:(j + 1) * P], du[:, ch, i * P:(i + 1) * P],
                                                    Wout[:, ch * P:(ch + 1) * P], start=(ch == 0), stop=(ch == NCH - 1))
                    last.then_inc(out_done, 1)
                pe.wait_ge(back_kept, 2)
                for half in range(2):
                    for j in range(4):
                        i = TPB - 1 - (4 * half + j)
                        last = nc.tensor.matmul(bspread[:, half, j * P:(j + 1) * P], back[:, i, :], m.flip[:],
                                                start=True, stop=True)
                    last.then_inc(flip_done, 1)

        @block.scalar
        def _(act):
            for k in range(NCH * NS):
                n, ch = k // NCH, k % NCH
                if k >= DECAYS:
                    act.wait_ge(scan_done, k - DECAYS + 1)
                a = (NCH * d + ch) * NS + n
                nc.scalar.activation(decay[:, k % DECAYS, :], delta[:, ch, :], ACT.Exp,
                                     scale=negA[:, a:a + 1]).then_inc(dec_done, 1)
                if ch == 0:
                    act.wait_ge(c_done, n + 1)
                    if n >= 2:
                        act.wait_ge(hc_done, 2 * (n - 1))
                    nc.scalar.activation(crow[:, n % 2, :], cspread[:].rearrange("p a t -> p (a t)"),
                                         ACT.Copy).then_inc(c_kept, 1)

        @block.gpsimd
        def _(pool):
            for k in range(LAST):
                n = k // NCH
                pool.wait_ge(scan_done, k + 1)
                pool.wait_ge(c_kept, n + 1)
                nc.gpsimd.tensor_tensor(state[:, k % STATES, :], crow[:, n % 2, :], state[:, k % STATES, :],
                                        ALU.mult).then_inc(hc_done, 1)

        @block.vector
        def _(dve):
            for n in range(NS):
                for ch in range(NCH):
                    k = NCH * n + ch
                    if k >= STATES:
                        dve.wait_ge(y_used, k - STATES + 1)
                    dve.wait_ge(b_done, n + 1)
                    nc.vector.tensor_tensor(state[:, k % STATES, :], bspread[:].rearrange("p a t -> p (a t)"), du[:, ch, :],
                                            ALU.mult).then_inc(in_done, 1)
                for ch in range(NCH):
                    k = NCH * n + ch
                    dve.wait_ge(in_done, k + 1)
                    dve.wait_ge(dec_done, k + 1)
                    nc.vector.tensor_tensor_scan(state[:, k % STATES, :], decay[:, k % DECAYS, :],
                                                 state[:, k % STATES, :], 0.0, ALU.mult, ALU.add).then_inc(scan_done, 1)
            dve.wait_ge(scan_done, NCH * NS)
            dve.wait_ge(c_kept, NS)
            nc.vector.tensor_tensor(state[:, LAST % STATES, :], crow[:, (NS - 1) % 2, :], state[:, LAST % STATES, :],
                                    ALU.mult).then_inc(hc_last, 1)
            dve.wait_ge(y_used, NCH * NS)
            for half in range(2):
                at = slice(half * BANK, (half + 1) * BANK)
                for ch in range(NCH):
                    nc.vector.scalar_tensor_tensor(out=du[:, ch, at], in0=xc[:, ch, at],
                                                   scalar=w["D"][:, NCH * d + ch:NCH * d + ch + 1],
                                                   in1=yacc[:, 2 * ch + half, :], op0=ALU.mult,
                                                   op1=ALU.add).then_inc(gate_sem, 1)
                for ch in range(NCH):
                    dve.wait_ge(gate_sem, NCH * half + ch + 1)
                    nc.vector.tensor_tensor(du[:, ch, at], du[:, ch, at], sz[:, ch, at], ALU.mult).then_inc(gated, 1)
            if d == 1:
                for half in range(2):
                    dve.wait_ge(out_done, half + 1)
                    nc.vector.tensor_copy(back[:, 4 * half:4 * half + 4, :].rearrange("p t n -> p (t n)"),
                                          cspread[:, half, :]).then_inc(back_kept, 1)
            for half in range(2):
                dve.wait_ge(flip_done, half + 1)
                at = b * SEQ + half * BANK
                nc.vector.scalar_tensor_tensor(out=outT[:, d, at:at + BANK], in0=bspread[:, half, :],
                                               scalar=w["bout"][:, d:d + 1], in1=m.HT[:, at:at + BANK], op0=ALU.add,
                                               op1=ALU.add).then_inc(fin, 1)


def mamba_gate(nc, m, w, outT):
    with Phase(nc, "mgate") as ph:
        total = ph.sb("total", [P, 2, BANK])
        gate = ph.sb("gate", [P, 2, BANK])
        mixed = ph.sb("mixed", [P, 2, BANK])
        gv = ph.ps("gv", 4)
        turned = ph.ps("turned", 2)
        chain_sem, gv_done, gate_done, mixed_done, turn_done, y_done = (
            ph.sem(x) for x in ("chain", "gv_done", "gate_done", "mixed_done", "turn_done", "y_done"))
        block = ph.block()
        CH = NT // 4

        def keep(act, c):
            act.wait_ge(turn_done, c + 1)
            nc.scalar.activation(m.Y[:, 4 * c:4 * c + 4, :].rearrange("p t n -> p (t n)"), turned[:, c % 2, :],
                                 ACT.Copy).then_inc(y_done, 1)

        @block.tensor
        def _(pe):
            def turn(c):
                pe.wait_ge(mixed_done, c + 1)
                if c >= 2:
                    pe.wait_ge(y_done, c - 1)
                for j in range(4):
                    last = nc.tensor.transpose(turned[:, c % 2, j * P:(j + 1) * P], mixed[:, c % 2, j * P:(j + 1) * P],
                                               m.ident[:])
                last.then_inc(turn_done, 1)
            for c in range(CH):
                if c >= 2:
                    pe.wait_ge(mixed_done, c - 1)
                for k, wt in enumerate((w["Wg"], w["Wv"])):
                    for d in range(2):
                        last = nc.tensor.matmul(gv[:, 2 * (c % 2) + k, :], wt[:, d * P:(d + 1) * P],
                                                outT[:, d, c * BANK:(c + 1) * BANK], start=(d == 0), stop=(d == 1))
                    last.then_inc(gv_done, 1)
                if c >= 1:
                    turn(c - 1)
            turn(CH - 1)

        @block.scalar
        def _(act):
            for c in range(CH):
                act.wait_ge(gv_done, 2 * c + 1)
                if c >= 2:
                    act.wait_ge(mixed_done, c - 1)
                nc.scalar.activation(gate[:, c % 2, :], gv[:, 2 * (c % 2), :], ACT.Sigmoid,
                                     bias=w["bg"][:, 0:1]).then_inc(gate_done, 1)
                if c >= 1:
                    keep(act, c - 1)
            keep(act, CH - 1)

        @block.vector
        def _(dve):
            chain = Chain(dve, chain_sem)
            for c in range(CH):
                tot, mix = total[:, c % 2, :], mixed[:, c % 2, :]
                chain.step(nc.vector.tensor_tensor(tot, outT[:, 0, c * BANK:(c + 1) * BANK],
                                                   outT[:, 1, c * BANK:(c + 1) * BANK], ALU.add))
                dve.wait_ge(gv_done, 2 * c + 2)
                if c >= 2:
                    dve.wait_ge(turn_done, c - 1)
                chain.step(nc.vector.scalar_tensor_tensor(out=mix, in0=gv[:, 2 * (c % 2) + 1, :], scalar=w["bv"][:, 0:1],
                                                          in1=tot, op0=ALU.add, op1=ALU.subtract))
                dve.wait_ge(gate_done, c + 1)
                chain.step(nc.vector.tensor_tensor(mix, mix, gate[:, c % 2, :], ALU.mult))
                chain.step(nc.vector.tensor_tensor(mix, mix, tot, ALU.add))
                nc.vector.tensor_scalar(mix, mix, 0.5, None, ALU.mult).then_inc(mixed_done, 1)


def bidirectional_mamba(nc, m, dram, s):
    w = weight_views(m, s)
    with ExitStack() as keep:
        def kept(name, shape, dt=F32):
            return keep.enter_context(nc.sbuf_tensor(f"mamba_{name}", shape, dt))
        xc = kept("xc", [P, NCH, SEQ])
        sz = kept("sz", [P, NCH, SEQ])
        delta = kept("delta", [P, NCH, SEQ])
        du = kept("du", [P, NCH, SEQ])
        BC3 = kept("BC3", [96, SEQ], BF16)
        select = kept("select", [96, 2 * NS, P], BF16)
        negA = kept("negA", [P, 2 * NCH * NS])
        Wx3 = kept("Wx3", [P, 2 * NCH, 96])
        outT = kept("outT", [P, 2, TOKENS])
        mamba_setup(nc, m, dram, s, w, m.Y, negA, Wx3)
        for d in range(2):
            for b in range(BATCH):
                mamba_front(nc, m, w, d, b, m.Y, xc, sz, delta, du, BC3, Wx3, select)
                mamba_scan(nc, m, w, d, b, xc, sz, delta, du, BC3, select, negA, outT)
        mamba_gate(nc, m, w, outT)


def grouped_experts(nc, m, dram, s):
    w = weight_views(m, s)
    E, G, PERG, CH = 32, 8, 4, 16
    UNITS = [(tc, c) for tc in range(NT // 4) for c in range(CH + 1)]
    with Phase(nc, "grouped") as ph:
        scores = ph.sb("scores", [P, NT, E])
        biased = ph.sb("biased", [P, NT, E])
        biasB = ph.sb("biasB", [P, E])
        hi1, lo1, hi2, lo2, first, second = (ph.sb(f"pair{k}", [P, NT, G]) for k in range(6))
        group = ph.sb("group", [P, NT, G])
        top = ph.sb("top", [P, NT, 8])
        where = ph.sb("where", [P, NT, 8], U32)
        wheref = ph.sb("wheref", [P, NT, 4])
        same = ph.sb("same", [P, NT, G, 4])
        gmask = ph.sb("gmask", [P, NT, G])
        replaced = ph.sb("replaced", [P, NT, E])
        stat = ph.sb("stat", [P, NT])
        parts = ph.sb("parts", [P, NT, 3, E], BF16)
        partsT = ph.sb("partsT", [96, TOKENS], BF16)
        select = ph.sb("select", [96, CH, P], BF16)
        silu = ph.sb("silu", [P, 2, BANK])
        wide_ones = ph.sb("wide_ones", [1, BANK])
        gated = ph.sb("gated", [P, 2, BANK])
        hidden = ph.sb("hidden", [P, 3, BANK])
        gate_up = ph.ps("gate_up", 4)
        spread = ph.ps("spread", 2)
        down = ph.ps("down", 1)
        turned = ph.ctx.enter_context(nc.psum_tensor("grouped_turned", [P, 1, 1024], BF16))
        (router_done, bias_done, chain_sem, sig_done, parts_done, turn_done, turn_kept, gu_done, silu_done, gated_done,
         hid_done, spread_done, down_done, y_done, sel_done) = (
            ph.sem(x) for x in ("router_done", "bias_done", "chain", "sig_done", "parts_done", "turn_done", "turn_kept",
                                "gu_done", "silu_done", "gated_done", "hid_done", "spread_done", "down_done", "y_done",
                                "sel_done"))
        block = ph.block()
        shared_w = (w["sg"], w["su"], w["sd"])

        @block.gpsimd
        def _(pool):
            nc.gpsimd.memset(wide_ones[:], 1.0).then_inc(sel_done, 1)
            nc.gpsimd.memset(select[:], 0.0).then_inc(sel_done, 1)
            for r in range(3):
                pool.wait_ge(sel_done, r + 2)
                nc.gpsimd.affine_select(out=select[:].rearrange("k c (j i) -> k c j i", j=2),
                                        in_=select[:].rearrange("k c (j i) -> k c j i", j=2),
                                        compare_op=ALU.not_equal, fill=1.0, base=-E * r,
                                        pattern=[[-2, CH], [-1, 2], [0, 64]], channel_multiplier=1).then_inc(sel_done, 1)

        @block.tensor
        def _(pe):
            pe.wait_ge(m.wsem[s], 16)
            nc.tensor.matmul(down[:, 0, 0:E], m.ones[0:1, :], w["bias"], start=True, stop=True).then_inc(bias_done, 1)
            for g in range(NT):
                last = nc.tensor.matmul(spread[:, 0, E * g:E * (g + 1)], m.HT[:, g * P:(g + 1) * P], w["gate"],
                                        start=True, stop=True)
            last.then_inc(router_done, 1)

            def gate_and_up(n):
                tc, c = UNITS[n]
                if n >= 2:
                    pe.wait_ge(gated_done, n - 1)
                for k in range(2):
                    wt = shared_w[k] if c == CH else w[("wg", "wu")[k]][:, c * P:(c + 1) * P]
                    nc.tensor.matmul(gate_up[:, 2 * (n % 2) + k, :], wt, m.HT[:, tc * BANK:(tc + 1) * BANK],
                                     start=True, stop=True).then_inc(gu_done, 1)
            gate_and_up(0)
            gate_and_up(1)
            pe.wait_ge(parts_done, 1)
            for half in range(2):
                if half:
                    pe.wait_ge(turn_kept, 1)
                for j in range(8):
                    g = 8 * half + j
                    last = nc.tensor.transpose(turned[0:96, 0, j * P:(j + 1) * P],
                                               parts[:, g, :, :].rearrange("p r e -> p (r e)"), m.identb[:])
                last.then_inc(turn_done, 1)
            pe.wait_ge(turn_kept, 2)
            pe.wait_ge(sel_done, 5)
            for n in range(len(UNITS) + 1):
                if n < len(UNITS):
                    tc, c = UNITS[n]
                    if n >= 2:
                        gate_and_up(n)
                        pe.wait_ge(hid_done, n - 1)
                    if c < CH:
                        nc.tensor.matmul(spread[:, n % 2, :], select[:, c, :], partsT[:, tc * BANK:(tc + 1) * BANK],
                                         start=True, stop=True).then_inc(spread_done, 1)
                    else:
                        nc.tensor.matmul(spread[:, n % 2, :], m.ones[0:1, :], wide_ones[0:1, :], start=True,
                                         stop=True).then_inc(spread_done, 1)
                if n >= 1:
                    tc, c = UNITS[n - 1]
                    pe.wait_ge(hid_done, n)
                    if c == 0 and tc > 0:
                        pe.wait_ge(y_done, tc)
                    for j in range(4):
                        wt = shared_w[2] if c == CH else w["wd"][:, c * P:(c + 1) * P]
                        last = nc.tensor.matmul(down[:, 0, j * P:(j + 1) * P], hidden[:, (n - 1) % 3, j * P:(j + 1) * P],
                                                wt, start=(c == 0 and j == 0), stop=(c == CH), skip_group_check=True)
                    last.then_inc(down_done, 1)

        @block.scalar
        def _(act):
            act.wait_ge(router_done, 1)
            nc.scalar.activation(scores[:].rearrange("p t e -> p (t e)"), spread[:, 0, :], ACT.Sigmoid).then_inc(sig_done, 1)
            for half in range(2):
                act.wait_ge(turn_done, half + 1)
                nc.scalar.activation(partsT[:, half * 1024:(half + 1) * 1024], turned[0:96, 0, :],
                                     ACT.Copy).then_inc(turn_kept, 1)
            for n in range(len(UNITS)):
                act.wait_ge(gu_done, 2 * n + 1)
                if n >= 2:
                    act.wait_ge(gated_done, n - 1)
                nc.scalar.activation(silu[:, n % 2, :], gate_up[:, 2 * (n % 2), :], ACT.Silu).then_inc(silu_done, 1)

        @block.vector
        def _(dve):
            chain = Chain(dve, chain_sem)

            def tt(out, a, b, op):
                chain.step(nc.vector.tensor_tensor(out, a, b, op))
            dve.wait_ge(bias_done, 1)
            chain.step(nc.vector.tensor_copy(biasB[:], down[:, 0, 0:E]))
            dve.wait_ge(sig_done, 1)
            tt(biased[:], scores[:], biasB[:].unsqueeze(1).broadcast_to([P, NT, E]), ALU.add)
            a, b, c, d = (biased[:].rearrange("p t (g k) -> p t g k", k=PERG)[:, :, :, k] for k in range(PERG))
            tt(hi1[:], a, b, ALU.max)
            tt(lo1[:], a, b, ALU.min)
            tt(hi2[:], c, d, ALU.max)
            tt(lo2[:], c, d, ALU.min)
            tt(first[:], hi1[:], hi2[:], ALU.max)
            tt(second[:], hi1[:], hi2[:], ALU.min)
            tt(lo1[:], lo1[:], lo2[:], ALU.max)
            tt(second[:], second[:], lo1[:], ALU.max)
            tt(group[:], first[:], second[:], ALU.add)
            for g in range(NT):
                last = nc.vector.max(out=top[:, g, :], in_=group[:, g, :])
            chain.step(last)
            for g in range(NT):
                last = nc.vector.max_index(where[:, g, :], top[:, g, :], group[:, g, :])
            chain.step(last)
            chain.step(nc.vector.tensor_copy(wheref[:], where[:, :, 0:4]))
            for k in range(4):
                tt(same[:, :, :, k], m.iota8[:].unsqueeze(1).broadcast_to([P, NT, G]),
                   wheref[:, :, k:k + 1].broadcast_to([P, NT, G]), ALU.is_equal)
            chain.step(nc.vector.tensor_reduce(gmask[:], same[:], AX, ALU.add))
            for k in range(PERG):
                bk = biased[:].rearrange("p t (g k) -> p t g k", k=PERG)[:, :, :, k]
                tt(bk, bk, gmask[:], ALU.mult)
            for g in range(NT):
                last = nc.vector.max(out=top[:, g, :], in_=biased[:, g, :])
            chain.step(last)
            for g in range(NT):
                last = nc.vector.match_replace(out=replaced[:, g, :], in_to_replace=top[:, g, :],
                                               in_values=biased[:, g, :], imm_value=-3.0e38)
            chain.step(last)
            tt(replaced[:], replaced[:], biased[:], ALU.not_equal)
            tt(scores[:], scores[:], replaced[:], ALU.mult)
            chain.step(nc.vector.tensor_reduce(stat[:], scores[:], AX, ALU.add))
            chain.step(nc.vector.tensor_scalar(stat[:], stat[:], 1e-20, None, ALU.add))
            chain.step(nc.vector.reciprocal(stat[:], stat[:]))
            chain.step(nc.vector.tensor_scalar(stat[:], stat[:], 2.5, None, ALU.mult))
            tt(scores[:], scores[:], stat[:].unsqueeze(2).broadcast_to([P, NT, E]), ALU.mult)
            split3(nc, chain, scores[:], parts[:, :, 0, :], parts[:, :, 1, :], parts[:, :, 2, :], replaced[:])
            dve.sem_inc(parts_done, 1)
            for n in range(len(UNITS) + 1):
                if n < len(UNITS):
                    dve.wait_ge(silu_done, n + 1)
                    dve.wait_ge(gu_done, 2 * n + 2)
                    nc.vector.tensor_tensor(gated[:, n % 2, :], gate_up[:, 2 * (n % 2) + 1, :], silu[:, n % 2, :],
                                            ALU.mult).then_inc(gated_done, 1)
                    dve.wait_ge(gated_done, n + 1)
                    dve.wait_ge(spread_done, n + 1)
                    if n >= 3:
                        dve.wait_ge(down_done, n - 2)
                    nc.vector.tensor_tensor(hidden[:, n % 3, :], spread[:, n % 2, :], gated[:, n % 2, :],
                                            ALU.mult).then_inc(hid_done, 1)
                if n >= 1 and UNITS[n - 1][1] == CH:
                    tc = UNITS[n - 1][0]
                    dve.wait_ge(down_done, n)
                    nc.vector.tensor_copy(m.Y[:, 4 * tc:4 * tc + 4, :].rearrange("p t n -> p (t n)"),
                                          down[:, 0, :]).then_inc(y_done, 1)


S0, S1 = 0, 8
PHASES = [linear_attention_phase, attention_and_top2, causal_single_head, swiglu_experts, causal_sixteen_heads, local_transformer, bidirectional_mamba, grouped_experts]



def program(nc, dram, out):
    with ExitStack() as ctx:
        m = Memory(nc, ctx)
        constants_phase(nc, m, dram)
        phases = PHASES
        with Phase(nc, "first") as ph:
            block = ph.block()

            @block.sync
            def _(sp):
                load_weights(sp, m, dram, S0)
        for s in range(S0, S1):
            norm_phase(nc, m, f"norm{s}", add=s > S0, norm=True)
            phases[s](nc, m, dram, s)
        norm_phase(nc, m, "last", add=True, norm=False, out=out)


def rotary_tables():
    half = np.arange(0, 64, 2, dtype=np.float32)
    inv = (1.0 / 10000.0 ** (half / 64)).astype(np.float32)
    t = np.arange(SEQ, dtype=np.float32)
    freqs = t[:, None] * inv[None, :]
    freqs = np.concatenate([freqs, freqs], -1)
    base = (half + 0.4 * 64) / (1.4 * 64)
    power = (t - SEQ // 2) / 32.0
    scale = (base[None, :] ** power[:, None]).astype(np.float32)
    scale = np.concatenate([scale, scale], -1)
    sign = np.concatenate([-np.ones(32, np.float32), np.ones(32, np.float32)])
    cos, sin = np.cos(freqs), np.sin(freqs) * sign
    fold = lambda a: np.ascontiguousarray(
        a.astype(np.float32).reshape(TPB, P, 64).transpose(1, 0, 2).reshape(P, TPB * 64))
    return fold(cos * scale), fold(sin * scale), fold(cos / scale), fold(sin / scale)


def packed(s, parts):
    out = np.zeros((P, WIDTHS[s]), np.float32)
    at = 0
    for name, rows, n in PACKS[s]:
        a = parts[name]
        out[0:a.shape[0], at:at + a.shape[1]] = a
        at += n
    return out


def row(a):
    return a.reshape(1, -1)


def cols(a):
    return a.reshape(-1, P).T


def chunks(a):
    return a.reshape(-1, P, a.shape[-1]).transpose(1, 0, 2).reshape(P, -1)


def layouts(i):
    flat = lambda a: a.transpose(1, 0, 2).reshape(a.shape[1], -1)
    w1 = i["L2_ffn_w1"]
    b1 = np.zeros((2, 6, P), np.float32)
    b1.reshape(2, 2, 3 * P)[:, :, 0:HID] = i["L2_ffn_b1"].reshape(2, 2, HID)
    w2 = np.zeros((2, 3 * P, P), np.float32)
    w2[:, 0:HID] = i["L2_ffn_w2"]
    cosq, sinq, cosk, sink = rotary_tables()
    return [
        {"Wq": i["L0_attn_Wq"], "Wk": i["L0_attn_Wk"], "Wv": i["L0_attn_Wv"], "Wo": chunks(i["L0_attn_Wo"]),
         "bo": row(i["L0_attn_bo"])},
        {"Wqkv": i["L0_ffn_W_qkv"], "bqkv": row(i["L0_ffn_b_qkv"]), "Wgate": i["L0_ffn_W_gate"],
         "bgate": row(i["L0_ffn_b_gate"]), "Wexp": flat(i["L0_ffn_W_experts"]), "bexp": i["L0_ffn_b_experts"]},
        {"Wq": i["L1_attn_Wq"], "Wk": i["L1_attn_Wk"], "Wv": i["L1_attn_Wv"]},
        {"gate": i["L1_ffn_gate_w"].T, "wg": i["L1_ffn_wg"].reshape(4096, P).T,
         "wu": i["L1_ffn_wu"].reshape(4096, P).T,
         "wd": i["L1_ffn_wd"].reshape(8, P, 4, P).transpose(3, 0, 2, 1).reshape(P, 4096)},
        {"Wq": i["L2_attn_W_Q"].reshape(1024, P).T, "Wk": i["L2_attn_W_K"].reshape(1024, P).T,
         "Wv": i["L2_attn_W_V"].reshape(1024, P).T, "Wo": chunks(i["L2_attn_W_O"].T)},
        {"wqkv": flat(i["L2_ffn_wqkv"]),
         "wo": i["L2_ffn_wo"].reshape(2, 4, P, P).transpose(2, 0, 1, 3).reshape(P, -1),
         "w1": flat(w1), "w2": w2.reshape(2, 3, P, P).transpose(2, 0, 1, 3).reshape(P, -1),
         "b1": cols(b1), "b2": row(i["L2_ffn_b2"]), "lng": cols(i["L2_ffn_ln_g"]), "lnb": cols(i["L2_ffn_ln_b"]),
         "qscale": row(i["L2_ffn_q_scale"]), "kscale": row(i["L2_ffn_k_scale"]),
         "cosq": cosq, "sinq": sinq, "cosk": cosk, "sink": sink},
        {"lnw": cols(i["L3_attn_ln_w"]), "lnb": cols(i["L3_attn_ln_b"]), "Win": flat(i["L3_attn_W_in"]),
         "bin": cols(i["L3_attn_b_in"]),
         "convw": i["L3_attn_conv_w"].reshape(2, 2, P, 4).transpose(2, 0, 1, 3).reshape(P, 16),
         "convb": cols(i["L3_attn_conv_b"]),
         "Wx": i["L3_attn_W_xproj"].reshape(2, 2, P, 96).transpose(2, 0, 1, 3).reshape(P, -1),
         "Wdt": flat(i["L3_attn_W_dt"]), "bdt": cols(i["L3_attn_b_dt"]),
         "Alog": i["L3_attn_A_log"].reshape(2, 2, P, 16).transpose(2, 0, 1, 3).reshape(P, -1),
         "D": cols(i["L3_attn_D"]),
         "Wout": i["L3_attn_W_out"].reshape(2, 2, P, P).transpose(2, 0, 1, 3).reshape(P, -1),
         "bout": cols(i["L3_attn_b_out"]), "Wg": chunks(i["L3_attn_Wg"]), "bg": cols(i["L3_attn_bg"]),
         "Wv": chunks(i["L3_attn_Wv"]), "bv": cols(i["L3_attn_bv"])},
        {"gate": i["L3_ffn_gate_w"].T, "bias": row(i["L3_ffn_gate_bias"]),
         "wg": i["L3_ffn_w_gate"].reshape(2048, P).T, "wu": i["L3_ffn_w_up"].reshape(2048, P).T,
         "wd": i["L3_ffn_w_down"].reshape(16, 2, P, 64).transpose(1, 3, 0, 2).reshape(P, 2048),
         "sg": i["L3_ffn_sh_gate"].T, "su": i["L3_ffn_sh_up"].T, "sd": i["L3_ffn_sh_down"].T},
    ]


_OUTS = [((BATCH, SEQ, P), "float32")]


def kernel(**inputs):
    import concourse.bacc as _bacc
    from concourse.bass_utils import run_bass_kernel_spmd as _run

    nc = _bacc.Bacc("TRN2", target_bir_lowering=False, num_devices=1)
    host = {k: np.asarray(v) for k, v in inputs.items()}
    feeds = {"x": np.ascontiguousarray(host["L0_attn_x"])}
    for s, parts in enumerate(layouts(host)):
        feeds[f"w{s}"] = packed(s, parts)
    dram = {k: nc.dram_tensor(f"in_{k}_dram", a.shape, mybir.dt.from_np(a.dtype), kind="ExternalInput").ap()
            for k, a in feeds.items()}
    outs = [nc.dram_tensor(f"out_{i}_dram", shape, mybir.dt.from_np(np.dtype(dtype)), kind="ExternalOutput").ap()
            for i, (shape, dtype) in enumerate(_OUTS)]
    program(nc, dram, outs[0])
    r = _run(nc, [{f"in_{k}_dram": a for k, a in feeds.items()}], core_ids=[0])
    return r.results[0]["out_0_dram"]
```
